# Optimizing a Trainium2 kernel written in Bass

```python
import numpy as np
import jax
import jax.numpy as jnp

def _softmax(x, axis=-1):
    return jax.nn.softmax(x, axis=axis)

def _gelu(x):
    return jax.nn.gelu(x, approximate=True)

def _silu(x):
    return jax.nn.silu(x)

def _sigmoid(x):
    return jax.nn.sigmoid(x)

def _layernorm(x, axis=-1, eps=1e-05):
    m = jnp.mean(x, axis=axis, keepdims=True)
    v = jnp.var(x, axis=axis, keepdims=True)
    return (x - m) / jnp.sqrt(v + eps)

def _scatter_add(tgt, idx, src, axis=0):
    return tgt.at[idx].add(src)

def _segment_sum(src, seg, n):
    return jax.ops.segment_sum(src, seg, n)
kernel_name = 'mk_gnn_ffn_d4_gnn_r32_f2af26'

def setup_inputs(seed: int=0):
    np.random.seed(seed)
    _w = jnp.asarray

    def _rec_inputs():
        import jax
        import jax.numpy as jnp
        _gk = jax.random.key(seed)
        x = -8.776e-05 + 1 * jax.random.normal(jax.random.fold_in(_gk, 1), (625, 256), jnp.float32)
        src = jax.random.randint(jax.random.fold_in(_gk, 2), (10000,), 0, 625, jnp.int32)
        dst = jax.random.randint(jax.random.fold_in(_gk, 3), (10000,), 0, 625, jnp.int32)
        _o = jnp.argsort(dst, stable=True)
        src = src[_o]
        dst = dst[_o]
        edge_attr_128 = -5.16925e-05 + 1.00005 * jax.random.normal(jax.random.fold_in(_gk, 12), (10000, 128), jnp.float32)
        edge_attr_18 = 0.000318098 + 1.00013 * jax.random.normal(jax.random.fold_in(_gk, 13), (10000, 18), jnp.float32)
        edge_attr_256 = -8.513e-05 + 0.999844 * jax.random.normal(jax.random.fold_in(_gk, 14), (10000, 256), jnp.float32)
        edge_attr_54 = 0.000309991 + 1.00005 * jax.random.normal(jax.random.fold_in(_gk, 15), (10000, 54), jnp.float32)
        return (x, src, dst, edge_attr_128, edge_attr_18, edge_attr_256, edge_attr_54)
    x, src, dst, edge_attr_128, edge_attr_18, edge_attr_256, edge_attr_54 = _rec_inputs()

    def _L0_gnn_setup():
        import jax, jax.numpy as jnp
        import numpy as np
        N, E, C, MID = (625, 10000, 256, 64)
        NR, NS = (6, 3)
        F1_IN = NR * NS * NS
        F2_IN = NR * NS
        G = 64
        EPS = 1e-05
        NEG_SLOPE = 0.1

        def leaky(v):
            return jnp.where(v > 0, v, NEG_SLOPE * v)
        key = jax.random.key(seed)
        ks = jax.random.split(key, 26)

        def w(k, shape):
            fan_in = shape[0]
            return jax.random.normal(k, shape, dtype=jnp.float32) / jnp.sqrt(jnp.float32(fan_in))
        return {'x': jax.random.normal(ks[0], (N, C), dtype=jnp.float32), 'gate_edge': jax.random.normal(ks[1], (E, C), dtype=jnp.float32), 'feature1': jax.random.normal(ks[2], (E, F1_IN), dtype=jnp.float32), 'feature2': jax.random.normal(ks[3], (E, F2_IN), dtype=jnp.float32), 'edge_index': jax.random.randint(ks[4], (2, E), 0, N, dtype=jnp.int32), 'batch': jnp.sort(jax.random.randint(ks[5], (N,), 0, G, dtype=jnp.int32)), 'w_f1a': w(ks[6], (F1_IN, MID)), 'w_f1b': w(ks[7], (MID, C)), 'w_f2a': w(ks[8], (F2_IN, MID)), 'w_f2b': w(ks[9], (MID, C)), 'c1_wl': w(ks[10], (C, C)), 'c1_bl': jnp.zeros((C,), jnp.float32), 'c1_wr': w(ks[11], (C, C)), 'c2_wl': w(ks[12], (C, C)), 'c2_bl': jnp.zeros((C,), jnp.float32), 'c2_wr': w(ks[13], (C, C)), 'lin1_w': w(ks[14], (C, C)), 'lin1_b': jnp.zeros((C,), jnp.float32), 'lin2_w': w(ks[15], (C, C)), 'lin2_b': jnp.zeros((C,), jnp.float32), 'cat_w': w(ks[16], (2 * C, C)), 'cat_b': jnp.zeros((C,), jnp.float32), 'gn_w': jnp.ones((C,), jnp.float32), 'gn_b': jnp.zeros((C,), jnp.float32), 'gn_ms': jnp.ones((C,), jnp.float32)}
    _L0_gnn_all = _L0_gnn_setup()
    _L0_gnn_in = {k: v for k, v in _L0_gnn_all.items() if k in ('w_f1a', 'w_f1b', 'w_f2a', 'w_f2b', 'c1_wl', 'c1_bl', 'c1_wr', 'c2_wl', 'c2_bl', 'c2_wr', 'lin1_w', 'lin1_b', 'lin2_w', 'lin2_b', 'cat_w', 'cat_b', 'gn_w', 'gn_b', 'gn_ms')}
    del _L0_gnn_all

    def _L0_ffn_setup():
        import math
        import jax, jax.numpy as jnp
        import numpy as np
        CAPACITY_FACTOR = 1.25
        TOP_K = 2
        LN_EPS = 1e-05

        def _layer_norm(x, gamma, beta):
            mu = jnp.mean(x, axis=-1, keepdims=True)
            var = jnp.var(x, axis=-1, keepdims=True)
            return (x - mu) * jax.lax.rsqrt(var + LN_EPS) * gamma + beta
        key = jax.random.key(seed)
        ks = jax.random.split(key, 4)
        B, S, D, F, E = (8, 128, 256, 512, 8)
        x = jax.random.normal(ks[0], (B, S, D), dtype=jnp.float32)
        Wr = jax.random.normal(ks[1], (D, E), dtype=jnp.float32) / np.sqrt(D)
        br = jnp.zeros((E,), jnp.float32)
        W1 = jax.random.normal(ks[2], (E, D, F), dtype=jnp.float32) / np.sqrt(D)
        b1 = jnp.zeros((E, F), jnp.float32)
        W2 = jax.random.normal(ks[3], (E, F, D), dtype=jnp.float32) / np.sqrt(F)
        b2 = jnp.zeros((E, D), jnp.float32)
        gamma = jnp.ones((D,), jnp.float32)
        beta = jnp.zeros((D,), jnp.float32)
        return {'x': x, 'Wr': Wr, 'br': br, 'W1': W1, 'b1': b1, 'W2': W2, 'b2': b2, 'gamma': gamma, 'beta': beta}
    _L0_ffn_all = _L0_ffn_setup()
    _L0_ffn_in = {k: v for k, v in _L0_ffn_all.items() if k in ('Wr', 'br', 'W1', 'b1', 'W2', 'b2', 'gamma', 'beta')}
    del _L0_ffn_all

    def _L1_gnn_setup():
        import jax, jax.numpy as jnp
        import numpy as np
        N_NODES = 50000
        N_EDGES = 25000
        IN_DIM = 256
        OUT_DIM = 256
        HEADS = 1
        EDGE_DIM = 128
        NEG_SLOPE = 0.01
        key = jax.random.key(seed)
        ks = jax.random.split(key, 8)
        x = jax.random.normal(ks[0], (N_NODES, IN_DIM), dtype=jnp.float32)
        edge_index = jax.random.randint(ks[1], (2, N_EDGES), 0, N_NODES, dtype=jnp.int64)
        edge_attr = jax.random.normal(ks[2], (N_EDGES, EDGE_DIM), dtype=jnp.float32)
        hc = HEADS * OUT_DIM
        Wn = jax.random.normal(ks[3], (hc, IN_DIM), dtype=jnp.float32) / np.sqrt(IN_DIM)
        bn = jnp.zeros((hc,), dtype=jnp.float32)
        We = jax.random.normal(ks[4], (hc, EDGE_DIM), dtype=jnp.float32) / np.sqrt(EDGE_DIM)
        be = jnp.zeros((hc,), dtype=jnp.float32)
        attn = jax.random.normal(ks[5], (1, HEADS, OUT_DIM), dtype=jnp.float32) * np.sqrt(2.0 / (HEADS * OUT_DIM + 1))
        return {'x': x, 'edge_index': edge_index, 'edge_attr': edge_attr, 'Wn': Wn, 'bn': bn, 'We': We, 'be': be, 'attn': attn}
    _L1_gnn_all = _L1_gnn_setup()
    _L1_gnn_in = {k: v for k, v in _L1_gnn_all.items() if k in ('Wn', 'bn', 'We', 'be', 'attn')}
    del _L1_gnn_all

    def _L1_ffn_setup():
        import jax, jax.numpy as jnp
        import numpy as np
        BN_EPS = 0.001

        def _bn(h, g, b, m, v):
            return g * (h - m) * jax.lax.rsqrt(v + BN_EPS) + b
        key = jax.random.key(seed)
        ks = jax.random.split(key, 8)
        B, F, Df = (256, 64, 256)
        E, H, D = (8, 256, 256)
        s1 = 1.0 / np.sqrt(Df)
        s2 = 1.0 / np.sqrt(H)
        return {'x': jax.random.normal(ks[0], (B, F, Df), jnp.float32), 'Wr': jax.random.normal(ks[1], (Df, E), jnp.float32) * s1, 'br': jnp.zeros((E,), jnp.float32), 'W1': jax.random.normal(ks[2], (E, Df, H), jnp.float32) * s1, 'b1': jnp.zeros((E, H), jnp.float32), 'g1': jnp.ones((E, H), jnp.float32), 'be1': jnp.zeros((E, H), jnp.float32), 'm1': jnp.zeros((E, H), jnp.float32), 'v1': jnp.ones((E, H), jnp.float32), 'W2': jax.random.normal(ks[3], (E, H, H), jnp.float32) * s2, 'b2': jnp.zeros((E, H), jnp.float32), 'g2': jnp.ones((E, H), jnp.float32), 'be2': jnp.zeros((E, H), jnp.float32), 'm2': jnp.zeros((E, H), jnp.float32), 'v2': jnp.ones((E, H), jnp.float32), 'Wo': jax.random.normal(ks[4], (E, H, D), jnp.float32) * s2, 'bo': jnp.zeros((E, D), jnp.float32)}
    _L1_ffn_all = _L1_ffn_setup()
    _L1_ffn_in = {k: v for k, v in _L1_ffn_all.items() if k in ('Wr', 'br', 'W1', 'b1', 'g1', 'be1', 'm1', 'v1', 'W2', 'b2', 'g2', 'be2', 'm2', 'v2', 'Wo', 'bo')}
    del _L1_ffn_all

    def _L2_gnn_setup():
        import jax, jax.numpy as jnp
        import numpy as np
        N_NODES = 3125
        BN_EPS = 1e-05

        def gcn_conv(x, src, dst, W, b, n):
            h = x @ W
            loop = jnp.arange(n, dtype=src.dtype)
            s = jnp.concatenate([src, loop])
            d = jnp.concatenate([dst, loop])
            deg = jax.ops.segment_sum(jnp.ones(s.shape, h.dtype), d, num_segments=n)
            dinv = jnp.where(deg > 0, jax.lax.rsqrt(jnp.maximum(deg, 1.0)), 0.0)
            norm = dinv[s] * dinv[d]
            msg = h[s] * norm[:, None]
            out = jax.ops.segment_sum(msg, d, num_segments=n)
            return out + b

        def batch_norm(x, gamma, beta):
            mean = jnp.mean(x, axis=0)
            var = jnp.mean(jnp.square(x - mean), axis=0)
            return (x - mean) * jax.lax.rsqrt(var + BN_EPS) * gamma + beta
        key = jax.random.key(seed)
        ks = jax.random.split(key, 10)
        d0, d1, d2 = (256, 128, 64)
        d_cat = d0 + d1 + d2
        inp = {'node_features': jax.random.normal(ks[0], (N_NODES, d0), jnp.float32), 'edge_idx': jax.random.randint(ks[1], (2, 50000), 0, N_NODES, jnp.int64), 'W1': jax.random.normal(ks[2], (d0, d1), jnp.float32) * (1.0 / np.sqrt(d0)), 'b1': jnp.zeros((d1,), jnp.float32), 'g1': jnp.ones((d1,), jnp.float32), 'be1': jnp.zeros((d1,), jnp.float32), 'W2': jax.random.normal(ks[3], (d1, d2), jnp.float32) * (1.0 / np.sqrt(d1)), 'b2': jnp.zeros((d2,), jnp.float32), 'g2': jnp.ones((d2,), jnp.float32), 'be2': jnp.zeros((d2,), jnp.float32), 'Wfc': jax.random.normal(ks[4], (d_cat, d0), jnp.float32) * (1.0 / np.sqrt(d_cat)), 'bfc': jnp.zeros((d0,), jnp.float32)}
        return inp
    _L2_gnn_all = _L2_gnn_setup()
    _L2_gnn_in = {k: v for k, v in _L2_gnn_all.items() if k in ('W1', 'b1', 'g1', 'be1', 'W2', 'b2', 'g2', 'be2', 'Wfc', 'bfc')}
    del _L2_gnn_all

    def _L2_ffn_setup():
        import jax, jax.numpy as jnp
        import numpy as np
        B, S, H, F, E, K = (8, 128, 256, 512, 16, 2)
        EPS = 1e-05
        key = jax.random.key(seed)
        ks = jax.random.split(key, 9)
        sc = 0.02
        return {'x': jax.random.normal(ks[0], (B, S, H), dtype=jnp.float32), 'gate_w': jax.random.normal(ks[1], (H, E), dtype=jnp.float32) * sc, 'gate_b': jnp.zeros((E,), dtype=jnp.float32), 'w1': jax.random.normal(ks[2], (E, H, F), dtype=jnp.float32) * sc, 'b1': jnp.zeros((E, F), dtype=jnp.float32), 'w2': jax.random.normal(ks[3], (E, F, H), dtype=jnp.float32) * sc, 'b2': jnp.zeros((E, H), dtype=jnp.float32), 'gamma': jnp.ones((H,), dtype=jnp.float32), 'beta': jnp.zeros((H,), dtype=jnp.float32)}
    _L2_ffn_all = _L2_ffn_setup()
    _L2_ffn_in = {k: v for k, v in _L2_ffn_all.items() if k in ('gate_w', 'gate_b', 'w1', 'b1', 'w2', 'b2', 'gamma', 'beta')}
    del _L2_ffn_all

    def _L3_gnn_setup():
        import jax, jax.numpy as jnp
        import numpy as np
        N = 3125
        D = 256
        E = 100000
        key = jax.random.key(seed)
        ks = jax.random.split(key, 8)
        x = jax.random.normal(ks[0], (N, D), dtype=jnp.float32)
        edge_index = jax.random.randint(ks[1], (2, E), 0, N, dtype=jnp.int64)
        s = 1.0 / np.sqrt(D)
        W_l = jax.random.uniform(ks[2], (D, D), dtype=jnp.float32, minval=-s, maxval=s)
        b_l = jax.random.uniform(ks[3], (D,), dtype=jnp.float32, minval=-s, maxval=s)
        W_r = jax.random.uniform(ks[4], (D, D), dtype=jnp.float32, minval=-s, maxval=s)
        ln_gamma = jnp.ones((D,), dtype=jnp.float32)
        ln_beta = jnp.zeros((D,), dtype=jnp.float32)
        return {'x': x, 'edge_index': edge_index, 'W_l': W_l, 'b_l': b_l, 'W_r': W_r, 'ln_gamma': ln_gamma, 'ln_beta': ln_beta}
    _L3_gnn_all = _L3_gnn_setup()
    _L3_gnn_in = {k: v for k, v in _L3_gnn_all.items() if k in ('W_l', 'b_l', 'W_r', 'ln_gamma', 'ln_beta')}
    del _L3_gnn_all

    def _L3_ffn_setup():
        import jax, jax.numpy as jnp
        import numpy as np
        DIM = 256
        H = 8
        D = 64
        G = 64
        INNER = H * D
        SCALE = D ** (-0.5)
        key = jax.random.key(seed)
        ks = jax.random.split(key, 12)
        B, N = (4, 512)
        x = jax.random.normal(ks[0], (B, N, DIM), dtype=jnp.float32)
        s = lambda fan_in: 1.0 / np.sqrt(fan_in)
        W_fx = jax.random.normal(ks[1], (DIM, INNER), dtype=jnp.float32) * s(DIM)
        b_fx = jnp.zeros((INNER,), dtype=jnp.float32)
        W_x = jax.random.normal(ks[2], (DIM, INNER), dtype=jnp.float32) * s(DIM)
        b_x = jnp.zeros((INNER,), dtype=jnp.float32)
        A = jax.random.normal(ks[3], (G, D), dtype=jnp.float32)
        Q, _ = jnp.linalg.qr(A.T)
        W_slice = Q[:, :G].astype(jnp.float32)
        b_slice = jnp.zeros((G,), dtype=jnp.float32)
        W_q = jax.random.normal(ks[4], (D, D), dtype=jnp.float32) * s(D)
        W_k = jax.random.normal(ks[5], (D, D), dtype=jnp.float32) * s(D)
        W_v = jax.random.normal(ks[6], (D, D), dtype=jnp.float32) * s(D)
        W_out = jax.random.normal(ks[7], (INNER, DIM), dtype=jnp.float32) * s(INNER)
        b_out = jnp.zeros((DIM,), dtype=jnp.float32)
        temperature = jnp.ones((1, H, 1, 1), dtype=jnp.float32) * 0.5
        return {'x': x, 'W_fx': W_fx, 'b_fx': b_fx, 'W_x': W_x, 'b_x': b_x, 'W_slice': W_slice, 'b_slice': b_slice, 'W_q': W_q, 'W_k': W_k, 'W_v': W_v, 'W_out': W_out, 'b_out': b_out, 'temperature': temperature}
    _L3_ffn_all = _L3_ffn_setup()
    _L3_ffn_in = {k: v for k, v in _L3_ffn_all.items() if k in ('W_fx', 'b_fx', 'W_x', 'b_x', 'W_slice', 'b_slice', 'W_q', 'W_k', 'W_v', 'W_out', 'b_out', 'temperature')}
    del _L3_ffn_all
    return {'x': x, 'src': src, 'dst': dst, 'edge_attr_128': edge_attr_128, 'edge_attr_18': edge_attr_18, 'edge_attr_256': edge_attr_256, 'edge_attr_54': edge_attr_54, 'L0_gnn_w_f1a': _L0_gnn_in['w_f1a'], 'L0_gnn_w_f1b': _L0_gnn_in['w_f1b'], 'L0_gnn_w_f2a': _L0_gnn_in['w_f2a'], 'L0_gnn_w_f2b': _L0_gnn_in['w_f2b'], 'L0_gnn_c1_wl': _L0_gnn_in['c1_wl'], 'L0_gnn_c1_bl': _L0_gnn_in['c1_bl'], 'L0_gnn_c1_wr': _L0_gnn_in['c1_wr'], 'L0_gnn_c2_wl': _L0_gnn_in['c2_wl'], 'L0_gnn_c2_bl': _L0_gnn_in['c2_bl'], 'L0_gnn_c2_wr': _L0_gnn_in['c2_wr'], 'L0_gnn_lin1_w': _L0_gnn_in['lin1_w'], 'L0_gnn_lin1_b': _L0_gnn_in['lin1_b'], 'L0_gnn_lin2_w': _L0_gnn_in['lin2_w'], 'L0_gnn_lin2_b': _L0_gnn_in['lin2_b'], 'L0_gnn_cat_w': _L0_gnn_in['cat_w'], 'L0_gnn_cat_b': _L0_gnn_in['cat_b'], 'L0_gnn_gn_w': _L0_gnn_in['gn_w'], 'L0_gnn_gn_b': _L0_gnn_in['gn_b'], 'L0_gnn_gn_ms': _L0_gnn_in['gn_ms'], 'L0_ffn_Wr': _L0_ffn_in['Wr'], 'L0_ffn_br': _L0_ffn_in['br'], 'L0_ffn_W1': _L0_ffn_in['W1'], 'L0_ffn_b1': _L0_ffn_in['b1'], 'L0_ffn_W2': _L0_ffn_in['W2'], 'L0_ffn_b2': _L0_ffn_in['b2'], 'L0_ffn_gamma': _L0_ffn_in['gamma'], 'L0_ffn_beta': _L0_ffn_in['beta'], 'L1_gnn_Wn': _L1_gnn_in['Wn'], 'L1_gnn_bn': _L1_gnn_in['bn'], 'L1_gnn_We': _L1_gnn_in['We'], 'L1_gnn_be': _L1_gnn_in['be'], 'L1_gnn_attn': _L1_gnn_in['attn'], 'L1_ffn_Wr': _L1_ffn_in['Wr'], 'L1_ffn_br': _L1_ffn_in['br'], 'L1_ffn_W1': _L1_ffn_in['W1'], 'L1_ffn_b1': _L1_ffn_in['b1'], 'L1_ffn_g1': _L1_ffn_in['g1'], 'L1_ffn_be1': _L1_ffn_in['be1'], 'L1_ffn_m1': _L1_ffn_in['m1'], 'L1_ffn_v1': _L1_ffn_in['v1'], 'L1_ffn_W2': _L1_ffn_in['W2'], 'L1_ffn_b2': _L1_ffn_in['b2'], 'L1_ffn_g2': _L1_ffn_in['g2'], 'L1_ffn_be2': _L1_ffn_in['be2'], 'L1_ffn_m2': _L1_ffn_in['m2'], 'L1_ffn_v2': _L1_ffn_in['v2'], 'L1_ffn_Wo': _L1_ffn_in['Wo'], 'L1_ffn_bo': _L1_ffn_in['bo'], 'L2_gnn_W1': _L2_gnn_in['W1'], 'L2_gnn_b1': _L2_gnn_in['b1'], 'L2_gnn_g1': _L2_gnn_in['g1'], 'L2_gnn_be1': _L2_gnn_in['be1'], 'L2_gnn_W2': _L2_gnn_in['W2'], 'L2_gnn_b2': _L2_gnn_in['b2'], 'L2_gnn_g2': _L2_gnn_in['g2'], 'L2_gnn_be2': _L2_gnn_in['be2'], 'L2_gnn_Wfc': _L2_gnn_in['Wfc'], 'L2_gnn_bfc': _L2_gnn_in['bfc'], 'L2_ffn_gate_w': _L2_ffn_in['gate_w'], 'L2_ffn_gate_b': _L2_ffn_in['gate_b'], 'L2_ffn_w1': _L2_ffn_in['w1'], 'L2_ffn_b1': _L2_ffn_in['b1'], 'L2_ffn_w2': _L2_ffn_in['w2'], 'L2_ffn_b2': _L2_ffn_in['b2'], 'L2_ffn_gamma': _L2_ffn_in['gamma'], 'L2_ffn_beta': _L2_ffn_in['beta'], 'L3_gnn_W_l': _L3_gnn_in['W_l'], 'L3_gnn_b_l': _L3_gnn_in['b_l'], 'L3_gnn_W_r': _L3_gnn_in['W_r'], 'L3_gnn_ln_gamma': _L3_gnn_in['ln_gamma'], 'L3_gnn_ln_beta': _L3_gnn_in['ln_beta'], 'L3_ffn_W_fx': _L3_ffn_in['W_fx'], 'L3_ffn_b_fx': _L3_ffn_in['b_fx'], 'L3_ffn_W_x': _L3_ffn_in['W_x'], 'L3_ffn_b_x': _L3_ffn_in['b_x'], 'L3_ffn_W_slice': _L3_ffn_in['W_slice'], 'L3_ffn_b_slice': _L3_ffn_in['b_slice'], 'L3_ffn_W_q': _L3_ffn_in['W_q'], 'L3_ffn_W_k': _L3_ffn_in['W_k'], 'L3_ffn_W_v': _L3_ffn_in['W_v'], 'L3_ffn_W_out': _L3_ffn_in['W_out'], 'L3_ffn_b_out': _L3_ffn_in['b_out'], 'L3_ffn_temperature': _L3_ffn_in['temperature']}

def reference(x, src, dst, edge_attr_128, edge_attr_18, edge_attr_256, edge_attr_54, L0_gnn_w_f1a, L0_gnn_w_f1b, L0_gnn_w_f2a, L0_gnn_w_f2b, L0_gnn_c1_wl, L0_gnn_c1_bl, L0_gnn_c1_wr, L0_gnn_c2_wl, L0_gnn_c2_bl, L0_gnn_c2_wr, L0_gnn_lin1_w, L0_gnn_lin1_b, L0_gnn_lin2_w, L0_gnn_lin2_b, L0_gnn_cat_w, L0_gnn_cat_b, L0_gnn_gn_w, L0_gnn_gn_b, L0_gnn_gn_ms, L0_ffn_Wr, L0_ffn_br, L0_ffn_W1, L0_ffn_b1, L0_ffn_W2, L0_ffn_b2, L0_ffn_gamma, L0_ffn_beta, L1_gnn_Wn, L1_gnn_bn, L1_gnn_We, L1_gnn_be, L1_gnn_attn, L1_ffn_Wr, L1_ffn_br, L1_ffn_W1, L1_ffn_b1, L1_ffn_g1, L1_ffn_be1, L1_ffn_m1, L1_ffn_v1, L1_ffn_W2, L1_ffn_b2, L1_ffn_g2, L1_ffn_be2, L1_ffn_m2, L1_ffn_v2, L1_ffn_Wo, L1_ffn_bo, L2_gnn_W1, L2_gnn_b1, L2_gnn_g1, L2_gnn_be1, L2_gnn_W2, L2_gnn_b2, L2_gnn_g2, L2_gnn_be2, L2_gnn_Wfc, L2_gnn_bfc, L2_ffn_gate_w, L2_ffn_gate_b, L2_ffn_w1, L2_ffn_b1, L2_ffn_w2, L2_ffn_b2, L2_ffn_gamma, L2_ffn_beta, L3_gnn_W_l, L3_gnn_b_l, L3_gnn_W_r, L3_gnn_ln_gamma, L3_gnn_ln_beta, L3_ffn_W_fx, L3_ffn_b_fx, L3_ffn_W_x, L3_ffn_b_x, L3_ffn_W_slice, L3_ffn_b_slice, L3_ffn_W_q, L3_ffn_W_k, L3_ffn_W_v, L3_ffn_W_out, L3_ffn_b_out, L3_ffn_temperature):
    import jax
    import jax.numpy as jnp

    def _L0_gnn_ref(x, gate_edge, feature1, feature2, edge_index, batch, w_f1a, w_f1b, w_f2a, w_f2b, c1_wl, c1_bl, c1_wr, c2_wl, c2_bl, c2_wr, lin1_w, lin1_b, lin2_w, lin2_b, cat_w, cat_b, gn_w, gn_b, gn_ms):
        import jax, jax.numpy as jnp
        import numpy as np
        N, E, C, MID = (625, 10000, 256, 64)
        NR, NS = (6, 3)
        F1_IN = NR * NS * NS
        F2_IN = NR * NS
        G = 64
        EPS = 1e-05
        NEG_SLOPE = 0.1

        def leaky(v):
            return jnp.where(v > 0, v, NEG_SLOPE * v)
        src, dst = (edge_index[0], edge_index[1])
        f1 = feature1 @ w_f1a @ w_f1b * gate_edge
        h1 = jax.ops.segment_sum(x[src] * f1, dst, num_segments=N)
        h1 = h1 @ c1_wl + c1_bl + x @ c1_wr
        h1 = leaky(h1 @ lin1_w + lin1_b)
        _dead = feature2 @ w_f2a @ w_f2b
        f2 = f1 * gate_edge
        h2 = jax.ops.segment_sum(x[src] * f2, dst, num_segments=N)
        h2 = h2 @ c2_wl + c2_bl + x @ c2_wr
        h2 = leaky(h2 @ lin2_w + lin2_b)
        h = jnp.concatenate([h1, h2], axis=1) @ cat_w + cat_b
        cnt = jnp.maximum(jax.ops.segment_sum(jnp.ones((N,), h.dtype), batch, num_segments=G), 1.0)[:, None]
        mean = jax.ops.segment_sum(h, batch, num_segments=G) / cnt
        out = h - mean[batch] * gn_ms
        var = jax.ops.segment_sum(out * out, batch, num_segments=G) / cnt
        std = jnp.sqrt(var + EPS)[batch]
        return gn_w * out / std + gn_b

    def _L0_ffn_ref(x, Wr, br, W1, b1, W2, b2, gamma, beta):
        import math
        import jax, jax.numpy as jnp
        import numpy as np
        CAPACITY_FACTOR = 1.25
        TOP_K = 2
        LN_EPS = 1e-05

        def _layer_norm(x, gamma, beta):
            mu = jnp.mean(x, axis=-1, keepdims=True)
            var = jnp.var(x, axis=-1, keepdims=True)
            return (x - mu) * jax.lax.rsqrt(var + LN_EPS) * gamma + beta
        B, S, D = x.shape
        E = Wr.shape[1]
        N = B * S
        K = TOP_K
        logits = jnp.mean(x, axis=1) @ Wr + br
        routing_weights = jax.nn.softmax(logits, axis=-1)
        capacity = float(math.ceil(N * CAPACITY_FACTOR / E))
        expected_loads = routing_weights.sum(axis=0) * (N / B)
        scale = jnp.where(expected_loads > capacity, capacity / expected_loads, 1.0)
        routing_weights = jax.nn.softmax(routing_weights * scale, axis=-1)
        rw_tok = jnp.broadcast_to(routing_weights[:, None, :], (B, S, E)).reshape(N, E)
        top_w, top_i = jax.lax.top_k(rw_tok, K)
        top_w = jax.nn.softmax(top_w, axis=-1)
        xf = x.reshape(N, D)
        h = jax.nn.gelu(jnp.einsum('nd,edf->enf', xf, W1) + b1[:, None, :], approximate=False)
        y = jnp.einsum('enf,efd->end', h, W2) + b2[:, None, :]
        w_dense = jnp.zeros((N, E), x.dtype).at[jnp.arange(N)[:, None], top_i].add(top_w)
        out = jnp.einsum('ne,end->nd', w_dense, y).reshape(B, S, D)
        out = _layer_norm(out + x, gamma, beta)
        return out

    def _L1_gnn_ref(x, edge_index, edge_attr, Wn, bn, We, be, attn):
        import jax, jax.numpy as jnp
        import numpy as np
        N_NODES = 50000
        N_EDGES = 25000
        IN_DIM = 256
        OUT_DIM = 256
        HEADS = 1
        EDGE_DIM = 128
        NEG_SLOPE = 0.01
        N = x.shape[0]
        H, C = (attn.shape[1], attn.shape[2])
        src, dst = (edge_index[0], edge_index[1])
        h = x @ Wn.T + bn
        e = edge_attr @ We.T + be
        xj = h[src].reshape(-1, H, C)
        ee = e.reshape(-1, H, C)
        a = jax.nn.leaky_relu(jnp.sum((xj + ee) * attn, axis=-1), NEG_SLOPE)
        m = jax.ops.segment_max(a, dst, num_segments=N)
        a = jnp.exp(a - m[dst])
        denom = jax.ops.segment_sum(a, dst, num_segments=N)
        a = a / (denom[dst] + 1e-16)
        msg = (xj * a[..., None]).reshape(-1, H * C)
        out = jax.ops.segment_sum(msg, dst, num_segments=N)
        return jax.nn.relu(out)

    def _L1_ffn_ref(x, Wr, br, W1, b1, g1, be1, m1, v1, W2, b2, g2, be2, m2, v2, Wo, bo):
        import jax, jax.numpy as jnp
        import numpy as np
        BN_EPS = 0.001

        def _bn(h, g, b, m, v):
            return g * (h - m) * jax.lax.rsqrt(v + BN_EPS) + b
        feat = jnp.mean(x, axis=0)
        w = jax.nn.softmax(feat @ Wr + br, axis=-1)
        h = jnp.einsum('bfd,edh->bfeh', x, W1) + b1
        h = jax.nn.relu(_bn(h, g1, be1, m1, v1))
        h = jnp.einsum('bfeh,ehk->bfek', h, W2) + b2
        h = jax.nn.relu(_bn(h, g2, be2, m2, v2))
        y = jnp.einsum('bfeh,ehd->bfed', h, Wo) + bo
        return jnp.einsum('bfed,fe->bfd', y, w)

    def _L2_gnn_ref(node_features, edge_idx, W1, b1, g1, be1, W2, b2, g2, be2, Wfc, bfc):
        import jax, jax.numpy as jnp
        import numpy as np
        N_NODES = 3125
        BN_EPS = 1e-05

        def gcn_conv(x, src, dst, W, b, n):
            h = x @ W
            loop = jnp.arange(n, dtype=src.dtype)
            s = jnp.concatenate([src, loop])
            d = jnp.concatenate([dst, loop])
            deg = jax.ops.segment_sum(jnp.ones(s.shape, h.dtype), d, num_segments=n)
            dinv = jnp.where(deg > 0, jax.lax.rsqrt(jnp.maximum(deg, 1.0)), 0.0)
            norm = dinv[s] * dinv[d]
            msg = h[s] * norm[:, None]
            out = jax.ops.segment_sum(msg, d, num_segments=n)
            return out + b

        def batch_norm(x, gamma, beta):
            mean = jnp.mean(x, axis=0)
            var = jnp.mean(jnp.square(x - mean), axis=0)
            return (x - mean) * jax.lax.rsqrt(var + BN_EPS) * gamma + beta
        n = node_features.shape[0]
        src, dst = (edge_idx[0], edge_idx[1])
        feats = [node_features]
        x = node_features
        x = gcn_conv(x, src, dst, W1, b1, n)
        x = jax.nn.relu(batch_norm(x, g1, be1))
        feats.append(x)
        x = gcn_conv(x, src, dst, W2, b2, n)
        x = jax.nn.relu(batch_norm(x, g2, be2))
        feats.append(x)
        cat = jnp.concatenate(feats, axis=1)
        return jax.nn.relu(cat @ Wfc + bfc)

    def _L2_ffn_ref(x, gate_w, gate_b, w1, b1, w2, b2, gamma, beta):
        import jax, jax.numpy as jnp
        import numpy as np
        B, S, H, F, E, K = (8, 128, 256, 512, 16, 2)
        EPS = 1e-05
        gate_logits = x @ gate_w + gate_b
        topk_vals, topk_idx = jax.lax.top_k(gate_logits, K)
        topk_w = jax.nn.softmax(topk_vals, axis=-1)
        h = jax.nn.relu(jnp.einsum('bsh,ehf->bsef', x, w1) + b1)
        expert_out = jnp.einsum('bsef,efh->bseh', h, w2) + b2
        sel = jnp.take_along_axis(expert_out, topk_idx[:, :, :, None], axis=2)
        moe = jnp.sum(topk_w[..., None] * sel, axis=2)
        y = x + moe
        mu = jnp.mean(y, axis=-1, keepdims=True)
        var = jnp.var(y, axis=-1, keepdims=True)
        return (y - mu) / jnp.sqrt(var + EPS) * gamma + beta

    def _L3_gnn_ref(x, edge_index, W_l, b_l, W_r, ln_gamma, ln_beta):
        import jax, jax.numpy as jnp
        import numpy as np
        N = 3125
        D = 256
        E = 100000
        src, dst = (edge_index[0], edge_index[1])
        n = x.shape[0]
        msg_sum = jax.ops.segment_sum(x[src], dst, num_segments=n)
        deg = jax.ops.segment_sum(jnp.ones((src.shape[0],), x.dtype), dst, num_segments=n)
        agg = msg_sum / jnp.maximum(deg, 1.0)[:, None]
        f = agg @ W_l.T + b_l + x @ W_r.T
        f = jax.nn.gelu(f, approximate=False)
        mu = jnp.mean(f, axis=-1, keepdims=True)
        var = jnp.var(f, axis=-1, keepdims=True)
        f = (f - mu) * jax.lax.rsqrt(var + 1e-05) * ln_gamma + ln_beta
        return f + x

    def _L3_ffn_ref(x, W_fx, b_fx, W_x, b_x, W_slice, b_slice, W_q, W_k, W_v, W_out, b_out, temperature):
        import jax, jax.numpy as jnp
        import numpy as np
        DIM = 256
        H = 8
        D = 64
        G = 64
        INNER = H * D
        SCALE = D ** (-0.5)
        B, N, _ = x.shape
        fx_mid = (x @ W_fx + b_fx).reshape(B, N, H, D).transpose(0, 2, 1, 3)
        x_mid = (x @ W_x + b_x).reshape(B, N, H, D).transpose(0, 2, 1, 3)
        temp = jnp.clip(temperature, 0.1, 5.0)
        slice_weights = jax.nn.softmax((x_mid @ W_slice + b_slice) / temp, axis=-1)
        slice_norm = slice_weights.sum(axis=2)
        slice_token = jnp.einsum('bhnc,bhng->bhgc', fx_mid, slice_weights)
        slice_token = slice_token / (slice_norm[..., None] + 1e-05)
        q = slice_token @ W_q
        k = slice_token @ W_k
        v = slice_token @ W_v
        attn = jax.nn.softmax(jnp.einsum('bhgc,bhkc->bhgk', q, k) * SCALE, axis=-1)
        out_slice = jnp.einsum('bhgk,bhkc->bhgc', attn, v)
        out_x = jnp.einsum('bhgc,bhng->bhnc', out_slice, slice_weights)
        out_x = out_x.transpose(0, 2, 1, 3).reshape(B, N, INNER)
        return out_x @ W_out + b_out
    edge_index = jnp.stack([src, dst])
    batch0 = jnp.zeros((625,), jnp.int32)
    x = x + _L0_gnn_ref(_layernorm(x, axis=-1), edge_attr_256, edge_attr_54, edge_attr_18, edge_index, batch0, L0_gnn_w_f1a, L0_gnn_w_f1b, L0_gnn_w_f2a, L0_gnn_w_f2b, L0_gnn_c1_wl, L0_gnn_c1_bl, L0_gnn_c1_wr, L0_gnn_c2_wl, L0_gnn_c2_bl, L0_gnn_c2_wr, L0_gnn_lin1_w, L0_gnn_lin1_b, L0_gnn_lin2_w, L0_gnn_lin2_b, L0_gnn_cat_w, L0_gnn_cat_b, L0_gnn_gn_w, L0_gnn_gn_b, L0_gnn_gn_ms)
    x = x + _L0_ffn_ref(_layernorm(x, axis=-1)[None], L0_ffn_Wr, L0_ffn_br, L0_ffn_W1, L0_ffn_b1, L0_ffn_W2, L0_ffn_b2, L0_ffn_gamma, L0_ffn_beta)[0]
    x = x + _L1_gnn_ref(_layernorm(x, axis=-1), edge_index, edge_attr_128, L1_gnn_Wn, L1_gnn_bn, L1_gnn_We, L1_gnn_be, L1_gnn_attn)
    x = x + _L1_ffn_ref(_layernorm(x, axis=-1)[None], L1_ffn_Wr, L1_ffn_br, L1_ffn_W1, L1_ffn_b1, L1_ffn_g1, L1_ffn_be1, L1_ffn_m1, L1_ffn_v1, L1_ffn_W2, L1_ffn_b2, L1_ffn_g2, L1_ffn_be2, L1_ffn_m2, L1_ffn_v2, L1_ffn_Wo, L1_ffn_bo)[0]
    x = x + _L2_gnn_ref(_layernorm(x, axis=-1), edge_index, L2_gnn_W1, L2_gnn_b1, L2_gnn_g1, L2_gnn_be1, L2_gnn_W2, L2_gnn_b2, L2_gnn_g2, L2_gnn_be2, L2_gnn_Wfc, L2_gnn_bfc)
    x = x + _L2_ffn_ref(_layernorm(x, axis=-1)[None], L2_ffn_gate_w, L2_ffn_gate_b, L2_ffn_w1, L2_ffn_b1, L2_ffn_w2, L2_ffn_b2, L2_ffn_gamma, L2_ffn_beta)[0]
    x = x + _L3_gnn_ref(_layernorm(x, axis=-1), edge_index, L3_gnn_W_l, L3_gnn_b_l, L3_gnn_W_r, L3_gnn_ln_gamma, L3_gnn_ln_beta)
    x = x + _L3_ffn_ref(_layernorm(x, axis=-1)[None], L3_ffn_W_fx, L3_ffn_b_fx, L3_ffn_W_x, L3_ffn_b_x, L3_ffn_W_slice, L3_ffn_b_slice, L3_ffn_W_q, L3_ffn_W_k, L3_ffn_W_v, L3_ffn_W_out, L3_ffn_b_out, L3_ffn_temperature)[0]
    return x

_drawn_inputs = setup_inputs


def setup_inputs(seed=0):
    import zlib

    import numpy as np

    out = dict(_drawn_inputs(seed))
    spreads = {'L0_gnn_c1_bl': (0.0, 0.8),
     'L0_gnn_c2_bl': (0.0, 0.8),
     'L0_gnn_lin1_b': (0.0, 0.8),
     'L0_gnn_lin2_b': (0.0, 0.8),
     'L0_gnn_cat_b': (0.0, 0.8),
     'L0_gnn_gn_w': (1.0, 0.2),
     'L0_gnn_gn_b': (0.0, 0.1),
     'L0_gnn_gn_ms': (1.0, 0.2),
     'L0_ffn_br': (0.0, 0.1),
     'L0_ffn_b1': (0.0, 0.42),
     'L0_ffn_b2': (0.0, 0.277),
     'L0_ffn_gamma': (1.0, 0.2),
     'L0_ffn_beta': (0.0, 0.1),
     'L1_gnn_bn': (0.0, 0.281),
     'L1_gnn_be': (0.0, 0.8),
     'L1_ffn_br': (0.0, 0.8),
     'L1_ffn_b1': (0.0, 0.67),
     'L1_ffn_g1': (1.0, 0.6),
     'L1_ffn_be1': (0.0, 0.733),
     'L1_ffn_m1': (0.0, 0.691),
     'L1_ffn_v1': (1.0, 0.6),
     'L1_ffn_b2': (0.0, 0.494),
     'L1_ffn_g2': (1.0, 0.6),
     'L1_ffn_be2': (0.0, 0.55),
     'L1_ffn_m2': (0.0, 0.479),
     'L1_ffn_v2': (1.0, 0.6),
     'L1_ffn_bo': (0.0, 0.378),
     'L2_gnn_b1': (0.0, 0.8),
     'L2_gnn_g1': (1.0, 0.562),
     'L2_gnn_be1': (0.0, 0.574),
     'L2_gnn_b2': (0.0, 0.8),
     'L2_gnn_g2': (1.0, 0.6),
     'L2_gnn_be2': (0.0, 0.8),
     'L2_gnn_bfc': (0.0, 0.279),
     'L2_ffn_gate_b': (0.0, 0.362),
     'L2_ffn_b1': (0.0, 0.8),
     'L2_ffn_b2': (0.0, 0.394),
     'L2_ffn_gamma': (1.0, 0.2),
     'L2_ffn_beta': (0.0, 0.279),
     'L3_gnn_ln_gamma': (1.0, 0.2),
     'L3_gnn_ln_beta': (0.0, 0.389),
     'L3_ffn_b_fx': (0.0, 0.404),
     'L3_ffn_b_x': (0.0, 0.8),
     'L3_ffn_b_slice': (0.0, 0.8),
     'L3_ffn_b_out': (0.0, 0.425),
     'L3_ffn_temperature': (0.5, 0.6)}
    factors = {'L0_ffn_Wr': 8.0,
     'L2_ffn_w1': 3.283,
     'L3_gnn_b_l': 4.246,
     'L3_ffn_W_x': 8.0,
     'L3_ffn_W_slice': 8.0,
     'L3_ffn_W_q': 8.0,
     'L3_ffn_W_k': 8.0}
    for name, (base, spread) in spreads.items():
        noise = np.random.default_rng([zlib.crc32(name.encode()), seed]).standard_normal(out[name].shape)
        drawn = base * np.exp(spread * noise) if base else spread * noise
        out[name] = jnp.asarray(drawn.astype(out[name].dtype))
    for name, factor in factors.items():
        out[name] = (out[name] * factor).astype(out[name].dtype)
    return out
```

```python
from contextlib import ExitStack

import numpy as np

import concourse.bass as bass
from concourse import mybir

F32 = mybir.dt.float32
BF16 = mybir.dt.bfloat16
F16 = mybir.dt.float16
I32 = mybir.dt.int32
ALU = mybir.AluOpType
ACT = mybir.ActivationFunctionType
AX = mybir.AxisListType

N, C, E = 625, 256, 10000
P, KC = 128, C // 128
NT, TP = 5, 125
ET = E // TP
LN_EPS = 1e-5
HALF = ((0, 313), (313, N))

COLS = ["L0_gnn_c1_bl", "L0_gnn_c2_bl", "L0_gnn_lin1_b", "L0_gnn_lin2_b", "L0_gnn_cat_b", "L0_gnn_gn_w",
        "L0_gnn_gn_b", "L0_gnn_gn_ms", "L1_ffn_b1", "L1_ffn_g1", "L1_ffn_be1", "L1_ffn_m1", "L1_ffn_v1",
        "L1_ffn_b2", "L1_ffn_g2", "L1_ffn_be2", "L1_ffn_m2", "L1_ffn_v2", "L2_gnn_b1", "L2_gnn_g1",
        "L2_gnn_be1", "L2_ffn_b1", "L1_gnn_attn"]
COL_WIDTH = {n: 2 for n in COLS} | {n: 16 for n in COLS if n.startswith("L1_ffn")} | \
    {"L2_gnn_b1": 1, "L2_gnn_g1": 1, "L2_gnn_be1": 1, "L2_ffn_b1": 64}
ROWS = {"L0_ffn_br": 8, "L0_ffn_gamma": C, "L0_ffn_beta": C, "L1_gnn_bn": C, "L1_gnn_attn": C, "L1_ffn_br": 8,
        "L2_gnn_bfc": C, "L2_ffn_gate_b": 16, "L2_ffn_gamma": C, "L2_ffn_beta": C, "L3_gnn_b_l": C,
        "L3_gnn_ln_gamma": C, "L3_gnn_ln_beta": C, "L3_ffn_b_fx": 512, "L3_ffn_b_slice": 64,
        "L3_ffn_b_out": C, "L3_ffn_temperature": 8}


def offsets(widths):
    at, out = 0, {}
    for name, w in widths.items():
        out[name] = (at, at + w)
        at += w
    return out, at


COL_AT, NCOL = offsets(COL_WIDTH)
ROW_AT, NROW = offsets(ROWS)


class Steps:

    def __init__(self, eng, own):
        self.eng, self.own, self.count, self.last = eng, own, {}, own

    def __call__(self, ins, sem=None):
        sem = sem or self.own
        ins.then_inc(sem, 1)
        self.count[sem.name] = self.count.get(sem.name, 0) + 1
        self.last = sem
        return ins

    def settle(self):
        self.eng.wait_ge(self.last, self.count[self.last.name])

    def do(self, ins, sem=None):
        self(ins, sem)
        self.settle()


class Memory:

    def __init__(self, nc, ctx):
        def sb(name, shape, dt=F32):
            return ctx.enter_context(nc.sbuf_tensor(name, shape, dt))

        self.x = sb("x", [TP, NT, C])
        self.xn = sb("xn", [TP, NT, C])
        self.xnT = sb("xnT", [P, KC, N])
        self.stats = sb("stats", [TP, NT, 6])
        self.mv = sb("mv", [TP, NT, 2])
        self.veps = sb("veps", [P, NT])
        self.rstd = sb("rstd", [P, NT])
        self.mhalf = sb("mhalf", [P, 16])
        self.ident = sb("ident", [P, P])
        self.ones = sb("ones", [P, P])
        self.iota = sb("iota", [P, 640])
        self.pcol = sb("pcol", [P, 1])
        self.cols = sb("cols", [P, NCOL])
        self.rows = sb("rows", [P, NROW])
        self.count = sb("count", [TP, NT, N])
        self.srci = sb("srci", [TP, ET], I32)
        self.dsti = sb("dsti", [TP, ET], I32)
        self.src = sb("src", [TP, ET])
        self.dst = sb("dst", [TP, ET])
        self.iota16 = sb("iota16", [P, 640], F16)
        self.score_e = sb("score_e", [TP, ET])
        self.score0 = sb("score0", [TP, 1])
        self.q = sb("q", [P, KC])
        self.w = [sb(f"w{i}", [P, 5120]) for i in range(2)]
        self.ps = ctx.enter_context(nc.psum_tensor("ps", [P, 8, 512], F32))

    def col(self, name):
        a, b = COL_AT[name]
        return self.cols[:, a:b]

    def row(self, name, n=TP):
        a, b = ROW_AT[name]
        return self.rows[0:n, a:b]


class Stage:

    def __init__(self, nc, ctx, name):
        self.nc, self.ctx, self.name = nc, ctx, name
        self.made = {}
        ctx.callback(self.clear)

    def clear(self):
        if self.made:
            self.nc.clear_and_free_semaphores(list(self.made.values()))
            self.nc.all_engine_barrier()

    def sem(self, name):
        if name not in self.made:
            self.made[name] = self.nc.alloc_semaphore(f"{self.name}_{name}")
        return self.made[name]

    def sb(self, name, shape, dt=F32):
        return self.ctx.enter_context(self.nc.sbuf_tensor(f"{self.name}_{name}", shape, dt))



def norm_vector(nc, m, dve, st, steps):
    for t in range(NT):
        steps(nc.vector.bn_stats(m.stats[:, t, :], m.x[:, t, :]))
    steps.settle()
    for t in range(NT):
        steps(nc.vector.bn_aggr(m.mv[:, t, :], m.stats[:, t, :]), st.sem("stats_done"))
    dve.wait_ge(st.sem("rstd_done"), 1)
    for t in range(NT):
        steps(nc.vector.tensor_scalar(m.xn[:, t, :], m.x[:, t, :], m.mv[:, t, 0:1], m.rstd[0:TP, t:t + 1],
                                      ALU.subtract, ALU.mult), st.sem("xn_done"))


def norm_pool(nc, m, pool, st, steps):
    pool.wait_ge(st.sem("stats_done"), NT)
    steps.do(nc.gpsimd.tensor_scalar(m.veps[0:TP, :], m.mv[:, :, 1], LN_EPS, None, ALU.add))
    steps(nc.gpsimd.tensor_tensor(m.rstd[0:TP, :], m.veps[0:TP, :], m.mhalf[0:TP, 0:NT], ALU.pow), st.sem("rstd_done"))


def norm_tensor(nc, m, pe, st):
    for t in range(NT):
        pe.wait_ge(st.sem("xn_done"), t + 1)
        for k in range(KC):
            out = m.ps[:, k, t * TP:(t + 1) * TP] if t < 4 else m.ps[:, 2, k * TP:(k + 1) * TP]
            nc.tensor.transpose(out, m.xn[:, t, k * P:(k + 1) * P], m.ident[0:TP, 0:TP]).then_inc(st.sem("xn_turned"), 1)


def norm_scalar(nc, m, act, st):
    act.wait_ge(st.sem("xn_turned"), 8)
    for k in range(KC):
        nc.scalar.activation(m.xnT[:, k, 0:4 * TP], m.ps[:, k, 0:4 * TP], ACT.Copy).then_inc(st.sem("xnT_done"), 1)
    act.wait_ge(st.sem("xn_turned"), 10)
    nc.scalar.activation(m.xnT[:, :, 4 * TP:N], m.ps[:, 2, 0:KC * TP].rearrange("p (k n) -> p k n", k=KC),
                         ACT.Copy).then_inc(st.sem("xnT_done"), 1)


XNT = 3



def setup(nc, m, A):
    with ExitStack() as ctx:
        st = Stage(nc, ctx, "setup")
        ramp = st.sb("ramp", [P, 640], I32)
        pint = st.sb("pint", [P, 1], I32)
        block = ctx.enter_context(nc.Block())

        @block.sync
        def _(sp):
            sp.dma_start(m.x[:, :, :], A["x"].rearrange("(t p) c -> p t c", p=TP)).then_inc(st.sem("loads"), 16)
            sp.dma_start(m.cols[:, :], A["cols"]).then_inc(st.sem("loads"), 16)
            sp.dma_start(m.rows[:, :], A["rows"][None, :].to_broadcast([P, NROW])).then_inc(st.sem("loads"), 16)
            sp.dma_start(m.srci[:, :], A["src_t"]).then_inc(st.sem("ends"), 16)
            sp.dma_start(m.dsti[:, :], A["dst_t"]).then_inc(st.sem("ends"), 16)
            sp.wait_ge(st.sem("loads"), 48)

        @block.gpsimd
        def _(pool):
            steps = Steps(pool, st.sem("pool"))
            steps(nc.gpsimd.memset(m.ident[:, :], 0.0))
            steps(nc.gpsimd.memset(m.ones[:, :], 1.0))
            steps(nc.gpsimd.memset(m.mhalf[:, :], -0.5))
            steps(nc.gpsimd.iota(pint[:, :], pattern=[[0, 1]], base=0, channel_multiplier=1))
            steps(nc.gpsimd.iota(ramp[:, :], pattern=[[1, 640]], base=0, channel_multiplier=0))
            steps.settle()
            steps(nc.gpsimd.affine_select(out=m.ident[:, :], in_=m.ident[:, :], compare_op=ALU.not_equal, fill=1.0,
                                          base=0, pattern=[[-1, P]], channel_multiplier=1))
            steps(nc.gpsimd.tensor_copy(m.iota[:, :], ramp[:, :]))
            steps(nc.gpsimd.tensor_copy(m.iota16[:, :], ramp[:, :]))
            steps(nc.gpsimd.tensor_copy(m.pcol[:, :], pint[:, :]))
            pool.wait_ge(st.sem("ends"), 32)
            steps(nc.gpsimd.tensor_copy(m.src[:, :], m.srci[:, :]))
            steps.do(nc.gpsimd.tensor_copy(m.dst[:, :], m.dsti[:, :]))



def l0_gnn(nc, m, A):
    W = m.w[0]
    names = ["c1_wl", "c1_wr", "c2_wl", "c2_wr", "lin1_w", "lin2_w"]
    wk = {n: W[:, 512 * i:512 * (i + 1)].rearrange("p (k n) -> p k n", k=2) for i, n in enumerate(names)}
    cat = W[:, 3072:4096].rearrange("p (k n) -> p k n", k=4)
    with ExitStack() as ctx:
        st = Stage(nc, ctx, "l0g")
        table = nc.dram_tensor("l0_nodes", (N, C), F32, kind="Internal").ap()
        agg = st.sb("agg", [TP, NT, 512])
        fa = st.sb("fa", [64, 54])
        fb = st.sb("fb", [64, C])
        wf = st.sb("wf", [54, C])

        with ExitStack() as inner:
            sb = Stage(nc, inner, "l0e").sb
            idx = sb("idx", [TP, 8], I32)
            gate = [sb(f"gate{h}", [TP, 4, C]) for h in range(2)]
            feat = [sb(f"feat{h}", [54, 4 * TP]) for h in range(2)]
            xg = [sb(f"xg{h}", [TP, 4, C]) for h in range(2)]
            fg = [sb(f"fg{s}", [TP, 2, C]) for s in range(2)]
            oh = [sb(f"oh{s}", [TP, 2, N]) for s in range(2)]
            msg = [sb(f"msg{s}", [TP, 2, 2, C]) for s in range(2)]
            gate_d = A["edge_attr_256"].rearrange("(q u p) c -> q p u c", p=TP, u=4)
            s = st.sem
            block = inner.enter_context(nc.Block())

            @block.sync
            def _(sp):
                sp.dma_start(fa[:, :], A["w_f1aT"]).then_inc(s("small"), 16)
                sp.dma_start(fb[:, :], A["L0_gnn_w_f1b"]).then_inc(s("small"), 16)
                sp.wait_ge(s("xn_done"), NT)
                sp.dma_start(table.rearrange("(t p) c -> p t c", p=TP), m.xn[:, :, :]).then_inc(s("table"), 16)
                sp.dma_start(W[:, 0:4096], A["w_l0g"]).then_inc(s("w"), 16)
                with sp.Fori(0, 10) as i:
                    for h in range(2):
                        sp.wait_ge(s(f"quad_used{h}"), i)
                        sp.wait_ge(s(f"feat_used{h}"), i)
                        sp.dma_start(gate[h][:, :, :], gate_d[bass.ds(i * 2 + h, 1)].rearrange("q p u c -> (q p) u c"))\
                            .then_inc(s(f"gate{h}"), 16)
                        sp.dma_start(feat[h][:, :], A["featT"][:, bass.ds(i * 1000 + h * 500, 500)])\
                            .then_inc(s(f"feat{h}"), 16)

            @block.gpsimd
            def _(pool):
                steps = Steps(pool, s("pool"))
                norm_pool(nc, m, pool, st, steps)
                pool.wait_ge(s("table"), 16)
                with pool.Fori(0, 10) as i:
                    for h in range(2):
                        pool.wait_ge(s(f"xg{h}"), i * 64)
                        pool.wait_ge(s(f"quad_used{h}"), i)
                        pool.nop(nofuse=True)
                        nc.gpsimd.tensor_copy(idx[:, 4 * h:4 * h + 4], m.srci[:, bass.ds(i * 8 + 4 * h, 4)])\
                            .then_inc(s("idx"), 1)
                        pool.wait_ge(s("idx"), i * 2 + (h + 1))
                        pool.nop(nofuse=True)
                        for u in range(4):
                            pool.indirect_dma_start(
                                out=xg[h][:, u, :], out_offset=None, in_=table,
                                in_offset=bass.IndirectOffsetOnAxis(ap=idx[:, 4 * h + u:4 * h + u + 1], axis=0),
                            ).then_inc(s(f"xg{h}"), 16)

            @block.scalar
            def _(act):
                norm_scalar(nc, m, act, st)
                act.wait_ge(s("wf_made"), 1)
                nc.scalar.activation(wf[:, :], m.ps[0:54, 3, 0:C], ACT.Copy).then_inc(s("wf"), 1)
                act.wait_ge(s("agg_made"), 1)
                for t in range(NT):
                    nc.scalar.activation(agg[:, t, :], m.ps[0:TP, t, :], ACT.Copy).then_inc(s("agg"), 1)

            @block.vector
            def _(dve):
                steps = Steps(dve, s("dve"))
                norm_vector(nc, m, dve, st, steps)
                with dve.Fori(0, 10) as i:
                    for q in range(4):
                        h, slot = q // 2, q % 2
                        u = 2 * (q % 2)
                        use = i * 2 + q // 2
                        dve.wait_ge(s(f"msg_used{slot}"), use)
                        for v in range(2):
                            nc.vector.tensor_scalar(oh[slot][:, v, :], m.iota[0:TP, 0:N],
                                                    m.dst[:, bass.ds(i * 8 + 2 * q + v, 1)], None, ALU.is_equal)\
                                .then_inc(s(f"oh{slot}"), 1)
                        if q % 2 == 0:
                            dve.wait_ge(s(f"gate{h}"), (i + 1) * 16)
                        dve.wait_ge(s(f"f1_made{slot}"), use + 1)
                        nc.vector.tensor_tensor(fg[slot][:, :, :], m.ps[0:TP, 5 + slot, :].rearrange("p (v c) -> p v c", v=2),
                                                gate[h][:, u:u + 2, :], ALU.mult).then_inc(s(f"fg{slot}"), 1)
                        if q % 2 == 0:
                            dve.wait_ge(s(f"xg{h}"), (i + 1) * 64)
                        dve.wait_ge(s(f"fg{slot}"), use + 1)
                        nc.vector.tensor_tensor(msg[slot][:, :, 0, :], fg[slot][:, :, :], xg[h][:, u:u + 2, :], ALU.mult)\
                            .then_inc(s(f"m1{slot}"), 1)
                        dve.wait_ge(s(f"m1{slot}"), use + 1)
                        ins = nc.vector.tensor_tensor(msg[slot][:, :, 1, :], msg[slot][:, :, 0, :], gate[h][:, u:u + 2, :],
                                                      ALU.mult)
                        ins.then_inc(s(f"msg{slot}"), 1)
                        if q % 2 == 1:
                            dve.wait_ge(s(f"msg{slot}"), use + 1)
                            dve.nop(nofuse=True).then_inc(s(f"quad_used{h}"), 1)

            @block.tensor
            def _(pe):
                norm_tensor(nc, m, pe, st)
                pe.wait_ge(s("small"), 32)
                nc.tensor.matmul(m.ps[0:54, 3, 0:C], fa[:, :], fb[:, :], start=True, stop=True).then_inc(s("wf_made"), 1)
                pe.wait_ge(s("wf"), 1)
                pe.wait_ge(s("xnT_done"), XNT)

                def features(i, q):
                    h, slot = q // 2, q % 2
                    if q % 2 == 0:
                        pe.wait_ge(s(f"feat{h}"), (i + 1) * 16)
                    pe.wait_ge(s(f"fg{slot}"), i * 2 + q // 2)
                    for v in range(2):
                        u = 2 * (q % 2) + v
                        ins = nc.tensor.matmul(m.ps[0:TP, 5 + slot, v * C:(v + 1) * C], feat[h][:, u * TP:(u + 1) * TP],
                                               wf[:, :], start=True, stop=True)
                    ins.then_inc(s(f"f1_made{slot}"), 1)
                    if q % 2 == 1:
                        ins2 = pe.nop(nofuse=True) if False else None

                def sums(i, q, first=False, last=False):
                    slot = q % 2
                    pe.wait_ge(s(f"msg{slot}"), i * 2 + (q // 2 + 1))
                    pe.wait_ge(s(f"oh{slot}"), i * 4 + 2 * (q // 2 + 1))
                    for v in range(2):
                        for t in range(NT):
                            ins = nc.tensor.matmul(m.ps[0:TP, t, :], oh[slot][:, v, t * TP:(t + 1) * TP],
                                                   msg[slot][:, v, :, :].rearrange("p a c -> p (a c)"),
                                                   start=first and v == 0, stop=last and v == 1)
                    ins.then_inc(s(f"msg_used{slot}"), 1)

                def turn(i, first=False, last=False):
                    for q in range(4):
                        if q < 3:
                            features(i, q + 1)
                            if q == 0:
                                pass
                        elif not last:
                            features(i + 1, 0)
                        sums(i, q, first and q == 0, last and q == 3)
                        if q % 2 == 1:
                            pe.wait_ge(s(f"f1_made1"), i * 2 + (q // 2 + 1))
                            pe.nop(nofuse=True).then_inc(s(f"feat_used{q // 2}"), 1)

                features(0, 0)
                turn(0, first=True)
                with pe.Fori(1, 9) as i:
                    turn(i)
                turn(9, last=True)
                pe.wait_ge(s("msg_used1"), 20)
                pe.wait_ge(s("msg_used0"), 20)
                pe.nop(nofuse=True).then_inc(s("agg_made"), 1)

        with ExitStack() as inner:
            sb = Stage(nc, inner, "l0m").sb
            aggT = sb("aggT", [P, 4, N])
            z = [sb(f"z{j}", [P, KC, N]) for j in range(2)]
            pre = [sb(f"pre{j}", [P, KC, N]) for j in range(2)]
            g = [sb(f"g{j}", [P, KC, N]) for j in range(2)]
            h = sb("h", [P, KC, N])
            hstat = sb("hstat", [P, KC, 5, 6])
            hmv = sb("hmv", [P, KC, 2])
            tmp = sb("tmp", [P, 4, KC])
            s = st.sem
            block = inner.enter_context(nc.Block())
            layers = [([("c1_wl", lambda k: aggT[:, k, :]), ("c1_wr", lambda k: m.xnT[:, k, :])], "c1_bl", z[0]),
                      ([("c2_wl", lambda k: aggT[:, 2 + k, :]), ("c2_wr", lambda k: m.xnT[:, k, :])], "c2_bl", z[1]),
                      ([("lin1_w", lambda k: z[0][:, k, :])], "lin1_b", pre[0]),
                      ([("lin2_w", lambda k: z[1][:, k, :])], "lin2_b", pre[1]),
                      ([("cat", lambda k: g[k // 2][:, k % 2, :])], "cat_b", h)]

            @block.tensor
            def _(pe):
                for t in range(NT):
                    for k in range(4):
                        ins = nc.tensor.transpose(m.ps[:, t, k * TP:(k + 1) * TP], agg[:, t, k * P:(k + 1) * P],
                                                  m.ident[0:TP, 0:TP])
                    ins.then_inc(s("agg_turned"), 1)
                pe.wait_ge(s("w"), 16)
                unit = 0
                for n, (terms, _, _) in enumerate(layers):
                    if n == 0:
                        pe.wait_ge(s("aggT"), NT)
                    elif n == 2:
                        pe.wait_ge(s("mlp_evac"), 4)
                    elif n == 3:
                        pe.wait_ge(s("mlp_evac"), 8)
                    elif n == 4:
                        pe.wait_ge(s("leaky"), 4)
                    for c in range(KC):
                        for (a, b) in HALF:
                            if unit >= 8:
                                pe.wait_ge(s("mlp_evac"), unit - 7)
                            ops = [(wk[w][:, k, c * P:(c + 1) * P] if w != "cat" else cat[:, k, c * P:(c + 1) * P],
                                    x(k)[:, a:b]) for w, x in terms for k in range(4 if w == "cat" else 2)]
                            for j, (lhsT, rhs) in enumerate(ops):
                                ins = nc.tensor.matmul(m.ps[:, unit % 8, 0:b - a], lhsT, rhs, start=j == 0,
                                                       stop=j == len(ops) - 1)
                            ins.then_inc(s("mlp_made"), 1)
                            unit += 1
                pe.wait_ge(s("hn"), 2)
                pe.wait_ge(s("mlp_evac"), 20)
                for t in range(NT):
                    for k in range(KC):
                        nc.tensor.transpose(m.ps[0:TP, t, k * P:(k + 1) * P],
                                            h[:, k, t * TP:(t + 1) * TP], m.ident[:, :]).then_inc(s("hn_turned"), 1)

            @block.scalar
            def _(act):
                for t in range(NT):
                    act.wait_ge(s("agg_turned"), t + 1)
                    nc.scalar.activation(aggT[:, :, t * TP:(t + 1) * TP],
                                         m.ps[:, t, 0:4 * TP].rearrange("p (k n) -> p k n", k=4), ACT.Copy)\
                        .then_inc(s("aggT"), 1)
                unit = 0
                for _, bias, out in layers:
                    for c in range(KC):
                        for (a, b) in HALF:
                            act.wait_ge(s("mlp_made"), unit + 1)
                            nc.scalar.activation(out[:, c, a:b], m.ps[:, unit % 8, 0:b - a], ACT.Identity,
                                                 bias=m.col("L0_gnn_" + bias)[:, c:c + 1]).then_inc(s("mlp_evac"), 1)
                            unit += 1
                act.wait_ge(s("gn_coef"), 1)
                for c in range(KC):
                    nc.scalar.activation(h[:, c, :], h[:, c, :], ACT.Identity, bias=tmp[:, 3, c:c + 1],
                                         scale=tmp[:, 2, c:c + 1]).then_inc(s("hn"), 1)

            @block.gpsimd
            def _(pool):
                steps = Steps(pool, s("pool_gn"))
                pool.wait_ge(s("gn_var"), 1)
                steps.do(nc.gpsimd.tensor_scalar(m.veps[:, 0:KC], tmp[:, 1, :], 1e-5, None, ALU.add))
                steps(nc.gpsimd.tensor_tensor(m.rstd[:, 0:KC], m.veps[:, 0:KC], m.mhalf[:, 0:KC], ALU.pow), s("gn_rstd"))

            @block.vector
            def _(dve):
                steps = Steps(dve, s("dve_mlp"))
                for j in range(2):
                    dve.wait_ge(s("mlp_evac"), 12 + 4 * j)
                    for c in range(KC):
                        steps(nc.vector.scalar_tensor_tensor(g[j][:, c, :], pre[j][:, c, :], 0.1, pre[j][:, c, :],
                                                             ALU.mult, ALU.max), s("leaky"))
                dve.wait_ge(s("mlp_evac"), 20)
                for c in range(KC):
                    for t in range(NT):
                        steps(nc.vector.bn_stats(hstat[:, c, t, :], h[:, c, t * TP:(t + 1) * TP]))
                steps.settle()
                for c in range(KC):
                    steps(nc.vector.bn_aggr(hmv[:, c, :], hstat[:, c, :, :].rearrange("p t s -> p (t s)")))
                steps.settle()
                steps.do(nc.vector.tensor_tensor(tmp[:, 0, :], hmv[:, :, 0], m.col("L0_gnn_gn_ms"), ALU.mult))
                steps.do(nc.vector.tensor_tensor(tmp[:, 1, :], hmv[:, :, 0], tmp[:, 0, :], ALU.subtract))
                steps.do(nc.vector.tensor_tensor(tmp[:, 1, :], tmp[:, 1, :], tmp[:, 1, :], ALU.mult))
                steps(nc.vector.tensor_tensor(tmp[:, 1, :], tmp[:, 1, :], hmv[:, :, 1], ALU.add), s("gn_var"))
                dve.wait_ge(s("gn_rstd"), 1)
                steps.do(nc.vector.tensor_tensor(tmp[:, 2, :], m.rstd[:, 0:KC], m.col("L0_gnn_gn_w"), ALU.mult))
                steps.do(nc.vector.tensor_tensor(tmp[:, 3, :], tmp[:, 0, :], tmp[:, 2, :], ALU.mult))
                steps(nc.vector.tensor_tensor(tmp[:, 3, :], m.col("L0_gnn_gn_b"), tmp[:, 3, :], ALU.subtract), s("gn_coef"))
                for t in range(NT):
                    dve.wait_ge(s("hn_turned"), 2 * t + 2)
                    steps(nc.vector.tensor_tensor(m.x[:, t, :], m.x[:, t, :],
                                                  m.ps[0:TP, t, 0:C], ALU.add))
                steps.settle()



def l0_ffn(nc, m, A):
    NE, F, FK = 8, 512, 4
    ROWLEN = 2052
    CAPACITY = float(int(np.ceil(N * 1.25 / NE)))
    with ExitStack() as ctx:
        st = Stage(nc, ctx, "l0f")
        s, sb = st.sem, st.sb
        wr = sb("wr", [P, KC, NE])
        b2 = sb("b2", [NE, C])
        expert = [m.w[1][:, ROWLEN * j:ROWLEN * (j + 1)] for j in range(2)]
        w1 = [e[:, 0:1024].rearrange("p (k f) -> p k f", k=KC) for e in expert]
        w2 = [e[:, 1024:2048].rearrange("p (k c) -> p k c", k=FK) for e in expert]
        b1 = [e[:, 2048:2052] for e in expert]
        hT = [sb(f"hT{j}", [P, FK, N]) for j in range(2)]
        xsum = sb("xsum", [P, KC])
        xmean = sb("xmean", [P, KC, P])
        r = sb("r", [P, 16, NE])
        c = sb("c", [P, 32])
        row_idx = sb("row_idx", [P, 2], I32)
        wdT = sb("wdT", [NE, P])
        z = sb("z", [TP, NT, C])
        zn = sb("zn", [TP, NT, C])
        block = ctx.enter_context(nc.Block())
        UNITS = 2 * FK * 2

        @block.sync
        def _(sp):
            sp.dma_start(wr[:, :, :], A["l0f_wr"].rearrange("p (k e) -> p k e", k=KC)).then_inc(s("small"), 16)
            sp.dma_start(b2[:, :], A["L0_ffn_b2"]).then_inc(s("small"), 16)

        @block.gpsimd
        def _(pool):
            steps = Steps(pool, s("pool"))
            norm_pool(nc, m, pool, st, steps)
            for j in range(2):
                pool.wait_ge(s("chosen"), j + 1)
                pool.indirect_dma_start(out=expert[j], out_offset=None, in_=A["l0f_experts"],
                                        in_offset=bass.IndirectOffsetOnAxis(ap=row_idx[:, j:j + 1], axis=0))\
                    .then_inc(s(f"expert{j}"), 16)
            pool.wait_ge(s("z_stats"), NT)
            steps.do(nc.gpsimd.tensor_scalar(m.veps[0:TP, :], m.mv[:, :, 1], LN_EPS, None, ALU.add))
            steps(nc.gpsimd.tensor_tensor(m.rstd[0:TP, :], m.veps[0:TP, :], m.mhalf[0:TP, 0:NT], ALU.pow), s("z_rstd"))

        @block.scalar
        def _(act):
            norm_scalar(nc, m, act, st)
            for n in range(2):
                act.wait_ge(s("exp_in"), n + 1)
                nc.scalar.activation(r[:, 3 * n + 2, :], r[:, 3 * n + 1, :], ACT.Exp, accum_out=c[:, n:n + 1])\
                    .then_inc(s("exp_out"), 1)
            act.wait_ge(s("exp_in"), 3)
            nc.scalar.activation(c[:, 11:12], c[:, 10:11], ACT.Exp).then_inc(s("exp_out"), 1)
            act.wait_ge(s("wdT_made"), 1)
            nc.scalar.activation(wdT[:, :], m.ps[0:NE, 4, 0:P], ACT.Copy).then_inc(s("wdT"), 1)
            unit = 0
            for j in range(2):
                for f in range(FK):
                    for (a, b) in HALF:
                        act.wait_ge(s("h_made"), unit + 1)
                        nc.scalar.activation(hT[j][:, f, a:b], m.ps[:, unit % 3, 0:b - a], ACT.Gelu,
                                             bias=b1[j][:, f:f + 1]).then_inc(s("hT"), 1)
                        unit += 1

        @block.vector
        def _(dve):
            steps = Steps(dve, s("dve"))
            norm_vector(nc, m, dve, st, steps)
            dve.wait_ge(s("xnT_done"), XNT)
            steps.do(nc.vector.tensor_reduce(xsum[:, :], m.xnT[:, :, :], AX.X, ALU.add))
            for k in range(KC):
                steps(nc.vector.tensor_scalar(xmean[:, k, :], m.ones[:, :], xsum[:, k:k + 1], 1.0 / N, ALU.mult, ALU.mult),
                      s("xmean"))
            dve.wait_ge(s("logits"), 1)

            def softmax_top(n, logits):
                steps.do(nc.vector.tensor_reduce(c[:, 2:3], logits, AX.X, ALU.max))
                steps(nc.vector.tensor_scalar(r[:, 3 * n + 1, :], logits, c[:, 2:3], None, ALU.subtract), s("exp_in"))

            def softmax_end(n):
                dve.wait_ge(s("exp_out"), n + 1)
                steps.do(nc.vector.reciprocal(c[:, 3:4], c[:, n:n + 1]))
                steps.do(nc.vector.tensor_scalar(r[:, 3 * n + 3, :], r[:, 3 * n + 2, :], c[:, 3:4], None, ALU.mult))

            steps.do(nc.vector.tensor_copy(r[:, 0, :], m.ps[:, 3, 0:NE]))
            softmax_top(0, r[:, 0, :])
            softmax_end(0)
            steps.do(nc.vector.tensor_scalar(r[:, 8, :], r[:, 3, :], float(N), None, ALU.mult))
            steps.do(nc.vector.tensor_scalar(r[:, 8, :], r[:, 8, :], CAPACITY, 1.0 / CAPACITY, ALU.max, ALU.mult))
            steps.do(nc.vector.reciprocal(r[:, 9, :], r[:, 8, :]))
            steps.do(nc.vector.tensor_tensor(r[:, 0, :], r[:, 3, :], r[:, 9, :], ALU.mult))
            softmax_top(1, r[:, 0, :])
            softmax_end(1)
            left = r[:, 6, :]
            for j in range(2):
                steps.do(nc.vector.tensor_reduce(c[:, 4 + j:5 + j], left, AX.X, ALU.max))
                steps.do(nc.vector.tensor_scalar(r[:, 10, :], left, c[:, 4 + j:5 + j], -1000.0, ALU.is_equal, ALU.mult))
                steps.do(nc.vector.tensor_tensor(r[:, 10, :], r[:, 10, :], m.iota[:, 0:NE], ALU.add))
                steps.do(nc.vector.tensor_reduce(c[:, 6 + j:7 + j], r[:, 10, :], AX.X, ALU.min))
                steps.do(nc.vector.tensor_scalar(c[:, 8:9], c[:, 6 + j:7 + j], 1000.0, float(P), ALU.add, ALU.mult))
                steps(nc.vector.tensor_tensor(row_idx[:, j:j + 1], c[:, 8:9], m.pcol[:, :], ALU.add), s("chosen"))
                steps.do(nc.vector.tensor_scalar(c[:, 9:10], c[:, 6 + j:7 + j], 1000.0, None, ALU.add))
                steps.do(nc.vector.tensor_scalar(r[:, 11 + j, :], m.iota[:, 0:NE], c[:, 9:10], None, ALU.is_equal))
                if j == 0:
                    steps.do(nc.vector.scalar_tensor_tensor(r[:, 13, :], r[:, 11, :], -2.0, left, ALU.mult, ALU.add))
                    left = r[:, 13, :]
            steps(nc.vector.tensor_tensor(c[:, 10:11], c[:, 5:6], c[:, 4:5], ALU.subtract), s("exp_in"))
            dve.wait_ge(s("exp_out"), 3)
            steps.do(nc.vector.tensor_scalar(c[:, 12:13], c[:, 11:12], 1.0, None, ALU.add))
            steps.do(nc.vector.reciprocal(c[:, 13:14], c[:, 12:13]))
            steps.do(nc.vector.tensor_tensor(c[:, 14:15], c[:, 11:12], c[:, 13:14], ALU.mult))
            steps.do(nc.vector.tensor_scalar(r[:, 14, :], r[:, 11, :], c[:, 13:14], None, ALU.mult))
            steps(nc.vector.scalar_tensor_tensor(r[:, 15, :], r[:, 12, :], c[:, 14:15], r[:, 14, :], ALU.mult, ALU.add),
                  s("wdense"))
            for j in range(2):
                dve.wait_ge(s(f"expert{j}"), 16)
                steps(nc.vector.tensor_scalar(expert[j][:, 1024:2048], expert[j][:, 1024:2048], c[:, 13 + j:14 + j],
                                              None, ALU.mult), s("w2_scaled"))
            for t in range(NT):
                dve.wait_ge(s("y_made"), t + 1)
                steps(nc.vector.tensor_tensor(z[:, t, :], m.ps[0:TP, 3 + t, 0:C], m.xn[:, t, :], ALU.add), s("z"))
                steps.settle()
                steps.do(nc.vector.bn_stats(m.stats[:, t, :], z[:, t, :]))
                steps(nc.vector.bn_aggr(m.mv[:, t, :], m.stats[:, t, :]), s("z_stats"))
            dve.wait_ge(s("z_rstd"), 1)
            for t in range(NT):
                steps(nc.vector.tensor_scalar(zn[:, t, :], z[:, t, :], m.mv[:, t, 0:1], m.rstd[0:TP, t:t + 1],
                                              ALU.subtract, ALU.mult))
            steps.settle()
            for t in range(NT):
                steps(nc.vector.tensor_tensor(z[:, t, :], zn[:, t, :], m.row("L0_ffn_gamma"), ALU.mult))
            steps.settle()
            for t in range(NT):
                steps(nc.vector.tensor_tensor(zn[:, t, :], z[:, t, :], m.row("L0_ffn_beta"), ALU.add))
            steps.settle()
            for t in range(NT):
                steps(nc.vector.tensor_tensor(m.x[:, t, :], m.x[:, t, :], zn[:, t, :], ALU.add))
            steps.settle()

        @block.tensor
        def _(pe):
            norm_tensor(nc, m, pe, st)
            pe.wait_ge(s("xmean"), KC)
            pe.wait_ge(s("small"), 32)
            for k in range(KC):
                nc.tensor.matmul(m.ps[:, 3, 0:NE], xmean[:, k, :], wr[:, k, :], start=k == 0, stop=False)
            nc.tensor.matmul(m.ps[:, 3, 0:NE], m.ones[0:1, :], m.row("L0_ffn_br", 1), start=False, stop=True)\
                .then_inc(s("logits"), 1)
            pe.wait_ge(s("wdense"), 1)
            nc.tensor.transpose(m.ps[0:NE, 4, 0:P], r[:, 15, :], m.ident[:, :]).then_inc(s("wdT_made"), 1)
            pe.wait_ge(s("wdT"), 1)
            for t in range(NT):
                nc.tensor.matmul(m.ps[0:TP, 3 + t, 0:C], wdT[:, 0:TP], b2[:, :], start=True, stop=False)
            pe.wait_ge(s("xnT_done"), XNT)
            unit = 0
            for j in range(2):
                pe.wait_ge(s(f"expert{j}"), 16)
                for f in range(FK):
                    for (a, b) in HALF:
                        if unit >= 3:
                            pe.wait_ge(s("hT"), unit - 2)
                        for k in range(KC):
                            ins = nc.tensor.matmul(m.ps[:, unit % 3, 0:b - a], w1[j][:, k, f * P:(f + 1) * P],
                                                   m.xnT[:, k, a:b], start=k == 0, stop=k == KC - 1)
                        ins.then_inc(s("h_made"), 1)
                        unit += 1
            for j in range(2):
                pe.wait_ge(s("hT"), UNITS // 2 * (j + 1))
                pe.wait_ge(s("w2_scaled"), j + 1)
                for t in range(NT):
                    for f in range(FK):
                        ins = nc.tensor.matmul(m.ps[0:TP, 3 + t, 0:C], hT[j][:, f, t * TP:(t + 1) * TP], w2[j][:, f, :],
                                               start=False, stop=j == 1 and f == FK - 1)
                    if j == 1:
                        ins.then_inc(s("y_made"), 1)



def edges(nc, m, A):
    with ExitStack() as ctx:
        st = Stage(nc, ctx, "edg")
        s, sb = st.sem, st.sb
        wn = sb("wn", [P, KC, C])
        we = sb("we", [P, KC, P + 1])
        attnB = sb("attnB", [P, KC, TP])
        vrow = sb("vrow", [TP, P])
        both = sb("both", [TP, C])
        junk = sb("junk", [TP, C])
        c0 = sb("c0", [TP, 2])
        ea = [sb(f"ea{h}", [TP, 4, P]) for h in range(2)]
        prod = [sb(f"prod{h}", [TP, 4, P]) for h in range(2)]
        ohs = [sb(f"ohs{v}", [TP, N], BF16) for v in range(2)]
        ohd = [sb(f"ohd{v}", [TP, N], BF16) for v in range(2)]
        ea_d = A["edge_attr_128"].rearrange("(q u p) c -> q p u c", p=TP, u=4)
        attn = m.col("L1_gnn_attn")
        block = ctx.enter_context(nc.Block())

        @block.sync
        def _(sp):
            sp.dma_start(wn[:, :, :], A["wn"].rearrange("p (k n) -> p k n", k=KC)).then_inc(s("w"), 16)
            sp.dma_start(we[:, :, :], A["we_be"].rearrange("p (k n) -> p k n", k=KC)).then_inc(s("w"), 16)
            with sp.Fori(0, 10) as i:
                for h in range(2):
                    sp.wait_ge(s(f"prod_made{h}"), i)
                    sp.dma_start(ea[h][:, :, :], ea_d[bass.ds(i * 2 + h, 1)].rearrange("q p u c -> (q p) u c"))\
                        .then_inc(s(f"ea{h}"), 16)

        @block.scalar
        def _(act):
            act.wait_ge(s("attn_done"), 1)
            nc.scalar.activation(vrow[:, :], m.ps[0:TP, 0, 0:P], ACT.Copy).then_inc(s("vrow"), 1)
            nc.scalar.activation(c0[:, 0:1], m.ps[0:TP, 0, P:P + 1], ACT.Copy).then_inc(s("vrow"), 1)
            act.wait_ge(s("q_made"), 1)
            nc.scalar.activation(m.q[:, :], m.ps[:, 1, 0:KC], ACT.Copy).then_inc(s("vrow"), 1)
            act.wait_ge(s("counted"), 2)
            for t in range(NT):
                nc.scalar.activation(m.count[:, t, 0:4 * TP], m.ps[0:TP, t, 0:4 * TP], ACT.Copy).then_inc(s("count"), 1)
            nc.scalar.activation(m.count[:, 0:4, 4 * TP:N], m.ps[0:TP, 5, 0:4 * TP].rearrange("p (t n) -> p t n", t=4),
                                 ACT.Copy).then_inc(s("count"), 1)
            nc.scalar.activation(m.count[:, 4, 4 * TP:N], m.ps[0:TP, 6, 0:TP], ACT.Copy).then_inc(s("count"), 1)

        @block.vector
        def _(dve):
            steps = Steps(dve, s("dve"))
            for k in range(KC):
                steps(nc.vector.tensor_scalar(attnB[:, k, :], m.ones[:, 0:TP], attn[:, k:k + 1], None, ALU.mult), s("attnB"))
            dve.wait_ge(s("vrow"), 2)
            steps.do(nc.vector.tensor_tensor_reduce(junk[:, :], m.row("L1_gnn_bn"), m.row("L1_gnn_attn"), 1.0, 0.0,
                                                    ALU.mult, ALU.add, c0[:, 1:2]))
            steps.do(nc.vector.tensor_tensor(m.score0[:, :], c0[:, 0:1], c0[:, 1:2], ALU.add))
            with dve.Fori(0, 10) as i:
                for h in range(2):
                    for v in range(4):
                        slot, use = v % 2, i * 4 + (2 * h + v // 2)
                        tile = i * 8 + (4 * h + v)
                        dve.wait_ge(s(f"oh_used{slot}"), use)
                        nc.vector.tensor_scalar(ohs[slot][:, :], m.iota16[0:TP, 0:N], m.src[:, bass.ds(tile, 1)], None,
                                                ALU.is_equal).then_inc(s(f"oh{slot}"), 1)
                        nc.vector.tensor_scalar(ohd[slot][:, :], m.iota16[0:TP, 0:N], m.dst[:, bass.ds(tile, 1)], None,
                                                ALU.is_equal).then_inc(s(f"oh{slot}"), 1)
                    dve.wait_ge(s(f"ea{h}"), (i + 1) * 16)
                    dve.wait_ge(s(f"t_made{h}"), i)
                    nc.vector.tensor_tensor(prod[h][:, :, :], ea[h][:, :, :],
                                            vrow[:, :].unsqueeze(1).to_broadcast([TP, 4, P]), ALU.mult)\
                        .then_inc(s(f"prod_made{h}"), 1)
                    dve.wait_ge(s(f"prod_made{h}"), i + 1)
                    nc.vector.tensor_reduce(m.score_e[:, bass.ds(i * 8 + 4 * h, 4)], prod[h][:, :, :], AX.X, ALU.add)\
                        .then_inc(s(f"t_made{h}"), 1)

        @block.tensor
        def _(pe):
            pe.wait_ge(s("w"), 32)
            pe.wait_ge(s("attnB"), KC)
            for k in range(KC):
                ins = nc.tensor.matmul(m.ps[0:TP, 0, 0:P + 1], attnB[:, k, :], we[:, k, :], start=k == 0, stop=k == KC - 1)
            ins.then_inc(s("attn_done"), 1)
            for c in range(KC):
                for k in range(KC):
                    ins = nc.tensor.matmul(m.ps[:, 1, c:c + 1], wn[:, k, c * P:(c + 1) * P], attn[:, k:k + 1],
                                           start=k == 0, stop=k == KC - 1)
            ins.then_inc(s("q_made"), 1)
            pe.wait_ge(s("vrow"), 3)

            def tile(slot, use, first, last):
                pe.wait_ge(s(f"oh{slot}"), 2 * use + 2)
                for t in range(NT):
                    lhsT = ohs[slot][:, t * TP:(t + 1) * TP]
                    nc.tensor.matmul(m.ps[0:TP, t, 0:4 * TP], lhsT, ohd[slot][:, 0:4 * TP], start=first, stop=last)
                    b, at = (5, t * TP) if t < 4 else (6, 0)
                    ins = nc.tensor.matmul(m.ps[0:TP, b, at:at + TP], lhsT, ohd[slot][:, 4 * TP:N],
                                           start=first and at == 0, stop=last, skip_group_check=True)
                ins.then_inc(s(f"oh_used{slot}"), 1)

            for v in range(4):
                tile(v % 2, v // 2, v == 0, False)
            with pe.Fori(1, 19) as i:
                for v in range(4):
                    tile(v % 2, i * 2 + v // 2, False, False)
            for v in range(4):
                tile(v % 2, 38 + v // 2, False, v == 3)
            pe.wait_ge(s("oh_used0"), ET // 2)
            pe.wait_ge(s("oh_used1"), ET // 2)
            pe.nop(nofuse=True).then_inc(s("counted"), 2)



def l1_gnn(nc, m, A):
    BIG = 1e30
    CH = 2500
    with ExitStack() as ctx:
        st = Stage(nc, ctx, "l1g")
        s, sb = st.sem, st.sb
        arow_d = nc.dram_tensor("l1_scores", (ET, TP), F32, kind="Internal").ap()
        table = nc.dram_tensor("l1_nodes", (N, C + 1), F32, kind="Internal").ap()
        wnT = sb("wnT", [P, KC, C])
        qB = sb("qB", [P, KC, TP])
        line = sb("line", [TP, N])
        junk = [sb(f"junk{v}", [TP, N]) for v in range(2)]
        got = sb("got", [TP, ET])
        ends8 = sb("ends8", [TP, 8])
        got8 = sb("got8", [TP, 8])
        a = sb("a", [TP, ET])
        w = sb("w", [TP, ET])
        at = sb("at", [ET, TP])
        dcol = sb("dcol", [TP, NT])
        dsti = [sb(f"dsti{h}", [TP, CH], I32) for h in range(2)]
        drow = sb("drow", [TP, E], F16)
        arow = [sb(f"arow{h}", [TP, CH]) for h in range(2)]
        off = [sb(f"off{h}", [TP, CH], BF16) for h in range(2)]
        mjunk = sb("mjunk", [TP, CH], BF16)
        mx = sb("mx", [TP, NT, 4])
        mcol = sb("mcol", [TP, NT])
        diag = sb("diag", [TP, NT, TP])
        hs = sb("hs", [TP, NT, C + 1])
        idx = sb("idx", [TP, 8], I32)
        hg = [sb(f"hg{h}", [TP, 4, C + 1]) for h in range(2)]
        woh = [sb(f"woh{v}", [TP, N]) for v in range(2)]
        res = sb("res", [TP, NT, C])
        den = sb("den", [TP, NT])
        block = ctx.enter_context(nc.Block())

        @block.sync
        def _(sp):
            sp.dma_start(wnT[:, :, :], A["wnT"].rearrange("p (k n) -> p k n", k=KC)).then_inc(s("w"), 16)
            with sp.Fori(0, 2) as i:
                for h in range(2):
                    sp.wait_ge(s(f"drow{h}"), i)
                    sp.dma_start(dsti[h][:, :], A["dst"][bass.ds(i * (2 * CH) + h * CH, CH)][None, :].to_broadcast([TP, CH]))\
                        .then_inc(s(f"dsti{h}"), 16)
            sp.wait_ge(s("hs"), NT)
            sp.wait_ge(s("hs1"), 1)
            sp.dma_start(table.rearrange("(t p) c -> p t c", p=TP), hs[:, :, :]).then_inc(s("table"), 16)
            sp.wait_ge(s("at"), 1)
            sp.dma_start(arow_d, at[:, :]).then_inc(s("arow_d"), 16)
            sp.wait_ge(s("arow_d"), 16)
            with sp.Fori(0, 2) as i:
                for h in range(2):
                    sp.wait_ge(s(f"max_done{h}"), i * NT)
                    sp.dma_start(arow[h][:, :],
                                 arow_d.rearrange("t p -> (t p)")[bass.ds(i * (2 * CH) + h * CH, CH)][None, :].to_broadcast([TP, CH]))\
                        .then_inc(s(f"arow{h}"), 16)

        @block.gpsimd
        def _(pool):
            steps = Steps(pool, s("pool"))
            norm_pool(nc, m, pool, st, steps)
            steps.do(nc.gpsimd.memset(hs[:, :, C:C + 1], 1.0), s("hs1"))
            pool.wait_ge(s("table"), 16)

            def gather(i, again=True):
                for h in range(2):
                    if again:
                        pool.wait_ge(s(f"hg{h}"), i * 64)
                        for v in range(2):
                            pool.wait_ge(s(f"woh_used{v}"), i * 4 + (2 * h - 2))
                        pool.nop(nofuse=True)
                    nc.gpsimd.tensor_copy(idx[:, 4 * h:4 * h + 4], m.srci[:, bass.ds(i * 8 + 4 * h, 4)]).then_inc(s("idx"), 1)
                    pool.wait_ge(s("idx"), i * 2 + (h + 1))
                    pool.nop(nofuse=True)
                    for u in range(4):
                        pool.indirect_dma_start(
                            out=hg[h][:, u, :], out_offset=None, in_=table,
                            in_offset=bass.IndirectOffsetOnAxis(ap=idx[:, 4 * h + u:4 * h + u + 1], axis=0),
                        ).then_inc(s(f"hg{h}"), 16)

            gather(0, again=False)
            with pool.Fori(1, 10) as i:
                gather(i)

        @block.scalar
        def _(act):
            norm_scalar(nc, m, act, st)
            act.wait_ge(s("line_made"), 2)
            for n, (x, y) in enumerate(HALF):
                nc.scalar.activation(line[:, x:y], m.ps[0:TP, n, 0:y - x], ACT.Copy).then_inc(s("line"), 1)
            for t in range(NT):
                act.wait_ge(s("h_made"), t + 1)
                nc.scalar.activation(hs[:, t, 0:C], m.ps[0:TP, 3 + t, 0:C], ACT.Copy).then_inc(s("hs"), 1)
            act.wait_ge(s("a_turned"), 1)
            nc.scalar.activation(at[:, :], m.ps[0:ET, 2, 0:TP], ACT.Copy).then_inc(s("at"), 1)
            act.wait_ge(s("mline_made"), 2)
            for n, (x, y) in enumerate(((0, 4 * TP), (4 * TP, N))):
                nc.scalar.activation(line[:, x:y], m.ps[0:TP, n, 0:y - x], ACT.Copy).then_inc(s("line"), 1)
            act.wait_ge(s("w_in"), 1)
            nc.scalar.activation(w[:, :], a[:, :], ACT.Exp).then_inc(s("w_edge"), 1)

        @block.vector
        def _(dve):
            steps = Steps(dve, s("dve"))
            norm_vector(nc, m, dve, st, steps)
            for k in range(KC):
                steps(nc.vector.tensor_scalar(qB[:, k, :], m.ones[:, 0:TP], m.q[:, k:k + 1], None, ALU.mult), s("qB"))
            for t in range(NT):
                steps(nc.vector.tensor_scalar(dcol[:, t:t + 1], m.pcol[0:TP, :], float(t * TP), None, ALU.add))
            with dve.Fori(0, 2) as i:
                for h in range(2):
                    dve.wait_ge(s(f"dsti{h}"), (i + 1) * 16)
                    nc.vector.tensor_copy(drow[:, bass.ds(i * (2 * CH) + h * CH, CH)], dsti[h][:, :]).then_inc(s(f"drow{h}"), 1)

            def pick(ends, name):
                with dve.Fori(0, ET // 8) as i:
                    nc.vector.tensor_copy(ends8[:, :], ends[:, bass.ds(i * 8, 8)]).then_inc(s(f"{name}_ends"), 1)
                    dve.wait_ge(s(f"{name}_ends"), i + 1)
                    dve.wait_ge(s(f"{name}_kept"), i)
                    for v in range(8):
                        dve.wait_ge(s(f"{name}{v % 2}"), i * 4 + v // 2)
                        nc.vector.scalar_tensor_tensor(junk[v % 2][:, :], m.iota[0:TP, 0:N], ends8[:, v:v + 1],
                                                       line[:, :], ALU.is_equal, ALU.mult,
                                                       accum_out=got8[:, v:v + 1]).then_inc(s(f"{name}{v % 2}"), 1)
                    for v in range(2):
                        dve.wait_ge(s(f"{name}{v}"), i * 4 + 4)
                    nc.vector.tensor_copy(got[:, bass.ds(i * 8, 8)], got8[:, :]).then_inc(s(f"{name}_kept"), 1)
                dve.wait_ge(s(f"{name}_kept"), ET // 8)

            dve.wait_ge(s("line"), 2)
            pick(m.src, "got_s")
            steps.do(nc.vector.tensor_tensor(got[:, :], got[:, :], m.score_e[:, :], ALU.add))
            steps.do(nc.vector.tensor_scalar(got[:, :], got[:, :], m.score0[:, :], None, ALU.add))
            steps.do(nc.vector.scalar_tensor_tensor(a[:, :], got[:, :], 0.01, got[:, :], ALU.mult, ALU.max), s("a"))
            for n in range(4):
                dve.wait_ge(s(f"arow{n % 2}"), (n // 2 + 1) * 16)
                for t in range(NT):
                    o = (n * NT + t) % 2
                    steps.do(nc.vector.tensor_scalar(off[o][:, :], drow[:, n * CH:(n + 1) * CH], dcol[:, t:t + 1],
                                                     -BIG, ALU.not_equal, ALU.mult))
                    steps(nc.vector.tensor_tensor_reduce(mjunk[:, :], arow[n % 2][:, :], off[o][:, :], 1.0, -BIG,
                                                         ALU.add, ALU.max, mx[:, t, n:n + 1]), s(f"max_done{n % 2}"))
            steps.settle()
            steps.do(nc.vector.tensor_reduce(mcol[:, :], mx[:, :, :], AX.X, ALU.max))
            for t in range(NT):
                steps(nc.vector.tensor_scalar(diag[:, t, :], m.ident[0:TP, 0:TP], mcol[:, t:t + 1], None, ALU.mult), s("diag"))
            dve.wait_ge(s("line"), 4)
            pick(m.dst, "got_m")
            steps(nc.vector.tensor_tensor(a[:, :], a[:, :], got[:, :], ALU.subtract), s("w_in"))
            dve.wait_ge(s("w_edge"), 1)
            with dve.Fori(0, ET // 4) as i:
                for v in range(4):
                    dve.wait_ge(s(f"woh_used{v % 2}"), i * 2 + v // 2)
                    nc.vector.tensor_scalar(woh[v % 2][:, :], m.iota[0:TP, 0:N], m.dst[:, bass.ds(i * 4 + v, 1)],
                                            w[:, bass.ds(i * 4 + v, 1)], ALU.is_equal, ALU.mult).then_inc(s(f"woh{v % 2}"), 1)
            dve.wait_ge(s("summed"), 1)
            for t in range(NT):
                steps(nc.vector.tensor_scalar(den[:, t:t + 1], m.ps[0:TP, 3 + t, C:C + 1], 1e-16, None, ALU.add))
            steps.settle()
            steps.do(nc.vector.reciprocal(den[:, :], den[:, :]))
            for t in range(NT):
                steps(nc.vector.tensor_scalar(res[:, t, :], m.ps[0:TP, 3 + t, 0:C], den[:, t:t + 1], 0.0, ALU.mult, ALU.max))
            steps.settle()
            for t in range(NT):
                steps(nc.vector.tensor_tensor(m.x[:, t, :], m.x[:, t, :], res[:, t, :], ALU.add))
            steps.settle()

        @block.tensor
        def _(pe):
            norm_tensor(nc, m, pe, st)
            pe.wait_ge(s("xnT_done"), XNT)
            pe.wait_ge(s("qB"), KC)
            for n, (x, y) in enumerate(HALF):
                for k in range(KC):
                    ins = nc.tensor.matmul(m.ps[0:TP, n, 0:y - x], qB[:, k, :], m.xnT[:, k, x:y], start=k == 0, stop=k == KC - 1)
                ins.then_inc(s("line_made"), 1)
            pe.wait_ge(s("w"), 16)
            for t in range(NT):
                for k in range(KC):
                    nc.tensor.matmul(m.ps[0:TP, 3 + t, 0:C], m.xnT[:, k, t * TP:(t + 1) * TP], wnT[:, k, :], start=k == 0,
                                     stop=False)
                nc.tensor.matmul(m.ps[0:TP, 3 + t, 0:C], m.ones[0:1, 0:TP], m.row("L1_gnn_bn", 1), start=False, stop=True)\
                    .then_inc(s("h_made"), 1)
            pe.wait_ge(s("a"), 1)
            nc.tensor.transpose(m.ps[0:ET, 2, 0:TP], a[:, :], m.ident[0:TP, 0:TP]).then_inc(s("a_turned"), 1)
            pe.wait_ge(s("diag"), NT)
            pe.wait_ge(s("line"), 2)
            for t in range(NT):
                b, c = (0, t * TP) if t < 4 else (1, 0)
                ins = nc.tensor.matmul(m.ps[0:TP, b, c:c + TP], m.ones[0:TP, 0:TP], diag[:, t, :], start=True, stop=True)
                if t >= 3:
                    ins.then_inc(s("mline_made"), 1)

            def tile(h, u, i, first, last):
                v = u % 2
                if u == 0:
                    pe.wait_ge(s(f"hg{h}"), (i + 1) * 64)
                pe.wait_ge(s(f"woh{v}"), i * 4 + (2 * h + u // 2 + 1))
                for t in range(NT):
                    ins = nc.tensor.matmul(m.ps[0:TP, 3 + t, 0:C + 1], woh[v][:, t * TP:(t + 1) * TP], hg[h][:, u, :],
                                           start=first, stop=last)
                ins.then_inc(s(f"woh_used{v}"), 1)

            def turn(i, first=False, last=False):
                for h in range(2):
                    for u in range(4):
                        tile(h, u, i, first and h + u == 0, last and h == 1 and u == 3)

            turn(0, first=True)
            with pe.Fori(1, 9) as i:
                turn(i)
            turn(9, last=True)
            for v in range(2):
                pe.wait_ge(s(f"woh_used{v}"), ET // 2)
            pe.nop(nofuse=True).then_inc(s("summed"), 1)



class Experts:

    def __init__(self, hidden):
        self.hidden = hidden
        self.units = []
        for layer, chunks_ in enumerate(hidden):
            for e in range(2):
                for half in range(2):
                    for c in range(chunks_):
                        self.units.append((layer, e, half, c))
        for e in range(2):
            for t in range(NT):
                self.units.append((len(hidden), e, t, 0))
        self.uses = [len(range(b, len(self.units), 8)) for b in range(8)]
        self.at = {u: k for k, u in enumerate(self.units)}

    def before(self, k, i):
        return i * self.uses[k % 8] + k // 8

    def after(self, k, i):
        return i * self.uses[k % 8] + (k // 8 + 1)

    def last_reader(self, layer, e):
        return max(k for k, u in enumerate(self.units) if u[0] == layer and u[1] == e)

    def load(self, sp, s, i, bufs, source, again=True):
        for layer in range(len(self.hidden) + 1):
            for e in range(2):
                if again:
                    k = self.last_reader(layer, e)
                    sp.wait_ge(s(f"made{k % 8}"), self.after(k, i) - self.uses[k % 8])
                sp.dma_start(bufs[layer][e][:, :], source[bass.ds(i * 2 + e, 1), layer].rearrange("a p n -> (a p) n"))\
                    .then_inc(s(f"w{layer}{e}"), 16)

    def tensor(self, nc, m, pe, s, i, bufs, hT):
        for k, (layer, e, part, c) in enumerate(self.units):
            pe.wait_ge(s(f"free{k % 8}"), self.before(k, i))
            if k == min(self.at[u] for u in self.units if u[0] == layer and u[1] == e):
                pe.wait_ge(s(f"w{layer}{e}"), (i + 1) * 16)
            final = layer == len(self.hidden)
            if layer:
                below = self.hidden[layer - 1]
                for half in ([part] if not final else [0] if part < 2 else [0, 1]):
                    for b in range(below):
                        j = self.at[(layer - 1, e, half, b)]
                        pe.wait_ge(s(f"free{j % 8}"), self.after(j, i))
            src = m.xnT if layer == 0 else hT[layer - 1][e]
            kin = KC if layer == 0 else self.hidden[layer - 1]
            w = bufs[layer][e][:, :].rearrange("p (k n) -> p k n", k=kin)
            for j in range(kin):
                if final:
                    ins = nc.tensor.matmul(m.ps[0:TP, k % 8, 0:C], src[:, j, part * TP:(part + 1) * TP], w[:, j, :],
                                           start=j == 0, stop=j == kin - 1)
                else:
                    a, b = HALF[part]
                    ins = nc.tensor.matmul(m.ps[:, k % 8, 0:b - a], w[:, j, c * P:(c + 1) * P], src[:, j, a:b],
                                           start=j == 0, stop=j == kin - 1)
            ins.then_inc(s(f"made{k % 8}"), 1)

    def scalar(self, nc, m, act, s, i, hT, coef):
        for k, (layer, e, part, c) in enumerate(self.units):
            if layer < len(self.hidden):
                a, b = HALF[part]
                scale, bias = coef(layer, i * 2 + e, c)
                act.wait_ge(s(f"made{k % 8}"), self.after(k, i))
                act.nop(nofuse=True)
                nc.scalar.activation(hT[layer][e][:, c, a:b], m.ps[:, k % 8, 0:b - a], ACT.Relu, bias=bias, scale=scale)\
                    .then_inc(s(f"free{k % 8}"), 1)

    def vector(self, nc, m, dve, s, i, gate, acc):
        final = len(self.hidden)
        for k, (layer, e, t, _) in enumerate(self.units):
            if layer == final:
                dve.wait_ge(s(f"made{k % 8}"), self.after(k, i))
                j = self.at[(final, 1 - e, t, 0)]
                dve.wait_ge(s(f"free{j % 8}"), self.after(j, i) - (self.uses[j % 8] if e == 0 else 0))
                nc.vector.scalar_tensor_tensor(acc[:, t, :], m.ps[0:TP, k % 8, 0:C], gate[:, t, bass.ds(i * 2 + e, 1)],
                                               acc[:, t, :], ALU.mult, ALU.add).then_inc(s(f"free{k % 8}"), 1)


def gate_tensor(nc, m, pe, s, wr, ne, bias, last_bias):
    pe.wait_ge(s("xnT_done"), XNT)
    pe.wait_ge(s("small"), 32)
    for t in range(NT):
        for k in range(KC):
            nc.tensor.matmul(m.ps[0:TP, 3, t * ne:(t + 1) * ne], m.xnT[:, k, t * TP:(t + 1) * TP], wr[:, k, :],
                             start=k == 0, stop=False)
        nc.tensor.matmul(m.ps[0:TP, 3, t * ne:(t + 1) * ne], m.ones[0:1, 0:TP], m.row(bias, 1), start=False, stop=True)\
            .then_inc(s("scores"), 1)


def gate_turn(nc, m, pe, s, gate, gateT, ne, last_bias):
    pe.wait_ge(s("gate"), 1)
    for t in range(NT):
        b, c = (4, t * TP) if t < 4 else (5, 0)
        nc.tensor.transpose(m.ps[0:ne, b, c:c + TP], gate[:, t, :], m.ident[0:TP, 0:TP]).then_inc(s("gate_turned"), 1)
    pe.wait_ge(s("gateT"), 2)
    for t in range(NT):
        b = t if t < 3 else t + 3
        nc.tensor.matmul(m.ps[0:TP, b, 0:C], gateT[:, t * TP:(t + 1) * TP], last_bias[:, :], start=True, stop=True)\
            .then_inc(s("bias_made"), 1)


def gate_scalar(nc, m, act, s, gateT, acc, ne):
    act.wait_ge(s("gate_turned"), NT)
    nc.scalar.activation(gateT[:, 0:4 * TP], m.ps[0:ne, 4, 0:4 * TP], ACT.Copy).then_inc(s("gateT"), 1)
    nc.scalar.activation(gateT[:, 4 * TP:N], m.ps[0:ne, 5, 0:TP], ACT.Copy).then_inc(s("gateT"), 1)
    for t in range(NT):
        act.wait_ge(s("bias_made"), t + 1)
        nc.scalar.activation(acc[:, t, :], m.ps[0:TP, t if t < 3 else t + 3, 0:C], ACT.Copy).then_inc(s("acc"), 1)


def l1_ffn(nc, m, A):
    NE = 8
    plan = Experts([2, 2])
    with ExitStack() as ctx:
        st = Stage(nc, ctx, "l1f")
        s, sb = st.sem, st.sb
        wr = sb("wr", [P, KC, NE])
        bo = sb("bo", [NE, C])
        bufs = [[m.w[e][:, 512 * l:512 * (l + 1)] for e in range(2)] for l in range(3)]
        hT = [[sb(f"h{l}{e}", [P, 2, N]) for e in range(2)] for l in range(2)]
        coefs = sb("coefs", [P, 4, 2 * NE])
        cv = sb("cv", [P, 2, 2 * NE])
        half16 = m.mhalf
        score = sb("score", [TP, NT, NE])
        top = sb("top", [TP, NT])
        tot = sb("tot", [TP, NT])
        gate = sb("gate", [TP, NT, NE])
        gateT = sb("gateT", [NE, N])
        acc = sb("acc", [TP, NT, C])
        block = ctx.enter_context(nc.Block())

        @block.sync
        def _(sp):
            sp.dma_start(wr[:, :, :], A["l1f_wr"].rearrange("p (k e) -> p k e", k=KC)).then_inc(s("small"), 16)
            sp.dma_start(bo[:, :], A["L1_ffn_bo"]).then_inc(s("small"), 16)
            plan.load(sp, s, 0, bufs, A["l1f_w"], again=False)
            with sp.Fori(1, NE // 2) as i:
                plan.load(sp, s, i, bufs, A["l1f_w"])

        @block.gpsimd
        def _(pool):
            steps = Steps(pool, s("pool"))
            norm_pool(nc, m, pool, st, steps)
            for n in range(2):
                p = lambda name: m.col(f"L1_ffn_{name}{n + 1}")
                steps.do(nc.gpsimd.tensor_scalar(cv[:, 0, :], p("v"), 1e-3, None, ALU.add))
                steps.do(nc.gpsimd.tensor_tensor(cv[:, 1, :], cv[:, 0, :], m.mhalf[:, :], ALU.pow))
                steps.do(nc.gpsimd.tensor_tensor(coefs[:, 2 * n, :], cv[:, 1, :], p("g"), ALU.mult))
                steps.do(nc.gpsimd.tensor_tensor(cv[:, 0, :], p("b"), p("m"), ALU.subtract))
                steps.do(nc.gpsimd.tensor_tensor(cv[:, 1, :], cv[:, 0, :], coefs[:, 2 * n, :], ALU.mult))
                steps.do(nc.gpsimd.tensor_tensor(coefs[:, 2 * n + 1, :], cv[:, 1, :], p("be"), ALU.add), s("coefs"))

        def coef(layer, e, c):
            return coefs[:, 2 * layer, bass.ds(e * 2 + c, 1)], coefs[:, 2 * layer + 1, bass.ds(e * 2 + c, 1)]

        @block.scalar
        def _(act):
            norm_scalar(nc, m, act, st)
            act.wait_ge(s("exp_in"), 1)
            nc.scalar.activation(gate[:, :, :], score[:, :, :], ACT.Exp).then_inc(s("exp_out"), 1)
            gate_scalar(nc, m, act, s, gateT, acc, NE)
            act.wait_ge(s("coefs"), 2)
            with act.Fori(0, NE // 2) as i:
                plan.scalar(nc, m, act, s, i, hT, coef)

        @block.vector
        def _(dve):
            steps = Steps(dve, s("dve"))
            norm_vector(nc, m, dve, st, steps)
            dve.wait_ge(s("scores"), NT)
            steps.do(nc.vector.tensor_copy(score[:, :, :], m.ps[0:TP, 3, 0:NT * NE].rearrange("p (t e) -> p t e", t=NT)))
            steps.do(nc.vector.tensor_reduce(top[:, :], score[:, :, :], AX.X, ALU.max))
            steps(nc.vector.tensor_tensor(score[:, :, :], score[:, :, :], top[:, :].unsqueeze(2).to_broadcast([TP, NT, NE]),
                                          ALU.subtract), s("exp_in"))
            dve.wait_ge(s("exp_out"), 1)
            steps.do(nc.vector.tensor_reduce(tot[:, :], gate[:, :, :], AX.X, ALU.add))
            steps.do(nc.vector.reciprocal(top[:, :], tot[:, :]))
            steps(nc.vector.tensor_tensor(gate[:, :, :], gate[:, :, :], top[:, :].unsqueeze(2).to_broadcast([TP, NT, NE]),
                                          ALU.mult), s("gate"))
            dve.wait_ge(s("acc"), NT)
            dve.wait_ge(s("gate"), 1)
            with dve.Fori(0, NE // 2) as i:
                plan.vector(nc, m, dve, s, i, gate, acc)
            for b in range(8):
                dve.wait_ge(s(f"free{b}"), plan.uses[b] * (NE // 2))
            for t in range(NT):
                steps(nc.vector.tensor_tensor(m.x[:, t, :], m.x[:, t, :], acc[:, t, :], ALU.add))
            steps.settle()

        @block.tensor
        def _(pe):
            norm_tensor(nc, m, pe, st)
            gate_tensor(nc, m, pe, s, wr, NE, "L1_ffn_br", bo)
            gate_turn(nc, m, pe, s, gate, gateT, NE, bo)
            pe.wait_ge(s("acc"), NT)
            with pe.Fori(0, NE // 2) as i:
                plan.tensor(nc, m, pe, s, i, bufs, hT)



def l2_gnn(nc, m, A):
    D1, D2 = 128, 64
    with ExitStack() as ctx:
        st = Stage(nc, ctx, "l2g")
        s, sb = st.sem, st.sb
        W = m.w[0]
        w1 = W[:, 0:256].rearrange("p (k n) -> p k n", k=KC)
        wfc = W[:, 256:1280].rearrange("p (k n) -> p k n", k=4)
        w2 = W[:, 1280:1344]
        adj = sb("adj", [TP, NT, N])
        dinvT = sb("dinvT", [P, N])
        diag = sb("diag", [TP, NT, TP])
        deg = sb("deg", [TP, NT])
        dinv = sb("dinv", [TP, NT])
        h1 = sb("h1", [TP, NT, D1])
        h2 = sb("h2", [TP, NT, D2])
        o = [sb(f"o{n}", [P, N]) for n in range(2)]
        xT = [sb(f"xT{n}", [P, N]) for n in range(2)]
        bst = sb("bst", [P, NT, 6])
        bmv = sb("bmv", [P, 2])
        bt = sb("bt", [P, 8])
        b2 = sb("b2", [D2, 4])
        res = sb("res", [TP, NT, C])
        block = ctx.enter_context(nc.Block())
        dims = [D1, D2]

        @block.sync
        def _(sp):
            sp.dma_start(W[:, 0:1344], A["w_l2g"]).then_inc(s("w"), 16)
            sp.dma_start(b2[:, 0:3], A["l2g_small"]).then_inc(s("w"), 16)

        @block.gpsimd
        def _(pool):
            steps = Steps(pool, s("pool"))
            norm_pool(nc, m, pool, st, steps)
            pool.wait_ge(s("deg"), 1)
            steps(nc.gpsimd.tensor_tensor(dinv[:, :], deg[:, :], m.mhalf[0:TP, 0:NT], ALU.pow), s("dinv"))
            for n, d in enumerate(dims):
                pool.wait_ge(s("bn_var"), n + 1)
                steps.do(nc.gpsimd.tensor_scalar(bt[0:d, 0:1], bmv[0:d, 1:2], 1e-5, None, ALU.add))
                steps(nc.gpsimd.tensor_tensor(bt[0:d, 1:2], bt[0:d, 0:1], m.mhalf[0:d, 0:1], ALU.pow), s("bn_rstd"))

        @block.scalar
        def _(act):
            norm_scalar(nc, m, act, st)
            act.wait_ge(s("deg_made"), 1)
            nc.scalar.activation(deg[:, :], m.ps[0:TP, 5, 0:NT], ACT.Copy).then_inc(s("deg"), 1)
            act.wait_ge(s("dinvT_made"), 2)
            for n, (a, b) in enumerate(((0, 4 * TP), (4 * TP, N))):
                nc.scalar.activation(dinvT[:, a:b], m.ps[:, 1 + n, 0:b - a], ACT.Copy).then_inc(s("dinvT"), 1)
            for n, (d, h) in enumerate(((D1, h1), (D2, h2))):
                for t in range(NT):
                    act.wait_ge(s(f"h_made{n}"), t + 1)
                    nc.scalar.activation(h[:, t, :], m.ps[0:TP, 3 + t, 0:d], ACT.Copy, scale=dinv[:, t:t + 1]).then_inc(s(f"h{n}"), 1)
                act.wait_ge(s("bn_coef"), n + 1)
                nc.scalar.activation(xT[n][0:d, :], o[n][0:d, :], ACT.Relu, bias=bt[0:d, 3:4], scale=bt[0:d, 2:3])\
                    .then_inc(s("xT"), 1)

        @block.vector
        def _(dve):
            steps = Steps(dve, s("dve"))
            for t in range(NT):
                steps(nc.vector.tensor_copy(adj[:, t, :], m.count[:, t, :]))
            steps.settle()
            for t in range(NT):
                steps(nc.vector.tensor_tensor(adj[:, t, t * TP:(t + 1) * TP], adj[:, t, t * TP:(t + 1) * TP],
                                              m.ident[0:TP, 0:TP], ALU.add), s("adj"))
            norm_vector(nc, m, dve, st, steps)
            dve.wait_ge(s("dinv"), 1)
            for t in range(NT):
                steps(nc.vector.tensor_scalar(diag[:, t, :], m.ident[0:TP, 0:TP], dinv[:, t:t + 1], None, ALU.mult), s("diag"))
            dve.wait_ge(s("dinvT"), 2)
            dve.wait_ge(s("w"), 32)
            for n, d in enumerate(dims):
                bias, gam, bet = [m.col("L2_gnn_" + x)[:, 0:1] for x in ("b1", "g1", "be1")] if n == 0 else \
                    [b2[:, x:x + 1] for x in range(3)]
                for i, (a, b) in enumerate(HALF):
                    dve.wait_ge(s(f"o_made{n}"), i + 1)
                    steps.do(nc.vector.tensor_tensor(o[n][0:d, a:b], m.ps[0:d, 1 + i, 0:b - a], dinvT[0:d, a:b], ALU.mult))
                    steps.do(nc.vector.tensor_scalar(o[n][0:d, a:b], o[n][0:d, a:b], bias, None, ALU.add))
                for t in range(NT):
                    steps(nc.vector.bn_stats(bst[0:d, t, :], o[n][0:d, t * TP:(t + 1) * TP]))
                steps.settle()
                steps(nc.vector.bn_aggr(bmv[0:d, :], bst[0:d, :, :].rearrange("p t s -> p (t s)")), s("bn_var"))
                dve.wait_ge(s("bn_rstd"), n + 1)
                steps.do(nc.vector.tensor_tensor(bt[0:d, 2:3], bt[0:d, 1:2], gam, ALU.mult))
                steps.do(nc.vector.tensor_tensor(bt[0:d, 4:5], bmv[0:d, 0:1], bt[0:d, 2:3], ALU.mult))
                steps(nc.vector.tensor_tensor(bt[0:d, 3:4], bet, bt[0:d, 4:5], ALU.subtract), s("bn_coef"))
                if n == 0:
                    dve.wait_ge(s("xT"), 1)
            for t in range(NT):
                dve.wait_ge(s("fc_made"), t + 1)
                steps.do(nc.vector.tensor_scalar(res[:, t, :], m.ps[0:TP, 3 + t, 0:C], 0.0, None, ALU.max))
                steps(nc.vector.tensor_tensor(m.x[:, t, :], m.x[:, t, :], res[:, t, :], ALU.add))
            steps.settle()

        @block.tensor
        def _(pe):
            pe.wait_ge(s("adj"), NT)
            for d in range(NT):
                for t in range(NT):
                    ins = nc.tensor.matmul(m.ps[0:TP, 5, d:d + 1], adj[:, t, d * TP:(d + 1) * TP], m.ones[0:TP, 0:1],
                                           start=t == 0, stop=t == NT - 1)
            ins.then_inc(s("deg_made"), 1)
            norm_tensor(nc, m, pe, st)
            pe.wait_ge(s("xnT_done"), XNT)
            pe.wait_ge(s("w"), 32)
            pe.wait_ge(s("diag"), NT)
            for t in range(NT):
                b, c = (1, t * TP) if t < 4 else (2, 0)
                ins = nc.tensor.matmul(m.ps[:, b, c:c + TP], m.ones[0:TP, :], diag[:, t, :], start=True, stop=True)
                if t >= 3:
                    ins.then_inc(s("dinvT_made"), 1)
            for t in range(NT):
                for k in range(KC):
                    ins = nc.tensor.matmul(m.ps[0:TP, 3 + t, 0:D1], m.xnT[:, k, t * TP:(t + 1) * TP], w1[:, k, :],
                                           start=k == 0, stop=k == KC - 1)
                ins.then_inc(s("h_made0"), 1)
            for n, (d, h) in enumerate(((D1, h1), (D2, h2))):
                if n == 1:
                    pe.wait_ge(s("xT"), 1)
                    for t in range(NT):
                        nc.tensor.matmul(m.ps[0:TP, 3 + t, 0:D2], xT[0][:, t * TP:(t + 1) * TP], w2[:, :], start=True,
                                         stop=True).then_inc(s("h_made1"), 1)
                pe.wait_ge(s(f"h{n}"), NT)
                pe.wait_ge(s("dinvT"), 2)
                for i, (a, b) in enumerate(HALF):
                    for t in range(NT):
                        ins = nc.tensor.matmul(m.ps[0:d, 1 + i, 0:b - a], h[:, t, :], adj[:, t, a:b], start=t == 0,
                                               stop=t == NT - 1)
                    ins.then_inc(s(f"o_made{n}"), 1)
            pe.wait_ge(s("xT"), 2)
            for t in range(NT):
                cols = slice(t * TP, (t + 1) * TP)
                parts = [(m.xnT[:, 0, cols], wfc[:, 0, :]), (m.xnT[:, 1, cols], wfc[:, 1, :]), (xT[0][:, cols], wfc[:, 2, :]),
                         (xT[1][0:D2, cols], wfc[0:D2, 3, :]), (m.ones[0:1, 0:TP], m.row("L2_gnn_bfc", 1))]
                for j, (lhsT, rhs) in enumerate(parts):
                    ins = nc.tensor.matmul(m.ps[0:TP, 3 + t, 0:C], lhsT, rhs, start=j == 0, stop=j == 4)
                ins.then_inc(s("fc_made"), 1)


def l2_ffn(nc, m, A):
    NE = 16
    plan = Experts([4])
    with ExitStack() as ctx:
        st = Stage(nc, ctx, "l2f")
        s, sb = st.sem, st.sb
        wr = sb("wr", [P, KC, NE])
        b2 = sb("b2", [NE, C])
        bufs = [[m.w[e][:, 1024 * l:1024 * (l + 1)] for e in range(2)] for l in range(2)]
        hT = [[sb(f"h{e}", [P, 4, N]) for e in range(2)]]
        score = sb("score", [TP, NT, NE])
        left = sb("left", [TP, NT, NE])
        pick = sb("pick", [TP, 2, NT, NE])
        low = sb("low", [TP, NT, NE])
        top = sb("top", [TP, 8, NT])
        gate = sb("gate", [TP, NT, NE])
        gateT = sb("gateT", [NE, N])
        acc = sb("acc", [TP, NT, C])
        z = sb("z", [TP, NT, C])
        block = ctx.enter_context(nc.Block())

        @block.sync
        def _(sp):
            sp.dma_start(wr[:, :, :], A["l2f_wr"].rearrange("p (k e) -> p k e", k=KC)).then_inc(s("small"), 16)
            sp.dma_start(b2[:, :], A["L2_ffn_b2"]).then_inc(s("small"), 16)
            plan.load(sp, s, 0, bufs, A["l2f_w"], again=False)
            with sp.Fori(1, NE // 2) as i:
                plan.load(sp, s, i, bufs, A["l2f_w"])

        @block.gpsimd
        def _(pool):
            steps = Steps(pool, s("pool"))
            norm_pool(nc, m, pool, st, steps)
            pool.wait_ge(s("z_stats"), NT)
            steps.do(nc.gpsimd.tensor_scalar(m.veps[0:TP, :], m.mv[:, :, 1], 1e-5, None, ALU.add))
            steps(nc.gpsimd.tensor_tensor(m.rstd[0:TP, :], m.veps[0:TP, :], m.mhalf[0:TP, 0:NT], ALU.pow), s("z_rstd"))

        def coef(layer, e, c):
            return 1.0, m.col("L2_ffn_b1")[:, bass.ds(e * 4 + c, 1)]

        @block.scalar
        def _(act):
            norm_scalar(nc, m, act, st)
            act.wait_ge(s("exp_in"), 1)
            nc.scalar.activation(top[:, 3, :], top[:, 2, :], ACT.Exp).then_inc(s("exp_out"), 1)
            gate_scalar(nc, m, act, s, gateT, acc, NE)
            with act.Fori(0, NE // 2) as i:
                plan.scalar(nc, m, act, s, i, hT, coef)

        @block.vector
        def _(dve):
            def wide(ap):
                return ap.unsqueeze(2).to_broadcast([TP, NT, NE])

            steps = Steps(dve, s("dve"))
            norm_vector(nc, m, dve, st, steps)
            dve.wait_ge(s("scores"), NT)
            steps.do(nc.vector.tensor_copy(score[:, :, :], m.ps[0:TP, 3, 0:NT * NE].rearrange("p (t e) -> p t e", t=NT)))
            iota = m.iota[0:TP, 0:NE].unsqueeze(1).to_broadcast([TP, NT, NE])
            src = score
            for j in range(2):
                steps.do(nc.vector.tensor_reduce(top[:, j, :], src[:, :, :], AX.X, ALU.max))
                steps.do(nc.vector.tensor_tensor(low[:, :, :], src[:, :, :], wide(top[:, j, :]), ALU.is_equal))
                steps.do(nc.vector.tensor_scalar(low[:, :, :], low[:, :, :], -1000.0, None, ALU.mult))
                steps.do(nc.vector.tensor_tensor(low[:, :, :], low[:, :, :], iota, ALU.add))
                steps.do(nc.vector.tensor_reduce(top[:, 4 + j, :], low[:, :, :], AX.X, ALU.min))
                steps.do(nc.vector.tensor_tensor(pick[:, j, :, :], low[:, :, :], wide(top[:, 4 + j, :]), ALU.is_equal))
                if j == 0:
                    steps.do(nc.vector.tensor_scalar(low[:, :, :], pick[:, 0, :, :], -1e30, None, ALU.mult))
                    steps.do(nc.vector.tensor_tensor(left[:, :, :], score[:, :, :], low[:, :, :], ALU.add))
                    src = left
            steps(nc.vector.tensor_tensor(top[:, 2, :], top[:, 1, :], top[:, 0, :], ALU.subtract), s("exp_in"))
            dve.wait_ge(s("exp_out"), 1)
            steps.do(nc.vector.tensor_scalar(top[:, 6, :], top[:, 3, :], 1.0, None, ALU.add))
            steps.do(nc.vector.reciprocal(top[:, 7, :], top[:, 6, :]))
            steps.do(nc.vector.tensor_tensor(top[:, 6, :], top[:, 3, :], top[:, 7, :], ALU.mult))
            steps.do(nc.vector.tensor_tensor(low[:, :, :], pick[:, 0, :, :], wide(top[:, 7, :]), ALU.mult))
            steps.do(nc.vector.tensor_tensor(left[:, :, :], pick[:, 1, :, :], wide(top[:, 6, :]), ALU.mult))
            steps(nc.vector.tensor_tensor(gate[:, :, :], low[:, :, :], left[:, :, :], ALU.add), s("gate"))
            dve.wait_ge(s("gate"), 1)
            dve.wait_ge(s("acc"), NT)
            with dve.Fori(0, NE // 2) as i:
                plan.vector(nc, m, dve, s, i, gate, acc)
            for b in range(8):
                dve.wait_ge(s(f"free{b}"), plan.uses[b] * (NE // 2))
            for t in range(NT):
                steps(nc.vector.tensor_tensor(z[:, t, :], acc[:, t, :], m.xn[:, t, :], ALU.add))
            steps.settle()
            norm_tail(nc, m, dve, s, steps, z, acc, "L2_ffn_gamma", "L2_ffn_beta")

        @block.tensor
        def _(pe):
            norm_tensor(nc, m, pe, st)
            gate_tensor(nc, m, pe, s, wr, NE, "L2_ffn_gate_b", b2)
            gate_turn(nc, m, pe, s, gate, gateT, NE, b2)
            pe.wait_ge(s("acc"), NT)
            with pe.Fori(0, NE // 2) as i:
                plan.tensor(nc, m, pe, s, i, bufs, hT)


def norm_tail(nc, m, dve, s, steps, z, other, gamma, beta, extra=None):
    for t in range(NT):
        steps(nc.vector.bn_stats(m.stats[:, t, :], z[:, t, :]))
    steps.settle()
    for t in range(NT):
        steps(nc.vector.bn_aggr(m.mv[:, t, :], m.stats[:, t, :]), s("z_stats"))
    if extra is not None:
        for t in range(NT):
            steps(nc.vector.tensor_tensor(m.x[:, t, :], m.x[:, t, :], extra[:, t, :], ALU.add))
    dve.wait_ge(s("z_rstd"), 1)
    for t in range(NT):
        steps(nc.vector.tensor_scalar(other[:, t, :], z[:, t, :], m.mv[:, t, 0:1], m.rstd[0:TP, t:t + 1],
                                      ALU.subtract, ALU.mult))
    steps.settle()
    for src, dst, op, with_ in ((other, z, ALU.mult, gamma), (z, other, ALU.add, beta)):
        for t in range(NT):
            steps(nc.vector.tensor_tensor(dst[:, t, :], src[:, t, :], m.row(with_), op))
        steps.settle()
    for t in range(NT):
        steps(nc.vector.tensor_tensor(m.x[:, t, :], m.x[:, t, :], other[:, t, :], ALU.add))
    steps.settle()



def l3_gnn(nc, m, A):
    with ExitStack() as ctx:
        st = Stage(nc, ctx, "l3g")
        s, sb = st.sem, st.sb
        W = m.w[0]
        wl = W[:, 0:512].rearrange("p (k n) -> p k n", k=KC)
        wr = W[:, 512:1024].rearrange("p (k n) -> p k n", k=KC)
        rdeg = sb("rdeg", [P, N])
        aggT = sb("aggT", [P, KC, N])
        f = sb("f", [TP, NT, C])
        g = sb("g", [TP, NT, C])
        block = ctx.enter_context(nc.Block())

        @block.sync
        def _(sp):
            sp.dma_start(W[:, 0:1024], A["w_l3g"]).then_inc(s("w"), 16)

        @block.gpsimd
        def _(pool):
            steps = Steps(pool, s("pool"))
            norm_pool(nc, m, pool, st, steps)
            pool.wait_ge(s("z_stats"), NT)
            steps.do(nc.gpsimd.tensor_scalar(m.veps[0:TP, :], m.mv[:, :, 1], 1e-5, None, ALU.add))
            steps(nc.gpsimd.tensor_tensor(m.rstd[0:TP, :], m.veps[0:TP, :], m.mhalf[0:TP, 0:NT], ALU.pow), s("z_rstd"))

        @block.scalar
        def _(act):
            norm_scalar(nc, m, act, st)
            for t in range(NT):
                act.wait_ge(s("f_made"), t + 1)
                nc.scalar.activation(f[:, t, :], m.ps[0:TP, t, 0:C], ACT.Gelu).then_inc(s("f"), 1)

        @block.vector
        def _(dve):
            steps = Steps(dve, s("dve"))
            norm_vector(nc, m, dve, st, steps)
            for n, (a, b) in enumerate(HALF):
                dve.wait_ge(s("deg_made"), n + 1)
                steps.do(nc.vector.tensor_scalar(rdeg[:, a:b], m.ps[:, 3 + n, 0:b - a], 1.0, None, ALU.max))
            steps.do(nc.vector.reciprocal(rdeg[:, :], rdeg[:, :]))
            unit = 0
            for c in range(KC):
                for (a, b) in HALF:
                    dve.wait_ge(s("agg_made"), unit + 1)
                    steps(nc.vector.tensor_tensor(aggT[:, c, a:b], m.ps[:, 3 + unit, 0:b - a], rdeg[:, a:b], ALU.mult), s("aggT"))
                    unit += 1
            dve.wait_ge(s("f"), NT)
            norm_tail(nc, m, dve, s, steps, f, g, "L3_gnn_ln_gamma", "L3_gnn_ln_beta", extra=m.xn)

        @block.tensor
        def _(pe):
            for n, (a, b) in enumerate(HALF):
                for t in range(NT):
                    ins = nc.tensor.matmul(m.ps[:, 3 + n, 0:b - a], m.ones[0:TP, :], m.count[:, t, a:b], start=t == 0,
                                           stop=t == NT - 1)
                ins.then_inc(s("deg_made"), 1)
            norm_tensor(nc, m, pe, st)
            pe.wait_ge(s("dve"), NT + 2)
            unit = 0
            for c in range(KC):
                for (a, b) in HALF:
                    for t in range(NT):
                        ins = nc.tensor.matmul(m.ps[:, 3 + unit, 0:b - a], m.xn[:, t, c * P:(c + 1) * P], m.count[:, t, a:b],
                                               start=t == 0, stop=t == NT - 1)
                    ins.then_inc(s("agg_made"), 1)
                    unit += 1
            pe.wait_ge(s("w"), 16)
            pe.wait_ge(s("xnT_done"), XNT)
            pe.wait_ge(s("aggT"), 4)
            for t in range(NT):
                cols = slice(t * TP, (t + 1) * TP)
                parts = [(aggT[:, k, cols], wl[:, k, :]) for k in range(KC)] + [(m.xnT[:, k, cols], wr[:, k, :]) for k in range(KC)] + \
                    [(m.ones[0:1, 0:TP], m.row("L3_gnn_b_l", 1))]
                for j, (lhsT, rhs) in enumerate(parts):
                    ins = nc.tensor.matmul(m.ps[0:TP, t, 0:C], lhsT, rhs, start=j == 0, stop=j == len(parts) - 1)
                ins.then_inc(s("f_made"), 1)



def l3_ffn(nc, m, A):
    NH, D, G = 8, 64, 64
    SCALE = D ** -0.5
    with ExitStack() as ctx:
        st = Stage(nc, ctx, "l3f")
        s, sb = st.sem, st.sb
        wfx = m.w[0][:, 0:1024].rearrange("p (k n) -> p k n", k=KC)
        wxT = m.w[1][0:D, 0:2048].rearrange("p (h c) -> p h c", h=NH)
        wout = m.w[1][0:D, 2048:4096].rearrange("p (h c) -> p h c", h=NH)
        small = m.w[1][0:D, 4096:4096 + 4 * D + NH].rearrange("p n -> p n")
        wsl, wq, wk, wv = [small[:, D * i:D * (i + 1)] for i in range(4)]
        bxT = small[:, 4 * D:4 * D + NH]
        itemp = sb("itemp", [P, NH])
        wc = sb("wc", [P, KC, NH, G])
        bc = sb("bc", [1, NH, G])
        sw = sb("sw", [TP, NT, NH, G])
        mx = sb("mx", [TP, NT, NH])
        rs = sb("rs", [TP, NT, NH])
        zT = sb("zT", [P, KC, NH * G])
        norm = sb("norm", [G, NH * G])
        rnorm = sb("rnorm", [G, NH * G])
        tokT = sb("tokT", [D, NH * G])
        qT = sb("qT", [D, NH * G])
        kT = sb("kT", [D, NH * G])
        v = sb("v", [G, NH, D])
        at = sb("at", [G, NH, G])
        amx = sb("amx", [G, NH])
        atT = sb("atT", [G, NH, G])
        osT = sb("osT", [D, NH, G])
        pw = sb("pw", [G, NH, C])
        swT = sb("swT", [G, NH, N])
        block = ctx.enter_context(nc.Block())

        @block.sync
        def _(sp):
            sp.dma_start(m.w[0][:, 0:1024], A["l3f_wfx"]).then_inc(s("w"), 16)
            sp.dma_start(m.w[1][0:D, 0:4096 + 4 * D + NH], A["l3f_w64"]).then_inc(s("w"), 16)

        @block.gpsimd
        def _(pool):
            steps = Steps(pool, s("pool"))
            norm_pool(nc, m, pool, st, steps)

        @block.scalar
        def _(act):
            norm_scalar(nc, m, act, st)
            for t in range(NT):
                act.wait_ge(s("sw_in"), t + 1)
                nc.scalar.activation(sw[:, t, :, :], sw[:, t, :, :], ACT.Exp).then_inc(s("sw_exp"), 1)
            for j in range(2):
                act.wait_ge(s("qk_made"), j + 1)
                nc.scalar.activation((qT, kT)[j][:, :], m.ps[0:D, 2 + j, :], ACT.Copy).then_inc(s("qk"), 1)
            act.wait_ge(s("v_made"), 1)
            nc.scalar.activation(v[:, :, :], m.ps[0:G, 4, :].rearrange("p (h d) -> p h d", h=NH), ACT.Copy).then_inc(s("v"), 1)
            for h in range(NH):
                for n in range(2):
                    act.wait_ge(s("sw_turned"), 2 * h + n + 1)
                    a, b = ((0, 4 * TP), (4 * TP, N))[n]
                    nc.scalar.activation(swT[:, h, a:b], m.ps[0:G, 6 + n, 0:b - a], ACT.Copy).then_inc(s("swT"), 1)
            act.wait_ge(s("at_in"), 1)
            nc.scalar.activation(at[:, :, :], at[:, :, :], ACT.Exp, scale=SCALE).then_inc(s("at_exp"), 1)
            act.wait_ge(s("atT_made"), 1)
            nc.scalar.activation(atT[:, :, :], m.ps[0:G, 0, :].rearrange("p (h d) -> p h d", h=NH), ACT.Copy).then_inc(s("atT"), 1)
            act.wait_ge(s("osT_made"), 1)
            nc.scalar.activation(osT[:, :, :], m.ps[0:D, 1, :].rearrange("p (h d) -> p h d", h=NH), ACT.Copy).then_inc(s("osT"), 1)
            for h in range(NH):
                act.wait_ge(s("pw_made"), h + 1)
                nc.scalar.activation(pw[:, h, :], m.ps[0:G, 2 + h % 4, 0:C], ACT.Copy).then_inc(s("pw"), 1)

        @block.vector
        def _(dve):
            steps = Steps(dve, s("dve"))
            steps.do(nc.vector.tensor_scalar(itemp[:, :], m.row("L3_ffn_temperature", P), 0.1, 5.0, ALU.max, ALU.min))
            steps.do(nc.vector.reciprocal(itemp[:, :], itemp[:, :]))
            for c in range(KC):
                dve.wait_ge(s("wc_made"), c + 1)
                steps(nc.vector.tensor_tensor(wc[:, c, :, :], m.ps[:, 3 + c, :].rearrange("p (h g) -> p h g", h=NH),
                                              itemp[:, :].unsqueeze(2).to_broadcast([P, NH, G]), ALU.mult), s("wc"))
            dve.wait_ge(s("bc_made"), 1)
            steps.do(nc.vector.tensor_tensor(bc[:, :, :], m.ps[0:1, 5, :].rearrange("p (h g) -> p h g", h=NH),
                                             m.row("L3_ffn_b_slice", 1).unsqueeze(1).to_broadcast([1, NH, G]), ALU.add))
            steps(nc.vector.tensor_tensor(bc[:, :, :], bc[:, :, :], itemp[0:1, :].unsqueeze(2).to_broadcast([1, NH, G]),
                                          ALU.mult), s("wc"))
            norm_vector(nc, m, dve, st, steps)
            for t in range(NT):
                dve.wait_ge(s("logits"), t + 1)
                lg = m.ps[0:TP, (3, 4, 5, 6, 7)[t], :].rearrange("p (h g) -> p h g", h=NH)
                steps.do(nc.vector.tensor_reduce(mx[:, t, :], lg, AX.X, ALU.max))
                steps(nc.vector.tensor_tensor(sw[:, t, :, :], lg, mx[:, t, :].unsqueeze(2).to_broadcast([TP, NH, G]),
                                              ALU.subtract), s("sw_in"))
            for t in range(NT):
                dve.wait_ge(s("sw_exp"), t + 1)
                steps.do(nc.vector.tensor_reduce(mx[:, t, :], sw[:, t, :, :], AX.X, ALU.add))
                steps.do(nc.vector.reciprocal(rs[:, t, :], mx[:, t, :]))
                steps(nc.vector.tensor_tensor(sw[:, t, :, :], sw[:, t, :, :], rs[:, t, :].unsqueeze(2).to_broadcast([TP, NH, G]),
                                              ALU.mult), s("sw"))
            dve.wait_ge(s("norm_made"), 1)
            steps(nc.vector.tensor_copy(norm[:, :], m.ps[0:G, 2, :]), s("norm"))
            steps.settle()
            steps.do(nc.vector.tensor_scalar(rnorm[:, :], norm[:, :], 1e-5, None, ALU.add))
            steps.do(nc.vector.reciprocal(rnorm[:, :], rnorm[:, :]))
            for c in range(KC):
                dve.wait_ge(s("z_made"), c + 1)
                steps(nc.vector.tensor_copy(zT[:, c, :], m.ps[:, c, :]), s("zT"))
            dve.wait_ge(s("tok_made"), 1)
            steps(nc.vector.tensor_tensor(tokT[:, :], m.ps[0:D, 5, :], rnorm[:, :], ALU.mult), s("tokT"))
            dve.wait_ge(s("att_made"), 1)
            lg = m.ps[0:G, 5, :].rearrange("p (h g) -> p h g", h=NH)
            steps.do(nc.vector.tensor_reduce(amx[:, :], lg, AX.X, ALU.max))
            steps(nc.vector.tensor_tensor(at[:, :, :], lg, amx[:, :].unsqueeze(2).to_broadcast([G, NH, G]), ALU.subtract), s("at_in"))
            dve.wait_ge(s("at_exp"), 1)
            steps.do(nc.vector.tensor_reduce(amx[:, :], at[:, :, :], AX.X, ALU.add))
            steps.do(nc.vector.reciprocal(amx[:, :], amx[:, :]))
            steps(nc.vector.tensor_tensor(at[:, :, :], at[:, :, :], amx[:, :].unsqueeze(2).to_broadcast([G, NH, G]), ALU.mult), s("at"))
            for t in range(NT):
                dve.wait_ge(s("out_made"), t + 1)
                steps(nc.vector.tensor_tensor(m.x[:, t, :], m.x[:, t, :], m.ps[0:TP, (6, 7, 0, 1, 2)[t], 0:C], ALU.add))
            steps.settle()

        @block.tensor
        def _(pe):
            pe.wait_ge(s("w"), 32)
            for c in range(KC):
                for h in range(NH):
                    ins = nc.tensor.matmul(m.ps[:, 3 + c, h * G:(h + 1) * G], wxT[:, h, c * P:(c + 1) * P], wsl, start=True, stop=True)
                ins.then_inc(s("wc_made"), 1)
            for h in range(NH):
                ins = nc.tensor.matmul(m.ps[0:1, 5, h * G:(h + 1) * G], bxT[:, h:h + 1], wsl, start=True, stop=True)
            ins.then_inc(s("bc_made"), 1)
            norm_tensor(nc, m, pe, st)
            pe.wait_ge(s("xnT_done"), XNT)
            pe.wait_ge(s("wc"), 3)
            for t in range(NT):
                b = (3, 4, 5, 6, 7)[t]
                for k in range(KC):
                    nc.tensor.matmul(m.ps[0:TP, b, :], m.xnT[:, k, t * TP:(t + 1) * TP], wc[:, k, :, :].rearrange("p h g -> p (h g)"),
                                     start=k == 0, stop=False)
                nc.tensor.matmul(m.ps[0:TP, b, :], m.ones[0:1, 0:TP], bc[:, :, :].rearrange("p h g -> p (h g)"), start=False,
                                 stop=True).then_inc(s("logits"), 1)
            for t in range(NT):
                pe.wait_ge(s("sw"), t + 1)
                w = sw[:, t, :, :].rearrange("p h g -> p (h g)")
                ins0 = nc.tensor.matmul(m.ps[0:G, 2, :], m.ones[0:TP, 0:G], w, start=t == 0, stop=t == NT - 1)
                for c in range(KC):
                    ins = nc.tensor.matmul(m.ps[:, c, :], m.xn[:, t, c * P:(c + 1) * P], w, start=t == 0, stop=t == NT - 1)
                    if t == NT - 1:
                        ins.then_inc(s("z_made"), 1)
                if t == NT - 1:
                    ins0.then_inc(s("norm_made"), 1)
            pe.wait_ge(s("norm"), 1)
            pe.wait_ge(s("zT"), KC)
            for h in range(NH):
                o = m.ps[0:D, 5, h * G:(h + 1) * G]
                for k in range(KC):
                    nc.tensor.matmul(o, wfx[:, k, h * D:(h + 1) * D], zT[:, k, h * G:(h + 1) * G], start=k == 0, stop=False)
                ins = nc.tensor.matmul(o, m.row("L3_ffn_b_fx", 1)[:, h * D:(h + 1) * D], norm[0:1, h * G:(h + 1) * G], start=False,
                                       stop=True)
            ins.then_inc(s("tok_made"), 1)
            pe.wait_ge(s("tokT"), 1)
            for j, wt in enumerate((wq, wk)):
                nc.tensor.matmul(m.ps[0:D, 2 + j, :], wt, tokT[:, :], start=True, stop=True).then_inc(s("qk_made"), 1)
            for h in range(NH):
                ins = nc.tensor.matmul(m.ps[0:G, 4, h * D:(h + 1) * D], tokT[:, h * G:(h + 1) * G], wv, start=True, stop=True)
            ins.then_inc(s("v_made"), 1)
            pe.wait_ge(s("qk"), 2)
            for h in range(NH):
                hg = slice(h * G, (h + 1) * G)
                ins = nc.tensor.matmul(m.ps[0:G, 5, hg], qT[:, hg], kT[:, hg], start=True, stop=True)
            ins.then_inc(s("att_made"), 1)
            for h in range(NH):
                for t in range(NT):
                    b, c = (6, t * TP) if t < 4 else (7, 0)
                    if t in (0, 4) and h:
                        pe.wait_ge(s("swT"), 2 * h - 1 + (t == 4))
                    ins = nc.tensor.transpose(m.ps[0:G, b, c:c + TP], sw[:, t, h, :], m.ident[0:TP, 0:TP])
                    if t >= 3:
                        ins.then_inc(s("sw_turned"), 1)
            pe.wait_ge(s("at"), 1)
            for h in range(NH):
                ins = nc.tensor.transpose(m.ps[0:G, 0, h * G:(h + 1) * G], at[:, h, :], m.ident[0:G, 0:G])
            ins.then_inc(s("atT_made"), 1)
            pe.wait_ge(s("atT"), 1)
            pe.wait_ge(s("v"), 1)
            for h in range(NH):
                ins = nc.tensor.matmul(m.ps[0:D, 1, h * G:(h + 1) * G], v[:, h, :], atT[:, h, :], start=True, stop=True)
            ins.then_inc(s("osT_made"), 1)
            pe.wait_ge(s("osT"), 1)
            for h in range(NH):
                if h >= 4:
                    pe.wait_ge(s("pw"), h - 3)
                nc.tensor.matmul(m.ps[0:G, 2 + h % 4, 0:C], osT[:, h, :], wout[:, h, :], start=True, stop=True).then_inc(s("pw_made"), 1)
            pe.wait_ge(s("pw"), NH)
            pe.wait_ge(s("swT"), 2 * NH)
            for t in range(NT):
                b = (6, 7, 0, 1, 2)[t]
                for h in range(NH):
                    nc.tensor.matmul(m.ps[0:TP, b, 0:C], swT[:, h, t * TP:(t + 1) * TP], pw[:, h, :], start=h == 0, stop=False)
                nc.tensor.matmul(m.ps[0:TP, b, 0:C], m.ones[0:1, 0:TP], m.row("L3_ffn_b_out", 1), start=False, stop=True)\
                    .then_inc(s("out_made"), 1)


LAYERS = [l0_gnn, l0_ffn, l1_gnn, l1_ffn, l2_gnn, l2_ffn, l3_gnn, l3_ffn]


def build(nc, A, out, upto=99):
    with ExitStack() as ctx:
        m = Memory(nc, ctx)
        setup(nc, m, A)
        edges(nc, m, A)
        for layer in LAYERS[:upto]:
            layer(nc, m, A)
        with ExitStack() as last:
            done = last.enter_context(nc.semaphore("stored"))
            block = last.enter_context(nc.Block())

            @block.sync
            def _(sp):
                sp.dma_start(out.rearrange("(t p) c -> p t c", p=TP), m.x[:, :, :]).then_inc(done, 16)
                sp.wait_ge(done, 16)



def chunks(w):
    return w.reshape(-1, P, w.shape[-1]).transpose(1, 0, 2).reshape(P, -1)


def laid_out(inputs):
    a = {k: np.asarray(v) for k, v in inputs.items()}
    out = {n: a[n] for n in ["x", "edge_attr_256", "edge_attr_128", "L0_gnn_w_f1b"]}
    cols = []
    for n in COLS:
        v = a[n].reshape(-1, P)
        cols.append(v.T)
    out["cols"] = np.concatenate(cols, axis=1)
    out["rows"] = np.concatenate([a[n].reshape(-1) for n in ROWS])
    out["w_f1aT"] = a["L0_gnn_w_f1a"].T
    out["featT"] = a["edge_attr_54"].T
    out["src_t"] = a["src"].reshape(ET, TP).T
    out["dst_t"] = a["dst"].reshape(ET, TP).T
    g = lambda n: a["L0_gnn_" + n]
    out["w_l0g"] = np.concatenate([chunks(g(n)) for n in ["c1_wl", "c1_wr", "c2_wl", "c2_wr", "lin1_w", "lin2_w", "cat_w"]], axis=1)
    out["dst"] = a["dst"]
    out["wn"] = chunks(a["L1_gnn_Wn"])
    out["wnT"] = chunks(a["L1_gnn_Wn"].T)
    out["we_be"] = chunks(np.concatenate([a["L1_gnn_We"], a["L1_gnn_be"][:, None]], axis=1))
    out["l1f_wr"] = chunks(a["L1_ffn_Wr"])
    out["L1_ffn_bo"] = a["L1_ffn_bo"]
    out["l1f_w"] = np.stack([np.stack([chunks(a["L1_ffn_" + n][e]) for n in ("W1", "W2", "Wo")]) for e in range(8)])
    fc = a["L2_gnn_Wfc"]
    fc = np.concatenate([fc, np.zeros((512 - fc.shape[0], fc.shape[1]), fc.dtype)])
    out["w_l2g"] = np.concatenate([chunks(a["L2_gnn_W1"]), chunks(fc), a["L2_gnn_W2"]], axis=1)
    out["l2g_small"] = np.stack([a["L2_gnn_" + n] for n in ("b2", "g2", "be2")], axis=1)
    out["l2f_wr"] = chunks(a["L2_ffn_gate_w"])
    out["L2_ffn_b2"] = a["L2_ffn_b2"]
    out["l2f_w"] = np.stack([np.stack([chunks(a["L2_ffn_" + n][e]) for n in ("w1", "w2")]) for e in range(16)])
    out["w_l3g"] = np.concatenate([chunks(a["L3_gnn_W_l"].T), chunks(a["L3_gnn_W_r"].T)], axis=1)
    f = lambda n: a["L3_ffn_" + n]
    heads = lambda w: w.reshape(8, 64, C).transpose(1, 0, 2).reshape(64, -1)
    out["l3f_wfx"] = chunks(f("W_fx"))
    out["l3f_w64"] = np.concatenate([heads(f("W_x").T), heads(f("W_out")), f("W_slice"), f("W_q"), f("W_k"), f("W_v"),
                                     f("b_x").reshape(8, 64).T], axis=1)
    out["l0f_wr"] = chunks(a["L0_ffn_Wr"])
    out["L0_ffn_b2"] = a["L0_ffn_b2"]
    out["l0f_experts"] = np.concatenate(
        [np.concatenate([chunks(a["L0_ffn_W1"][e]), chunks(a["L0_ffn_W2"][e]), a["L0_ffn_b1"][e].reshape(4, P).T], axis=1)
         for e in range(8)], axis=0)
    return {k: np.ascontiguousarray(v) for k, v in out.items()}


def kernel(**inputs):
    import concourse.bacc as bacc
    from concourse.bass_utils import run_bass_kernel_spmd

    nc = bacc.Bacc("TRN2", target_bir_lowering=False, num_devices=1)
    arrays = laid_out(inputs)
    A = {n: nc.dram_tensor("in_" + n, a.shape, mybir.dt.from_np(a.dtype), kind="ExternalInput").ap()
         for n, a in arrays.items()}
    out = nc.dram_tensor("out_x", (N, C), F32, kind="ExternalOutput").ap()
    build(nc, A, out)
    r = run_bass_kernel_spmd(nc, [{"in_" + n: a for n, a in arrays.items()}], core_ids=[0])
    return r.results[0]["out_x"]
```

```python
from contextlib import ExitStack

import numpy as np

import concourse.bass as bass
from concourse import mybir

F32 = mybir.dt.float32
BF16 = mybir.dt.bfloat16
F16 = mybir.dt.float16
I32 = mybir.dt.int32
ALU = mybir.AluOpType
ACT = mybir.ActivationFunctionType
AX = mybir.AxisListType

N, C, E = 625, 256, 10000
P, KC = 128, C // 128
NT, TP = 5, 125
ET = E // TP
NQ = ET // 4
LN_EPS = 1e-5
HALF = ((0, 313), (313, N))

COLS = ["L0_gnn_c1_bl", "L0_gnn_c2_bl", "L0_gnn_lin1_b", "L0_gnn_lin2_b", "L0_gnn_cat_b", "L0_gnn_gn_w",
        "L0_gnn_gn_b", "L0_gnn_gn_ms", "L1_ffn_b1", "L1_ffn_g1", "L1_ffn_be1", "L1_ffn_m1", "L1_ffn_v1",
        "L1_ffn_b2", "L1_ffn_g2", "L1_ffn_be2", "L1_ffn_m2", "L1_ffn_v2", "L2_gnn_b1", "L2_gnn_g1",
        "L2_gnn_be1", "L2_ffn_b1", "L1_gnn_attn"]
COL_WIDTH = {n: 2 for n in COLS} | {n: 16 for n in COLS if n.startswith("L1_ffn")} | \
    {"L2_gnn_b1": 1, "L2_gnn_g1": 1, "L2_gnn_be1": 1, "L2_ffn_b1": 64}
ROWS = {"L0_ffn_br": 8, "L0_ffn_gamma": C, "L0_ffn_beta": C, "L1_gnn_bn": C, "L1_gnn_attn": C, "L1_ffn_br": 8,
        "L2_gnn_bfc": C, "L2_ffn_gate_b": 16, "L2_ffn_gamma": C, "L2_ffn_beta": C, "L3_gnn_b_l": C,
        "L3_gnn_ln_gamma": C, "L3_gnn_ln_beta": C, "L3_ffn_b_fx": 512, "L3_ffn_b_slice": 64,
        "L3_ffn_b_out": C, "L3_ffn_temperature": 8}


def offsets(widths):
    at, out = 0, {}
    for name, w in widths.items():
        out[name] = (at, at + w)
        at += w
    return out, at


COL_AT, NCOL = offsets(COL_WIDTH)
ROW_AT, NROW = offsets(ROWS)


class Steps:

    def __init__(self, eng, own):
        self.eng, self.own, self.count, self.last = eng, own, {}, own

    def __call__(self, ins, sem=None):
        sem = sem or self.own
        ins.then_inc(sem, 1)
        self.count[sem.name] = self.count.get(sem.name, 0) + 1
        self.last = sem
        return ins

    def settle(self):
        self.eng.wait_ge(self.last, self.count[self.last.name])

    def do(self, ins, sem=None):
        self(ins, sem)
        self.settle()


class Memory:

    def __init__(self, nc, ctx):
        def sb(name, shape, dt=F32):
            return ctx.enter_context(nc.sbuf_tensor(name, shape, dt))

        self.x = sb("x", [TP, NT, C])
        self.xn = sb("xn", [TP, NT, C])
        self.xnT = sb("xnT", [P, KC, N])
        self.stats = sb("stats", [TP, NT, 6])
        self.mv = sb("mv", [TP, NT, 2])
        self.veps = sb("veps", [P, NT])
        self.rstd = sb("rstd", [P, NT])
        self.mhalf = sb("mhalf", [P, 16])
        self.ident = sb("ident", [P, P])
        self.ones = sb("ones", [P, P])
        self.iota = sb("iota", [P, 640])
        self.pcol = sb("pcol", [P, 1])
        self.cols = sb("cols", [P, NCOL])
        self.rows = sb("rows", [P, NROW])
        self.count = sb("count", [TP, NT, N])
        self.srci = sb("srci", [TP, ET], I32)
        self.dsti = sb("dsti", [TP, ET], I32)
        self.src = sb("src", [TP, ET])
        self.dst = sb("dst", [TP, ET])
        self.iota16 = sb("iota16", [P, 640], F16)
        self.score_e = sb("score_e", [TP, ET])
        self.score0 = sb("score0", [TP, 1])
        self.q = sb("q", [P, KC])
        self.dst16 = sb("dst16", [TP, ET], F16)
        self.zeros = sb("zeros", [1, 512], BF16)
        self.inside = {n: sb("inside_" + n, [TP, NT, ET]) for n in ("src", "dst")}
        self.mask_s = sb("mask_s", [TP, E], BF16)
        self.end_rows = nc.dram_tensor("end_rows", (3, ET, TP), F16, kind="Internal").ap()
        self.words = sb("words", [1, NQ // 2], I32)
        self.ps = ctx.enter_context(nc.psum_tensor("ps", [P, 8, 512], F32))

    def col(self, name):
        a, b = COL_AT[name]
        return self.cols[:, a:b]

    def row(self, name, n=TP):
        a, b = ROW_AT[name]
        return self.rows[0:n, a:b]


class Stage:

    def __init__(self, nc, ctx, name):
        self.nc, self.ctx, self.name = nc, ctx, name
        self.made = {}
        ctx.callback(self.clear)

    def clear(self):
        if self.made:
            self.nc.clear_and_free_semaphores(list(self.made.values()))
            self.nc.all_engine_barrier()

    def sem(self, name):
        if name not in self.made:
            self.made[name] = self.nc.alloc_semaphore(f"{self.name}_{name}")
        return self.made[name]

    def sb(self, name, shape, dt=F32):
        return self.ctx.enter_context(self.nc.sbuf_tensor(f"{self.name}_{name}", shape, dt))

    def credit(self, eng, *names):
        for name in names:
            eng.nop(nofuse=True).then_inc(self.sem(name), 1)



def norm_vector(nc, m, dve, st, steps):
    for t in range(NT):
        steps(nc.vector.bn_stats(m.stats[:, t, :], m.x[:, t, :]))
    steps.settle()
    for t in range(NT):
        steps(nc.vector.bn_aggr(m.mv[:, t, :], m.stats[:, t, :]), st.sem("stats_done"))
    dve.wait_ge(st.sem("rstd_done"), 1)
    for t in range(NT):
        steps(nc.vector.tensor_scalar(m.xn[:, t, :], m.x[:, t, :], m.mv[:, t, 0:1], m.rstd[0:TP, t:t + 1],
                                      ALU.subtract, ALU.mult), st.sem("xn_done"))


def norm_pool(nc, m, pool, st, steps):
    pool.wait_ge(st.sem("stats_done"), NT)
    steps.do(nc.gpsimd.tensor_scalar(m.veps[0:TP, :], m.mv[:, :, 1], LN_EPS, None, ALU.add))
    steps(nc.gpsimd.tensor_tensor(m.rstd[0:TP, :], m.veps[0:TP, :], m.mhalf[0:TP, 0:NT], ALU.pow), st.sem("rstd_done"))


def norm_tensor(nc, m, pe, st):
    for t in range(NT):
        pe.wait_ge(st.sem("xn_done"), t + 1)
        for k in range(KC):
            out = m.ps[:, k, t * TP:(t + 1) * TP] if t < 4 else m.ps[:, 2, k * TP:(k + 1) * TP]
            nc.tensor.transpose(out, m.xn[:, t, k * P:(k + 1) * P], m.ident[0:TP, 0:TP]).then_inc(st.sem("xn_turned"), 1)


def norm_scalar(nc, m, act, st):
    act.wait_ge(st.sem("xn_turned"), 8)
    for k in range(KC):
        nc.scalar.activation(m.xnT[:, k, 0:4 * TP], m.ps[:, k, 0:4 * TP], ACT.Copy).then_inc(st.sem("xnT_done"), 1)
    act.wait_ge(st.sem("xn_turned"), 10)
    nc.scalar.activation(m.xnT[:, :, 4 * TP:N], m.ps[:, 2, 0:KC * TP].rearrange("p (k n) -> p k n", k=KC),
                         ACT.Copy).then_inc(st.sem("xnT_done"), 1)


XNT = 3



def setup(nc, m, A):
    with ExitStack() as ctx:
        st = Stage(nc, ctx, "setup")
        ramp = st.sb("ramp", [P, 640], I32)
        pint = st.sb("pint", [P, 1], I32)
        block = ctx.enter_context(nc.Block())

        @block.sync
        def _(sp):
            sp.dma_start(m.x[:, :, :], A["x"].rearrange("(t p) c -> p t c", p=TP)).then_inc(st.sem("loads"), 16)
            sp.dma_start(m.cols[:, :], A["cols"]).then_inc(st.sem("loads"), 16)
            sp.dma_start(m.rows[:, :], A["rows"][None, :].to_broadcast([P, NROW])).then_inc(st.sem("loads"), 16)
            sp.dma_start(m.srci[:, :], A["src_t"]).then_inc(st.sem("ends"), 16)
            sp.dma_start(m.dsti[:, :], A["dst_t"]).then_inc(st.sem("ends"), 16)
            sp.wait_ge(st.sem("loads"), 48)

        @block.gpsimd
        def _(pool):
            steps = Steps(pool, st.sem("pool"))
            steps(nc.gpsimd.memset(m.ident[:, :], 0.0))
            steps(nc.gpsimd.memset(m.ones[:, :], 1.0))
            steps(nc.gpsimd.memset(m.mhalf[:, :], -0.5))
            steps(nc.gpsimd.memset(m.zeros[:, :], 0.0))
            steps(nc.gpsimd.iota(pint[:, :], pattern=[[0, 1]], base=0, channel_multiplier=1))
            steps(nc.gpsimd.iota(ramp[:, :], pattern=[[1, 640]], base=0, channel_multiplier=0))
            steps.settle()
            steps(nc.gpsimd.affine_select(out=m.ident[:, :], in_=m.ident[:, :], compare_op=ALU.not_equal, fill=1.0,
                                          base=0, pattern=[[-1, P]], channel_multiplier=1))
            steps(nc.gpsimd.tensor_copy(m.iota[:, :], ramp[:, :]))
            steps(nc.gpsimd.tensor_copy(m.iota16[:, :], ramp[:, :]))
            steps(nc.gpsimd.tensor_copy(m.pcol[:, :], pint[:, :]))
            pool.wait_ge(st.sem("ends"), 32)
            steps(nc.gpsimd.tensor_copy(m.src[:, :], m.srci[:, :]))
            steps(nc.gpsimd.tensor_copy(m.dst[:, :], m.dsti[:, :]))
            steps.do(nc.gpsimd.tensor_copy(m.dst16[:, :], m.dsti[:, :]))



def l0_gnn(nc, m, A):
    names = ["c1_wl", "c1_wr", "c2_wl", "c2_wr", "lin1_w", "lin2_w"]
    with ExitStack() as ctx:
        st = Stage(nc, ctx, "l0g")
        W = st.sb("W", [P, 4096])
        wk = {n: W[:, 512 * i:512 * (i + 1)].rearrange("p (k n) -> p k n", k=2) for i, n in enumerate(names)}
        cat = W[:, 3072:4096].rearrange("p (k n) -> p k n", k=4)
        table = nc.dram_tensor("l0_nodes", (N, C), F32, kind="Internal").ap()
        agg = st.sb("agg", [TP, NT, 512])
        fa = st.sb("fa", [64, 54])
        fb = st.sb("fb", [64, C])
        wf = st.sb("wf", [54, C])

        with ExitStack() as inner:
            sb = Stage(nc, inner, "l0e").sb
            idx = sb("idx", [TP, 8], I32)
            gate = [sb(f"gate{h}", [TP, 4, C]) for h in range(2)]
            feat = [sb(f"feat{h}", [54, 4 * TP]) for h in range(2)]
            xg = [sb(f"xg{h}", [TP, 4, C]) for h in range(2)]
            fg = [sb(f"fg{v}", [TP, 2, C]) for v in range(2)]
            oh = [sb(f"oh{h}", [TP, 4, N]) for h in range(2)]
            msg = [sb(f"msg{h}", [TP, 4, 2, C]) for h in range(2)]
            gate_d = A["edge_attr_256"].rearrange("(q u p) c -> q p u c", p=TP, u=4)
            s = st.sem
            block = inner.enter_context(nc.Block())

            @block.sync
            def _(sp):
                sp.dma_start(fa[:, :], A["w_f1aT"]).then_inc(s("small"), 16)
                sp.dma_start(fb[:, :], A["L0_gnn_w_f1b"]).then_inc(s("small"), 16)
                sp.wait_ge(s("xn_done"), NT)
                sp.dma_start(table.rearrange("(t p) c -> p t c", p=TP), m.xn[:, :, :]).then_inc(s("table"), 16)
                with sp.Fori(0, NQ // 2) as i:
                    for h in range(2):
                        sp.wait_ge(s(f"feat_used{h}"), i + 1)
                        sp.dma_start(feat[h][:, :], A["featT"][:, bass.ds(i * 1000 + h * 500, 500)])\
                            .then_inc(s(f"feat{h}"), 16)
                        sp.wait_ge(s(f"quad_used{h}"), i + 1)
                        sp.dma_start(gate[h][:, :, :], gate_d[bass.ds(i * 2 + h, 1)].rearrange("q p u c -> (q p) u c"))\
                            .then_inc(s(f"gate{h}"), 16)
                sp.dma_start(W[:, :], A["w_l0g"]).then_inc(s("w"), 16)

            @block.gpsimd
            def _(pool):
                steps = Steps(pool, s("pool"))
                norm_pool(nc, m, pool, st, steps)
                pool.wait_ge(s("table"), 16)
                with pool.Fori(0, NQ // 2) as i:
                    for h in range(2):
                        pool.wait_ge(s(f"quad_used{h}"), i + 1)
                        pool.nop(nofuse=True)
                        nc.gpsimd.tensor_copy(idx[:, 4 * h:4 * h + 4], m.srci[:, bass.ds(i * 8 + 4 * h, 4)])\
                            .then_inc(s("idx"), 1)
                        pool.wait_ge(s("idx"), i * 2 + (h + 1))
                        pool.nop(nofuse=True)
                        for u in range(4):
                            pool.indirect_dma_start(
                                out=xg[h][:, u, :], out_offset=None, in_=table,
                                in_offset=bass.IndirectOffsetOnAxis(ap=idx[:, 4 * h + u:4 * h + u + 1], axis=0),
                            ).then_inc(s(f"xg{h}"), 16)

            @block.scalar
            def _(act):
                norm_scalar(nc, m, act, st)
                act.wait_ge(s("wf_made"), 1)
                nc.scalar.activation(wf[:, :], m.ps[0:54, 3, 0:C], ACT.Copy).then_inc(s("wf"), 1)
                act.wait_ge(s("agg_made"), 1)
                for t in range(NT):
                    nc.scalar.activation(agg[:, t, :], m.ps[0:TP, t, :], ACT.Copy).then_inc(s("agg"), 1)

            @block.vector
            def _(dve):
                steps = Steps(dve, s("dve"))
                st.credit(dve, "quad_used0", "quad_used1", "fg0", "fg1")
                norm_vector(nc, m, dve, st, steps)
                with dve.Fori(0, NQ // 2) as i:
                    word = word_of(dve, m, i)
                    for h in range(2):
                        dve.wait_ge(s(f"msg_used{h}"), i + 1)
                        for t in range(NT):
                            with dve.If(has(word, h, t)):
                                nc.vector.tensor_tensor(oh[h][:, :, t * TP:(t + 1) * TP],
                                                        m.iota16[0:TP, t * TP:(t + 1) * TP].unsqueeze(1).to_broadcast([TP, 4, TP]),
                                                        m.dst16[:, bass.ds(i * 8 + 4 * h, 4)].unsqueeze(2).to_broadcast([TP, 4, TP]),
                                                        ALU.is_equal)
                        use = i * 2 + h
                        for v in range(2):
                            if v == 0:
                                dve.wait_ge(s(f"gate{h}"), (i + 1) * 16)
                            dve.wait_ge(s(f"f1_made{v}"), use + 1)
                            nc.vector.tensor_tensor(fg[v][:, :, :], m.ps[0:TP, 5 + v, :].rearrange("p (u c) -> p u c", u=2),
                                                    gate[h][:, 2 * v:2 * v + 2, :], ALU.mult).then_inc(s(f"fg{v}"), 1)
                        dve.wait_ge(s(f"xg{h}"), (i + 1) * 64)
                        for v in range(2):
                            dve.wait_ge(s(f"fg{v}"), use + 2)
                            nc.vector.tensor_tensor(msg[h][:, 2 * v:2 * v + 2, 0, :], fg[v][:, :, :], xg[h][:, 2 * v:2 * v + 2, :],
                                                    ALU.mult).then_inc(s(f"m1{v}"), 1)
                        for v in range(2):
                            dve.wait_ge(s(f"m1{v}"), use + 1)
                            nc.vector.tensor_tensor(msg[h][:, 2 * v:2 * v + 2, 1, :], msg[h][:, 2 * v:2 * v + 2, 0, :],
                                                    gate[h][:, 2 * v:2 * v + 2, :], ALU.mult)\
                                .then_inc(s(f"quad_used{h}" if v else "m2"), 1)

            @block.tensor
            def _(pe):
                st.credit(pe, "msg_used0", "msg_used1", "feat_used0", "feat_used1")
                norm_tensor(nc, m, pe, st)
                pe.wait_ge(s("small"), 32)
                nc.tensor.matmul(m.ps[0:54, 3, 0:C], fa[:, :], fb[:, :], start=True, stop=True).then_inc(s("wf_made"), 1)
                pe.wait_ge(s("wf"), 1)
                pe.wait_ge(s("xnT_done"), XNT)
                zero_banks(nc, m, NT, 512, start=True)

                def features(i, h):
                    pe.wait_ge(s(f"feat{h}"), (i + 1) * 16)
                    for v in range(2):
                        pe.wait_ge(s(f"fg{v}"), i * 2 + (h + 1))
                        for u in range(2):
                            ins = nc.tensor.matmul(m.ps[0:TP, 5 + v, u * C:(u + 1) * C],
                                                   feat[h][:, (2 * v + u) * TP:(2 * v + u + 1) * TP], wf[:, :],
                                                   start=True, stop=True)
                        ins.then_inc(s(f"f1_made{v}"), 1)
                    mark(nc, m).then_inc(s(f"feat_used{h}"), 1)

                def sums(word, i, h):
                    pe.wait_ge(s(f"quad_used{h}"), i + 2)
                    for t in range(NT):
                        with pe.If(has(word, h, t)):
                            for u in range(4):
                                nc.tensor.matmul(m.ps[0:TP, t, :], oh[h][:, u, t * TP:(t + 1) * TP],
                                                 msg[h][:, u, :, :].rearrange("p a c -> p (a c)"), start=False, stop=False,
                                                 skip_group_check=True)
                    mark(nc, m).then_inc(s(f"msg_used{h}"), 1)

                features(0, 0)
                with pe.Fori(0, NQ // 2 - 1) as i:
                    word = word_of(pe, m, i)
                    features(i, 1)
                    sums(word, i, 0)
                    features(i + 1, 0)
                    sums(word, i, 1)
                word = word_of(pe, m, NQ // 2 - 1)
                features(NQ // 2 - 1, 1)
                sums(word, NQ // 2 - 1, 0)
                sums(word, NQ // 2 - 1, 1)
                zero_banks(nc, m, NT, 512, start=False).then_inc(s("agg_made"), 1)

        with ExitStack() as inner:
            sb = Stage(nc, inner, "l0m").sb
            aggT = sb("aggT", [P, 4, N])
            z = [sb(f"z{j}", [P, KC, N]) for j in range(2)]
            pre = [sb(f"pre{j}", [P, KC, N]) for j in range(2)]
            g = [sb(f"g{j}", [P, KC, N]) for j in range(2)]
            h = sb("h", [P, KC, N])
            hstat = sb("hstat", [P, KC, 5, 6])
            hmv = sb("hmv", [P, KC, 2])
            tmp = sb("tmp", [P, 4, KC])
            s = st.sem
            block = inner.enter_context(nc.Block())
            layers = [([("c1_wl", lambda k: aggT[:, k, :]), ("c1_wr", lambda k: m.xnT[:, k, :])], "c1_bl", z[0]),
                      ([("c2_wl", lambda k: aggT[:, 2 + k, :]), ("c2_wr", lambda k: m.xnT[:, k, :])], "c2_bl", z[1]),
                      ([("lin1_w", lambda k: z[0][:, k, :])], "lin1_b", pre[0]),
                      ([("lin2_w", lambda k: z[1][:, k, :])], "lin2_b", pre[1]),
                      ([("cat", lambda k: g[k // 2][:, k % 2, :])], "cat_b", h)]

            @block.tensor
            def _(pe):
                for t in range(NT):
                    for k in range(4):
                        ins = nc.tensor.transpose(m.ps[:, t, k * TP:(k + 1) * TP], agg[:, t, k * P:(k + 1) * P],
                                                  m.ident[0:TP, 0:TP])
                    ins.then_inc(s("agg_turned"), 1)
                pe.wait_ge(s("w"), 16)
                unit = 0
                for n, (terms, _, _) in enumerate(layers):
                    if n == 0:
                        pe.wait_ge(s("aggT"), NT)
                    elif n == 2:
                        pe.wait_ge(s("mlp_evac"), 4)
                    elif n == 3:
                        pe.wait_ge(s("mlp_evac"), 8)
                    elif n == 4:
                        pe.wait_ge(s("leaky"), 4)
                    for c in range(KC):
                        for (a, b) in HALF:
                            if unit >= 8:
                                pe.wait_ge(s("mlp_evac"), unit - 7)
                            ops = [(wk[w][:, k, c * P:(c + 1) * P] if w != "cat" else cat[:, k, c * P:(c + 1) * P],
                                    x(k)[:, a:b]) for w, x in terms for k in range(4 if w == "cat" else 2)]
                            for j, (lhsT, rhs) in enumerate(ops):
                                ins = nc.tensor.matmul(m.ps[:, unit % 8, 0:b - a], lhsT, rhs, start=j == 0,
                                                       stop=j == len(ops) - 1)
                            ins.then_inc(s("mlp_made"), 1)
                            unit += 1
                pe.wait_ge(s("hn"), 2)
                pe.wait_ge(s("mlp_evac"), 20)
                for t in range(NT):
                    for k in range(KC):
                        nc.tensor.transpose(m.ps[0:TP, t, k * P:(k + 1) * P],
                                            h[:, k, t * TP:(t + 1) * TP], m.ident[:, :]).then_inc(s("hn_turned"), 1)

            @block.scalar
            def _(act):
                for t in range(NT):
                    act.wait_ge(s("agg_turned"), t + 1)
                    nc.scalar.activation(aggT[:, :, t * TP:(t + 1) * TP],
                                         m.ps[:, t, 0:4 * TP].rearrange("p (k n) -> p k n", k=4), ACT.Copy)\
                        .then_inc(s("aggT"), 1)
                unit = 0
                for _, bias, out in layers:
                    for c in range(KC):
                        for (a, b) in HALF:
                            act.wait_ge(s("mlp_made"), unit + 1)
                            nc.scalar.activation(out[:, c, a:b], m.ps[:, unit % 8, 0:b - a], ACT.Identity,
                                                 bias=m.col("L0_gnn_" + bias)[:, c:c + 1]).then_inc(s("mlp_evac"), 1)
                            unit += 1
                act.wait_ge(s("gn_coef"), 1)
                for c in range(KC):
                    nc.scalar.activation(h[:, c, :], h[:, c, :], ACT.Identity, bias=tmp[:, 3, c:c + 1],
                                         scale=tmp[:, 2, c:c + 1]).then_inc(s("hn"), 1)

            @block.gpsimd
            def _(pool):
                steps = Steps(pool, s("pool_gn"))
                pool.wait_ge(s("gn_var"), 1)
                steps.do(nc.gpsimd.tensor_scalar(m.veps[:, 0:KC], tmp[:, 1, :], 1e-5, None, ALU.add))
                steps(nc.gpsimd.tensor_tensor(m.rstd[:, 0:KC], m.veps[:, 0:KC], m.mhalf[:, 0:KC], ALU.pow), s("gn_rstd"))

            @block.vector
            def _(dve):
                steps = Steps(dve, s("dve_mlp"))
                for j in range(2):
                    dve.wait_ge(s("mlp_evac"), 12 + 4 * j)
                    for c in range(KC):
                        steps(nc.vector.scalar_tensor_tensor(g[j][:, c, :], pre[j][:, c, :], 0.1, pre[j][:, c, :],
                                                             ALU.mult, ALU.max), s("leaky"))
                dve.wait_ge(s("mlp_evac"), 20)
                for c in range(KC):
                    for t in range(NT):
                        steps(nc.vector.bn_stats(hstat[:, c, t, :], h[:, c, t * TP:(t + 1) * TP]))
                steps.settle()
                for c in range(KC):
                    steps(nc.vector.bn_aggr(hmv[:, c, :], hstat[:, c, :, :].rearrange("p t s -> p (t s)")))
                steps.settle()
                steps.do(nc.vector.tensor_tensor(tmp[:, 0, :], hmv[:, :, 0], m.col("L0_gnn_gn_ms"), ALU.mult))
                steps.do(nc.vector.tensor_tensor(tmp[:, 1, :], hmv[:, :, 0], tmp[:, 0, :], ALU.subtract))
                steps.do(nc.vector.tensor_tensor(tmp[:, 1, :], tmp[:, 1, :], tmp[:, 1, :], ALU.mult))
                steps(nc.vector.tensor_tensor(tmp[:, 1, :], tmp[:, 1, :], hmv[:, :, 1], ALU.add), s("gn_var"))
                dve.wait_ge(s("gn_rstd"), 1)
                steps.do(nc.vector.tensor_tensor(tmp[:, 2, :], m.rstd[:, 0:KC], m.col("L0_gnn_gn_w"), ALU.mult))
                steps.do(nc.vector.tensor_tensor(tmp[:, 3, :], tmp[:, 0, :], tmp[:, 2, :], ALU.mult))
                steps(nc.vector.tensor_tensor(tmp[:, 3, :], m.col("L0_gnn_gn_b"), tmp[:, 3, :], ALU.subtract), s("gn_coef"))
                for t in range(NT):
                    dve.wait_ge(s("hn_turned"), 2 * t + 2)
                    steps(nc.vector.tensor_tensor(m.x[:, t, :], m.x[:, t, :],
                                                  m.ps[0:TP, t, 0:C], ALU.add))
                steps.settle()



def l0_ffn(nc, m, A):
    NE, F, FK = 8, 512, 4
    ROWLEN = 2052
    CAPACITY = float(int(np.ceil(N * 1.25 / NE)))
    with ExitStack() as ctx:
        st = Stage(nc, ctx, "l0f")
        s, sb = st.sem, st.sb
        wr = sb("wr", [P, KC, NE])
        b2 = sb("b2", [NE, C])
        expert = [sb(f"expert{j}", [P, ROWLEN]) for j in range(2)]
        w1 = [e[:, 0:1024].rearrange("p (k f) -> p k f", k=KC) for e in expert]
        w2 = [e[:, 1024:2048].rearrange("p (k c) -> p k c", k=FK) for e in expert]
        b1 = [e[:, 2048:2052] for e in expert]
        hT = [sb(f"hT{j}", [P, FK, N]) for j in range(2)]
        xsum = sb("xsum", [P, KC])
        xmean = sb("xmean", [P, KC, P])
        r = sb("r", [P, 16, NE])
        c = sb("c", [P, 32])
        row_idx = sb("row_idx", [P, 2], I32)
        wdT = sb("wdT", [NE, P])
        z = sb("z", [TP, NT, C])
        zn = sb("zn", [TP, NT, C])
        block = ctx.enter_context(nc.Block())
        UNITS = 2 * FK * 2

        @block.sync
        def _(sp):
            sp.dma_start(wr[:, :, :], A["l0f_wr"].rearrange("p (k e) -> p k e", k=KC)).then_inc(s("small"), 16)
            sp.dma_start(b2[:, :], A["L0_ffn_b2"]).then_inc(s("small"), 16)

        @block.gpsimd
        def _(pool):
            steps = Steps(pool, s("pool"))
            norm_pool(nc, m, pool, st, steps)
            for j in range(2):
                pool.wait_ge(s("chosen"), j + 1)
                pool.indirect_dma_start(out=expert[j][:, :], out_offset=None, in_=A["l0f_experts"],
                                        in_offset=bass.IndirectOffsetOnAxis(ap=row_idx[:, j:j + 1], axis=0))\
                    .then_inc(s(f"expert{j}"), 16)
            pool.wait_ge(s("z_stats"), NT)
            steps.do(nc.gpsimd.tensor_scalar(m.veps[0:TP, :], m.mv[:, :, 1], LN_EPS, None, ALU.add))
            steps(nc.gpsimd.tensor_tensor(m.rstd[0:TP, :], m.veps[0:TP, :], m.mhalf[0:TP, 0:NT], ALU.pow), s("z_rstd"))

        @block.scalar
        def _(act):
            norm_scalar(nc, m, act, st)
            for n in range(2):
                act.wait_ge(s("exp_in"), n + 1)
                nc.scalar.activation(r[:, 3 * n + 2, :], r[:, 3 * n + 1, :], ACT.Exp, accum_out=c[:, n:n + 1])\
                    .then_inc(s("exp_out"), 1)
            act.wait_ge(s("exp_in"), 3)
            nc.scalar.activation(c[:, 11:12], c[:, 10:11], ACT.Exp).then_inc(s("exp_out"), 1)
            act.wait_ge(s("wdT_made"), 1)
            nc.scalar.activation(wdT[:, :], m.ps[0:NE, 4, 0:P], ACT.Copy).then_inc(s("wdT"), 1)
            unit = 0
            for j in range(2):
                for f in range(FK):
                    for (a, b) in HALF:
                        act.wait_ge(s("h_made"), unit + 1)
                        nc.scalar.activation(hT[j][:, f, a:b], m.ps[:, unit % 3, 0:b - a], ACT.Gelu,
                                             bias=b1[j][:, f:f + 1]).then_inc(s("hT"), 1)
                        unit += 1

        @block.vector
        def _(dve):
            steps = Steps(dve, s("dve"))
            norm_vector(nc, m, dve, st, steps)
            dve.wait_ge(s("xnT_done"), XNT)
            steps.do(nc.vector.tensor_reduce(xsum[:, :], m.xnT[:, :, :], AX.X, ALU.add))
            for k in range(KC):
                steps(nc.vector.tensor_scalar(xmean[:, k, :], m.ones[:, :], xsum[:, k:k + 1], 1.0 / N, ALU.mult, ALU.mult),
                      s("xmean"))
            dve.wait_ge(s("logits"), 1)

            def softmax_top(n, logits):
                steps.do(nc.vector.tensor_reduce(c[:, 2:3], logits, AX.X, ALU.max))
                steps(nc.vector.tensor_scalar(r[:, 3 * n + 1, :], logits, c[:, 2:3], None, ALU.subtract), s("exp_in"))

            def softmax_end(n):
                dve.wait_ge(s("exp_out"), n + 1)
                steps.do(nc.vector.reciprocal(c[:, 3:4], c[:, n:n + 1]))
                steps.do(nc.vector.tensor_scalar(r[:, 3 * n + 3, :], r[:, 3 * n + 2, :], c[:, 3:4], None, ALU.mult))

            steps.do(nc.vector.tensor_copy(r[:, 0, :], m.ps[:, 3, 0:NE]))
            softmax_top(0, r[:, 0, :])
            softmax_end(0)
            steps.do(nc.vector.tensor_scalar(r[:, 8, :], r[:, 3, :], float(N), None, ALU.mult))
            steps.do(nc.vector.tensor_scalar(r[:, 8, :], r[:, 8, :], CAPACITY, 1.0 / CAPACITY, ALU.max, ALU.mult))
            steps.do(nc.vector.reciprocal(r[:, 9, :], r[:, 8, :]))
            steps.do(nc.vector.tensor_tensor(r[:, 0, :], r[:, 3, :], r[:, 9, :], ALU.mult))
            softmax_top(1, r[:, 0, :])
            softmax_end(1)
            left = r[:, 6, :]
            for j in range(2):
                steps.do(nc.vector.tensor_reduce(c[:, 4 + j:5 + j], left, AX.X, ALU.max))
                steps.do(nc.vector.tensor_scalar(r[:, 10, :], left, c[:, 4 + j:5 + j], -1000.0, ALU.is_equal, ALU.mult))
                steps.do(nc.vector.tensor_tensor(r[:, 10, :], r[:, 10, :], m.iota[:, 0:NE], ALU.add))
                steps.do(nc.vector.tensor_reduce(c[:, 6 + j:7 + j], r[:, 10, :], AX.X, ALU.min))
                steps.do(nc.vector.tensor_scalar(c[:, 8:9], c[:, 6 + j:7 + j], 1000.0, float(P), ALU.add, ALU.mult))
                steps(nc.vector.tensor_tensor(row_idx[:, j:j + 1], c[:, 8:9], m.pcol[:, :], ALU.add), s("chosen"))
                steps.do(nc.vector.tensor_scalar(c[:, 9:10], c[:, 6 + j:7 + j], 1000.0, None, ALU.add))
                steps.do(nc.vector.tensor_scalar(r[:, 11 + j, :], m.iota[:, 0:NE], c[:, 9:10], None, ALU.is_equal))
                if j == 0:
                    steps.do(nc.vector.scalar_tensor_tensor(r[:, 13, :], r[:, 11, :], -2.0, left, ALU.mult, ALU.add))
                    left = r[:, 13, :]
            steps(nc.vector.tensor_tensor(c[:, 10:11], c[:, 5:6], c[:, 4:5], ALU.subtract), s("exp_in"))
            dve.wait_ge(s("exp_out"), 3)
            steps.do(nc.vector.tensor_scalar(c[:, 12:13], c[:, 11:12], 1.0, None, ALU.add))
            steps.do(nc.vector.reciprocal(c[:, 13:14], c[:, 12:13]))
            steps.do(nc.vector.tensor_tensor(c[:, 14:15], c[:, 11:12], c[:, 13:14], ALU.mult))
            steps.do(nc.vector.tensor_scalar(r[:, 14, :], r[:, 11, :], c[:, 13:14], None, ALU.mult))
            steps(nc.vector.scalar_tensor_tensor(r[:, 15, :], r[:, 12, :], c[:, 14:15], r[:, 14, :], ALU.mult, ALU.add),
                  s("wdense"))
            for j in range(2):
                dve.wait_ge(s(f"expert{j}"), 16)
                steps(nc.vector.tensor_scalar(expert[j][:, 1024:2048], expert[j][:, 1024:2048], c[:, 13 + j:14 + j],
                                              None, ALU.mult), s("w2_scaled"))
            for t in range(NT):
                dve.wait_ge(s("y_made"), t + 1)
                steps(nc.vector.tensor_tensor(z[:, t, :], m.ps[0:TP, 3 + t, 0:C], m.xn[:, t, :], ALU.add), s("z"))
                steps.settle()
                steps.do(nc.vector.bn_stats(m.stats[:, t, :], z[:, t, :]))
                steps(nc.vector.bn_aggr(m.mv[:, t, :], m.stats[:, t, :]), s("z_stats"))
            dve.wait_ge(s("z_rstd"), 1)
            for t in range(NT):
                steps(nc.vector.tensor_scalar(zn[:, t, :], z[:, t, :], m.mv[:, t, 0:1], m.rstd[0:TP, t:t + 1],
                                              ALU.subtract, ALU.mult))
            steps.settle()
            for t in range(NT):
                steps(nc.vector.tensor_tensor(z[:, t, :], zn[:, t, :], m.row("L0_ffn_gamma"), ALU.mult))
            steps.settle()
            for t in range(NT):
                steps(nc.vector.tensor_tensor(zn[:, t, :], z[:, t, :], m.row("L0_ffn_beta"), ALU.add))
            steps.settle()
            for t in range(NT):
                steps(nc.vector.tensor_tensor(m.x[:, t, :], m.x[:, t, :], zn[:, t, :], ALU.add))
            steps.settle()

        @block.tensor
        def _(pe):
            norm_tensor(nc, m, pe, st)
            pe.wait_ge(s("xmean"), KC)
            pe.wait_ge(s("small"), 32)
            for k in range(KC):
                nc.tensor.matmul(m.ps[:, 3, 0:NE], xmean[:, k, :], wr[:, k, :], start=k == 0, stop=False)
            nc.tensor.matmul(m.ps[:, 3, 0:NE], m.ones[0:1, :], m.row("L0_ffn_br", 1), start=False, stop=True)\
                .then_inc(s("logits"), 1)
            pe.wait_ge(s("wdense"), 1)
            nc.tensor.transpose(m.ps[0:NE, 4, 0:P], r[:, 15, :], m.ident[:, :]).then_inc(s("wdT_made"), 1)
            pe.wait_ge(s("wdT"), 1)
            for t in range(NT):
                nc.tensor.matmul(m.ps[0:TP, 3 + t, 0:C], wdT[:, 0:TP], b2[:, :], start=True, stop=False)
            pe.wait_ge(s("xnT_done"), XNT)
            unit = 0
            for j in range(2):
                pe.wait_ge(s(f"expert{j}"), 16)
                for f in range(FK):
                    for (a, b) in HALF:
                        if unit >= 3:
                            pe.wait_ge(s("hT"), unit - 2)
                        for k in range(KC):
                            ins = nc.tensor.matmul(m.ps[:, unit % 3, 0:b - a], w1[j][:, k, f * P:(f + 1) * P],
                                                   m.xnT[:, k, a:b], start=k == 0, stop=k == KC - 1)
                        ins.then_inc(s("h_made"), 1)
                        unit += 1
            for j in range(2):
                pe.wait_ge(s("hT"), UNITS // 2 * (j + 1))
                pe.wait_ge(s("w2_scaled"), j + 1)
                for t in range(NT):
                    for f in range(FK):
                        ins = nc.tensor.matmul(m.ps[0:TP, 3 + t, 0:C], hT[j][:, f, t * TP:(t + 1) * TP], w2[j][:, f, :],
                                               start=False, stop=j == 1 and f == FK - 1)
                    if j == 1:
                        ins.then_inc(s("y_made"), 1)



def word_of(eng, m, i):
    return eng.value_load(m.words[0:1, bass.ds(i, 1)], min_val=0, max_val=1023)


def has(word, h, t):
    return (word & (1 << (NT * h + t))) > 0


def edges(nc, m, A):
    with ExitStack() as ctx:
        st = Stage(nc, ctx, "edg")
        s, sb = st.sem, st.sb
        wn = sb("wn", [P, KC, C])
        we = sb("we", [P, KC, P + 1])
        attnB = sb("attnB", [P, KC, TP])
        vrow = sb("vrow", [TP, P])
        junk = sb("junk", [TP, C])
        c0 = sb("c0", [TP, 2])
        above = sb("above", [TP, NT + 1, ET])
        place = sb("place", [TP, 2, ET])
        ends16 = sb("ends16", [ET, 3, TP], F16)
        srow = sb("srow", [TP, E], F16)
        per_quad = sb("per_quad", [TP, NQ, NT])
        bits = sb("bits", [1, NQ // 2, 2 * NT])
        power = sb("power", [1, 2 * NT])
        ea = [sb(f"ea{h}", [TP, 4, P]) for h in range(2)]
        prod = [sb(f"prod{h}", [TP, 4, P]) for h in range(2)]
        ohs = [sb(f"ohs{v}", [TP, 4, N], BF16) for v in range(2)]
        ohd = [sb(f"ohd{v}", [TP, 4, N], BF16) for v in range(2)]
        ea_d = A["edge_attr_128"].rearrange("(q u p) c -> q p u c", p=TP, u=4)
        attn = m.col("L1_gnn_attn")
        block = ctx.enter_context(nc.Block())

        @block.sync
        def _(sp):
            sp.dma_start(we[:, :, :], A["we_be"].rearrange("p (k n) -> p k n", k=KC)).then_inc(s("w"), 16)
            sp.dma_start(wn[:, :, :], A["wn"].rearrange("p (k n) -> p k n", k=KC)).then_inc(s("w"), 16)
            sp.wait_ge(s("ends16"), 1)
            sp.dma_start(m.end_rows.rearrange("n t p -> t n p"), ends16[:, :, :]).then_inc(s("end_rows"), 16)
            sp.wait_ge(s("end_rows"), 16)
            sp.dma_start(srow[:, :], m.end_rows[0].rearrange("t p -> (t p)")[None, :].to_broadcast([TP, E])).then_inc(s("srow"), 16)
            with sp.Fori(0, NQ // 2) as i:
                for h in range(2):
                    sp.wait_ge(s(f"ea_used{h}"), i + 1)
                    sp.dma_start(ea[h][:, :, :], ea_d[bass.ds(i * 2 + h, 1)].rearrange("q p u c -> (q p) u c"))\
                        .then_inc(s(f"ea{h}"), 16)

        @block.gpsimd
        def _(pool):
            st.credit(pool, "ea_used0", "ea_used1")
            pool.wait_ge(s("vrow"), 2)
            with pool.Fori(0, NQ // 2) as i:
                for h in range(2):
                    pool.wait_ge(s(f"ea{h}"), (i + 1) * 16)
                    pool.wait_ge(s(f"prod_used{h}"), i + 1)
                    nc.gpsimd.tensor_tensor(prod[h][:, :, :], ea[h][:, :, :],
                                            vrow[:, :].unsqueeze(1).to_broadcast([TP, 4, P]), ALU.mult)\
                        .then_inc(s(f"ea_used{h}"), 1)

        @block.scalar
        def _(act):
            act.wait_ge(s("ends_turned"), 1)
            nc.scalar.activation(ends16[:, :, :], m.ps[0:ET, 3, 0:3 * TP].rearrange("t (n p) -> t n p", n=3), ACT.Copy)\
                .then_inc(s("ends16"), 1)
            act.wait_ge(s("attn_done"), 1)
            nc.scalar.activation(vrow[:, :], m.ps[0:TP, 0, 0:P], ACT.Copy).then_inc(s("vrow"), 1)
            nc.scalar.activation(c0[:, 0:1], m.ps[0:TP, 0, P:P + 1], ACT.Copy).then_inc(s("vrow"), 1)
            act.wait_ge(s("q_made"), 1)
            nc.scalar.activation(m.q[:, :], m.ps[:, 1, 0:KC], ACT.Copy).then_inc(s("vrow"), 1)
            act.wait_ge(s("counted"), 1)
            for t in range(NT):
                nc.scalar.activation(m.count[:, t, 0:4 * TP], m.ps[0:TP, t, 0:4 * TP], ACT.Copy).then_inc(s("count"), 1)
            nc.scalar.activation(m.count[:, 0:4, 4 * TP:N], m.ps[0:TP, 5, 0:4 * TP].rearrange("p (t n) -> p t n", t=4),
                                 ACT.Copy).then_inc(s("count"), 1)
            nc.scalar.activation(m.count[:, 4, 4 * TP:N], m.ps[0:TP, 6, 0:TP], ACT.Copy).then_inc(s("count"), 1)

        @block.vector
        def _(dve):
            steps = Steps(dve, s("dve"))
            st.credit(dve, "prod_used0", "prod_used1")
            for k in range(KC):
                steps(nc.vector.tensor_scalar(attnB[:, k, :], m.ones[:, 0:TP], attn[:, k:k + 1], None, ALU.mult), s("attnB"))
            for j, (n, ends) in enumerate((("src", m.src), ("dst", m.dst))):
                for t in range(NT + 1):
                    steps(nc.vector.tensor_scalar(above[:, t, :], ends[:, :], float(t * TP), None, ALU.is_ge))
                steps.settle()
                steps(nc.vector.tensor_tensor(m.inside[n][:, :, :], above[:, 0:NT, :], above[:, 1:NT + 1, :], ALU.subtract))
                steps.do(nc.vector.tensor_reduce(place[:, j, :], above[:, 1:NT, :].rearrange("p t e -> p e t"), AX.X, ALU.add))
                steps.do(nc.vector.scalar_tensor_tensor(place[:, j, :], place[:, j, :], -float(TP), ends[:, :], ALU.mult, ALU.add),
                         s("places"))
            steps(nc.vector.tensor_reduce(per_quad[:, :, :].rearrange("p q t -> p t q"),
                                          m.inside["dst"][:, :, :].rearrange("p t (q u) -> p t q u", u=4), AX.X, ALU.add), s("per_group"))
            for k in range(2 * NT):
                steps(nc.vector.memset(power[:, k:k + 1], float(1 << k)))
            dve.wait_ge(s("groups"), 1)
            counts = m.ps[0:1, 2, 0:NQ * NT].rearrange("p (w k) -> p w k", k=2 * NT)
            steps.do(nc.vector.tensor_scalar(bits[:, :, :], counts, 1.0, None, ALU.min))
            steps.do(nc.vector.tensor_tensor(bits[:, :, :], bits[:, :, :],
                                             power[:, :].unsqueeze(1).to_broadcast([1, NQ // 2, 2 * NT]), ALU.mult))
            with nc.allow_low_precision("sums of powers of two under 1024"):
                steps(nc.vector.tensor_reduce(m.words[:, :], bits[:, :, :], AX.X, ALU.add), s("tables"))
            dve.wait_ge(s("vrow"), 2)
            steps.do(nc.vector.tensor_tensor_reduce(junk[:, :], m.row("L1_gnn_bn"), m.row("L1_gnn_attn"), 1.0, 0.0,
                                                    ALU.mult, ALU.add, c0[:, 1:2]))
            steps.do(nc.vector.tensor_tensor(m.score0[:, :], c0[:, 0:1], c0[:, 1:2], ALU.add))
            dve.wait_ge(s("tables"), 1)
            with dve.Fori(0, NQ // 2) as i:
                word = word_of(dve, m, i)
                for h in range(2):
                    dve.wait_ge(s(f"oh_used{h}"), i + 1)
                    for u in range(4):
                        nc.vector.tensor_scalar(ohs[h][:, u, :], m.iota16[0:TP, 0:N], m.src[:, bass.ds(i * 8 + (4 * h + u), 1)],
                                                None, ALU.is_equal).then_inc(s("ohs"), 1)
                    for t in range(NT):
                        with dve.If(has(word, h, t)):
                            nc.vector.tensor_tensor(ohd[h][:, :, t * TP:(t + 1) * TP],
                                                    m.iota16[0:TP, t * TP:(t + 1) * TP].unsqueeze(1).to_broadcast([TP, 4, TP]),
                                                    m.dst16[:, bass.ds(i * 8 + 4 * h, 4)].unsqueeze(2).to_broadcast([TP, 4, TP]),
                                                    ALU.is_equal)
                    dve.wait_ge(s(f"ea_used{h}"), i + 2)
                    nc.vector.tensor_reduce(m.score_e[:, bass.ds(i * 8 + 4 * h, 4)], prod[h][:, :, :], AX.X, ALU.add)\
                        .then_inc(s(f"prod_used{h}"), 1)
            dve.wait_ge(s("srow"), 16)
            steps.do(nc.vector.tensor_scalar(m.mask_s[:, :], srow[:, :], m.pcol[0:TP, :], None, ALU.is_equal))

        @block.tensor
        def _(pe):
            st.credit(pe, "oh_used0", "oh_used1")
            pe.wait_ge(s("places"), 2)
            for j, ends in enumerate((place[:, 0, :], place[:, 1, :], m.dst[:, :])):
                ins = nc.tensor.transpose(m.ps[0:ET, 3, j * TP:(j + 1) * TP], ends, m.ident[0:TP, 0:TP])
            ins.then_inc(s("ends_turned"), 1)
            pe.wait_ge(s("per_group"), 1)
            nc.tensor.matmul(m.ps[0:1, 2, 0:NQ * NT], m.ones[0:TP, 0:1], per_quad[:, :, :].rearrange("p q t -> p (q t)"),
                             start=True, stop=True).then_inc(s("groups"), 1)
            pe.wait_ge(s("w"), 32)
            pe.wait_ge(s("attnB"), KC)
            for k in range(KC):
                ins = nc.tensor.matmul(m.ps[0:TP, 0, 0:P + 1], attnB[:, k, :], we[:, k, :], start=k == 0, stop=k == KC - 1)
            ins.then_inc(s("attn_done"), 1)
            for c in range(KC):
                for k in range(KC):
                    ins = nc.tensor.matmul(m.ps[:, 1, c:c + 1], wn[:, k, c * P:(c + 1) * P], attn[:, k:k + 1],
                                           start=k == 0, stop=k == KC - 1)
            ins.then_inc(s("q_made"), 1)
            pe.wait_ge(s("vrow"), 3)
            pe.wait_ge(s("tables"), 1)
            pe.wait_ge(s("ends16"), 1)
            zero_banks(nc, m, 7, 4 * TP, start=True)
            with pe.Fori(0, NQ // 2) as i:
                word = word_of(pe, m, i)
                for h in range(2):
                    pe.wait_ge(s(f"prod_used{h}"), i + 2)
                    for t in range(NT):
                        with pe.If(has(word, h, t)):
                            for u in range(4):
                                for r in range(NT):
                                    out = m.ps[0:TP, r, t * TP:(t + 1) * TP] if t < 4 else \
                                        m.ps[0:TP, 5, r * TP:(r + 1) * TP] if r < 4 else m.ps[0:TP, 6, 0:TP]
                                    nc.tensor.matmul(out, ohs[h][:, u, r * TP:(r + 1) * TP],
                                                     ohd[h][:, u, t * TP:(t + 1) * TP], start=False, stop=False,
                                                     skip_group_check=True)
                    mark(nc, m).then_inc(s(f"oh_used{h}"), 1)
            zero_banks(nc, m, 7, 4 * TP, start=False).then_inc(s("counted"), 1)


def zero_banks(nc, m, banks, width, start):
    for b in range(banks):
        ins = nc.tensor.matmul(m.ps[0:TP, b, 0:width], m.zeros[:, 0:TP], m.zeros[:, 0:width], start=start, stop=not start,
                               skip_group_check=True)
    return ins


def mark(nc, m):
    return nc.tensor.matmul(m.ps[0:1, 7, 511:512], m.zeros[:, 0:1], m.zeros[:, 0:1], start=True, stop=True,
                            skip_group_check=True)



def l1_gnn(nc, m, A):
    BIG = 1e30
    CH = 1000
    PW = 16
    with ExitStack() as ctx:
        st = Stage(nc, ctx, "l1g")
        s, sb = st.sem, st.sb
        arow_d = nc.dram_tensor("l1_scores", (ET, TP), F32, kind="Internal").ap()
        table = nc.dram_tensor("l1_nodes", (N, C), F32, kind="Internal").ap()
        wnT = sb("wnT", [P, KC, C])
        score = sb("score", [TP, NT])
        mcol = sb("mcol", [TP, NT])
        rest = sb("rest", [TP, NT])
        parts = sb("parts", [TP, 3, NT], BF16)
        drow = sb("drow", [TP, E], F16)
        got = sb("got", [TP, ET])
        a = sb("a", [TP, ET])
        w = sb("w", [TP, ET])
        at = sb("at", [ET, TP])
        dcol = sb("dcol", [TP, NT])
        tick = sb("tick", [1, 5])
        hs = m.xn
        idx = sb("idx", [TP, 8], I32)
        hg = [sb(f"hg{h}", [TP, 4, C]) for h in range(2)]
        G = sb("G", [TP, ET, C + 1])
        woh = sb("woh", [TP, 2, 4, N])
        flat = woh[:, :, :, :].rearrange("p h u n -> p (h u n)")
        arow = [flat[:, h * CH:(h + 1) * CH] for h in range(5)]
        off = sb("off", [TP, CH], BF16)
        mjunk = sb("mjunk", [TP, CH], BF16)
        sel = {"src": G[:, ET - 5:ET, :].rearrange("p e c -> p (e c)"), "dst": flat}
        sel = {n: v[:, 0:ET * 3 * NT].rearrange("p (e k) -> p e k", k=3 * NT) for n, v in sel.items()}
        places = flat.bitcast(F16)
        mask = m.mask_s
        res = m.xn
        den = sb("den", [TP, NT])
        block = ctx.enter_context(nc.Block())

        @block.sync
        def _(sp):
            sp.dma_start(wnT[:, :, :], A["wnT"].rearrange("p (k n) -> p k n", k=KC)).then_inc(s("w"), 16)
            row = lambda n: m.end_rows[n].rearrange("t p -> (t p)")[None, :].to_broadcast([TP, E])
            sp.wait_ge(s("hs"), NT)
            sp.dma_start(table.rearrange("(t p) c -> p t c", p=TP), hs[:, :, :]).then_inc(s("table"), 16)
            sp.dma_start(places, row(1)).then_inc(s("places"), 16)
            sp.dma_start(drow[:, :], row(2)).then_inc(s("drow"), 16)
            sp.wait_ge(s("at"), 1)
            sp.dma_start(arow_d, at[:, :]).then_inc(s("arow_d"), 16)
            sp.wait_ge(s("arow_d"), 16)
            sp.wait_ge(s("mask_d"), 1)
            with sp.Fori(0, E // (5 * CH)) as i:
                for h in range(5):
                    sp.wait_ge(s(f"max_done{h}"), i + 1)
                    sp.dma_start(arow[h],
                                 arow_d.rearrange("t p -> (t p)")[bass.ds(i * (5 * CH) + h * CH, CH)][None, :].to_broadcast([TP, CH]))\
                        .then_inc(s(f"arow{h}"), 16)

        @block.gpsimd
        def _(pool):
            steps = Steps(pool, s("pool"))
            norm_pool(nc, m, pool, st, steps)
            pool.wait_ge(s("table"), 16)
            with pool.Fori(0, NQ // 2) as i:
                for h in range(2):
                    pool.wait_ge(s(f"kept{h}"), i + 1)
                    pool.nop(nofuse=True)
                    nc.gpsimd.tensor_copy(idx[:, 4 * h:4 * h + 4], m.srci[:, bass.ds(i * 8 + 4 * h, 4)]).then_inc(s("idx"), 1)
                    pool.wait_ge(s("idx"), i * 2 + (h + 1))
                    pool.nop(nofuse=True)
                    for u in range(4):
                        pool.indirect_dma_start(
                            out=hg[h][:, u, :], out_offset=None, in_=table,
                            in_offset=bass.IndirectOffsetOnAxis(ap=idx[:, 4 * h + u:4 * h + u + 1], axis=0),
                        ).then_inc(s(f"hg{h}"), 16)

        @block.scalar
        def _(act):
            st.credit(act, "kept0", "kept1")
            norm_scalar(nc, m, act, st)
            act.wait_ge(s("score_made"), 1)
            nc.scalar.activation(score[:, :], m.ps[0:TP, 3, 0:NT], ACT.Copy).then_inc(s("score"), 1)
            for t in range(NT):
                act.wait_ge(s("h_made"), t + 1)
                nc.scalar.activation(hs[:, t, 0:C], m.ps[0:TP, 4 + t if t < 4 else 3, 0:C], ACT.Copy).then_inc(s("hs"), 1)

            def keep(first, last):
                with act.Fori(first, last) as i:
                    for h in range(2):
                        act.wait_ge(s(f"hg{h}"), (i + 1) * 64)
                        act.nop(nofuse=True)
                        nc.scalar.activation(G[:, bass.ds(i * 8 + 4 * h, 4), 0:C], hg[h][:, :, :], ACT.Copy)\
                            .then_inc(s(f"kept{h}"), 1)

            keep(0, 8)
            act.wait_ge(s("w_in"), 1)
            nc.scalar.activation(w[:, :], a[:, :], ACT.Exp).then_inc(s("w_edge"), 1)
            keep(8, NQ // 2)

        @block.vector
        def _(dve):
            steps = Steps(dve, s("dve"))
            st.credit(dve, *[f"max_done{h}" for h in range(5)])
            norm_vector(nc, m, dve, st, steps)
            for t in range(NT):
                steps(nc.vector.tensor_scalar(dcol[:, t:t + 1], m.pcol[0:TP, :], float(t * TP), None, ALU.add))
            steps(nc.vector.memset(mcol[:, :], -BIG))

            def split(value):
                steps.do(nc.vector.tensor_copy(parts[:, 0, :], value))
                steps.do(nc.vector.tensor_tensor(rest[:, :], value, parts[:, 0, :], ALU.subtract))
                steps.do(nc.vector.tensor_copy(parts[:, 1, :], rest[:, :]))
                steps.do(nc.vector.tensor_tensor(rest[:, :], rest[:, :], parts[:, 1, :], ALU.subtract))
                steps(nc.vector.tensor_copy(parts[:, 2, :], rest[:, :]), s("parts"))

            def picked(n, bank, turn):
                dve.wait_ge(s("picked"), turn)
                values = m.ps[0:TP, bank:bank + 3, :].rearrange("p b c -> p (b c)")[:, 0:ET * PW]
                values = values.rearrange("p (e k) -> p e k", k=PW)[:, :, 0:3 * NT].rearrange("p e (j t) -> p e j t", t=NT)
                steps.do(nc.vector.tensor_tensor(sel[n].rearrange("p e (j t) -> p e j t", t=NT), values,
                                                 m.inside[n][:, :, :].rearrange("p t e -> p e t").unsqueeze(2).to_broadcast([TP, ET, 3, NT]),
                                                 ALU.mult))
                steps.do(nc.vector.tensor_reduce(got[:, :], sel[n], AX.X, ALU.add))

            dve.wait_ge(s("score"), 1)
            split(score[:, :])
            picked("src", 0, 1)
            steps.do(nc.vector.tensor_tensor(got[:, :], got[:, :], m.score_e[:, :], ALU.add))
            steps.do(nc.vector.tensor_scalar(got[:, :], got[:, :], m.score0[:, :], None, ALU.add))
            steps.do(nc.vector.scalar_tensor_tensor(a[:, :], got[:, :], 0.01, got[:, :], ALU.mult, ALU.max), s("a"))
            steps(nc.vector.memset(G[:, :, C:C + 1], 1.0), s("ones"))
            dve.wait_ge(s("a_turned"), 1)
            steps(nc.vector.tensor_copy(at[:, :], m.ps[0:ET, 3, 0:TP]), s("at"))
            dve.wait_ge(s("places"), 16)
            steps(nc.vector.tensor_scalar(mask[:, :], places, m.pcol[0:TP, :], None, ALU.is_equal), s("mask_d"))
            dve.wait_ge(s("drow"), 16)
            with dve.Fori(0, E // (5 * CH)) as i:
                for h in range(5):
                    word = word_of(dve, m, i * 5 + h)
                    dve.wait_ge(s(f"arow{h}"), (i + 1) * 16)
                    for t in range(NT):
                        edges_of_t = (word & ((1 << t) | (1 << (NT + t)))) > 0
                        with dve.If(edges_of_t) as branch:
                            nc.vector.tensor_scalar(off[:, :], drow[:, bass.ds(i * (5 * CH) + h * CH, CH)], dcol[:, t:t + 1],
                                                    -BIG, ALU.not_equal, ALU.mult).then_inc(s("off"), 1)
                            dve.wait_ge(s("off"), i * (10 * NT) + (2 * (h * NT + t) + 1))
                            dve.nop(nofuse=True)
                            nc.vector.tensor_tensor_reduce(mjunk[:, :], arow[h], off[:, :], 1.0, mcol[:, t:t + 1],
                                                           ALU.add, ALU.max, mcol[:, t:t + 1]).then_inc(s("off"), 1)
                            dve.wait_ge(s("off"), i * (10 * NT) + (2 * (h * NT + t) + 2))
                            dve.nop(nofuse=True)
                        with dve.Else():
                            dve.nop(nofuse=True).then_inc(s("off"), 2)
                    nc.vector.memset(tick[:, h:h + 1], 0.0).then_inc(s(f"max_done{h}"), 1)
            dve.wait_ge(s("max_done4"), E // (5 * CH) + 1)
            split(mcol[:, :])
            picked("dst", 5, 2)
            steps(nc.vector.tensor_tensor(a[:, :], a[:, :], got[:, :], ALU.subtract), s("w_in"))
            dve.wait_ge(s("w_edge"), 1)
            with dve.Fori(0, NQ // 2) as i:
                word = word_of(dve, m, i)
                for h in range(2):
                    dve.wait_ge(s(f"woh_used{h}"), i + 1)
                    for t in range(NT):
                        with dve.If(has(word, h, t)):
                            for u in range(4):
                                nc.vector.tensor_scalar(woh[:, h, u, t * TP:(t + 1) * TP], m.iota[0:TP, t * TP:(t + 1) * TP],
                                                        m.dst[:, bass.ds(i * 8 + (4 * h + u), 1)],
                                                        w[:, bass.ds(i * 8 + (4 * h + u), 1)], ALU.is_equal, ALU.mult)
                    nc.vector.memset(tick[:, h:h + 1], 0.0).then_inc(s(f"woh{h}"), 1)
            dve.wait_ge(s("summed"), 1)
            for t in range(NT):
                steps(nc.vector.tensor_scalar(den[:, t:t + 1], m.ps[0:TP, t, C:C + 1], 1e-16, None, ALU.add))
            steps.settle()
            steps.do(nc.vector.reciprocal(den[:, :], den[:, :]))
            for t in range(NT):
                steps(nc.vector.tensor_scalar(res[:, t, 0:C], m.ps[0:TP, t, 0:C], den[:, t:t + 1], 0.0, ALU.mult, ALU.max))
            steps.settle()
            for t in range(NT):
                steps(nc.vector.tensor_tensor(m.x[:, t, :], m.x[:, t, :], res[:, t, 0:C], ALU.add))
            steps.settle()

        @block.tensor
        def _(pe):
            st.credit(pe, "woh_used0", "woh_used1")
            norm_tensor(nc, m, pe, st)
            pe.wait_ge(s("xnT_done"), XNT)
            for t in range(NT):
                for k in range(KC):
                    ins = nc.tensor.matmul(m.ps[0:TP, 3, t:t + 1], m.xnT[:, k, t * TP:(t + 1) * TP], m.q[:, k:k + 1],
                                           start=k == 0, stop=k == KC - 1)
            ins.then_inc(s("score_made"), 1)
            pe.wait_ge(s("w"), 16)
            for t in range(NT):
                if t == 4:
                    pe.wait_ge(s("score"), 1)
                out = m.ps[0:TP, 4 + t if t < 4 else 3, 0:C]
                for k in range(KC):
                    nc.tensor.matmul(out, m.xnT[:, k, t * TP:(t + 1) * TP], wnT[:, k, :], start=k == 0, stop=False)
                nc.tensor.matmul(out, m.ones[0:1, 0:TP], m.row("L1_gnn_bn", 1), start=False, stop=True).then_inc(s("h_made"), 1)

            def pick(bank):
                space = m.ps[0:TP, bank:bank + 3, :].rearrange("p b c -> p (b c)")
                for e in range(ET):
                    ins = nc.tensor.matmul(space[:, e * PW:e * PW + 3 * NT], mask[:, e * TP:(e + 1) * TP],
                                           parts[:, :, :].rearrange("p j t -> p (j t)"), start=True, stop=True)
                ins.then_inc(s("picked"), 1)

            pe.wait_ge(s("parts"), 1)
            pick(0)
            pe.wait_ge(s("a"), 1)
            pe.wait_ge(s("hs"), NT)
            nc.tensor.transpose(m.ps[0:ET, 3, 0:TP], a[:, :], m.ident[0:TP, 0:TP]).then_inc(s("a_turned"), 1)
            pe.wait_ge(s("at"), 1)
            pe.wait_ge(s("ones"), 1)
            zero_banks(nc, m, NT, C + 1, start=True)
            pe.wait_ge(s("mask_d"), 1)
            pe.wait_ge(s("parts"), 2)
            pick(5)
            with pe.Fori(0, NQ // 2) as i:
                word = word_of(pe, m, i)
                for h in range(2):
                    pe.wait_ge(s(f"kept{h}"), i + 2)
                    pe.wait_ge(s(f"woh{h}"), i + 1)
                    for t in range(NT):
                        with pe.If(has(word, h, t)):
                            for u in range(4):
                                nc.tensor.matmul(m.ps[0:TP, t, 0:C + 1], woh[:, h, u, t * TP:(t + 1) * TP],
                                                 G[:, bass.ds(i * 8 + (4 * h + u), 1), :].rearrange("p a c -> p (a c)"),
                                                 start=False, stop=False, skip_group_check=True)
                    mark(nc, m).then_inc(s(f"woh_used{h}"), 1)
            zero_banks(nc, m, NT, C + 1, start=False).then_inc(s("summed"), 1)



class Experts:

    def __init__(self, hidden):
        self.hidden = hidden
        self.units = []
        for layer, chunks_ in enumerate(hidden):
            for e in range(2):
                for half in range(2):
                    for c in range(chunks_):
                        self.units.append((layer, e, half, c))
        for e in range(2):
            for t in range(NT):
                self.units.append((len(hidden), e, t, 0))
        self.uses = [len(range(b, len(self.units), 8)) for b in range(8)]
        self.at = {u: k for k, u in enumerate(self.units)}

    def before(self, k, i):
        return i * self.uses[k % 8] + (k // 8 + 1)

    def left(self, k, i):
        return i * self.uses[k % 8] + (k // 8 + 2)

    def after(self, k, i):
        return i * self.uses[k % 8] + (k // 8 + 1)

    def credit(self, st, dve):
        st.credit(dve, *[f"free{b}" for b in range(8)])

    def last_reader(self, layer, e):
        return max(k for k, u in enumerate(self.units) if u[0] == layer and u[1] == e)

    def load(self, sp, s, i, bufs, source, again=True):
        for layer in range(len(self.hidden) + 1):
            for e in range(2):
                if again:
                    k = self.last_reader(layer, e)
                    sp.wait_ge(s(f"made{k % 8}"), self.after(k, i) - self.uses[k % 8])
                sp.dma_start(bufs[layer][e][:, :], source[bass.ds(i * 2 + e, 1), layer].rearrange("a p n -> (a p) n"))\
                    .then_inc(s(f"w{layer}{e}"), 16)

    def tensor(self, nc, m, pe, s, i, bufs, hT):
        for k, (layer, e, part, c) in enumerate(self.units):
            pe.wait_ge(s(f"free{k % 8}"), self.before(k, i))
            if k == min(self.at[u] for u in self.units if u[0] == layer and u[1] == e):
                pe.wait_ge(s(f"w{layer}{e}"), (i + 1) * 16)
            final = layer == len(self.hidden)
            if layer:
                below = self.hidden[layer - 1]
                for half in ([part] if not final else [0] if part < 2 else [0, 1]):
                    for b in range(below):
                        j = self.at[(layer - 1, e, half, b)]
                        pe.wait_ge(s(f"free{j % 8}"), self.left(j, i))
            src = m.xnT if layer == 0 else hT[layer - 1][e]
            kin = KC if layer == 0 else self.hidden[layer - 1]
            w = bufs[layer][e][:, :].rearrange("p (k n) -> p k n", k=kin)
            for j in range(kin):
                if final:
                    ins = nc.tensor.matmul(m.ps[0:TP, k % 8, 0:C], src[:, j, part * TP:(part + 1) * TP], w[:, j, :],
                                           start=j == 0, stop=j == kin - 1)
                else:
                    a, b = HALF[part]
                    ins = nc.tensor.matmul(m.ps[:, k % 8, 0:b - a], w[:, j, c * P:(c + 1) * P], src[:, j, a:b],
                                           start=j == 0, stop=j == kin - 1)
            ins.then_inc(s(f"made{k % 8}"), 1)

    def scalar(self, nc, m, act, s, i, hT, coef):
        for k, (layer, e, part, c) in enumerate(self.units):
            if layer < len(self.hidden):
                a, b = HALF[part]
                scale, bias = coef(layer, i * 2 + e, c)
                act.wait_ge(s(f"made{k % 8}"), self.after(k, i))
                act.nop(nofuse=True)
                nc.scalar.activation(hT[layer][e][:, c, a:b], m.ps[:, k % 8, 0:b - a], ACT.Relu, bias=bias, scale=scale)\
                    .then_inc(s(f"free{k % 8}"), 1)

    def vector(self, nc, m, dve, s, i, gate, acc):
        final = len(self.hidden)
        for k, (layer, e, t, _) in enumerate(self.units):
            if layer == final:
                dve.wait_ge(s(f"made{k % 8}"), self.after(k, i))
                j = self.at[(final, 1 - e, t, 0)]
                dve.wait_ge(s(f"free{j % 8}"), self.left(j, i) - (self.uses[j % 8] if e == 0 else 0))
                nc.vector.scalar_tensor_tensor(acc[:, t, :], m.ps[0:TP, k % 8, 0:C], gate[:, t, bass.ds(i * 2 + e, 1)],
                                               acc[:, t, :], ALU.mult, ALU.add).then_inc(s(f"free{k % 8}"), 1)


def gate_tensor(nc, m, pe, s, wr, ne, bias, last_bias):
    pe.wait_ge(s("xnT_done"), XNT)
    pe.wait_ge(s("small"), 32)
    for t in range(NT):
        for k in range(KC):
            nc.tensor.matmul(m.ps[0:TP, 3, t * ne:(t + 1) * ne], m.xnT[:, k, t * TP:(t + 1) * TP], wr[:, k, :],
                             start=k == 0, stop=False)
        nc.tensor.matmul(m.ps[0:TP, 3, t * ne:(t + 1) * ne], m.ones[0:1, 0:TP], m.row(bias, 1), start=False, stop=True)\
            .then_inc(s("scores"), 1)


def gate_turn(nc, m, pe, s, gate, gateT, ne, last_bias):
    pe.wait_ge(s("gate"), 1)
    for t in range(NT):
        b, c = (4, t * TP) if t < 4 else (5, 0)
        nc.tensor.transpose(m.ps[0:ne, b, c:c + TP], gate[:, t, :], m.ident[0:TP, 0:TP]).then_inc(s("gate_turned"), 1)
    pe.wait_ge(s("gateT"), 2)
    for t in range(NT):
        b = t if t < 3 else t + 3
        nc.tensor.matmul(m.ps[0:TP, b, 0:C], gateT[:, t * TP:(t + 1) * TP], last_bias[:, :], start=True, stop=True)\
            .then_inc(s("bias_made"), 1)


def gate_scalar(nc, m, act, s, gateT, acc, ne):
    act.wait_ge(s("gate_turned"), NT)
    nc.scalar.activation(gateT[:, 0:4 * TP], m.ps[0:ne, 4, 0:4 * TP], ACT.Copy).then_inc(s("gateT"), 1)
    nc.scalar.activation(gateT[:, 4 * TP:N], m.ps[0:ne, 5, 0:TP], ACT.Copy).then_inc(s("gateT"), 1)
    for t in range(NT):
        act.wait_ge(s("bias_made"), t + 1)
        nc.scalar.activation(acc[:, t, :], m.ps[0:TP, t if t < 3 else t + 3, 0:C], ACT.Copy).then_inc(s("acc"), 1)


def l1_ffn(nc, m, A):
    NE = 8
    plan = Experts([2, 2])
    with ExitStack() as ctx:
        st = Stage(nc, ctx, "l1f")
        s, sb = st.sem, st.sb
        wr = sb("wr", [P, KC, NE])
        bo = sb("bo", [NE, C])
        bufs = [[sb(f"w{l}{e}", [P, 512]) for e in range(2)] for l in range(3)]
        hT = [[sb(f"h{l}{e}", [P, 2, N]) for e in range(2)] for l in range(2)]
        coefs = sb("coefs", [P, 4, 2 * NE])
        cv = sb("cv", [P, 2, 2 * NE])
        half16 = m.mhalf
        score = sb("score", [TP, NT, NE])
        top = sb("top", [TP, NT])
        tot = sb("tot", [TP, NT])
        gate = sb("gate", [TP, NT, NE])
        gateT = sb("gateT", [NE, N])
        acc = sb("acc", [TP, NT, C])
        block = ctx.enter_context(nc.Block())

        @block.sync
        def _(sp):
            sp.dma_start(wr[:, :, :], A["l1f_wr"].rearrange("p (k e) -> p k e", k=KC)).then_inc(s("small"), 16)
            sp.dma_start(bo[:, :], A["L1_ffn_bo"]).then_inc(s("small"), 16)
            plan.load(sp, s, 0, bufs, A["l1f_w"], again=False)
            with sp.Fori(1, NE // 2) as i:
                plan.load(sp, s, i, bufs, A["l1f_w"])

        @block.gpsimd
        def _(pool):
            steps = Steps(pool, s("pool"))
            norm_pool(nc, m, pool, st, steps)
            for n in range(2):
                p = lambda name: m.col(f"L1_ffn_{name}{n + 1}")
                steps.do(nc.gpsimd.tensor_scalar(cv[:, 0, :], p("v"), 1e-3, None, ALU.add))
                steps.do(nc.gpsimd.tensor_tensor(cv[:, 1, :], cv[:, 0, :], m.mhalf[:, :], ALU.pow))
                steps.do(nc.gpsimd.tensor_tensor(coefs[:, 2 * n, :], cv[:, 1, :], p("g"), ALU.mult))
                steps.do(nc.gpsimd.tensor_tensor(cv[:, 0, :], p("b"), p("m"), ALU.subtract))
                steps.do(nc.gpsimd.tensor_tensor(cv[:, 1, :], cv[:, 0, :], coefs[:, 2 * n, :], ALU.mult))
                steps.do(nc.gpsimd.tensor_tensor(coefs[:, 2 * n + 1, :], cv[:, 1, :], p("be"), ALU.add), s("coefs"))

        def coef(layer, e, c):
            return coefs[:, 2 * layer, bass.ds(e * 2 + c, 1)], coefs[:, 2 * layer + 1, bass.ds(e * 2 + c, 1)]

        @block.scalar
        def _(act):
            norm_scalar(nc, m, act, st)
            act.wait_ge(s("exp_in"), 1)
            nc.scalar.activation(gate[:, :, :], score[:, :, :], ACT.Exp).then_inc(s("exp_out"), 1)
            gate_scalar(nc, m, act, s, gateT, acc, NE)
            act.wait_ge(s("coefs"), 2)
            with act.Fori(0, NE // 2) as i:
                plan.scalar(nc, m, act, s, i, hT, coef)

        @block.vector
        def _(dve):
            steps = Steps(dve, s("dve"))
            plan.credit(st, dve)
            norm_vector(nc, m, dve, st, steps)
            dve.wait_ge(s("scores"), NT)
            steps.do(nc.vector.tensor_copy(score[:, :, :], m.ps[0:TP, 3, 0:NT * NE].rearrange("p (t e) -> p t e", t=NT)))
            steps.do(nc.vector.tensor_reduce(top[:, :], score[:, :, :], AX.X, ALU.max))
            steps(nc.vector.tensor_tensor(score[:, :, :], score[:, :, :], top[:, :].unsqueeze(2).to_broadcast([TP, NT, NE]),
                                          ALU.subtract), s("exp_in"))
            dve.wait_ge(s("exp_out"), 1)
            steps.do(nc.vector.tensor_reduce(tot[:, :], gate[:, :, :], AX.X, ALU.add))
            steps.do(nc.vector.reciprocal(top[:, :], tot[:, :]))
            steps(nc.vector.tensor_tensor(gate[:, :, :], gate[:, :, :], top[:, :].unsqueeze(2).to_broadcast([TP, NT, NE]),
                                          ALU.mult), s("gate"))
            dve.wait_ge(s("acc"), NT)
            dve.wait_ge(s("gate"), 1)
            with dve.Fori(0, NE // 2) as i:
                plan.vector(nc, m, dve, s, i, gate, acc)
            for b in range(8):
                dve.wait_ge(s(f"free{b}"), plan.uses[b] * (NE // 2) + 1)
            for t in range(NT):
                steps(nc.vector.tensor_tensor(m.x[:, t, :], m.x[:, t, :], acc[:, t, :], ALU.add))
            steps.settle()

        @block.tensor
        def _(pe):
            norm_tensor(nc, m, pe, st)
            gate_tensor(nc, m, pe, s, wr, NE, "L1_ffn_br", bo)
            gate_turn(nc, m, pe, s, gate, gateT, NE, bo)
            pe.wait_ge(s("acc"), NT)
            with pe.Fori(0, NE // 2) as i:
                plan.tensor(nc, m, pe, s, i, bufs, hT)



def l2_gnn(nc, m, A):
    D1, D2 = 128, 64
    with ExitStack() as ctx:
        st = Stage(nc, ctx, "l2g")
        s, sb = st.sem, st.sb
        W = sb("W", [P, 1344])
        w1 = W[:, 0:256].rearrange("p (k n) -> p k n", k=KC)
        wfc = W[:, 256:1280].rearrange("p (k n) -> p k n", k=4)
        w2 = W[:, 1280:1344]
        adj = sb("adj", [TP, NT, N])
        dinvT = sb("dinvT", [P, N])
        diag = sb("diag", [TP, NT, TP])
        deg = sb("deg", [TP, NT])
        dinv = sb("dinv", [TP, NT])
        h1 = sb("h1", [TP, NT, D1])
        h2 = sb("h2", [TP, NT, D2])
        o = [sb(f"o{n}", [P, N]) for n in range(2)]
        xT = [sb(f"xT{n}", [P, N]) for n in range(2)]
        bst = sb("bst", [P, NT, 6])
        bmv = sb("bmv", [P, 2])
        bt = sb("bt", [P, 8])
        b2 = sb("b2", [D2, 4])
        res = sb("res", [TP, NT, C])
        block = ctx.enter_context(nc.Block())
        dims = [D1, D2]

        @block.sync
        def _(sp):
            sp.dma_start(W[:, 0:1344], A["w_l2g"]).then_inc(s("w"), 16)
            sp.dma_start(b2[:, 0:3], A["l2g_small"]).then_inc(s("w"), 16)

        @block.gpsimd
        def _(pool):
            steps = Steps(pool, s("pool"))
            norm_pool(nc, m, pool, st, steps)
            pool.wait_ge(s("deg"), 1)
            steps(nc.gpsimd.tensor_tensor(dinv[:, :], deg[:, :], m.mhalf[0:TP, 0:NT], ALU.pow), s("dinv"))
            for n, d in enumerate(dims):
                pool.wait_ge(s("bn_var"), n + 1)
                steps.do(nc.gpsimd.tensor_scalar(bt[0:d, 0:1], bmv[0:d, 1:2], 1e-5, None, ALU.add))
                steps(nc.gpsimd.tensor_tensor(bt[0:d, 1:2], bt[0:d, 0:1], m.mhalf[0:d, 0:1], ALU.pow), s("bn_rstd"))

        @block.scalar
        def _(act):
            norm_scalar(nc, m, act, st)
            act.wait_ge(s("deg_made"), 1)
            nc.scalar.activation(deg[:, :], m.ps[0:TP, 5, 0:NT], ACT.Copy).then_inc(s("deg"), 1)
            act.wait_ge(s("dinvT_made"), 2)
            for n, (a, b) in enumerate(((0, 4 * TP), (4 * TP, N))):
                nc.scalar.activation(dinvT[:, a:b], m.ps[:, 1 + n, 0:b - a], ACT.Copy).then_inc(s("dinvT"), 1)
            for n, (d, h) in enumerate(((D1, h1), (D2, h2))):
                for t in range(NT):
                    act.wait_ge(s(f"h_made{n}"), t + 1)
                    nc.scalar.activation(h[:, t, :], m.ps[0:TP, 3 + t, 0:d], ACT.Copy, scale=dinv[:, t:t + 1]).then_inc(s(f"h{n}"), 1)
                act.wait_ge(s("bn_coef"), n + 1)
                nc.scalar.activation(xT[n][0:d, :], o[n][0:d, :], ACT.Relu, bias=bt[0:d, 3:4], scale=bt[0:d, 2:3])\
                    .then_inc(s("xT"), 1)

        @block.vector
        def _(dve):
            steps = Steps(dve, s("dve"))
            for t in range(NT):
                steps(nc.vector.tensor_copy(adj[:, t, :], m.count[:, t, :]))
            steps.settle()
            for t in range(NT):
                steps(nc.vector.tensor_tensor(adj[:, t, t * TP:(t + 1) * TP], adj[:, t, t * TP:(t + 1) * TP],
                                              m.ident[0:TP, 0:TP], ALU.add), s("adj"))
            norm_vector(nc, m, dve, st, steps)
            dve.wait_ge(s("dinv"), 1)
            for t in range(NT):
                steps(nc.vector.tensor_scalar(diag[:, t, :], m.ident[0:TP, 0:TP], dinv[:, t:t + 1], None, ALU.mult), s("diag"))
            dve.wait_ge(s("dinvT"), 2)
            dve.wait_ge(s("w"), 32)
            for n, d in enumerate(dims):
                bias, gam, bet = [m.col("L2_gnn_" + x)[:, 0:1] for x in ("b1", "g1", "be1")] if n == 0 else \
                    [b2[:, x:x + 1] for x in range(3)]
                for i, (a, b) in enumerate(HALF):
                    dve.wait_ge(s(f"o_made{n}"), i + 1)
                    steps.do(nc.vector.tensor_tensor(o[n][0:d, a:b], m.ps[0:d, 1 + i, 0:b - a], dinvT[0:d, a:b], ALU.mult))
                    steps.do(nc.vector.tensor_scalar(o[n][0:d, a:b], o[n][0:d, a:b], bias, None, ALU.add))
                for t in range(NT):
                    steps(nc.vector.bn_stats(bst[0:d, t, :], o[n][0:d, t * TP:(t + 1) * TP]))
                steps.settle()
                steps(nc.vector.bn_aggr(bmv[0:d, :], bst[0:d, :, :].rearrange("p t s -> p (t s)")), s("bn_var"))
                dve.wait_ge(s("bn_rstd"), n + 1)
                steps.do(nc.vector.tensor_tensor(bt[0:d, 2:3], bt[0:d, 1:2], gam, ALU.mult))
                steps.do(nc.vector.tensor_tensor(bt[0:d, 4:5], bmv[0:d, 0:1], bt[0:d, 2:3], ALU.mult))
                steps(nc.vector.tensor_tensor(bt[0:d, 3:4], bet, bt[0:d, 4:5], ALU.subtract), s("bn_coef"))
                if n == 0:
                    dve.wait_ge(s("xT"), 1)
            for t in range(NT):
                dve.wait_ge(s("fc_made"), t + 1)
                steps.do(nc.vector.tensor_scalar(res[:, t, :], m.ps[0:TP, 3 + t, 0:C], 0.0, None, ALU.max))
                steps(nc.vector.tensor_tensor(m.x[:, t, :], m.x[:, t, :], res[:, t, :], ALU.add))
            steps.settle()

        @block.tensor
        def _(pe):
            pe.wait_ge(s("adj"), NT)
            for d in range(NT):
                for t in range(NT):
                    ins = nc.tensor.matmul(m.ps[0:TP, 5, d:d + 1], adj[:, t, d * TP:(d + 1) * TP], m.ones[0:TP, 0:1],
                                           start=t == 0, stop=t == NT - 1)
            ins.then_inc(s("deg_made"), 1)
            norm_tensor(nc, m, pe, st)
            pe.wait_ge(s("xnT_done"), XNT)
            pe.wait_ge(s("w"), 32)
            pe.wait_ge(s("diag"), NT)
            for t in range(NT):
                b, c = (1, t * TP) if t < 4 else (2, 0)
                ins = nc.tensor.matmul(m.ps[:, b, c:c + TP], m.ones[0:TP, :], diag[:, t, :], start=True, stop=True)
                if t >= 3:
                    ins.then_inc(s("dinvT_made"), 1)
            for t in range(NT):
                for k in range(KC):
                    ins = nc.tensor.matmul(m.ps[0:TP, 3 + t, 0:D1], m.xnT[:, k, t * TP:(t + 1) * TP], w1[:, k, :],
                                           start=k == 0, stop=k == KC - 1)
                ins.then_inc(s("h_made0"), 1)
            for n, (d, h) in enumerate(((D1, h1), (D2, h2))):
                if n == 1:
                    pe.wait_ge(s("xT"), 1)
                    for t in range(NT):
                        nc.tensor.matmul(m.ps[0:TP, 3 + t, 0:D2], xT[0][:, t * TP:(t + 1) * TP], w2[:, :], start=True,
                                         stop=True).then_inc(s("h_made1"), 1)
                pe.wait_ge(s(f"h{n}"), NT)
                pe.wait_ge(s("dinvT"), 2)
                for i, (a, b) in enumerate(HALF):
                    for t in range(NT):
                        ins = nc.tensor.matmul(m.ps[0:d, 1 + i, 0:b - a], h[:, t, :], adj[:, t, a:b], start=t == 0,
                                               stop=t == NT - 1)
                    ins.then_inc(s(f"o_made{n}"), 1)
            pe.wait_ge(s("xT"), 2)
            for t in range(NT):
                cols = slice(t * TP, (t + 1) * TP)
                parts = [(m.xnT[:, 0, cols], wfc[:, 0, :]), (m.xnT[:, 1, cols], wfc[:, 1, :]), (xT[0][:, cols], wfc[:, 2, :]),
                         (xT[1][0:D2, cols], wfc[0:D2, 3, :]), (m.ones[0:1, 0:TP], m.row("L2_gnn_bfc", 1))]
                for j, (lhsT, rhs) in enumerate(parts):
                    ins = nc.tensor.matmul(m.ps[0:TP, 3 + t, 0:C], lhsT, rhs, start=j == 0, stop=j == 4)
                ins.then_inc(s("fc_made"), 1)


def l2_ffn(nc, m, A):
    NE, NB = 16, 26
    with ExitStack() as ctx:
        st = Stage(nc, ctx, "l2f")
        s, sb = st.sem, st.sb
        xs_d = nc.dram_tensor("l2_sorted", ((NB + 2) * P, C), F32, kind="Internal").ap()
        y_d = nc.dram_tensor("l2_results", (NB * P, C), F32, kind="Internal").ap()
        wr = sb("wr", [P, KC, NE])
        b2 = sb("b2", [NE, C])
        w1 = [sb(f"w1{h}", [P, 1024]) for h in range(2)]
        w2 = [sb(f"w2{h}", [P, 1024]) for h in range(2)]
        empty = sb("empty", [P, C])
        xb = [sb(f"xb{h}", [P, C]) for h in range(2)]
        xT = [sb(f"xT{h}", [P, KC, P]) for h in range(2)]
        hT = [sb(f"hT{h}", [P, 4, P]) for h in range(2)]
        yb = [sb(f"yb{h}", [P, C]) for h in range(2)]
        yg = sb("yg", [TP, 2, NT, C])
        score = sb("score", [TP, NT, NE])
        left = sb("left", [TP, NT, NE])
        pick = sb("pick", [TP, 2, NT, NE])
        at = sb("at", [TP, 2, NT, NE])
        low = sb("low", [TP, NT, NE])
        top = sb("top", [TP, 8, NT])
        gate = sb("gate", [TP, NT, NE])
        gateT = sb("gateT", [NE, N])
        chosen = sb("chosen", [TP, NT, NE], BF16)
        lower = sb("lower", [TP, TP], BF16)
        all16 = sb("all16", [TP, TP], BF16)
        blocks = sb("blocks", [TP, NE])
        ends = [sb(f"ends{v}", [TP, NE]) for v in range(2)]
        first = sb("first", [TP, NE])
        slot = sb("slot", [TP, 2, NT])
        slot_i = sb("slot_i", [TP, 2, NT], I32)
        after = sb("after", [1, NB, NE])
        owner = sb("owner", [1, NB])
        uses = sb("uses", [1, 2])
        uses_i = sb("uses_i", [1, 2], I32)
        table = sb("table", [1, 2, NB], I32)
        acc = sb("acc", [TP, NT, C])
        z = sb("z", [TP, NT, C])
        block = ctx.enter_context(nc.Block())

        def expert_of(eng, b):
            return eng.value_load(table[0:1, 0, bass.ds(b, 1)], min_val=0, max_val=NE - 1)

        def used(eng, b):
            return eng.value_load(table[0:1, 1, bass.ds(b, 1)], min_val=0, max_val=1) > 0


        @block.sync
        def _(sp):
            sp.dma_start(wr[:, :, :], A["l2f_wr"].rearrange("p (k e) -> p k e", k=KC)).then_inc(s("small"), 16)
            sp.dma_start(b2[:, :], A["L2_ffn_b2"]).then_inc(s("small"), 16)
            sp.wait_ge(s("empty"), 1)
            sp.dma_start(xs_d.rearrange("(b p) c -> p b c", p=P), empty[:, :].unsqueeze(1).to_broadcast([P, NB + 2, C]))\
                .then_inc(s("cleared"), 16)
            sp.wait_ge(s("tables"), 1)
            with sp.Fori(0, NB // 2) as i:
                for h in range(2):
                    e = expert_of(sp, i * 2 + h)
                    with sp.If(used(sp, i * 2 + h)):
                        for l, (w, last_use) in enumerate(((w1, "h_made1"), (w2, "y_made"))):
                            sp.wait_ge(s(f"{last_use}{h}"), i + 1)
                            sp.dma_start(w[h][:, :], A["l2f_w"][bass.ds(e, 1), l].rearrange("a p n -> (a p) n"))\
                                .then_inc(s(f"w{l}{h}"), 16)
                        sp.nop(nofuse=True).then_inc(s("no_results"), 16)
                    with sp.Else():
                        sp.dma_start(y_d[bass.ds((i * 2 + h) * P, P), :], empty[:, :]).then_inc(s("no_results"), 16)

        @block.gpsimd
        def _(pool):
            steps = Steps(pool, s("pool"))
            st.credit(pool, "yb_free0", "yb_free1")
            steps(nc.gpsimd.memset(empty[:, :], 0.0), s("empty"))
            norm_pool(nc, m, pool, st, steps)
            pool.wait_ge(s("cleared"), 16)
            pool.wait_ge(s("slots"), 1)
            for t in range(NT):
                for j in range(2):
                    pool.indirect_dma_start(out=xs_d, out_offset=bass.IndirectOffsetOnAxis(ap=slot_i[:, j, t:t + 1], axis=0),
                                            in_=m.xn[:, t, :], in_offset=None).then_inc(s("sorted"), 16)
            pool.wait_ge(s("sorted"), 160)
            pool.wait_ge(s("tables"), 1)
            pool.nop(nofuse=True).then_inc(s("rows_sorted"), 1)
            with pool.Fori(0, NB // 2) as i:
                for h in range(2):
                    with pool.If(used(pool, i * 2 + h)):
                        pool.wait_ge(s(f"y_taken{h}"), i + 2)
                        pool.dma_start(y_d[bass.ds((i * 2 + h) * P, P), :], yb[h][:, :]).then_inc(s(f"y_out{h}"), 16)
                        pool.wait_ge(s(f"y_out{h}"), i * 16 + 16)
                        pool.nop(nofuse=True).then_inc(s(f"yb_free{h}"), 1)
            pool.wait_ge(s("no_results"), 16 * NB)
            for t in range(NT):
                for j in range(2):
                    pool.indirect_dma_start(out=yg[:, j, t, :], out_offset=None, in_=y_d,
                                            in_offset=bass.IndirectOffsetOnAxis(ap=slot_i[:, j, t:t + 1], axis=0))\
                        .then_inc(s(f"yg{t}"), 16)
            pool.wait_ge(s("z_stats"), NT)
            steps.do(nc.gpsimd.tensor_scalar(m.veps[0:TP, :], m.mv[:, :, 1], 1e-5, None, ALU.add))
            steps(nc.gpsimd.tensor_tensor(m.rstd[0:TP, :], m.veps[0:TP, :], m.mhalf[0:TP, 0:NT], ALU.pow), s("z_rstd"))

        @block.scalar
        def _(act):
            st.credit(act, "hT0", "hT1")
            norm_scalar(nc, m, act, st)
            act.wait_ge(s("exp_in"), 1)
            nc.scalar.activation(top[:, 3, :], top[:, 2, :], ACT.Exp).then_inc(s("exp_out"), 1)
            gate_scalar(nc, m, act, s, gateT, acc, NE)
            act.wait_ge(s("tables"), 1)
            act.wait_ge(s("rows_sorted"), 1)
            for h in range(2):
                act.dma_start(xb[h][:, :], xs_d[h * P:(h + 1) * P, :]).then_inc(s(f"xb{h}"), 16)
            with act.Fori(0, NB // 2) as i:
                for h in range(2):
                    e = expert_of(act, i * 2 + h)
                    with act.If(used(act, i * 2 + h)):
                        for c in range(4):
                            if c % 2 == 0:
                                act.wait_ge(s(f"h_made{c // 2}{h}"), i + 2)
                                act.nop(nofuse=True)
                            nc.scalar.activation(hT[h][:, c, :], m.ps[:, 2 + c // 2 * 2 + h, (c % 2) * P:(c % 2 + 1) * P], ACT.Relu,
                                                 bias=m.col("L2_ffn_b1")[:, bass.ds(e * 4 + c, 1)]).then_inc(s(f"hT{h}"), 1)
                        act.wait_ge(s(f"x_turned{h}"), i + 2)
                        act.dma_start(xb[h][:, :], xs_d[bass.ds((i * 2 + (h + 2)) * P, P), :]).then_inc(s(f"xb{h}"), 16)

            for h in range(2):
                n = act.value_load(uses_i[0:1, h:h + 1], min_val=1, max_val=NB // 2)
                act.wait_ge(s(f"xb{h}"), n * 16 + 16)
                act.nop(nofuse=True)

        @block.vector
        def _(dve):
            def wide(ap):
                return ap.unsqueeze(2).to_broadcast([TP, NT, NE])

            steps = Steps(dve, s("dve"))
            st.credit(dve, "y_taken0", "y_taken1")
            steps(nc.vector.memset(all16[:, :], 1.0))
            steps(nc.vector.tensor_scalar(lower[:, :], m.iota16[0:TP, 0:TP], m.pcol[0:TP, :], None, ALU.is_gt), s("lower"))
            norm_vector(nc, m, dve, st, steps)
            dve.wait_ge(s("scores"), NT)
            steps.do(nc.vector.tensor_copy(score[:, :, :], m.ps[0:TP, 3, 0:NT * NE].rearrange("p (t e) -> p t e", t=NT)))
            iota = m.iota[0:TP, 0:NE].unsqueeze(1).to_broadcast([TP, NT, NE])
            src = score
            for j in range(2):
                steps.do(nc.vector.tensor_reduce(top[:, j, :], src[:, :, :], AX.X, ALU.max))
                steps.do(nc.vector.tensor_tensor(low[:, :, :], src[:, :, :], wide(top[:, j, :]), ALU.is_equal))
                steps.do(nc.vector.tensor_scalar(low[:, :, :], low[:, :, :], -1000.0, None, ALU.mult))
                steps.do(nc.vector.tensor_tensor(low[:, :, :], low[:, :, :], iota, ALU.add))
                steps.do(nc.vector.tensor_reduce(top[:, 4 + j, :], low[:, :, :], AX.X, ALU.min))
                steps.do(nc.vector.tensor_tensor(pick[:, j, :, :], low[:, :, :], wide(top[:, 4 + j, :]), ALU.is_equal))
                if j == 0:
                    steps.do(nc.vector.tensor_scalar(low[:, :, :], pick[:, 0, :, :], -1e30, None, ALU.mult))
                    steps.do(nc.vector.tensor_tensor(left[:, :, :], score[:, :, :], low[:, :, :], ALU.add))
                    src = left
            steps(nc.vector.tensor_tensor(chosen[:, :, :], pick[:, 0, :, :], pick[:, 1, :, :], ALU.add), s("chosen"))
            steps(nc.vector.tensor_tensor(top[:, 2, :], top[:, 1, :], top[:, 0, :], ALU.subtract), s("exp_in"))
            dve.wait_ge(s("ranked"), 1)
            nodes = m.ps[0:TP, 7, 0:NE]
            steps.do(nc.vector.tensor_scalar(blocks[:, :], nodes, 0.5, None, ALU.is_ge))
            for k in range(1, NT):
                steps.do(nc.vector.scalar_tensor_tensor(blocks[:, :], nodes, k * P + 0.5, blocks[:, :], ALU.is_ge, ALU.add))
            src, d = blocks, 1
            while d < NE:
                dst = ends[1] if src is ends[0] else ends[0]
                steps(nc.vector.tensor_copy(dst[:, 0:d], src[:, 0:d]))
                steps.do(nc.vector.tensor_tensor(dst[:, d:NE], src[:, d:NE], src[:, 0:NE - d], ALU.add))
                src, d = dst, 2 * d
            end = src
            steps.do(nc.vector.tensor_tensor(first[:, :], end[:, :], blocks[:, :], ALU.subtract))
            steps.do(nc.vector.scalar_tensor_tensor(low[:, :, :], first[:, :].unsqueeze(1).to_broadcast([TP, NT, NE]), float(P),
                                                    m.ps[0:TP, 6, 0:NT * NE].rearrange("p (t e) -> p t e", t=NT), ALU.mult, ALU.add))
            for j in range(2):
                steps(nc.vector.tensor_tensor(at[:, j, :, :], pick[:, j, :, :], low[:, :, :], ALU.mult))
            steps.settle()
            steps.do(nc.vector.tensor_reduce(slot[:, :, :], at[:, :, :, :], AX.X, ALU.add))
            steps(nc.vector.tensor_copy(slot_i[:, :, :], slot[:, :, :]), s("slots"))
            steps.do(nc.vector.tensor_tensor(after[:, :, :], m.iota[0:1, 0:NB].unsqueeze(2).to_broadcast([1, NB, NE]),
                                             end[0:1, :].unsqueeze(1).to_broadcast([1, NB, NE]), ALU.is_ge))
            steps.do(nc.vector.tensor_reduce(owner[:, :], after[:, :, :], AX.X, ALU.add))
            steps(nc.vector.tensor_scalar(table[:, 0, :], owner[:, :], float(NE - 1), None, ALU.min))
            steps(nc.vector.tensor_scalar(table[:, 1, :], owner[:, :], NE - 0.5, None, ALU.is_lt))
            steps.do(nc.vector.tensor_scalar(owner[:, :], owner[:, :], NE - 0.5, None, ALU.is_lt))
            steps.do(nc.vector.tensor_reduce(uses[:, :], owner[:, :].rearrange("p (i h) -> p h i", h=2), AX.X, ALU.add))
            steps.do(nc.vector.tensor_copy(uses_i[:, :], uses[:, :]), s("tables"))
            dve.wait_ge(s("exp_out"), 1)
            steps.do(nc.vector.tensor_scalar(top[:, 6, :], top[:, 3, :], 1.0, None, ALU.add))
            steps.do(nc.vector.reciprocal(top[:, 7, :], top[:, 6, :]))
            steps.do(nc.vector.tensor_tensor(top[:, 6, :], top[:, 3, :], top[:, 7, :], ALU.mult))
            steps.do(nc.vector.tensor_tensor(low[:, :, :], pick[:, 0, :, :], wide(top[:, 7, :]), ALU.mult))
            steps.do(nc.vector.tensor_tensor(left[:, :, :], pick[:, 1, :, :], wide(top[:, 6, :]), ALU.mult))
            steps(nc.vector.tensor_tensor(gate[:, :, :], low[:, :, :], left[:, :, :], ALU.add), s("gate"))

            def turned(i, h, more):
                dve.wait_ge(s(f"x_turned{h}"), i + (more + 1))
                nc.vector.tensor_copy(xT[h][:, :, :], m.ps[:, h, 0:KC * P].rearrange("p (k n) -> p k n", k=KC))\
                    .then_inc(s(f"xT{h}"), 1)

            turned(0, 0, 1)
            with dve.Fori(0, NB // 2) as i:
                for h in range(2):
                    with dve.If(used(dve, i * 2 + h)):
                        turned(i, 1 - h, h + 1)
                        dve.wait_ge(s(f"y_made{h}"), i + 2)
                        dve.wait_ge(s(f"yb_free{h}"), i + 1)
                        nc.vector.tensor_copy(yb[h][:, :], m.ps[:, 6 + h, 0:C]).then_inc(s(f"y_taken{h}"), 1)
            dve.wait_ge(s("acc"), NT)
            for t in range(NT):
                dve.wait_ge(s(f"yg{t}"), 32)
                for j in range(2):
                    steps.do(nc.vector.scalar_tensor_tensor(acc[:, t, :], yg[:, j, t, :], top[:, 7 - j, t:t + 1], acc[:, t, :],
                                                            ALU.mult, ALU.add))
            for t in range(NT):
                steps(nc.vector.tensor_tensor(z[:, t, :], acc[:, t, :], m.xn[:, t, :], ALU.add))
            steps.settle()
            norm_tail(nc, m, dve, s, steps, z, acc, "L2_ffn_gamma", "L2_ffn_beta")

        @block.tensor
        def _(pe):
            st.credit(pe, *[f"{n}{h}" for n in ("x_turned", "h_made0", "h_made1", "y_made") for h in range(2)])
            norm_tensor(nc, m, pe, st)
            gate_tensor(nc, m, pe, s, wr, NE, "L2_ffn_gate_b", b2)
            pe.wait_ge(s("lower"), 1)
            pe.wait_ge(s("chosen"), 1)
            for t in range(NT):
                for u in range(t + 1):
                    nc.tensor.matmul(m.ps[0:TP, 6, t * NE:(t + 1) * NE], (lower if u == t else all16)[:, :], chosen[:, u, :],
                                     start=u == 0, stop=u == t)
            for u in range(NT):
                ins = nc.tensor.matmul(m.ps[0:TP, 7, 0:NE], all16[:, :], chosen[:, u, :], start=u == 0, stop=u == NT - 1)
            ins.then_inc(s("ranked"), 1)
            pe.wait_ge(s("slots"), 1)
            gate_turn(nc, m, pe, s, gate, gateT, NE, b2)
            pe.wait_ge(s("acc"), NT)

            def turn(i, h, more):
                pe.wait_ge(s(f"xb{h}"), i * 16 + 16 * more)
                for k in range(KC):
                    ins = nc.tensor.transpose(m.ps[:, h, k * P:(k + 1) * P], xb[h][:, k * P:(k + 1) * P], m.ident[:, :])
                ins.then_inc(s(f"x_turned{h}"), 1)

            turn(0, 0, 1)
            with pe.Fori(0, NB // 2) as i:
                for h in range(2):
                    with pe.If(used(pe, i * 2 + h)):
                        pe.wait_ge(s(f"w0{h}"), (i + 1) * 16)
                        pe.wait_ge(s(f"xT{h}"), i + 1)
                        pe.wait_ge(s(f"hT{h}"), i * 4 + 1)
                        for c in range(4):
                            for k in range(KC):
                                ins = nc.tensor.matmul(m.ps[:, 2 + c // 2 * 2 + h, (c % 2) * P:(c % 2 + 1) * P],
                                                       w1[h][:, (k * 4 + c) * P:(k * 4 + c + 1) * P], xT[h][:, k, :],
                                                       start=k == 0, stop=k == KC - 1)
                            if c % 2:
                                ins.then_inc(s(f"h_made{c // 2}{h}"), 1)
                        turn(i, 1 - h, h + 1)
                        pe.wait_ge(s(f"w1{h}"), (i + 1) * 16)
                        pe.wait_ge(s(f"y_taken{h}"), i + 1)
                        for c in range(4):
                            pe.wait_ge(s(f"hT{h}"), i * 4 + (c + 2))
                            ins = nc.tensor.matmul(m.ps[:, 6 + h, 0:C], hT[h][:, c, :], w2[h][:, c * C:(c + 1) * C],
                                                   start=c == 0, stop=c == 3)
                        ins.then_inc(s(f"y_made{h}"), 1)


def norm_tail(nc, m, dve, s, steps, z, other, gamma, beta, extra=None):
    for t in range(NT):
        steps(nc.vector.bn_stats(m.stats[:, t, :], z[:, t, :]))
    steps.settle()
    for t in range(NT):
        steps(nc.vector.bn_aggr(m.mv[:, t, :], m.stats[:, t, :]), s("z_stats"))
    if extra is not None:
        for t in range(NT):
            steps(nc.vector.tensor_tensor(m.x[:, t, :], m.x[:, t, :], extra[:, t, :], ALU.add))
    dve.wait_ge(s("z_rstd"), 1)
    for t in range(NT):
        steps(nc.vector.tensor_scalar(other[:, t, :], z[:, t, :], m.mv[:, t, 0:1], m.rstd[0:TP, t:t + 1],
                                      ALU.subtract, ALU.mult))
    steps.settle()
    for src, dst, op, with_ in ((other, z, ALU.mult, gamma), (z, other, ALU.add, beta)):
        for t in range(NT):
            steps(nc.vector.tensor_tensor(dst[:, t, :], src[:, t, :], m.row(with_), op))
        steps.settle()
    for t in range(NT):
        steps(nc.vector.tensor_tensor(m.x[:, t, :], m.x[:, t, :], other[:, t, :], ALU.add))
    steps.settle()



def l3_gnn(nc, m, A):
    with ExitStack() as ctx:
        st = Stage(nc, ctx, "l3g")
        s, sb = st.sem, st.sb
        W = sb("W", [P, 1024])
        wl = W[:, 0:512].rearrange("p (k n) -> p k n", k=KC)
        wr = W[:, 512:1024].rearrange("p (k n) -> p k n", k=KC)
        rdeg = sb("rdeg", [P, N])
        aggT = sb("aggT", [P, KC, N])
        f = sb("f", [TP, NT, C])
        g = sb("g", [TP, NT, C])
        block = ctx.enter_context(nc.Block())

        @block.sync
        def _(sp):
            sp.dma_start(W[:, 0:1024], A["w_l3g"]).then_inc(s("w"), 16)

        @block.gpsimd
        def _(pool):
            steps = Steps(pool, s("pool"))
            norm_pool(nc, m, pool, st, steps)
            pool.wait_ge(s("z_stats"), NT)
            steps.do(nc.gpsimd.tensor_scalar(m.veps[0:TP, :], m.mv[:, :, 1], 1e-5, None, ALU.add))
            steps(nc.gpsimd.tensor_tensor(m.rstd[0:TP, :], m.veps[0:TP, :], m.mhalf[0:TP, 0:NT], ALU.pow), s("z_rstd"))

        @block.scalar
        def _(act):
            norm_scalar(nc, m, act, st)
            for t in range(NT):
                act.wait_ge(s("f_made"), t + 1)
                nc.scalar.activation(f[:, t, :], m.ps[0:TP, t, 0:C], ACT.Gelu).then_inc(s("f"), 1)

        @block.vector
        def _(dve):
            steps = Steps(dve, s("dve"))
            norm_vector(nc, m, dve, st, steps)
            for n, (a, b) in enumerate(HALF):
                dve.wait_ge(s("deg_made"), n + 1)
                steps.do(nc.vector.tensor_scalar(rdeg[:, a:b], m.ps[:, 3 + n, 0:b - a], 1.0, None, ALU.max))
            steps.do(nc.vector.reciprocal(rdeg[:, :], rdeg[:, :]))
            unit = 0
            for c in range(KC):
                for (a, b) in HALF:
                    dve.wait_ge(s("agg_made"), unit + 1)
                    steps(nc.vector.tensor_tensor(aggT[:, c, a:b], m.ps[:, 3 + unit, 0:b - a], rdeg[:, a:b], ALU.mult), s("aggT"))
                    unit += 1
            dve.wait_ge(s("f"), NT)
            norm_tail(nc, m, dve, s, steps, f, g, "L3_gnn_ln_gamma", "L3_gnn_ln_beta", extra=m.xn)

        @block.tensor
        def _(pe):
            for n, (a, b) in enumerate(HALF):
                for t in range(NT):
                    ins = nc.tensor.matmul(m.ps[:, 3 + n, 0:b - a], m.ones[0:TP, :], m.count[:, t, a:b], start=t == 0,
                                           stop=t == NT - 1)
                ins.then_inc(s("deg_made"), 1)
            norm_tensor(nc, m, pe, st)
            pe.wait_ge(s("dve"), NT + 2)
            unit = 0
            for c in range(KC):
                for (a, b) in HALF:
                    for t in range(NT):
                        ins = nc.tensor.matmul(m.ps[:, 3 + unit, 0:b - a], m.xn[:, t, c * P:(c + 1) * P], m.count[:, t, a:b],
                                               start=t == 0, stop=t == NT - 1)
                    ins.then_inc(s("agg_made"), 1)
                    unit += 1
            pe.wait_ge(s("w"), 16)
            pe.wait_ge(s("xnT_done"), XNT)
            pe.wait_ge(s("aggT"), 4)
            for t in range(NT):
                cols = slice(t * TP, (t + 1) * TP)
                parts = [(aggT[:, k, cols], wl[:, k, :]) for k in range(KC)] + [(m.xnT[:, k, cols], wr[:, k, :]) for k in range(KC)] + \
                    [(m.ones[0:1, 0:TP], m.row("L3_gnn_b_l", 1))]
                for j, (lhsT, rhs) in enumerate(parts):
                    ins = nc.tensor.matmul(m.ps[0:TP, t, 0:C], lhsT, rhs, start=j == 0, stop=j == len(parts) - 1)
                ins.then_inc(s("f_made"), 1)



def l3_ffn(nc, m, A):
    NH, D, G = 8, 64, 64
    SCALE = D ** -0.5
    with ExitStack() as ctx:
        st = Stage(nc, ctx, "l3f")
        s, sb = st.sem, st.sb
        wbig = sb("wbig", [P, 1024])
        w64 = sb("w64", [D, 4096 + 4 * D + NH])
        wfx = wbig[:, 0:1024].rearrange("p (k n) -> p k n", k=KC)
        wxT = w64[:, 0:2048].rearrange("p (h c) -> p h c", h=NH)
        wout = w64[:, 2048:4096].rearrange("p (h c) -> p h c", h=NH)
        small = w64[:, 4096:4096 + 4 * D + NH].rearrange("p n -> p n")
        wsl, wq, wk, wv = [small[:, D * i:D * (i + 1)] for i in range(4)]
        bxT = small[:, 4 * D:4 * D + NH]
        itemp = sb("itemp", [P, NH])
        wc = sb("wc", [P, KC, NH, G])
        bc = sb("bc", [1, NH, G])
        sw = sb("sw", [TP, NT, NH, G])
        mx = sb("mx", [TP, NT, NH])
        rs = sb("rs", [TP, NT, NH])
        zT = sb("zT", [P, KC, NH * G])
        norm = sb("norm", [G, NH * G])
        rnorm = sb("rnorm", [G, NH * G])
        tokT = sb("tokT", [D, NH * G])
        qT = sb("qT", [D, NH * G])
        kT = sb("kT", [D, NH * G])
        v = sb("v", [G, NH, D])
        at = sb("at", [G, NH, G])
        amx = sb("amx", [G, NH])
        atT = sb("atT", [G, NH, G])
        osT = sb("osT", [D, NH, G])
        pw = sb("pw", [G, NH, C])
        swT = sb("swT", [G, NH, N])
        block = ctx.enter_context(nc.Block())

        @block.sync
        def _(sp):
            sp.dma_start(wbig[:, :], A["l3f_wfx"]).then_inc(s("w"), 16)
            sp.dma_start(w64[:, 0:4096 + 4 * D + NH], A["l3f_w64"]).then_inc(s("w"), 16)

        @block.gpsimd
        def _(pool):
            steps = Steps(pool, s("pool"))
            norm_pool(nc, m, pool, st, steps)

        @block.scalar
        def _(act):
            norm_scalar(nc, m, act, st)
            for t in range(NT):
                act.wait_ge(s("sw_in"), t + 1)
                nc.scalar.activation(sw[:, t, :, :], sw[:, t, :, :], ACT.Exp).then_inc(s("sw_exp"), 1)
            for j in range(2):
                act.wait_ge(s("qk_made"), j + 1)
                nc.scalar.activation((qT, kT)[j][:, :], m.ps[0:D, 2 + j, :], ACT.Copy).then_inc(s("qk"), 1)
            act.wait_ge(s("v_made"), 1)
            nc.scalar.activation(v[:, :, :], m.ps[0:G, 4, :].rearrange("p (h d) -> p h d", h=NH), ACT.Copy).then_inc(s("v"), 1)
            for h in range(NH):
                for n in range(2):
                    act.wait_ge(s("sw_turned"), 2 * h + n + 1)
                    a, b = ((0, 4 * TP), (4 * TP, N))[n]
                    nc.scalar.activation(swT[:, h, a:b], m.ps[0:G, 6 + n, 0:b - a], ACT.Copy).then_inc(s("swT"), 1)
            act.wait_ge(s("at_in"), 1)
            nc.scalar.activation(at[:, :, :], at[:, :, :], ACT.Exp, scale=SCALE).then_inc(s("at_exp"), 1)
            act.wait_ge(s("atT_made"), 1)
            nc.scalar.activation(atT[:, :, :], m.ps[0:G, 0, :].rearrange("p (h d) -> p h d", h=NH), ACT.Copy).then_inc(s("atT"), 1)
            act.wait_ge(s("osT_made"), 1)
            nc.scalar.activation(osT[:, :, :], m.ps[0:D, 1, :].rearrange("p (h d) -> p h d", h=NH), ACT.Copy).then_inc(s("osT"), 1)
            for h in range(NH):
                act.wait_ge(s("pw_made"), h + 1)
                nc.scalar.activation(pw[:, h, :], m.ps[0:G, 2 + h % 4, 0:C], ACT.Copy).then_inc(s("pw"), 1)

        @block.vector
        def _(dve):
            steps = Steps(dve, s("dve"))
            steps.do(nc.vector.tensor_scalar(itemp[:, :], m.row("L3_ffn_temperature", P), 0.1, 5.0, ALU.max, ALU.min))
            steps.do(nc.vector.reciprocal(itemp[:, :], itemp[:, :]))
            for c in range(KC):
                dve.wait_ge(s("wc_made"), c + 1)
                steps(nc.vector.tensor_tensor(wc[:, c, :, :], m.ps[:, 3 + c, :].rearrange("p (h g) -> p h g", h=NH),
                                              itemp[:, :].unsqueeze(2).to_broadcast([P, NH, G]), ALU.mult), s("wc"))
            dve.wait_ge(s("bc_made"), 1)
            steps.do(nc.vector.tensor_tensor(bc[:, :, :], m.ps[0:1, 5, :].rearrange("p (h g) -> p h g", h=NH),
                                             m.row("L3_ffn_b_slice", 1).unsqueeze(1).to_broadcast([1, NH, G]), ALU.add))
            steps(nc.vector.tensor_tensor(bc[:, :, :], bc[:, :, :], itemp[0:1, :].unsqueeze(2).to_broadcast([1, NH, G]),
                                          ALU.mult), s("wc"))
            norm_vector(nc, m, dve, st, steps)
            for t in range(NT):
                dve.wait_ge(s("logits"), t + 1)
                lg = m.ps[0:TP, (3, 4, 5, 6, 7)[t], :].rearrange("p (h g) -> p h g", h=NH)
                steps.do(nc.vector.tensor_reduce(mx[:, t, :], lg, AX.X, ALU.max))
                steps(nc.vector.tensor_tensor(sw[:, t, :, :], lg, mx[:, t, :].unsqueeze(2).to_broadcast([TP, NH, G]),
                                              ALU.subtract), s("sw_in"))
            for t in range(NT):
                dve.wait_ge(s("sw_exp"), t + 1)
                steps.do(nc.vector.tensor_reduce(mx[:, t, :], sw[:, t, :, :], AX.X, ALU.add))
                steps.do(nc.vector.reciprocal(rs[:, t, :], mx[:, t, :]))
                steps(nc.vector.tensor_tensor(sw[:, t, :, :], sw[:, t, :, :], rs[:, t, :].unsqueeze(2).to_broadcast([TP, NH, G]),
                                              ALU.mult), s("sw"))
            dve.wait_ge(s("norm_made"), 1)
            steps(nc.vector.tensor_copy(norm[:, :], m.ps[0:G, 2, :]), s("norm"))
            steps.settle()
            steps.do(nc.vector.tensor_scalar(rnorm[:, :], norm[:, :], 1e-5, None, ALU.add))
            steps.do(nc.vector.reciprocal(rnorm[:, :], rnorm[:, :]))
            for c in range(KC):
                dve.wait_ge(s("z_made"), c + 1)
                steps(nc.vector.tensor_copy(zT[:, c, :], m.ps[:, c, :]), s("zT"))
            dve.wait_ge(s("tok_made"), 1)
            steps(nc.vector.tensor_tensor(tokT[:, :], m.ps[0:D, 5, :], rnorm[:, :], ALU.mult), s("tokT"))
            dve.wait_ge(s("att_made"), 1)
            lg = m.ps[0:G, 5, :].rearrange("p (h g) -> p h g", h=NH)
            steps.do(nc.vector.tensor_reduce(amx[:, :], lg, AX.X, ALU.max))
            steps(nc.vector.tensor_tensor(at[:, :, :], lg, amx[:, :].unsqueeze(2).to_broadcast([G, NH, G]), ALU.subtract), s("at_in"))
            dve.wait_ge(s("at_exp"), 1)
            steps.do(nc.vector.tensor_reduce(amx[:, :], at[:, :, :], AX.X, ALU.add))
            steps.do(nc.vector.reciprocal(amx[:, :], amx[:, :]))
            steps(nc.vector.tensor_tensor(at[:, :, :], at[:, :, :], amx[:, :].unsqueeze(2).to_broadcast([G, NH, G]), ALU.mult), s("at"))
            for t in range(NT):
                dve.wait_ge(s("out_made"), t + 1)
                steps(nc.vector.tensor_tensor(m.x[:, t, :], m.x[:, t, :], m.ps[0:TP, (6, 7, 0, 1, 2)[t], 0:C], ALU.add))
            steps.settle()

        @block.tensor
        def _(pe):
            pe.wait_ge(s("w"), 32)
            for c in range(KC):
                for h in range(NH):
                    ins = nc.tensor.matmul(m.ps[:, 3 + c, h * G:(h + 1) * G], wxT[:, h, c * P:(c + 1) * P], wsl, start=True, stop=True)
                ins.then_inc(s("wc_made"), 1)
            for h in range(NH):
                ins = nc.tensor.matmul(m.ps[0:1, 5, h * G:(h + 1) * G], bxT[:, h:h + 1], wsl, start=True, stop=True)
            ins.then_inc(s("bc_made"), 1)
            norm_tensor(nc, m, pe, st)
            pe.wait_ge(s("xnT_done"), XNT)
            pe.wait_ge(s("wc"), 3)
            for t in range(NT):
                b = (3, 4, 5, 6, 7)[t]
                for k in range(KC):
                    nc.tensor.matmul(m.ps[0:TP, b, :], m.xnT[:, k, t * TP:(t + 1) * TP], wc[:, k, :, :].rearrange("p h g -> p (h g)"),
                                     start=k == 0, stop=False)
                nc.tensor.matmul(m.ps[0:TP, b, :], m.ones[0:1, 0:TP], bc[:, :, :].rearrange("p h g -> p (h g)"), start=False,
                                 stop=True).then_inc(s("logits"), 1)
            for t in range(NT):
                pe.wait_ge(s("sw"), t + 1)
                w = sw[:, t, :, :].rearrange("p h g -> p (h g)")
                ins0 = nc.tensor.matmul(m.ps[0:G, 2, :], m.ones[0:TP, 0:G], w, start=t == 0, stop=t == NT - 1)
                for c in range(KC):
                    ins = nc.tensor.matmul(m.ps[:, c, :], m.xn[:, t, c * P:(c + 1) * P], w, start=t == 0, stop=t == NT - 1)
                    if t == NT - 1:
                        ins.then_inc(s("z_made"), 1)
                if t == NT - 1:
                    ins0.then_inc(s("norm_made"), 1)
            pe.wait_ge(s("norm"), 1)
            pe.wait_ge(s("zT"), KC)
            for h in range(NH):
                o = m.ps[0:D, 5, h * G:(h + 1) * G]
                for k in range(KC):
                    nc.tensor.matmul(o, wfx[:, k, h * D:(h + 1) * D], zT[:, k, h * G:(h + 1) * G], start=k == 0, stop=False)
                ins = nc.tensor.matmul(o, m.row("L3_ffn_b_fx", 1)[:, h * D:(h + 1) * D], norm[0:1, h * G:(h + 1) * G], start=False,
                                       stop=True)
            ins.then_inc(s("tok_made"), 1)
            pe.wait_ge(s("tokT"), 1)
            for j, wt in enumerate((wq, wk)):
                nc.tensor.matmul(m.ps[0:D, 2 + j, :], wt, tokT[:, :], start=True, stop=True).then_inc(s("qk_made"), 1)
            for h in range(NH):
                ins = nc.tensor.matmul(m.ps[0:G, 4, h * D:(h + 1) * D], tokT[:, h * G:(h + 1) * G], wv, start=True, stop=True)
            ins.then_inc(s("v_made"), 1)
            pe.wait_ge(s("qk"), 2)
            for h in range(NH):
                hg = slice(h * G, (h + 1) * G)
                ins = nc.tensor.matmul(m.ps[0:G, 5, hg], qT[:, hg], kT[:, hg], start=True, stop=True)
            ins.then_inc(s("att_made"), 1)
            for h in range(NH):
                for t in range(NT):
                    b, c = (6, t * TP) if t < 4 else (7, 0)
                    if t in (0, 4) and h:
                        pe.wait_ge(s("swT"), 2 * h - 1 + (t == 4))
                    ins = nc.tensor.transpose(m.ps[0:G, b, c:c + TP], sw[:, t, h, :], m.ident[0:TP, 0:TP])
                    if t >= 3:
                        ins.then_inc(s("sw_turned"), 1)
            pe.wait_ge(s("at"), 1)
            for h in range(NH):
                ins = nc.tensor.transpose(m.ps[0:G, 0, h * G:(h + 1) * G], at[:, h, :], m.ident[0:G, 0:G])
            ins.then_inc(s("atT_made"), 1)
            pe.wait_ge(s("atT"), 1)
            pe.wait_ge(s("v"), 1)
            for h in range(NH):
                ins = nc.tensor.matmul(m.ps[0:D, 1, h * G:(h + 1) * G], v[:, h, :], atT[:, h, :], start=True, stop=True)
            ins.then_inc(s("osT_made"), 1)
            pe.wait_ge(s("osT"), 1)
            for h in range(NH):
                if h >= 4:
                    pe.wait_ge(s("pw"), h - 3)
                nc.tensor.matmul(m.ps[0:G, 2 + h % 4, 0:C], osT[:, h, :], wout[:, h, :], start=True, stop=True).then_inc(s("pw_made"), 1)
            pe.wait_ge(s("pw"), NH)
            pe.wait_ge(s("swT"), 2 * NH)
            for t in range(NT):
                b = (6, 7, 0, 1, 2)[t]
                for h in range(NH):
                    nc.tensor.matmul(m.ps[0:TP, b, 0:C], swT[:, h, t * TP:(t + 1) * TP], pw[:, h, :], start=h == 0, stop=False)
                nc.tensor.matmul(m.ps[0:TP, b, 0:C], m.ones[0:1, 0:TP], m.row("L3_ffn_b_out", 1), start=False, stop=True)\
                    .then_inc(s("out_made"), 1)


LAYERS = [l0_gnn, l0_ffn, l1_gnn, l1_ffn, l2_gnn, l2_ffn, l3_gnn, l3_ffn]


def build(nc, A, out, upto=99):
    with ExitStack() as ctx:
        m = Memory(nc, ctx)
        setup(nc, m, A)
        edges(nc, m, A)
        for layer in LAYERS[:upto]:
            layer(nc, m, A)
        with ExitStack() as last:
            done = last.enter_context(nc.semaphore("stored"))
            block = last.enter_context(nc.Block())

            @block.sync
            def _(sp):
                sp.dma_start(out.rearrange("(t p) c -> p t c", p=TP), m.x[:, :, :]).then_inc(done, 16)
                sp.wait_ge(done, 16)



def chunks(w):
    return w.reshape(-1, P, w.shape[-1]).transpose(1, 0, 2).reshape(P, -1)


def laid_out(inputs):
    a = {k: np.asarray(v) for k, v in inputs.items()}
    out = {n: a[n] for n in ["x", "edge_attr_256", "edge_attr_128", "L0_gnn_w_f1b"]}
    cols = []
    for n in COLS:
        v = a[n].reshape(-1, P)
        cols.append(v.T)
    out["cols"] = np.concatenate(cols, axis=1)
    out["rows"] = np.concatenate([a[n].reshape(-1) for n in ROWS])
    out["w_f1aT"] = a["L0_gnn_w_f1a"].T
    out["featT"] = a["edge_attr_54"].T
    out["src_t"] = a["src"].reshape(ET, TP).T
    out["dst_t"] = a["dst"].reshape(ET, TP).T
    g = lambda n: a["L0_gnn_" + n]
    out["w_l0g"] = np.concatenate([chunks(g(n)) for n in ["c1_wl", "c1_wr", "c2_wl", "c2_wr", "lin1_w", "lin2_w", "cat_w"]], axis=1)
    out["dst"] = a["dst"]
    out["wn"] = chunks(a["L1_gnn_Wn"])
    out["wnT"] = chunks(a["L1_gnn_Wn"].T)
    out["we_be"] = chunks(np.concatenate([a["L1_gnn_We"], a["L1_gnn_be"][:, None]], axis=1))
    out["l1f_wr"] = chunks(a["L1_ffn_Wr"])
    out["L1_ffn_bo"] = a["L1_ffn_bo"]
    out["l1f_w"] = np.stack([np.stack([chunks(a["L1_ffn_" + n][e]) for n in ("W1", "W2", "Wo")]) for e in range(8)])
    fc = a["L2_gnn_Wfc"]
    fc = np.concatenate([fc, np.zeros((512 - fc.shape[0], fc.shape[1]), fc.dtype)])
    out["w_l2g"] = np.concatenate([chunks(a["L2_gnn_W1"]), chunks(fc), a["L2_gnn_W2"]], axis=1)
    out["l2g_small"] = np.stack([a["L2_gnn_" + n] for n in ("b2", "g2", "be2")], axis=1)
    out["l2f_wr"] = chunks(a["L2_ffn_gate_w"])
    out["L2_ffn_b2"] = a["L2_ffn_b2"]
    out["l2f_w"] = np.stack([np.stack([chunks(a["L2_ffn_" + n][e]) for n in ("w1", "w2")]) for e in range(16)])
    out["w_l3g"] = np.concatenate([chunks(a["L3_gnn_W_l"].T), chunks(a["L3_gnn_W_r"].T)], axis=1)
    f = lambda n: a["L3_ffn_" + n]
    heads = lambda w: w.reshape(8, 64, C).transpose(1, 0, 2).reshape(64, -1)
    out["l3f_wfx"] = chunks(f("W_fx"))
    out["l3f_w64"] = np.concatenate([heads(f("W_x").T), heads(f("W_out")), f("W_slice"), f("W_q"), f("W_k"), f("W_v"),
                                     f("b_x").reshape(8, 64).T], axis=1)
    out["l0f_wr"] = chunks(a["L0_ffn_Wr"])
    out["L0_ffn_b2"] = a["L0_ffn_b2"]
    out["l0f_experts"] = np.concatenate(
        [np.concatenate([chunks(a["L0_ffn_W1"][e]), chunks(a["L0_ffn_W2"][e]), a["L0_ffn_b1"][e].reshape(4, P).T], axis=1)
         for e in range(8)], axis=0)
    return {k: np.ascontiguousarray(v) for k, v in out.items()}


def kernel(**inputs):
    import concourse.bacc as bacc
    from concourse.bass_utils import run_bass_kernel_spmd

    nc = bacc.Bacc("TRN2", target_bir_lowering=False, num_devices=1)
    arrays = laid_out(inputs)
    A = {n: nc.dram_tensor("in_" + n, a.shape, mybir.dt.from_np(a.dtype), kind="ExternalInput").ap()
         for n, a in arrays.items()}
    out = nc.dram_tensor("out_x", (N, C), F32, kind="ExternalOutput").ap()
    build(nc, A, out)
    r = run_bass_kernel_spmd(nc, [{"in_" + n: a for n, a in arrays.items()}], core_ids=[0])
    return r.results[0]["out_x"]
```

```python
from contextlib import ExitStack

import numpy as np

import concourse.bass as bass
from concourse import mybir

F32 = mybir.dt.float32
BF16 = mybir.dt.bfloat16
F16 = mybir.dt.float16
I32 = mybir.dt.int32
ALU = mybir.AluOpType
ACT = mybir.ActivationFunctionType
AX = mybir.AxisListType

N, C, E = 625, 256, 10000
P, KC = 128, C // 128
NT, TP = 5, 125
ET = E // TP
NQ = ET // 4
LN_EPS = 1e-5
HALF = ((0, 313), (313, N))

COLS = ["L0_gnn_c1_bl", "L0_gnn_c2_bl", "L0_gnn_lin1_b", "L0_gnn_lin2_b", "L0_gnn_cat_b", "L0_gnn_gn_w",
        "L0_gnn_gn_b", "L0_gnn_gn_ms", "L1_ffn_b1", "L1_ffn_g1", "L1_ffn_be1", "L1_ffn_m1", "L1_ffn_v1",
        "L1_ffn_b2", "L1_ffn_g2", "L1_ffn_be2", "L1_ffn_m2", "L1_ffn_v2", "L2_gnn_b1", "L2_gnn_g1",
        "L2_gnn_be1", "L2_ffn_b1", "L1_gnn_attn"]
COL_WIDTH = {n: 2 for n in COLS} | {n: 16 for n in COLS if n.startswith("L1_ffn")} | \
    {"L2_gnn_b1": 1, "L2_gnn_g1": 1, "L2_gnn_be1": 1, "L2_ffn_b1": 64}
ROWS = {"L0_ffn_br": 8, "L0_ffn_gamma": C, "L0_ffn_beta": C, "L1_gnn_bn": C, "L1_gnn_attn": C, "L1_ffn_br": 8,
        "L2_gnn_bfc": C, "L2_ffn_gate_b": 16, "L2_ffn_gamma": C, "L2_ffn_beta": C, "L3_gnn_b_l": C,
        "L3_gnn_ln_gamma": C, "L3_gnn_ln_beta": C, "L3_ffn_b_fx": 512, "L3_ffn_b_slice": 64,
        "L3_ffn_b_out": C, "L3_ffn_temperature": 8}


def offsets(widths):
    at, out = 0, {}
    for name, w in widths.items():
        out[name] = (at, at + w)
        at += w
    return out, at


COL_AT, NCOL = offsets(COL_WIDTH)
ROW_AT, NROW = offsets(ROWS)


class Steps:

    def __init__(self, eng, own):
        self.eng, self.own, self.count, self.last = eng, own, {}, own

    def __call__(self, ins, sem=None):
        sem = sem or self.own
        ins.then_inc(sem, 1)
        self.count[sem.name] = self.count.get(sem.name, 0) + 1
        self.last = sem
        return ins

    def settle(self):
        self.eng.wait_ge(self.last, self.count[self.last.name])

    def do(self, ins, sem=None):
        self(ins, sem)
        self.settle()


class Memory:

    def __init__(self, nc, ctx):
        def sb(name, shape, dt=F32):
            return ctx.enter_context(nc.sbuf_tensor(name, shape, dt))

        self.x = sb("x", [TP, NT, C])
        self.xn = sb("xn", [TP, NT, C])
        self.xnT = sb("xnT", [P, KC, N])
        self.stats = sb("stats", [TP, NT, 6])
        self.mv = sb("mv", [TP, NT, 2])
        self.veps = sb("veps", [P, NT])
        self.rstd = sb("rstd", [P, NT])
        self.mhalf = sb("mhalf", [P, 16])
        self.ident = sb("ident", [P, P])
        self.ones = sb("ones", [P, P])
        self.iota = sb("iota", [P, 640])
        self.pcol = sb("pcol", [P, 1])
        self.cols = sb("cols", [P, NCOL])
        self.rows = sb("rows", [P, NROW])
        self.count = sb("count", [TP, NT, N])
        self.srci = sb("srci", [TP, ET], I32)
        self.dsti = sb("dsti", [TP, ET], I32)
        self.src = sb("src", [TP, ET])
        self.dst = sb("dst", [TP, ET])
        self.iota16 = sb("iota16", [P, 8 * TP], F16)
        self.score_e = sb("score_e", [TP, ET])
        self.score0 = sb("score0", [TP, 1])
        self.q = sb("q", [P, KC])
        self.dst16 = sb("dst16", [TP, ET], F16)
        self.zeros = sb("zeros", [1, 512], BF16)
        self.inside = {n: sb("inside_" + n, [TP, NT, ET]) for n in ("src", "dst")}
        self.mask_s = sb("mask_s", [TP, E], BF16)
        self.nodes0 = nc.dram_tensor("l0_nodes", (N, C), F32, kind="Internal").ap()
        self.deg = sb("deg", [TP, NT])
        self.end_rows = nc.dram_tensor("end_rows", (3, ET, TP), F16, kind="Internal").ap()
        self.windows = sb("windows", [1, NQ, NT + 1], I32)
        self.windows2 = sb("windows2", [1, NQ // 2, NT + 1], I32)
        self.words = sb("words", [1, NQ // 2], I32)
        self.words2 = sb("words2", [1, NQ // 2], I32)
        self.ps = ctx.enter_context(nc.psum_tensor("ps", [P, 8, 512], F32))

    def col(self, name):
        a, b = COL_AT[name]
        return self.cols[:, a:b]

    def row(self, name, n=TP):
        a, b = ROW_AT[name]
        return self.rows[0:n, a:b]


class Stage:

    def __init__(self, nc, ctx, name):
        self.nc, self.ctx, self.name = nc, ctx, name
        self.made = {}
        ctx.callback(self.clear)

    def clear(self):
        if self.made:
            self.nc.clear_and_free_semaphores(list(self.made.values()))
            self.nc.all_engine_barrier()

    def sem(self, name):
        if name not in self.made:
            self.made[name] = self.nc.alloc_semaphore(f"{self.name}_{name}")
        return self.made[name]

    def sb(self, name, shape, dt=F32):
        return self.ctx.enter_context(self.nc.sbuf_tensor(f"{self.name}_{name}", shape, dt))

    def credit(self, eng, *names):
        for name in names:
            eng.nop(nofuse=True).then_inc(self.sem(name), 1)



def norm_vector(nc, m, dve, st, steps):
    for t in range(NT):
        steps(nc.vector.bn_stats(m.stats[:, t, :], m.x[:, t, :]))
    steps.settle()
    for t in range(NT):
        steps(nc.vector.bn_aggr(m.mv[:, t, :], m.stats[:, t, :]), st.sem("stats_done"))
    dve.wait_ge(st.sem("rstd_done"), 1)
    for t in range(NT):
        steps(nc.vector.tensor_scalar(m.xn[:, t, :], m.x[:, t, :], m.mv[:, t, 0:1], m.rstd[0:TP, t:t + 1],
                                      ALU.subtract, ALU.mult), st.sem("xn_done"))


def norm_pool(nc, m, pool, st, steps):
    pool.wait_ge(st.sem("stats_done"), NT)
    steps.do(nc.gpsimd.tensor_scalar(m.veps[0:TP, :], m.mv[:, :, 1], LN_EPS, None, ALU.add))
    steps(nc.gpsimd.tensor_tensor(m.rstd[0:TP, :], m.veps[0:TP, :], m.mhalf[0:TP, 0:NT], ALU.pow), st.sem("rstd_done"))


def norm_tensor(nc, m, pe, st, bank=0):
    for t in range(NT):
        pe.wait_ge(st.sem("xn_done"), t + 1)
        for k in range(KC):
            out = m.ps[:, bank + k, t * TP:(t + 1) * TP] if t < 4 else m.ps[:, bank + 2, k * TP:(k + 1) * TP]
            nc.tensor.transpose(out, m.xn[:, t, k * P:(k + 1) * P], m.ident[0:TP, 0:TP]).then_inc(st.sem("xn_turned"), 1)


def norm_scalar(nc, m, act, st, bank=0):
    act.wait_ge(st.sem("xn_turned"), 8)
    for k in range(KC):
        nc.scalar.activation(m.xnT[:, k, 0:4 * TP], m.ps[:, bank + k, 0:4 * TP], ACT.Copy).then_inc(st.sem("xnT_done"), 1)
    act.wait_ge(st.sem("xn_turned"), 10)
    nc.scalar.activation(m.xnT[:, :, 4 * TP:N], m.ps[:, bank + 2, 0:KC * TP].rearrange("p (k n) -> p k n", k=KC),
                         ACT.Copy).then_inc(st.sem("xnT_done"), 1)


XNT = 3



def setup(nc, m, A):
    with ExitStack() as ctx:
        st = Stage(nc, ctx, "setup")
        ramp = st.sb("ramp", [P, 8 * TP], I32)
        pint = st.sb("pint", [P, 1], I32)
        block = ctx.enter_context(nc.Block())

        @block.sync
        def _(sp):
            sp.dma_start(m.x[:, :, :], A["x"].rearrange("(t p) c -> p t c", p=TP)).then_inc(st.sem("loads"), 16)
            sp.dma_start(m.cols[:, :], A["cols"]).then_inc(st.sem("loads"), 16)
            sp.dma_start(m.rows[:, :], A["rows"][None, :].to_broadcast([P, NROW])).then_inc(st.sem("loads"), 16)
            sp.dma_start(m.srci[:, :], A["src_t"]).then_inc(st.sem("ends"), 16)
            sp.dma_start(m.dsti[:, :], A["dst_t"]).then_inc(st.sem("ends"), 16)
            sp.wait_ge(st.sem("loads"), 48)

        @block.gpsimd
        def _(pool):
            steps = Steps(pool, st.sem("pool"))
            steps(nc.gpsimd.memset(m.ident[:, :], 0.0))
            steps(nc.gpsimd.memset(m.ones[:, :], 1.0))
            steps(nc.gpsimd.memset(m.mhalf[:, :], -0.5))
            steps(nc.gpsimd.memset(m.zeros[:, :], 0.0))
            steps(nc.gpsimd.iota(pint[:, :], pattern=[[0, 1]], base=0, channel_multiplier=1))
            steps(nc.gpsimd.iota(ramp[:, :], pattern=[[1, 8 * TP]], base=0, channel_multiplier=0))
            steps.settle()
            steps(nc.gpsimd.affine_select(out=m.ident[:, :], in_=m.ident[:, :], compare_op=ALU.not_equal, fill=1.0,
                                          base=0, pattern=[[-1, P]], channel_multiplier=1))
            steps(nc.gpsimd.tensor_copy(m.iota[:, :], ramp[:, 0:640]))
            steps(nc.gpsimd.tensor_copy(m.iota16[:, :], ramp[:, :]))
            steps(nc.gpsimd.tensor_copy(m.pcol[:, :], pint[:, :]))
            pool.wait_ge(st.sem("ends"), 32)
            steps(nc.gpsimd.tensor_copy(m.src[:, :], m.srci[:, :]))
            steps(nc.gpsimd.tensor_copy(m.dst[:, :], m.dsti[:, :]))
            steps.do(nc.gpsimd.tensor_copy(m.dst16[:, :], m.dsti[:, :]))



def l0_gnn(nc, m, A):
    names = ["c1_wl", "c1_wr", "c2_wl", "c2_wr", "lin1_w", "lin2_w"]
    with ExitStack() as ctx:
        st = Stage(nc, ctx, "l0g")
        W = st.sb("W", [P, 4096])
        wk = {n: W[:, 512 * i:512 * (i + 1)].rearrange("p (k n) -> p k n", k=2) for i, n in enumerate(names)}
        cat = W[:, 3072:4096].rearrange("p (k n) -> p k n", k=4)
        table = m.nodes0
        agg = st.sb("agg", [TP, NT, 512])
        fa = st.sb("fa", [64, 54])
        fb = st.sb("fb", [64, C])
        wf = st.sb("wf", [54, C])

        with ExitStack() as inner:
            sb = Stage(nc, inner, "l0e").sb
            idx = sb("idx", [TP, 8], I32)
            gate = [sb(f"gate{h}", [TP, 4, C]) for h in range(2)]
            feat = [sb(f"feat{h}", [54, 4 * TP]) for h in range(2)]
            xg = [sb(f"xg{h}", [TP, 4, C]) for h in range(2)]
            fg = [sb(f"fg{v}", [TP, 2, C]) for v in range(2)]
            oh = [sb(f"oh{h}", [TP, 4, N]) for h in range(2)]
            msg = [sb(f"msg{h}", [TP, 4, 2, C]) for h in range(2)]
            gate_d = A["edge_attr_256"].rearrange("(q u p) c -> q p u c", p=TP, u=4)
            s = st.sem
            block = inner.enter_context(nc.Block())

            @block.sync
            def _(sp):
                sp.dma_start(fa[:, :], A["w_f1aT"]).then_inc(s("small"), 16)
                sp.dma_start(fb[:, :], A["L0_gnn_w_f1b"]).then_inc(s("small"), 16)
                with sp.Fori(0, NQ // 2) as i:
                    for h in range(2):
                        sp.wait_ge(s(f"feat_used{h}"), i + 1)
                        sp.dma_start(feat[h][:, :], A["featT"][:, bass.ds(i * 1000 + h * 500, 500)])\
                            .then_inc(s(f"feat{h}"), 16)
                        sp.wait_ge(s(f"quad_used{h}"), i + 1)
                        sp.dma_start(gate[h][:, :, :], gate_d[bass.ds(i * 2 + h, 1)].rearrange("q p u c -> (q p) u c"))\
                            .then_inc(s(f"gate{h}"), 16)
                sp.dma_start(W[:, :], A["w_l0g"]).then_inc(s("w"), 16)

            @block.gpsimd
            def _(pool):
                with pool.Fori(0, NQ // 2) as i:
                    for h in range(2):
                        pool.wait_ge(s(f"quad_used{h}"), i + 1)
                        pool.nop(nofuse=True)
                        nc.gpsimd.tensor_copy(idx[:, 4 * h:4 * h + 4], m.srci[:, bass.ds(i * 8 + 4 * h, 4)])\
                            .then_inc(s("idx"), 1)
                        pool.wait_ge(s("idx"), i * 2 + (h + 1))
                        pool.nop(nofuse=True)
                        for u in range(4):
                            pool.indirect_dma_start(
                                out=xg[h][:, u, :], out_offset=None, in_=table,
                                in_offset=bass.IndirectOffsetOnAxis(ap=idx[:, 4 * h + u:4 * h + u + 1], axis=0),
                            ).then_inc(s(f"xg{h}"), 16)

            @block.scalar
            def _(act):
                act.wait_ge(s("wf_made"), 1)
                nc.scalar.activation(wf[:, :], m.ps[0:54, 3, 0:C], ACT.Copy).then_inc(s("wf"), 1)
                act.wait_ge(s("agg_made"), 1)
                for t in range(NT):
                    nc.scalar.activation(agg[:, t, :], m.ps[0:TP, t, :], ACT.Copy).then_inc(s("agg"), 1)

            @block.vector
            def _(dve):
                st.credit(dve, "quad_used0", "quad_used1", "fg0", "fg1")
                with dve.Fori(0, NQ // 2) as i:
                    word = word_of(dve, m.words, i)
                    for h in range(2):
                        dve.wait_ge(s(f"msg_used{h}"), i + 1)

                        def onehot(k, tile):
                            nc.vector.tensor_tensor(oh[h][:, :, k * TP:(k + 1) * TP],
                                                    m.iota16[0:TP, bass.ds(tile * TP, TP)].unsqueeze(1).to_broadcast([TP, 4, TP]),
                                                    m.dst16[:, bass.ds(i * 8 + 4 * h, 4)].unsqueeze(2).to_broadcast([TP, 4, TP]),
                                                    ALU.is_equal)

                        for_windows(dve, word, h, m.windows, i * 2 + h, onehot)
                        use = i * 2 + h
                        for v in range(2):
                            if v == 0:
                                dve.wait_ge(s(f"gate{h}"), (i + 1) * 16)
                            dve.wait_ge(s(f"f1_made{v}"), use + 1)
                            nc.vector.tensor_tensor(fg[v][:, :, :], m.ps[0:TP, 5 + v, :].rearrange("p (u c) -> p u c", u=2),
                                                    gate[h][:, 2 * v:2 * v + 2, :], ALU.mult).then_inc(s(f"fg{v}"), 1)
                        dve.wait_ge(s(f"xg{h}"), (i + 1) * 64)
                        for v in range(2):
                            dve.wait_ge(s(f"fg{v}"), use + 2)
                            nc.vector.tensor_tensor(msg[h][:, 2 * v:2 * v + 2, 0, :], fg[v][:, :, :], xg[h][:, 2 * v:2 * v + 2, :],
                                                    ALU.mult).then_inc(s(f"m1{v}"), 1)
                        for v in range(2):
                            dve.wait_ge(s(f"m1{v}"), use + 1)
                            nc.vector.tensor_tensor(msg[h][:, 2 * v:2 * v + 2, 1, :], msg[h][:, 2 * v:2 * v + 2, 0, :],
                                                    gate[h][:, 2 * v:2 * v + 2, :], ALU.mult)\
                                .then_inc(s(f"quad_used{h}" if v else "m2"), 1)

            @block.tensor
            def _(pe):
                st.credit(pe, "msg_used0", "msg_used1", "feat_used0", "feat_used1")
                pe.wait_ge(s("small"), 32)
                nc.tensor.matmul(m.ps[0:54, 3, 0:C], fa[:, :], fb[:, :], start=True, stop=True).then_inc(s("wf_made"), 1)
                pe.wait_ge(s("wf"), 1)
                zero_banks(nc, m, NT, 512, start=True)

                def features(i, h):
                    pe.wait_ge(s(f"feat{h}"), (i + 1) * 16)
                    for v in range(2):
                        pe.wait_ge(s(f"fg{v}"), i * 2 + (h + 1))
                        for u in range(2):
                            ins = nc.tensor.matmul(m.ps[0:TP, 5 + v, u * C:(u + 1) * C],
                                                   feat[h][:, (2 * v + u) * TP:(2 * v + u + 1) * TP], wf[:, :],
                                                   start=True, stop=True)
                        ins.then_inc(s(f"f1_made{v}"), 1)
                    mark(nc, m).then_inc(s(f"feat_used{h}"), 1)

                def sums(word, i, h):
                    def window(k, tile):
                        for u in range(4):
                            nc.tensor.matmul(m.ps[0:TP, bass.ds(tile, 1), :].rearrange("p b c -> p (b c)"),
                                             oh[h][:, u, k * TP:(k + 1) * TP],
                                             msg[h][:, u, :, :].rearrange("p a c -> p (a c)"), start=False, stop=False,
                                             skip_group_check=True)

                    pe.wait_ge(s(f"quad_used{h}"), i + 2)
                    for_windows(pe, word, h, m.windows, i * 2 + h, window)
                    mark(nc, m).then_inc(s(f"msg_used{h}"), 1)

                features(0, 0)
                with pe.Fori(0, NQ // 2 - 1) as i:
                    word = word_of(pe, m.words, i)
                    features(i, 1)
                    sums(word, i, 0)
                    features(i + 1, 0)
                    sums(word, i, 1)
                word = word_of(pe, m.words, NQ // 2 - 1)
                features(NQ // 2 - 1, 1)
                sums(word, NQ // 2 - 1, 0)
                sums(word, NQ // 2 - 1, 1)
                zero_banks(nc, m, NT, 512, start=False).then_inc(s("agg_made"), 1)

        with ExitStack() as inner:
            sb = Stage(nc, inner, "l0m").sb
            aggT = sb("aggT", [P, 4, N])
            z = [sb(f"z{j}", [P, KC, N]) for j in range(2)]
            pre = [sb(f"pre{j}", [P, KC, N]) for j in range(2)]
            g = [sb(f"g{j}", [P, KC, N]) for j in range(2)]
            h = sb("h", [P, KC, N])
            hstat = sb("hstat", [P, KC, 5, 6])
            hmv = sb("hmv", [P, KC, 2])
            tmp = sb("tmp", [P, 4, KC])
            s = st.sem
            block = inner.enter_context(nc.Block())
            layers = [([("c1_wl", lambda k: aggT[:, k, :]), ("c1_wr", lambda k: m.xnT[:, k, :])], "c1_bl", z[0]),
                      ([("c2_wl", lambda k: aggT[:, 2 + k, :]), ("c2_wr", lambda k: m.xnT[:, k, :])], "c2_bl", z[1]),
                      ([("lin1_w", lambda k: z[0][:, k, :])], "lin1_b", pre[0]),
                      ([("lin2_w", lambda k: z[1][:, k, :])], "lin2_b", pre[1]),
                      ([("cat", lambda k: g[k // 2][:, k % 2, :])], "cat_b", h)]

            @block.tensor
            def _(pe):
                for t in range(NT):
                    for k in range(4):
                        ins = nc.tensor.transpose(m.ps[:, t, k * TP:(k + 1) * TP], agg[:, t, k * P:(k + 1) * P],
                                                  m.ident[0:TP, 0:TP])
                    ins.then_inc(s("agg_turned"), 1)
                pe.wait_ge(s("w"), 16)
                unit = 0
                for n, (terms, _, _) in enumerate(layers):
                    if n == 0:
                        pe.wait_ge(s("aggT"), NT)
                    elif n == 2:
                        pe.wait_ge(s("mlp_evac"), 4)
                    elif n == 3:
                        pe.wait_ge(s("mlp_evac"), 8)
                    elif n == 4:
                        pe.wait_ge(s("leaky"), 4)
                    for c in range(KC):
                        for (a, b) in HALF:
                            if unit >= 8:
                                pe.wait_ge(s("mlp_evac"), unit - 7)
                            ops = [(wk[w][:, k, c * P:(c + 1) * P] if w != "cat" else cat[:, k, c * P:(c + 1) * P],
                                    x(k)[:, a:b]) for w, x in terms for k in range(4 if w == "cat" else 2)]
                            for j, (lhsT, rhs) in enumerate(ops):
                                ins = nc.tensor.matmul(m.ps[:, unit % 8, 0:b - a], lhsT, rhs, start=j == 0,
                                                       stop=j == len(ops) - 1)
                            ins.then_inc(s("mlp_made"), 1)
                            unit += 1
                pe.wait_ge(s("hn"), 2)
                pe.wait_ge(s("mlp_evac"), 20)
                for t in range(NT):
                    for k in range(KC):
                        nc.tensor.transpose(m.ps[0:TP, t, k * P:(k + 1) * P],
                                            h[:, k, t * TP:(t + 1) * TP], m.ident[:, :]).then_inc(s("hn_turned"), 1)

            @block.scalar
            def _(act):
                for t in range(NT):
                    act.wait_ge(s("agg_turned"), t + 1)
                    nc.scalar.activation(aggT[:, :, t * TP:(t + 1) * TP],
                                         m.ps[:, t, 0:4 * TP].rearrange("p (k n) -> p k n", k=4), ACT.Copy)\
                        .then_inc(s("aggT"), 1)
                unit = 0
                for _, bias, out in layers:
                    for c in range(KC):
                        for (a, b) in HALF:
                            act.wait_ge(s("mlp_made"), unit + 1)
                            nc.scalar.activation(out[:, c, a:b], m.ps[:, unit % 8, 0:b - a], ACT.Identity,
                                                 bias=m.col("L0_gnn_" + bias)[:, c:c + 1]).then_inc(s("mlp_evac"), 1)
                            unit += 1
                act.wait_ge(s("gn_coef"), 1)
                for c in range(KC):
                    nc.scalar.activation(h[:, c, :], h[:, c, :], ACT.Identity, bias=tmp[:, 3, c:c + 1],
                                         scale=tmp[:, 2, c:c + 1]).then_inc(s("hn"), 1)

            @block.gpsimd
            def _(pool):
                steps = Steps(pool, s("pool_gn"))
                pool.wait_ge(s("gn_var"), 1)
                steps.do(nc.gpsimd.tensor_scalar(m.veps[:, 0:KC], tmp[:, 1, :], 1e-5, None, ALU.add))
                steps(nc.gpsimd.tensor_tensor(m.rstd[:, 0:KC], m.veps[:, 0:KC], m.mhalf[:, 0:KC], ALU.pow), s("gn_rstd"))

            @block.vector
            def _(dve):
                steps = Steps(dve, s("dve_mlp"))
                for j in range(2):
                    dve.wait_ge(s("mlp_evac"), 12 + 4 * j)
                    for c in range(KC):
                        steps(nc.vector.scalar_tensor_tensor(g[j][:, c, :], pre[j][:, c, :], 0.1, pre[j][:, c, :],
                                                             ALU.mult, ALU.max), s("leaky"))
                dve.wait_ge(s("mlp_evac"), 20)
                for c in range(KC):
                    for t in range(NT):
                        steps(nc.vector.bn_stats(hstat[:, c, t, :], h[:, c, t * TP:(t + 1) * TP]))
                steps.settle()
                for c in range(KC):
                    steps(nc.vector.bn_aggr(hmv[:, c, :], hstat[:, c, :, :].rearrange("p t s -> p (t s)")))
                steps.settle()
                steps.do(nc.vector.tensor_tensor(tmp[:, 0, :], hmv[:, :, 0], m.col("L0_gnn_gn_ms"), ALU.mult))
                steps.do(nc.vector.tensor_tensor(tmp[:, 1, :], hmv[:, :, 0], tmp[:, 0, :], ALU.subtract))
                steps.do(nc.vector.tensor_tensor(tmp[:, 1, :], tmp[:, 1, :], tmp[:, 1, :], ALU.mult))
                steps(nc.vector.tensor_tensor(tmp[:, 1, :], tmp[:, 1, :], hmv[:, :, 1], ALU.add), s("gn_var"))
                dve.wait_ge(s("gn_rstd"), 1)
                steps.do(nc.vector.tensor_tensor(tmp[:, 2, :], m.rstd[:, 0:KC], m.col("L0_gnn_gn_w"), ALU.mult))
                steps.do(nc.vector.tensor_tensor(tmp[:, 3, :], tmp[:, 0, :], tmp[:, 2, :], ALU.mult))
                steps(nc.vector.tensor_tensor(tmp[:, 3, :], m.col("L0_gnn_gn_b"), tmp[:, 3, :], ALU.subtract), s("gn_coef"))
                for t in range(NT):
                    dve.wait_ge(s("hn_turned"), 2 * t + 2)
                    steps(nc.vector.tensor_tensor(m.x[:, t, :], m.x[:, t, :],
                                                  m.ps[0:TP, t, 0:C], ALU.add))
                steps.settle()



def l0_ffn(nc, m, A):
    NE, F, FK = 8, 512, 4
    ROWLEN = 2052
    CAPACITY = float(int(np.ceil(N * 1.25 / NE)))
    with ExitStack() as ctx:
        st = Stage(nc, ctx, "l0f")
        s, sb = st.sem, st.sb
        wr = sb("wr", [P, KC, NE])
        b2 = sb("b2", [NE, C])
        expert = [sb(f"expert{j}", [P, ROWLEN]) for j in range(2)]
        w1 = [e[:, 0:1024].rearrange("p (k f) -> p k f", k=KC) for e in expert]
        w2 = [e[:, 1024:2048].rearrange("p (k c) -> p k c", k=FK) for e in expert]
        b1 = [e[:, 2048:2052] for e in expert]
        hT = [sb(f"hT{j}", [P, FK, N]) for j in range(2)]
        xsum = sb("xsum", [P, KC])
        xmean = sb("xmean", [P, KC, P])
        r = sb("r", [P, 16, NE])
        c = sb("c", [P, 32])
        row_idx = sb("row_idx", [P, 2], I32)
        wdT = sb("wdT", [NE, P])
        z = sb("z", [TP, NT, C])
        zn = sb("zn", [TP, NT, C])
        block = ctx.enter_context(nc.Block())
        UNITS = 2 * FK * 2

        @block.sync
        def _(sp):
            sp.dma_start(wr[:, :, :], A["l0f_wr"].rearrange("p (k e) -> p k e", k=KC)).then_inc(s("small"), 16)
            sp.dma_start(b2[:, :], A["L0_ffn_b2"]).then_inc(s("small"), 16)

        @block.gpsimd
        def _(pool):
            steps = Steps(pool, s("pool"))
            norm_pool(nc, m, pool, st, steps)
            for j in range(2):
                pool.wait_ge(s("chosen"), j + 1)
                pool.indirect_dma_start(out=expert[j][:, :], out_offset=None, in_=A["l0f_experts"],
                                        in_offset=bass.IndirectOffsetOnAxis(ap=row_idx[:, j:j + 1], axis=0))\
                    .then_inc(s(f"expert{j}"), 16)
            pool.wait_ge(s("z_stats"), NT)
            steps.do(nc.gpsimd.tensor_scalar(m.veps[0:TP, :], m.mv[:, :, 1], LN_EPS, None, ALU.add))
            steps(nc.gpsimd.tensor_tensor(m.rstd[0:TP, :], m.veps[0:TP, :], m.mhalf[0:TP, 0:NT], ALU.pow), s("z_rstd"))

        @block.scalar
        def _(act):
            norm_scalar(nc, m, act, st)
            for n in range(2):
                act.wait_ge(s("exp_in"), n + 1)
                nc.scalar.activation(r[:, 3 * n + 2, :], r[:, 3 * n + 1, :], ACT.Exp, accum_out=c[:, n:n + 1])\
                    .then_inc(s("exp_out"), 1)
            act.wait_ge(s("exp_in"), 3)
            nc.scalar.activation(c[:, 11:12], c[:, 10:11], ACT.Exp).then_inc(s("exp_out"), 1)
            act.wait_ge(s("wdT_made"), 1)
            nc.scalar.activation(wdT[:, :], m.ps[0:NE, 4, 0:P], ACT.Copy).then_inc(s("wdT"), 1)
            unit = 0
            for j in range(2):
                for f in range(FK):
                    for (a, b) in HALF:
                        act.wait_ge(s("h_made"), unit + 1)
                        nc.scalar.activation(hT[j][:, f, a:b], m.ps[:, unit % 3, 0:b - a], ACT.Gelu,
                                             bias=b1[j][:, f:f + 1]).then_inc(s("hT"), 1)
                        unit += 1

        @block.vector
        def _(dve):
            steps = Steps(dve, s("dve"))
            norm_vector(nc, m, dve, st, steps)
            dve.wait_ge(s("xnT_done"), XNT)
            steps.do(nc.vector.tensor_reduce(xsum[:, :], m.xnT[:, :, :], AX.X, ALU.add))
            for k in range(KC):
                steps(nc.vector.tensor_scalar(xmean[:, k, :], m.ones[:, :], xsum[:, k:k + 1], 1.0 / N, ALU.mult, ALU.mult),
                      s("xmean"))
            dve.wait_ge(s("logits"), 1)

            def softmax_top(n, logits):
                steps.do(nc.vector.tensor_reduce(c[:, 2:3], logits, AX.X, ALU.max))
                steps(nc.vector.tensor_scalar(r[:, 3 * n + 1, :], logits, c[:, 2:3], None, ALU.subtract), s("exp_in"))

            def softmax_end(n):
                dve.wait_ge(s("exp_out"), n + 1)
                steps.do(nc.vector.reciprocal(c[:, 3:4], c[:, n:n + 1]))
                steps.do(nc.vector.tensor_scalar(r[:, 3 * n + 3, :], r[:, 3 * n + 2, :], c[:, 3:4], None, ALU.mult))

            steps.do(nc.vector.tensor_copy(r[:, 0, :], m.ps[:, 3, 0:NE]))
            softmax_top(0, r[:, 0, :])
            softmax_end(0)
            steps.do(nc.vector.tensor_scalar(r[:, 8, :], r[:, 3, :], float(N), None, ALU.mult))
            steps.do(nc.vector.tensor_scalar(r[:, 8, :], r[:, 8, :], CAPACITY, 1.0 / CAPACITY, ALU.max, ALU.mult))
            steps.do(nc.vector.reciprocal(r[:, 9, :], r[:, 8, :]))
            steps.do(nc.vector.tensor_tensor(r[:, 0, :], r[:, 3, :], r[:, 9, :], ALU.mult))
            softmax_top(1, r[:, 0, :])
            softmax_end(1)
            left = r[:, 6, :]
            for j in range(2):
                steps.do(nc.vector.tensor_reduce(c[:, 4 + j:5 + j], left, AX.X, ALU.max))
                steps.do(nc.vector.tensor_scalar(r[:, 10, :], left, c[:, 4 + j:5 + j], -1000.0, ALU.is_equal, ALU.mult))
                steps.do(nc.vector.tensor_tensor(r[:, 10, :], r[:, 10, :], m.iota[:, 0:NE], ALU.add))
                steps.do(nc.vector.tensor_reduce(c[:, 6 + j:7 + j], r[:, 10, :], AX.X, ALU.min))
                steps.do(nc.vector.tensor_scalar(c[:, 8:9], c[:, 6 + j:7 + j], 1000.0, float(P), ALU.add, ALU.mult))
                steps(nc.vector.tensor_tensor(row_idx[:, j:j + 1], c[:, 8:9], m.pcol[:, :], ALU.add), s("chosen"))
                steps.do(nc.vector.tensor_scalar(c[:, 9:10], c[:, 6 + j:7 + j], 1000.0, None, ALU.add))
                steps.do(nc.vector.tensor_scalar(r[:, 11 + j, :], m.iota[:, 0:NE], c[:, 9:10], None, ALU.is_equal))
                if j == 0:
                    steps.do(nc.vector.scalar_tensor_tensor(r[:, 13, :], r[:, 11, :], -2.0, left, ALU.mult, ALU.add))
                    left = r[:, 13, :]
            steps(nc.vector.tensor_tensor(c[:, 10:11], c[:, 5:6], c[:, 4:5], ALU.subtract), s("exp_in"))
            dve.wait_ge(s("exp_out"), 3)
            steps.do(nc.vector.tensor_scalar(c[:, 12:13], c[:, 11:12], 1.0, None, ALU.add))
            steps.do(nc.vector.reciprocal(c[:, 13:14], c[:, 12:13]))
            steps.do(nc.vector.tensor_tensor(c[:, 14:15], c[:, 11:12], c[:, 13:14], ALU.mult))
            steps.do(nc.vector.tensor_scalar(r[:, 14, :], r[:, 11, :], c[:, 13:14], None, ALU.mult))
            steps(nc.vector.scalar_tensor_tensor(r[:, 15, :], r[:, 12, :], c[:, 14:15], r[:, 14, :], ALU.mult, ALU.add),
                  s("wdense"))
            for j in range(2):
                dve.wait_ge(s(f"expert{j}"), 16)
                steps(nc.vector.tensor_scalar(expert[j][:, 1024:2048], expert[j][:, 1024:2048], c[:, 13 + j:14 + j],
                                              None, ALU.mult), s("w2_scaled"))
            def with_input(t):
                dve.wait_ge(s("y_made"), t + 1)
                steps.do(nc.vector.tensor_tensor(z[:, t, :], m.ps[0:TP, 3 + t, 0:C], m.xn[:, t, :], ALU.add))

            norm_tail(nc, m, dve, s, steps, z, zn, "L0_ffn_gamma", "L0_ffn_beta", make=with_input)

        @block.tensor
        def _(pe):
            norm_tensor(nc, m, pe, st)
            pe.wait_ge(s("xmean"), KC)
            pe.wait_ge(s("small"), 32)
            for k in range(KC):
                nc.tensor.matmul(m.ps[:, 3, 0:NE], xmean[:, k, :], wr[:, k, :], start=k == 0, stop=False)
            nc.tensor.matmul(m.ps[:, 3, 0:NE], m.ones[0:1, :], m.row("L0_ffn_br", 1), start=False, stop=True)\
                .then_inc(s("logits"), 1)
            pe.wait_ge(s("wdense"), 1)
            nc.tensor.transpose(m.ps[0:NE, 4, 0:P], r[:, 15, :], m.ident[:, :]).then_inc(s("wdT_made"), 1)
            pe.wait_ge(s("wdT"), 1)
            for t in range(NT):
                nc.tensor.matmul(m.ps[0:TP, 3 + t, 0:C], wdT[:, 0:TP], b2[:, :], start=True, stop=False)
            pe.wait_ge(s("xnT_done"), XNT)
            unit = 0
            for j in range(2):
                pe.wait_ge(s(f"expert{j}"), 16)
                for f in range(FK):
                    for (a, b) in HALF:
                        if unit >= 3:
                            pe.wait_ge(s("hT"), unit - 2)
                        for k in range(KC):
                            ins = nc.tensor.matmul(m.ps[:, unit % 3, 0:b - a], w1[j][:, k, f * P:(f + 1) * P],
                                                   m.xnT[:, k, a:b], start=k == 0, stop=k == KC - 1)
                        ins.then_inc(s("h_made"), 1)
                        unit += 1
            for j in range(2):
                pe.wait_ge(s("hT"), UNITS // 2 * (j + 1))
                pe.wait_ge(s("w2_scaled"), j + 1)
                for t in range(NT):
                    for f in range(FK):
                        ins = nc.tensor.matmul(m.ps[0:TP, 3 + t, 0:C], hT[j][:, f, t * TP:(t + 1) * TP], w2[j][:, f, :],
                                               start=False, stop=j == 1 and f == FK - 1)
                    if j == 1:
                        ins.then_inc(s("y_made"), 1)



def word_of(eng, words, i):
    return eng.value_load(words[0:1, bass.ds(i, 1)], min_val=0, max_val=4095)


def for_windows(eng, word, h, table, q, body, otherwise=None):
    rows = table[0:1, :, :].rearrange("p q k -> p (q k)")
    fields = word >> (6 * h) if h else word
    number = (fields >> 3) & 7

    def window(k):
        body(k, eng.value_load(rows[:, bass.ds(q * (NT + 1) + k, 1)], min_val=0, max_val=NT - 1) if k else fields & 7)
        if k + 1 < NT:
            with eng.If(number > k + 1):
                window(k + 1)
            if otherwise:
                with eng.Else():
                    otherwise(NT - 1 - k)

    window(0)


def edges(nc, m, A):
    with ExitStack() as ctx:
        st = Stage(nc, ctx, "edg")
        s, sb = st.sem, st.sb
        wn = sb("wn", [P, KC, C])
        we = sb("we", [P, KC, P + 1])
        attnB = sb("attnB", [P, KC, TP])
        vrow = sb("vrow", [TP, P])
        junk = sb("junk", [TP, C])
        c0 = sb("c0", [TP, 2])
        above = sb("above", [TP, NT + 1, ET])
        place = sb("place", [TP, 2, ET])
        ends16 = sb("ends16", [ET, 3, TP], F16)
        srow = sb("srow", [TP, E], F16)
        countT = sb("countT", [TP, NT, N])
        per_quad = sb("per_quad", [TP, NQ, NT])
        rev = sb("rev", [1, NT])
        counts = sb("counts", [1, NQ, NT])
        span = {n: sb(f"span{n}", [1, n, NT]) for n in (NQ, NQ // 2)}
        some = {n: sb(f"some{n}", [1, n, NT]) for n in (NQ, NQ // 2)}
        last = {n: sb(f"last{n}", [1, n]) for n in (NQ, NQ // 2)}
        back = {n: sb(f"back{n}", [1, n]) for n in (NQ, NQ // 2)}
        tmp = {n: sb(f"tmp{n}", [1, n]) for n in (NQ, NQ // 2)}
        ea = [sb(f"ea{h}", [TP, 4, P]) for h in range(2)]
        prod = [sb(f"prod{h}", [TP, 4, P]) for h in range(2)]
        waste = [sb(f"waste{h}", [TP, 4, P]) for h in range(2)]
        sums = [sb(f"sums{h}", [TP, 4]) for h in range(2)]
        ohs = [sb(f"ohs{h}", [TP, 4, N], BF16) for h in range(4)]
        ohd = [sb(f"ohd{h}", [TP, 4, N], BF16) for h in range(4)]
        ea_d = A["edge_attr_128"].rearrange("(q u p) c -> q p u c", p=TP, u=4)
        attn = m.col("L1_gnn_attn")
        block = ctx.enter_context(nc.Block())

        @block.sync
        def _(sp):
            sp.dma_start(we[:, :, :], A["we_be"].rearrange("p (k n) -> p k n", k=KC)).then_inc(s("w"), 16)
            sp.dma_start(wn[:, :, :], A["wn"].rearrange("p (k n) -> p k n", k=KC)).then_inc(s("w"), 16)
            with sp.Fori(0, NQ // 2) as i:
                for h in range(2):
                    sp.wait_ge(s(f"ea_used{h}"), i + 1)
                    sp.dma_start(ea[h][:, :, :], ea_d[bass.ds(i * 2 + h, 1)].rearrange("q p u c -> (q p) u c"))\
                        .then_inc(s(f"ea{h}"), 16)

        @block.gpsimd
        def _(pool):
            st.credit(pool, "ea_used0", "ea_used1")
            norm_pool(nc, m, pool, st, Steps(pool, s("pool")))
            pool.wait_ge(s("vrow"), 2)
            with pool.Fori(0, NQ // 2) as i:
                for h in range(2):
                    pool.wait_ge(s(f"ea{h}"), (i + 1) * 16)
                    pool.wait_ge(s(f"prod_used{h}"), i + 1)
                    nc.gpsimd.tensor_tensor(prod[h][:, :, :], ea[h][:, :, :],
                                            vrow[:, :].unsqueeze(1).to_broadcast([TP, 4, P]), ALU.mult)\
                        .then_inc(s(f"ea_used{h}"), 1)

        @block.scalar
        def _(act):
            st.credit(act, "prod_used0", "prod_used1")
            act.wait_ge(s("ends_turned"), 1)
            nc.scalar.activation(ends16[:, :, :], m.ps[0:ET, 3, 0:3 * TP].rearrange("t (n p) -> t n p", n=3), ACT.Copy)\
                .then_inc(s("ends16"), 1)
            act.wait_ge(s("ends16"), 1)
            act.dma_start(m.end_rows.rearrange("n t p -> t n p"), ends16[:, :, :]).then_inc(s("end_rows"), 16)
            act.wait_ge(s("attn_done"), 1)
            nc.scalar.activation(vrow[:, :], m.ps[0:TP, 0, 0:P], ACT.Copy).then_inc(s("vrow"), 1)
            nc.scalar.activation(c0[:, 0:1], m.ps[0:TP, 0, P:P + 1], ACT.Copy).then_inc(s("vrow"), 1)
            act.wait_ge(s("q_made"), 1)
            nc.scalar.activation(m.q[:, :], m.ps[:, 1, 0:KC], ACT.Copy).then_inc(s("vrow"), 1)
            norm_scalar(nc, m, act, st, bank=4)
            act.dma_start(m.nodes0.rearrange("(t p) c -> p t c", p=TP), m.xn[:, :, :]).then_inc(s("nodes0"), 16)
            act.wait_ge(s("end_rows"), 16)
            act.dma_start(srow[:, :], m.end_rows[0].rearrange("t p -> (t p)")[None, :].to_broadcast([TP, E])).then_inc(s("srow"), 16)
            with act.Fori(0, NQ // 2) as i:
                for h in range(2):
                    act.wait_ge(s(f"ea_used{h}"), i + 2)
                    act.nop(nofuse=True)
                    for u in range(4):
                        nc.scalar.activation(waste[h][:, u, :], prod[h][:, u, :], ACT.Copy, accum_out=sums[h][:, u:u + 1])\
                            .then_inc(s("sums"), 1)
                    act.wait_ge(s("sums"), i * 8 + (4 * h + 4))
                    act.nop(nofuse=True)
                    nc.scalar.activation(m.score_e[:, bass.ds(i * 8 + 4 * h, 4)], sums[h][:, :], ACT.Copy)\
                        .then_inc(s(f"prod_used{h}"), 1)
            act.wait_ge(s("nodes0"), 16)
            act.wait_ge(s("counted"), 1)
            for t in range(NT):
                nc.scalar.activation(countT[:, t, 0:4 * TP], m.ps[0:TP, t, 0:4 * TP], ACT.Copy).then_inc(s("countT"), 1)
            nc.scalar.activation(countT[:, 0:4, 4 * TP:N], m.ps[0:TP, 5, :].rearrange("p (t n) -> p t n", t=4)[:, :, 0:TP],
                                 ACT.Copy).then_inc(s("countT"), 1)
            nc.scalar.activation(countT[:, 4, 4 * TP:N], m.ps[0:TP, 6, 0:TP], ACT.Copy).then_inc(s("countT"), 1)
            for t in range(NT):
                act.wait_ge(s("count_turned"), t + 1)
                nc.scalar.activation(m.count[:, t, 0:4 * TP], m.ps[0:TP, t, 0:4 * TP], ACT.Copy).then_inc(s("count"), 1)
            nc.scalar.activation(m.count[:, 0:4, 4 * TP:N], m.ps[0:TP, 5, 0:4 * TP].rearrange("p (t n) -> p t n", t=4),
                                 ACT.Copy).then_inc(s("count"), 1)
            nc.scalar.activation(m.count[:, 4, 4 * TP:N], m.ps[0:TP, 6, 0:TP], ACT.Copy).then_inc(s("count"), 1)

        @block.vector
        def _(dve):
            steps = Steps(dve, s("dve"))
            for k in range(KC):
                steps(nc.vector.tensor_scalar(attnB[:, k, :], m.ones[:, 0:TP], attn[:, k:k + 1], None, ALU.mult), s("attnB"))
            for j, (n, ends) in enumerate((("src", m.src), ("dst", m.dst))):
                for t in range(NT + 1):
                    steps(nc.vector.tensor_scalar(above[:, t, :], ends[:, :], float(t * TP), None, ALU.is_ge))
                steps.settle()
                steps(nc.vector.tensor_tensor(m.inside[n][:, :, :], above[:, 0:NT, :], above[:, 1:NT + 1, :], ALU.subtract))
                steps.do(nc.vector.tensor_reduce(place[:, j, :], above[:, 1:NT, :].rearrange("p t e -> p e t"), AX.X, ALU.add))
                steps.do(nc.vector.scalar_tensor_tensor(place[:, j, :], place[:, j, :], -float(TP), ends[:, :], ALU.mult, ALU.add),
                         s("places"))
            steps(nc.vector.tensor_reduce(per_quad[:, :, :].rearrange("p q t -> p t q"),
                                          m.inside["dst"][:, :, :].rearrange("p t (q u) -> p t q u", u=4), AX.X, ALU.add), s("per_group"))
            norm_vector(nc, m, dve, st, steps)
            steps(nc.vector.tensor_scalar(rev[:, :], m.iota[0:1, 0:NT], -1.0, float(NT - 1), ALU.mult, ALU.add))
            dve.wait_ge(s("groups"), 1)
            steps.do(nc.vector.tensor_copy(counts[:, :, :], m.ps[0:1, 2, 0:NQ * NT].rearrange("p (q k) -> p q k", k=NT)))
            steps(nc.vector.tensor_scalar(some[NQ][:, :, :], counts[:, :, :], 1.0, None, ALU.min))
            pairs = counts[:, :, :].rearrange("p (q h) k -> p q h k", h=2)
            steps.do(nc.vector.tensor_tensor(some[NQ // 2][:, :, :], pairs[:, :, 0, :], pairs[:, :, 1, :], ALU.add))
            steps.do(nc.vector.tensor_scalar(some[NQ // 2][:, :, :], some[NQ // 2][:, :, :], 1.0, None, ALU.min))
            for n, table in ((NQ, m.windows), (NQ // 2, m.windows2)):
                def ramp(ap):
                    return ap.unsqueeze(1).to_broadcast([1, n, NT])

                steps.do(nc.vector.tensor_tensor(span[n][:, :, :], some[n][:, :, :], ramp(m.iota[0:1, 0:NT]), ALU.mult))
                steps.do(nc.vector.tensor_reduce(last[n][:, :], span[n][:, :, :], AX.X, ALU.max))
                steps.do(nc.vector.tensor_tensor(span[n][:, :, :], some[n][:, :, :], ramp(rev[:, :]), ALU.mult))
                steps.do(nc.vector.tensor_reduce(back[n][:, :], span[n][:, :, :], AX.X, ALU.max))
                steps.do(nc.vector.tensor_scalar(tmp[n][:, :], back[n][:, :], -1.0, float(NT - 1), ALU.mult, ALU.add))
                for k in range(NT):
                    steps(nc.vector.tensor_scalar(table[:, :, k], tmp[n][:, :], float(k), float(NT - 1), ALU.add, ALU.min))
                steps.do(nc.vector.tensor_tensor(last[n][:, :], last[n][:, :], tmp[n][:, :], ALU.subtract))
                steps(nc.vector.tensor_scalar(table[:, :, NT], last[n][:, :], 1.0, None, ALU.add))
                steps.do(nc.vector.tensor_scalar(last[n][:, :], last[n][:, :], 8.0, 8.0, ALU.mult, ALU.add))
                steps.do(nc.vector.tensor_tensor(back[n][:, :], tmp[n][:, :], last[n][:, :], ALU.add))
            steps(nc.vector.tensor_copy(m.words2[:, :], back[NQ // 2][:, :]))
            pair = back[NQ][:, :].rearrange("p (q h) -> p q h", h=2)
            steps.do(nc.vector.scalar_tensor_tensor(tmp[NQ // 2][:, :], pair[:, :, 1], 64.0, pair[:, :, 0], ALU.mult, ALU.add))
            steps.do(nc.vector.tensor_copy(m.words[:, :], tmp[NQ // 2][:, :]), s("tables"))
            dve.wait_ge(s("vrow"), 2)
            steps.do(nc.vector.tensor_tensor_reduce(junk[:, :], m.row("L1_gnn_bn"), m.row("L1_gnn_attn"), 1.0, 0.0,
                                                    ALU.mult, ALU.add, c0[:, 1:2]))
            steps.do(nc.vector.tensor_tensor(m.score0[:, :], c0[:, 0:1], c0[:, 1:2], ALU.add))
            dve.wait_ge(s("tables"), 1)
            with dve.Fori(0, NQ // 4) as i:
                for h in range(4):
                    if h % 2 == 0:
                        word = word_of(dve, m.words, i * 2 + h // 2)
                    dve.wait_ge(s(f"oh_used{h}"), i + 1)
                    def onehot(k, tile):
                        nc.vector.tensor_tensor(ohd[h][:, :, k * TP:(k + 1) * TP],
                                                m.iota16[0:TP, bass.ds(tile * TP, TP)].unsqueeze(1).to_broadcast([TP, 4, TP]),
                                                m.dst16[:, bass.ds(i * 16 + 4 * h, 4)].unsqueeze(2).to_broadcast([TP, 4, TP]),
                                                ALU.is_equal)

                    for_windows(dve, word, h % 2, m.windows, i * 4 + h, onehot)
                    for u in range(4):
                        ins = nc.vector.tensor_scalar(ohs[h][:, u, :], m.iota16[0:TP, 0:N], m.src[:, bass.ds(i * 16 + (4 * h + u), 1)],
                                                      None, ALU.is_equal)
                    ins.then_inc(s(f"oh{h}"), 1)
            dve.wait_ge(s("srow"), 16)
            steps(nc.vector.tensor_scalar(m.mask_s[:, :], srow[:, :], m.pcol[0:TP, :], None, ALU.is_equal))
            dve.wait_ge(s("countT"), NT + 2)
            steps.do(nc.vector.tensor_reduce(m.deg[:, :], countT[:, :, :], AX.X, ALU.add))

        @block.tensor
        def _(pe):
            st.credit(pe, *[f"oh_used{h}" for h in range(4)])
            pe.wait_ge(s("places"), 2)
            for j, ends in enumerate((place[:, 0, :], place[:, 1, :], m.dst[:, :])):
                ins = nc.tensor.transpose(m.ps[0:ET, 3, j * TP:(j + 1) * TP], ends, m.ident[0:TP, 0:TP])
            ins.then_inc(s("ends_turned"), 1)
            pe.wait_ge(s("per_group"), 1)
            nc.tensor.matmul(m.ps[0:1, 2, 0:NQ * NT], m.ones[0:TP, 0:1], per_quad[:, :, :].rearrange("p q t -> p (q t)"),
                             start=True, stop=True).then_inc(s("groups"), 1)
            pe.wait_ge(s("w"), 32)
            pe.wait_ge(s("attnB"), KC)
            for k in range(KC):
                ins = nc.tensor.matmul(m.ps[0:TP, 0, 0:P + 1], attnB[:, k, :], we[:, k, :], start=k == 0, stop=k == KC - 1)
            ins.then_inc(s("attn_done"), 1)
            for c in range(KC):
                for k in range(KC):
                    ins = nc.tensor.matmul(m.ps[:, 1, c:c + 1], wn[:, k, c * P:(c + 1) * P], attn[:, k:k + 1],
                                           start=k == 0, stop=k == KC - 1)
            ins.then_inc(s("q_made"), 1)
            pe.wait_ge(s("vrow"), 3)
            pe.wait_ge(s("tables"), 1)
            pe.wait_ge(s("ends16"), 1)
            norm_tensor(nc, m, pe, st, bank=4)
            pe.wait_ge(s("xnT_done"), XNT)
            zero_banks(nc, m, 7, 512, start=True)
            rest = m.ps[0:TP, 5:7, :].rearrange("p b c -> p (b c)")

            with pe.Fori(0, NQ // 4) as i:
                for h in range(4):
                    if h % 2 == 0:
                        word = word_of(pe, m.words, i * 2 + h // 2)

                    def window(k, tile):
                        for u in range(4):
                            dst = ohd[h][:, u, k * TP:(k + 1) * TP]
                            nc.tensor.matmul(m.ps[0:TP, bass.ds(tile, 1), 0:4 * TP].rearrange("p b c -> p (b c)"), dst,
                                             ohs[h][:, u, 0:4 * TP], start=False, stop=False, skip_group_check=True)
                            nc.tensor.matmul(rest[:, bass.ds(tile * P, TP)], dst, ohs[h][:, u, 4 * TP:N],
                                             start=False, stop=False, skip_group_check=True)

                    pe.wait_ge(s(f"oh{h}"), i + 1)
                    for_windows(pe, word, h % 2, m.windows, i * 4 + h, window)
                    mark(nc, m).then_inc(s(f"oh_used{h}"), 1)
            zero_banks(nc, m, 7, 512, start=False).then_inc(s("counted"), 1)
            for r in range(NT):
                pe.wait_ge(s("countT"), NT + 2)
                for t in range(NT):
                    out = m.ps[0:TP, r, t * TP:(t + 1) * TP] if t < 4 else \
                        m.ps[0:TP, 5, r * TP:(r + 1) * TP] if r < 4 else m.ps[0:TP, 6, 0:TP]
                    ins = nc.tensor.transpose(out, countT[:, t, r * TP:(r + 1) * TP], m.ident[0:TP, 0:TP])
                ins.then_inc(s("count_turned"), 1)


def zero_banks(nc, m, banks, width, start):
    for b in range(banks):
        ins = nc.tensor.matmul(m.ps[0:TP, b, 0:width], m.zeros[:, 0:TP], m.zeros[:, 0:width], start=start, stop=not start,
                               skip_group_check=True)
    return ins


def mark(nc, m):
    return nc.tensor.matmul(m.ps[0:1, 7, 511:512], m.zeros[:, 0:1], m.zeros[:, 0:1], start=True, stop=True,
                            skip_group_check=True)



def l1_gnn(nc, m, A):
    BIG = 1e30
    CH = 1000
    PW = 16
    with ExitStack() as ctx:
        st = Stage(nc, ctx, "l1g")
        s, sb = st.sem, st.sb
        arow_d = nc.dram_tensor("l1_scores", (ET, TP), F32, kind="Internal").ap()
        table = nc.dram_tensor("l1_nodes", (N, C), F32, kind="Internal").ap()
        wnT = sb("wnT", [P, KC, C])
        score = sb("score", [TP, NT])
        mcol = sb("mcol", [TP, 8])
        rest = sb("rest", [TP, NT])
        parts = sb("parts", [TP, 3, NT], BF16)
        drow = sb("drow", [TP, E], F16)
        got = sb("got", [TP, ET])
        a = sb("a", [TP, ET])
        w = sb("w", [TP, ET])
        at = sb("at", [ET, TP])
        dcol = sb("dcol", [TP, 8])
        part = sb("part", [TP, 1])
        tick = sb("tick", [1, 5])
        hs = m.xn
        idx = sb("idx", [TP, 8], I32)
        hg = [sb(f"hg{h}", [TP, 4, C]) for h in range(2)]
        G = sb("G", [TP, ET, C + 1])
        woh = sb("woh", [TP, 2, 4, N])
        flat = woh[:, :, :, :].rearrange("p h u n -> p (h u n)")
        arow = [flat[:, h * CH:(h + 1) * CH] for h in range(5)]
        off = wnT[0:TP, :, :].rearrange("p k n -> p (k n)").bitcast(BF16)[:, 0:CH]
        mjunk = sb("mjunk", [TP, CH], BF16)
        sel = {"src": G[:, ET - 5:ET, :].rearrange("p e c -> p (e c)"), "dst": flat}
        sel = {n: v[:, 0:ET * 3 * NT].rearrange("p (e k) -> p e k", k=3 * NT) for n, v in sel.items()}
        places = flat.bitcast(F16)
        mask = m.mask_s
        res = m.xn
        den = sb("den", [TP, NT])
        block = ctx.enter_context(nc.Block())

        @block.sync
        def _(sp):
            sp.dma_start(wnT[:, :, :], A["wnT"].rearrange("p (k n) -> p k n", k=KC)).then_inc(s("w"), 16)
            row = lambda n: m.end_rows[n].rearrange("t p -> (t p)")[None, :].to_broadcast([TP, E])
            sp.wait_ge(s("hs"), NT)
            sp.dma_start(table.rearrange("(t p) c -> p t c", p=TP), hs[:, :, :]).then_inc(s("table"), 16)
            sp.dma_start(places, row(1)).then_inc(s("places"), 16)
            sp.dma_start(drow[:, :], row(2)).then_inc(s("drow"), 16)
            sp.wait_ge(s("at"), 1)
            sp.dma_start(arow_d, at[:, :]).then_inc(s("arow_d"), 16)
            sp.wait_ge(s("arow_d"), 16)
            sp.wait_ge(s("mask_d"), 1)
            with sp.Fori(0, E // (5 * CH)) as i:
                for h in range(5):
                    sp.wait_ge(s(f"max_done{h}"), i + 1)
                    sp.dma_start(arow[h],
                                 arow_d.rearrange("t p -> (t p)")[bass.ds(i * (5 * CH) + h * CH, CH)][None, :].to_broadcast([TP, CH]))\
                        .then_inc(s(f"arow{h}"), 16)

        @block.gpsimd
        def _(pool):
            steps = Steps(pool, s("pool"))
            norm_pool(nc, m, pool, st, steps)
            pool.wait_ge(s("table"), 16)
            with pool.Fori(0, NQ // 2) as i:
                for h in range(2):
                    pool.wait_ge(s(f"kept{h}"), i + 1)
                    pool.nop(nofuse=True)
                    nc.gpsimd.tensor_copy(idx[:, 4 * h:4 * h + 4], m.srci[:, bass.ds(i * 8 + 4 * h, 4)]).then_inc(s("idx"), 1)
                    pool.wait_ge(s("idx"), i * 2 + (h + 1))
                    pool.nop(nofuse=True)
                    for u in range(4):
                        pool.indirect_dma_start(
                            out=hg[h][:, u, :], out_offset=None, in_=table,
                            in_offset=bass.IndirectOffsetOnAxis(ap=idx[:, 4 * h + u:4 * h + u + 1], axis=0),
                        ).then_inc(s(f"hg{h}"), 16)

        @block.scalar
        def _(act):
            st.credit(act, "kept0", "kept1")
            norm_scalar(nc, m, act, st)
            act.wait_ge(s("score_made"), 1)
            nc.scalar.activation(score[:, :], m.ps[0:TP, 3, 0:NT], ACT.Copy).then_inc(s("score"), 1)
            for t in range(NT):
                act.wait_ge(s("h_made"), t + 1)
                nc.scalar.activation(hs[:, t, 0:C], m.ps[0:TP, 4 + t if t < 4 else 3, 0:C], ACT.Copy).then_inc(s("hs"), 1)

            def keep(first, last):
                with act.Fori(first, last) as i:
                    for h in range(2):
                        act.wait_ge(s(f"hg{h}"), (i + 1) * 64)
                        act.nop(nofuse=True)
                        nc.scalar.activation(G[:, bass.ds(i * 8 + 4 * h, 4), 0:C], hg[h][:, :, :], ACT.Copy)\
                            .then_inc(s(f"kept{h}"), 1)

            keep(0, 8)
            act.wait_ge(s("w_in"), 1)
            nc.scalar.activation(w[:, :], a[:, :], ACT.Exp).then_inc(s("w_edge"), 1)
            keep(8, NQ // 2)

        @block.vector
        def _(dve):
            steps = Steps(dve, s("dve"))
            st.credit(dve, *[f"max_done{h}" for h in range(5)])
            norm_vector(nc, m, dve, st, steps)
            for t in range(8):
                steps(nc.vector.tensor_scalar(dcol[:, t:t + 1], m.pcol[0:TP, :], float(t * TP), None, ALU.add))
            steps(nc.vector.memset(mcol[:, :], -BIG))

            def split(value):
                steps.do(nc.vector.tensor_copy(parts[:, 0, :], value))
                steps.do(nc.vector.tensor_tensor(rest[:, :], value, parts[:, 0, :], ALU.subtract))
                steps.do(nc.vector.tensor_copy(parts[:, 1, :], rest[:, :]))
                steps.do(nc.vector.tensor_tensor(rest[:, :], rest[:, :], parts[:, 1, :], ALU.subtract))
                steps(nc.vector.tensor_copy(parts[:, 2, :], rest[:, :]), s("parts"))

            def picked(n, bank, turn):
                dve.wait_ge(s("picked"), turn)
                values = m.ps[0:TP, bank:bank + 3, :].rearrange("p b c -> p (b c)")[:, 0:ET * PW]
                values = values.rearrange("p (e k) -> p e k", k=PW)[:, :, 0:3 * NT].rearrange("p e (j t) -> p e j t", t=NT)
                steps.do(nc.vector.tensor_tensor(sel[n].rearrange("p e (j t) -> p e j t", t=NT), values,
                                                 m.inside[n][:, :, :].rearrange("p t e -> p e t").unsqueeze(2).to_broadcast([TP, ET, 3, NT]),
                                                 ALU.mult))
                steps.do(nc.vector.tensor_reduce(got[:, :], sel[n], AX.X, ALU.add))

            dve.wait_ge(s("score"), 1)
            split(score[:, :])
            picked("src", 0, 1)
            steps.do(nc.vector.tensor_tensor(got[:, :], got[:, :], m.score_e[:, :], ALU.add))
            steps.do(nc.vector.tensor_scalar(got[:, :], got[:, :], m.score0[:, :], None, ALU.add))
            steps.do(nc.vector.scalar_tensor_tensor(a[:, :], got[:, :], 0.01, got[:, :], ALU.mult, ALU.max), s("a"))
            steps(nc.vector.memset(G[:, :, C:C + 1], 1.0), s("ones"))
            dve.wait_ge(s("a_turned"), 1)
            steps(nc.vector.tensor_copy(at[:, :], m.ps[0:ET, 3, 0:TP]), s("at"))
            dve.wait_ge(s("places"), 16)
            steps(nc.vector.tensor_scalar(mask[:, :], places, m.pcol[0:TP, :], None, ALU.is_equal), s("mask_d"))
            dve.wait_ge(s("drow"), 16)
            with dve.Fori(0, E // (5 * CH)) as i:
                for h in range(5):
                    word = word_of(dve, m.words2, i * 5 + h)
                    dve.wait_ge(s(f"arow{h}"), (i + 1) * 16)

                    def window(k, tile):
                        done = i * (15 * NT) + (3 * (h * NT + k))
                        nc.vector.tensor_scalar(off, drow[:, bass.ds(i * (5 * CH) + h * CH, CH)], dcol[:, bass.ds(tile, 1)],
                                                -BIG, ALU.not_equal, ALU.mult).then_inc(s("off"), 1)
                        dve.wait_ge(s("off"), done + 1)
                        dve.nop(nofuse=True)
                        nc.vector.tensor_tensor_reduce(mjunk[:, :], arow[h], off, 1.0, -BIG,
                                                       ALU.add, ALU.max, part[:, :]).then_inc(s("off"), 1)
                        dve.wait_ge(s("off"), done + 2)
                        nc.vector.tensor_tensor(mcol[:, bass.ds(tile, 1)], mcol[:, bass.ds(tile, 1)], part[:, :], ALU.max)\
                            .then_inc(s("off"), 1)
                        dve.wait_ge(s("off"), done + 3)
                        dve.nop(nofuse=True)

                    for_windows(dve, word, 0, m.windows2, i * 5 + h, window,
                                otherwise=lambda n: dve.nop(nofuse=True).then_inc(s("off"), 3 * n))
                    nc.vector.memset(tick[:, h:h + 1], 0.0).then_inc(s(f"max_done{h}"), 1)
            dve.wait_ge(s("max_done4"), E // (5 * CH) + 1)
            split(mcol[:, 0:NT])
            picked("dst", 5, 2)
            steps(nc.vector.tensor_tensor(a[:, :], a[:, :], got[:, :], ALU.subtract), s("w_in"))
            dve.wait_ge(s("w_edge"), 1)
            with dve.Fori(0, NQ // 2) as i:
                word = word_of(dve, m.words, i)
                for h in range(2):
                    def weighted(k, tile):
                        for u in range(4):
                            nc.vector.tensor_scalar(woh[:, h, u, k * TP:(k + 1) * TP], m.iota16[0:TP, bass.ds(tile * TP, TP)],
                                                    m.dst[:, bass.ds(i * 8 + (4 * h + u), 1)],
                                                    w[:, bass.ds(i * 8 + (4 * h + u), 1)], ALU.is_equal, ALU.mult)

                    dve.wait_ge(s(f"woh_used{h}"), i + 1)
                    for_windows(dve, word, h, m.windows, i * 2 + h, weighted)
                    nc.vector.memset(tick[:, h:h + 1], 0.0).then_inc(s(f"woh{h}"), 1)
            dve.wait_ge(s("summed"), 1)
            for t in range(NT):
                steps(nc.vector.tensor_scalar(den[:, t:t + 1], m.ps[0:TP, t, C:C + 1], 1e-16, None, ALU.add))
            steps.settle()
            steps.do(nc.vector.reciprocal(den[:, :], den[:, :]))
            for t in range(NT):
                steps(nc.vector.tensor_scalar(res[:, t, 0:C], m.ps[0:TP, t, 0:C], den[:, t:t + 1], 0.0, ALU.mult, ALU.max))
            steps.settle()
            for t in range(NT):
                steps(nc.vector.tensor_tensor(m.x[:, t, :], m.x[:, t, :], res[:, t, 0:C], ALU.add))
            steps.settle()

        @block.tensor
        def _(pe):
            st.credit(pe, "woh_used0", "woh_used1")
            norm_tensor(nc, m, pe, st)
            pe.wait_ge(s("xnT_done"), XNT)
            for t in range(NT):
                for k in range(KC):
                    ins = nc.tensor.matmul(m.ps[0:TP, 3, t:t + 1], m.xnT[:, k, t * TP:(t + 1) * TP], m.q[:, k:k + 1],
                                           start=k == 0, stop=k == KC - 1)
            ins.then_inc(s("score_made"), 1)
            pe.wait_ge(s("w"), 16)
            for t in range(NT):
                if t == 4:
                    pe.wait_ge(s("score"), 1)
                out = m.ps[0:TP, 4 + t if t < 4 else 3, 0:C]
                for k in range(KC):
                    nc.tensor.matmul(out, m.xnT[:, k, t * TP:(t + 1) * TP], wnT[:, k, :], start=k == 0, stop=False)
                nc.tensor.matmul(out, m.ones[0:1, 0:TP], m.row("L1_gnn_bn", 1), start=False, stop=True).then_inc(s("h_made"), 1)

            def pick(bank):
                space = m.ps[0:TP, bank:bank + 3, :].rearrange("p b c -> p (b c)")
                for e in range(ET):
                    ins = nc.tensor.matmul(space[:, e * PW:e * PW + 3 * NT], mask[:, e * TP:(e + 1) * TP],
                                           parts[:, :, :].rearrange("p j t -> p (j t)"), start=True, stop=True)
                ins.then_inc(s("picked"), 1)

            pe.wait_ge(s("parts"), 1)
            pick(0)
            pe.wait_ge(s("a"), 1)
            pe.wait_ge(s("hs"), NT)
            nc.tensor.transpose(m.ps[0:ET, 3, 0:TP], a[:, :], m.ident[0:TP, 0:TP]).then_inc(s("a_turned"), 1)
            pe.wait_ge(s("at"), 1)
            pe.wait_ge(s("ones"), 1)
            zero_banks(nc, m, NT, C + 1, start=True)
            pe.wait_ge(s("mask_d"), 1)
            pe.wait_ge(s("parts"), 2)
            pick(5)
            with pe.Fori(0, NQ // 2) as i:
                word = word_of(pe, m.words, i)
                for h in range(2):
                    def window(k, tile):
                        for u in range(4):
                            nc.tensor.matmul(m.ps[0:TP, bass.ds(tile, 1), 0:C + 1].rearrange("p b c -> p (b c)"),
                                             woh[:, h, u, k * TP:(k + 1) * TP],
                                             G[:, bass.ds(i * 8 + (4 * h + u), 1), :].rearrange("p a c -> p (a c)"),
                                             start=False, stop=False, skip_group_check=True)

                    pe.wait_ge(s(f"kept{h}"), i + 2)
                    pe.wait_ge(s(f"woh{h}"), i + 1)
                    for_windows(pe, word, h, m.windows, i * 2 + h, window)
                    mark(nc, m).then_inc(s(f"woh_used{h}"), 1)
            zero_banks(nc, m, NT, C + 1, start=False).then_inc(s("summed"), 1)



class Experts:

    def __init__(self, hidden):
        self.hidden = hidden
        self.units = []
        for layer, chunks_ in enumerate(hidden):
            for e in range(2):
                for half in range(2):
                    for c in range(chunks_):
                        self.units.append((layer, e, half, c))
        for e in range(2):
            for t in range(NT):
                self.units.append((len(hidden), e, t, 0))
        self.uses = [len(range(b, len(self.units), 8)) for b in range(8)]
        self.at = {u: k for k, u in enumerate(self.units)}

    def before(self, k, i):
        return i * self.uses[k % 8] + (k // 8 + 1)

    def left(self, k, i):
        return i * self.uses[k % 8] + (k // 8 + 2)

    def after(self, k, i):
        return i * self.uses[k % 8] + (k // 8 + 1)

    def credit(self, st, dve):
        st.credit(dve, *[f"free{b}" for b in range(8)])

    def last_reader(self, layer, e):
        return max(k for k, u in enumerate(self.units) if u[0] == layer and u[1] == e)

    def load(self, sp, s, i, bufs, source, again=True):
        for layer in range(len(self.hidden) + 1):
            for e in range(2):
                if again:
                    k = self.last_reader(layer, e)
                    sp.wait_ge(s(f"made{k % 8}"), self.after(k, i) - self.uses[k % 8])
                sp.dma_start(bufs[layer][e][:, :], source[bass.ds(i * 2 + e, 1), layer].rearrange("a p n -> (a p) n"))\
                    .then_inc(s(f"w{layer}{e}"), 16)

    def tensor(self, nc, m, pe, s, i, bufs, hT):
        for k, (layer, e, part, c) in enumerate(self.units):
            pe.wait_ge(s(f"free{k % 8}"), self.before(k, i))
            if k == min(self.at[u] for u in self.units if u[0] == layer and u[1] == e):
                pe.wait_ge(s(f"w{layer}{e}"), (i + 1) * 16)
            final = layer == len(self.hidden)
            if layer:
                below = self.hidden[layer - 1]
                for half in ([part] if not final else [0] if part < 2 else [0, 1]):
                    for b in range(below):
                        j = self.at[(layer - 1, e, half, b)]
                        pe.wait_ge(s(f"free{j % 8}"), self.left(j, i))
            src = m.xnT if layer == 0 else hT[layer - 1][e]
            kin = KC if layer == 0 else self.hidden[layer - 1]
            w = bufs[layer][e][:, :].rearrange("p (k n) -> p k n", k=kin)
            for j in range(kin):
                if final:
                    ins = nc.tensor.matmul(m.ps[0:TP, k % 8, 0:C], src[:, j, part * TP:(part + 1) * TP], w[:, j, :],
                                           start=j == 0, stop=j == kin - 1)
                else:
                    a, b = HALF[part]
                    ins = nc.tensor.matmul(m.ps[:, k % 8, 0:b - a], w[:, j, c * P:(c + 1) * P], src[:, j, a:b],
                                           start=j == 0, stop=j == kin - 1)
            ins.then_inc(s(f"made{k % 8}"), 1)

    def scalar(self, nc, m, act, s, i, hT, coef):
        for k, (layer, e, part, c) in enumerate(self.units):
            if layer < len(self.hidden):
                a, b = HALF[part]
                scale, bias = coef(layer, i * 2 + e, c)
                act.wait_ge(s(f"made{k % 8}"), self.after(k, i))
                act.nop(nofuse=True)
                nc.scalar.activation(hT[layer][e][:, c, a:b], m.ps[:, k % 8, 0:b - a], ACT.Relu, bias=bias, scale=scale)\
                    .then_inc(s(f"free{k % 8}"), 1)

    def vector(self, nc, m, dve, s, i, gate, acc):
        final = len(self.hidden)
        for k, (layer, e, t, _) in enumerate(self.units):
            if layer == final:
                dve.wait_ge(s(f"made{k % 8}"), self.after(k, i))
                j = self.at[(final, 1 - e, t, 0)]
                dve.wait_ge(s(f"free{j % 8}"), self.left(j, i) - (self.uses[j % 8] if e == 0 else 0))
                nc.vector.scalar_tensor_tensor(acc[:, t, :], m.ps[0:TP, k % 8, 0:C], gate[:, t, bass.ds(i * 2 + e, 1)],
                                               acc[:, t, :], ALU.mult, ALU.add).then_inc(s(f"free{k % 8}"), 1)


def gate_tensor(nc, m, pe, s, wr, ne, bias, last_bias):
    pe.wait_ge(s("xnT_done"), XNT)
    pe.wait_ge(s("small"), 32)
    for t in range(NT):
        for k in range(KC):
            nc.tensor.matmul(m.ps[0:TP, 3, t * ne:(t + 1) * ne], m.xnT[:, k, t * TP:(t + 1) * TP], wr[:, k, :],
                             start=k == 0, stop=False)
        nc.tensor.matmul(m.ps[0:TP, 3, t * ne:(t + 1) * ne], m.ones[0:1, 0:TP], m.row(bias, 1), start=False, stop=True)\
            .then_inc(s("scores"), 1)


def gate_turn(nc, m, pe, s, gate, gateT, ne, last_bias):
    pe.wait_ge(s("gate"), 1)
    for t in range(NT):
        b, c = (4, t * TP) if t < 4 else (5, 0)
        nc.tensor.transpose(m.ps[0:ne, b, c:c + TP], gate[:, t, :], m.ident[0:TP, 0:TP]).then_inc(s("gate_turned"), 1)
    pe.wait_ge(s("gateT"), 2)
    for t in range(NT):
        b = t if t < 3 else t + 3
        nc.tensor.matmul(m.ps[0:TP, b, 0:C], gateT[:, t * TP:(t + 1) * TP], last_bias[:, :], start=True, stop=True)\
            .then_inc(s("bias_made"), 1)


def gate_scalar(nc, m, act, s, gateT, acc, ne):
    act.wait_ge(s("gate_turned"), NT)
    nc.scalar.activation(gateT[:, 0:4 * TP], m.ps[0:ne, 4, 0:4 * TP], ACT.Copy).then_inc(s("gateT"), 1)
    nc.scalar.activation(gateT[:, 4 * TP:N], m.ps[0:ne, 5, 0:TP], ACT.Copy).then_inc(s("gateT"), 1)
    for t in range(NT):
        act.wait_ge(s("bias_made"), t + 1)
        nc.scalar.activation(acc[:, t, :], m.ps[0:TP, t if t < 3 else t + 3, 0:C], ACT.Copy).then_inc(s("acc"), 1)


def l1_ffn(nc, m, A):
    NE = 8
    plan = Experts([2, 2])
    with ExitStack() as ctx:
        st = Stage(nc, ctx, "l1f")
        s, sb = st.sem, st.sb
        wr = sb("wr", [P, KC, NE])
        bo = sb("bo", [NE, C])
        bufs = [[sb(f"w{l}{e}", [P, 512]) for e in range(2)] for l in range(3)]
        hT = [[sb(f"h{l}{e}", [P, 2, N]) for e in range(2)] for l in range(2)]
        coefs = sb("coefs", [P, 4, 2 * NE])
        cv = sb("cv", [P, 2, 2 * NE])
        half16 = m.mhalf
        score = sb("score", [TP, NT, NE])
        top = sb("top", [TP, NT])
        tot = sb("tot", [TP, NT])
        gate = sb("gate", [TP, NT, NE])
        gateT = sb("gateT", [NE, N])
        acc = sb("acc", [TP, NT, C])
        block = ctx.enter_context(nc.Block())

        @block.sync
        def _(sp):
            sp.dma_start(wr[:, :, :], A["l1f_wr"].rearrange("p (k e) -> p k e", k=KC)).then_inc(s("small"), 16)
            sp.dma_start(bo[:, :], A["L1_ffn_bo"]).then_inc(s("small"), 16)
            plan.load(sp, s, 0, bufs, A["l1f_w"], again=False)
            with sp.Fori(1, NE // 2) as i:
                plan.load(sp, s, i, bufs, A["l1f_w"])

        @block.gpsimd
        def _(pool):
            steps = Steps(pool, s("pool"))
            norm_pool(nc, m, pool, st, steps)
            for n in range(2):
                p = lambda name: m.col(f"L1_ffn_{name}{n + 1}")
                steps.do(nc.gpsimd.tensor_scalar(cv[:, 0, :], p("v"), 1e-3, None, ALU.add))
                steps.do(nc.gpsimd.tensor_tensor(cv[:, 1, :], cv[:, 0, :], m.mhalf[:, :], ALU.pow))
                steps.do(nc.gpsimd.tensor_tensor(coefs[:, 2 * n, :], cv[:, 1, :], p("g"), ALU.mult))
                steps.do(nc.gpsimd.tensor_tensor(cv[:, 0, :], p("b"), p("m"), ALU.subtract))
                steps.do(nc.gpsimd.tensor_tensor(cv[:, 1, :], cv[:, 0, :], coefs[:, 2 * n, :], ALU.mult))
                steps.do(nc.gpsimd.tensor_tensor(coefs[:, 2 * n + 1, :], cv[:, 1, :], p("be"), ALU.add), s("coefs"))

        def coef(layer, e, c):
            return coefs[:, 2 * layer, bass.ds(e * 2 + c, 1)], coefs[:, 2 * layer + 1, bass.ds(e * 2 + c, 1)]

        @block.scalar
        def _(act):
            norm_scalar(nc, m, act, st)
            act.wait_ge(s("exp_in"), 1)
            nc.scalar.activation(gate[:, :, :], score[:, :, :], ACT.Exp).then_inc(s("exp_out"), 1)
            gate_scalar(nc, m, act, s, gateT, acc, NE)
            act.wait_ge(s("coefs"), 2)
            with act.Fori(0, NE // 2) as i:
                plan.scalar(nc, m, act, s, i, hT, coef)

        @block.vector
        def _(dve):
            steps = Steps(dve, s("dve"))
            plan.credit(st, dve)
            norm_vector(nc, m, dve, st, steps)
            dve.wait_ge(s("scores"), NT)
            steps.do(nc.vector.tensor_copy(score[:, :, :], m.ps[0:TP, 3, 0:NT * NE].rearrange("p (t e) -> p t e", t=NT)))
            steps.do(nc.vector.tensor_reduce(top[:, :], score[:, :, :], AX.X, ALU.max))
            steps(nc.vector.tensor_tensor(score[:, :, :], score[:, :, :], top[:, :].unsqueeze(2).to_broadcast([TP, NT, NE]),
                                          ALU.subtract), s("exp_in"))
            dve.wait_ge(s("exp_out"), 1)
            steps.do(nc.vector.tensor_reduce(tot[:, :], gate[:, :, :], AX.X, ALU.add))
            steps.do(nc.vector.reciprocal(top[:, :], tot[:, :]))
            steps(nc.vector.tensor_tensor(gate[:, :, :], gate[:, :, :], top[:, :].unsqueeze(2).to_broadcast([TP, NT, NE]),
                                          ALU.mult), s("gate"))
            dve.wait_ge(s("acc"), NT)
            dve.wait_ge(s("gate"), 1)
            with dve.Fori(0, NE // 2) as i:
                plan.vector(nc, m, dve, s, i, gate, acc)
            for b in range(8):
                dve.wait_ge(s(f"free{b}"), plan.uses[b] * (NE // 2) + 1)
            for t in range(NT):
                steps(nc.vector.tensor_tensor(m.x[:, t, :], m.x[:, t, :], acc[:, t, :], ALU.add))
            steps.settle()

        @block.tensor
        def _(pe):
            norm_tensor(nc, m, pe, st)
            gate_tensor(nc, m, pe, s, wr, NE, "L1_ffn_br", bo)
            gate_turn(nc, m, pe, s, gate, gateT, NE, bo)
            pe.wait_ge(s("acc"), NT)
            with pe.Fori(0, NE // 2) as i:
                plan.tensor(nc, m, pe, s, i, bufs, hT)



def l2_gnn(nc, m, A):
    D1, D2 = 128, 64
    with ExitStack() as ctx:
        st = Stage(nc, ctx, "l2g")
        s, sb = st.sem, st.sb
        W = sb("W", [P, 1344])
        w1 = W[:, 0:256].rearrange("p (k n) -> p k n", k=KC)
        wfc = W[:, 256:1280].rearrange("p (k n) -> p k n", k=4)
        w2 = W[:, 1280:1344]
        adj = sb("adj", [TP, NT, N])
        dinvT = sb("dinvT", [P, N])
        diag = sb("diag", [TP, NT, TP])
        dinv = sb("dinv", [TP, NT])
        h1 = sb("h1", [TP, NT, D1])
        h2 = sb("h2", [TP, NT, D2])
        o = [sb(f"o{n}", [P, N]) for n in range(2)]
        xT = [sb(f"xT{n}", [P, N]) for n in range(2)]
        bst = sb("bst", [P, NT, 6])
        bmv = sb("bmv", [P, 2])
        bt = sb("bt", [P, 8])
        b2 = sb("b2", [D2, 4])
        res = sb("res", [TP, NT, C])
        block = ctx.enter_context(nc.Block())
        dims = [D1, D2]

        def h_place(t, d):
            return (6, t * d) if t < 4 else (7, 0)

        def fc_place(t):
            return 3 + t // 2, (t % 2) * C

        @block.sync
        def _(sp):
            sp.dma_start(W[:, 0:1344], A["w_l2g"]).then_inc(s("w"), 16)
            sp.dma_start(b2[:, 0:3], A["l2g_small"]).then_inc(s("w"), 16)

        @block.gpsimd
        def _(pool):
            steps = Steps(pool, s("pool"))
            steps.do(nc.gpsimd.tensor_scalar(dinv[:, :], m.deg[:, :], 1.0, None, ALU.add))
            steps(nc.gpsimd.tensor_tensor(dinv[:, :], dinv[:, :], m.mhalf[0:TP, 0:NT], ALU.pow), s("dinv"))
            norm_pool(nc, m, pool, st, steps)
            for n, d in enumerate(dims):
                pool.wait_ge(s("bn_var"), n + 1)
                steps.do(nc.gpsimd.tensor_scalar(bt[0:d, 0:1], bmv[0:d, 1:2], 1e-5, None, ALU.add))
                steps(nc.gpsimd.tensor_tensor(bt[0:d, 1:2], bt[0:d, 0:1], m.mhalf[0:d, 0:1], ALU.pow), s("bn_rstd"))

        @block.scalar
        def _(act):
            norm_scalar(nc, m, act, st)
            act.wait_ge(s("dinvT_made"), 2)
            for n, (a, b) in enumerate(((0, 4 * TP), (4 * TP, N))):
                nc.scalar.activation(dinvT[:, a:b], m.ps[:, 1 + n, 0:b - a], ACT.Copy).then_inc(s("dinvT"), 1)
            for n, (d, h) in enumerate(((D1, h1), (D2, h2))):
                for t in range(NT):
                    act.wait_ge(s(f"h_made{n}"), 1 if t < 4 else 2)
                    b, c = h_place(t, d)
                    nc.scalar.activation(h[:, t, :], m.ps[0:TP, b, c:c + d], ACT.Copy, scale=dinv[:, t:t + 1]).then_inc(s(f"h{n}"), 1)
                act.wait_ge(s("bn_coef"), n + 1)
                nc.scalar.activation(xT[n][0:d, :], o[n][0:d, :], ACT.Relu, bias=bt[0:d, 3:4], scale=bt[0:d, 2:3])\
                    .then_inc(s("xT"), 1)

        @block.vector
        def _(dve):
            steps = Steps(dve, s("dve"))
            norm_vector(nc, m, dve, st, steps)
            for t in range(NT):
                steps(nc.vector.tensor_copy(adj[:, t, :], m.count[:, t, :]))
            steps.settle()
            for t in range(NT):
                steps(nc.vector.tensor_tensor(adj[:, t, t * TP:(t + 1) * TP], adj[:, t, t * TP:(t + 1) * TP],
                                              m.ident[0:TP, 0:TP], ALU.add), s("adj"))
            dve.wait_ge(s("dinv"), 1)
            for t in range(NT):
                steps(nc.vector.tensor_scalar(diag[:, t, :], m.ident[0:TP, 0:TP], dinv[:, t:t + 1], None, ALU.mult), s("diag"))
            dve.wait_ge(s("dinvT"), 2)
            dve.wait_ge(s("w"), 32)
            for n, d in enumerate(dims):
                bias, gam, bet = [m.col("L2_gnn_" + x)[:, 0:1] for x in ("b1", "g1", "be1")] if n == 0 else \
                    [b2[:, x:x + 1] for x in range(3)]
                for i, (a, b) in enumerate(HALF):
                    dve.wait_ge(s(f"o_made{n}"), i + 1)
                    steps.do(nc.vector.tensor_tensor(o[n][0:d, a:b], m.ps[0:d, 1 + i, 0:b - a], dinvT[0:d, a:b], ALU.mult))
                    steps.do(nc.vector.tensor_scalar(o[n][0:d, a:b], o[n][0:d, a:b], bias, None, ALU.add))
                for t in range(NT):
                    steps(nc.vector.bn_stats(bst[0:d, t, :], o[n][0:d, t * TP:(t + 1) * TP]))
                steps.settle()
                steps(nc.vector.bn_aggr(bmv[0:d, :], bst[0:d, :, :].rearrange("p t s -> p (t s)")), s("bn_var"))
                dve.wait_ge(s("bn_rstd"), n + 1)
                steps.do(nc.vector.tensor_tensor(bt[0:d, 2:3], bt[0:d, 1:2], gam, ALU.mult))
                steps.do(nc.vector.tensor_tensor(bt[0:d, 4:5], bmv[0:d, 0:1], bt[0:d, 2:3], ALU.mult))
                steps(nc.vector.tensor_tensor(bt[0:d, 3:4], bet, bt[0:d, 4:5], ALU.subtract), s("bn_coef"))
                if n == 0:
                    dve.wait_ge(s("xT"), 1)
            for t in range(NT):
                dve.wait_ge(s("fc_made"), min(t // 2, 2) + 1)
                b, c = fc_place(t)
                steps.do(nc.vector.tensor_scalar(res[:, t, :], m.ps[0:TP, b, c:c + C], 0.0, None, ALU.max))
                steps(nc.vector.tensor_tensor(m.x[:, t, :], m.x[:, t, :], res[:, t, :], ALU.add))
            steps.settle()

        @block.tensor
        def _(pe):
            norm_tensor(nc, m, pe, st)
            pe.wait_ge(s("xnT_done"), XNT)
            pe.wait_ge(s("w"), 32)
            for t in range(NT):
                b, c = h_place(t, D1)
                for k in range(KC):
                    ins = nc.tensor.matmul(m.ps[0:TP, b, c:c + D1], m.xnT[:, k, t * TP:(t + 1) * TP], w1[:, k, :],
                                           start=k == 0, stop=k == KC - 1)
                if t >= 3:
                    ins.then_inc(s("h_made0"), 1)
            pe.wait_ge(s("diag"), NT)
            for t in range(NT):
                b, c = (1, t * TP) if t < 4 else (2, 0)
                ins = nc.tensor.matmul(m.ps[:, b, c:c + TP], m.ones[0:TP, :], diag[:, t, :], start=True, stop=True)
                if t >= 3:
                    ins.then_inc(s("dinvT_made"), 1)

            def fc(*parts):
                for t in range(NT):
                    b, c = fc_place(t)
                    for lhsT, rhs in parts:
                        if lhsT is not None:
                            lhsT = lhsT[:, t * TP:(t + 1) * TP]
                        nc.tensor.matmul(m.ps[0:TP, b, c:c + C], m.ones[0:1, 0:TP] if lhsT is None else lhsT, rhs,
                                         start=False, stop=False, skip_group_check=True)

            pe.wait_ge(s("adj"), NT)
            for n, (d, h) in enumerate(((D1, h1), (D2, h2))):
                if n == 1:
                    pe.wait_ge(s("xT"), 1)
                    for t in range(NT):
                        b, c = h_place(t, D2)
                        ins = nc.tensor.matmul(m.ps[0:TP, b, c:c + D2], xT[0][:, t * TP:(t + 1) * TP], w2[:, :], start=True,
                                               stop=True)
                        if t >= 3:
                            ins.then_inc(s("h_made1"), 1)
                pe.wait_ge(s(f"h{n}"), NT)
                pe.wait_ge(s("dinvT"), 2)
                for i, (a, b) in enumerate(HALF):
                    for t in range(NT):
                        ins = nc.tensor.matmul(m.ps[0:d, 1 + i, 0:b - a], h[:, t, :], adj[:, t, a:b], start=t == 0,
                                               stop=t == NT - 1)
                    ins.then_inc(s(f"o_made{n}"), 1)
                if n == 0:
                    for b in range(3, 6):
                        nc.tensor.matmul(m.ps[0:TP, b, :], m.zeros[:, 0:TP], m.zeros[:, :], start=True, stop=False,
                                         skip_group_check=True)
                    fc((None, m.row("L2_gnn_bfc", 1)), (m.xnT[:, 0, :], wfc[:, 0, :]), (m.xnT[:, 1, :], wfc[:, 1, :]))
                else:
                    fc((xT[0], wfc[:, 2, :]))
            pe.wait_ge(s("xT"), 2)
            fc((xT[1][0:D2, :], wfc[0:D2, 3, :]))
            for b in range(3, 6):
                nc.tensor.matmul(m.ps[0:TP, b, :], m.zeros[:, 0:TP], m.zeros[:, :], start=False, stop=True,
                                 skip_group_check=True).then_inc(s("fc_made"), 1)


def l2_ffn(nc, m, A):
    NE, NB = 16, 26
    with ExitStack() as ctx:
        st = Stage(nc, ctx, "l2f")
        s, sb = st.sem, st.sb
        xs_d = nc.dram_tensor("l2_sorted", ((NB + 2) * P, C), F32, kind="Internal").ap()
        y_d = nc.dram_tensor("l2_results", (NB * P, C), F32, kind="Internal").ap()
        wr = sb("wr", [P, KC, NE])
        b2 = sb("b2", [NE, C])
        w1 = [sb(f"w1{h}", [P, 1024]) for h in range(2)]
        w2 = [sb(f"w2{h}", [P, 1024]) for h in range(2)]
        empty = sb("empty", [P, C])
        xb = [sb(f"xb{h}", [P, C]) for h in range(2)]
        xT = [sb(f"xT{h}", [P, KC, P]) for h in range(2)]
        hT = [sb(f"hT{h}", [P, 4, P]) for h in range(2)]
        yb = [sb(f"yb{h}", [P, C]) for h in range(2)]
        yg = sb("yg", [TP, 2, NT, C])
        score = sb("score", [TP, NT, NE])
        left = sb("left", [TP, NT, NE])
        pick = sb("pick", [TP, 2, NT, NE])
        at = sb("at", [TP, 2, NT, NE])
        low = sb("low", [TP, NT, NE])
        top = sb("top", [TP, 8, NT])
        gate = sb("gate", [TP, NT, NE])
        gateT = sb("gateT", [NE, N])
        chosen = sb("chosen", [TP, NT, NE], BF16)
        lower = sb("lower", [TP, TP], BF16)
        all16 = sb("all16", [TP, TP], BF16)
        blocks = sb("blocks", [TP, NE])
        ends = [sb(f"ends{v}", [TP, NE]) for v in range(2)]
        first = sb("first", [TP, NE])
        slot = sb("slot", [TP, 2, NT])
        slot_i = sb("slot_i", [TP, 2, NT], I32)
        after = sb("after", [1, NB, NE])
        owner = sb("owner", [1, NB])
        uses = sb("uses", [1, 2])
        uses_i = sb("uses_i", [1, 2], I32)
        info = sb("info", [1, NB])
        info2 = sb("info2", [1, NB // 2])
        table = sb("table", [1, NB // 2], I32)
        acc = sb("acc", [TP, NT, C])
        z = sb("z", [TP, NT, C])
        block = ctx.enter_context(nc.Block())

        def turn_of(eng, i):
            return eng.value_load(table[0:1, bass.ds(i, 1)], min_val=0, max_val=1023)

        def expert_of(word, h):
            return (word >> 5 if h else word) & (NE - 1)

        def used(word, h):
            return (word & (16 << (5 * h))) > 0


        @block.sync
        def _(sp):
            sp.dma_start(wr[:, :, :], A["l2f_wr"].rearrange("p (k e) -> p k e", k=KC)).then_inc(s("small"), 16)
            sp.dma_start(b2[:, :], A["L2_ffn_b2"]).then_inc(s("small"), 16)
            sp.wait_ge(s("empty"), 1)
            sp.dma_start(xs_d.rearrange("(b p) c -> p b c", p=P), empty[:, :].unsqueeze(1).to_broadcast([P, NB + 2, C]))\
                .then_inc(s("cleared"), 16)
            sp.dma_start(y_d.rearrange("(b p) c -> p b c", p=P), empty[:, :].unsqueeze(1).to_broadcast([P, NB, C]))\
                .then_inc(s("cleared"), 16)
            sp.wait_ge(s("tables"), 1)
            with sp.Fori(0, NB // 2) as i:
                word = turn_of(sp, i)
                for h in range(2):
                    e = expert_of(word, h)
                    with sp.If(used(word, h)):
                        for l, (w, last_use) in enumerate(((w1, "h_made1"), (w2, "y_made"))):
                            sp.wait_ge(s(f"{last_use}{h}"), i + 1)
                            sp.nop(nofuse=True)
                            sp.dma_start(w[h][:, :], A["l2f_w"][bass.ds(e, 1), l].rearrange("a p n -> (a p) n"))\
                                .then_inc(s(f"w{l}{h}"), 16)

        @block.gpsimd
        def _(pool):
            steps = Steps(pool, s("pool"))
            st.credit(pool, "yb_free0", "yb_free1")
            steps(nc.gpsimd.memset(empty[:, :], 0.0), s("empty"))
            norm_pool(nc, m, pool, st, steps)
            pool.wait_ge(s("cleared"), 32)
            pool.wait_ge(s("slots"), 1)
            for t in range(NT):
                for j in range(2):
                    pool.indirect_dma_start(out=xs_d, out_offset=bass.IndirectOffsetOnAxis(ap=slot_i[:, j, t:t + 1], axis=0),
                                            in_=m.xn[:, t, :], in_offset=None).then_inc(s("sorted"), 16)
            pool.wait_ge(s("sorted"), 160)
            pool.wait_ge(s("tables"), 1)
            pool.nop(nofuse=True).then_inc(s("rows_sorted"), 1)
            with pool.Fori(0, NB // 2) as i:
                word = turn_of(pool, i)
                for h in range(2):
                    with pool.If(used(word, h)):
                        pool.wait_ge(s(f"y_taken{h}"), i + 2)
                        pool.dma_start(y_d[bass.ds((i * 2 + h) * P, P), :], yb[h][:, :]).then_inc(s(f"y_out{h}"), 16)
                        pool.wait_ge(s(f"y_out{h}"), i * 16 + 16)
                        pool.nop(nofuse=True).then_inc(s(f"yb_free{h}"), 1)
            for t in range(NT):
                for j in range(2):
                    pool.indirect_dma_start(out=yg[:, j, t, :], out_offset=None, in_=y_d,
                                            in_offset=bass.IndirectOffsetOnAxis(ap=slot_i[:, j, t:t + 1], axis=0))\
                        .then_inc(s(f"yg{t}"), 16)
            pool.wait_ge(s("z_stats"), NT)
            steps.do(nc.gpsimd.tensor_scalar(m.veps[0:TP, :], m.mv[:, :, 1], 1e-5, None, ALU.add))
            steps(nc.gpsimd.tensor_tensor(m.rstd[0:TP, :], m.veps[0:TP, :], m.mhalf[0:TP, 0:NT], ALU.pow), s("z_rstd"))

        @block.scalar
        def _(act):
            st.credit(act, "hT0", "hT1")
            norm_scalar(nc, m, act, st)
            act.wait_ge(s("exp_in"), 1)
            nc.scalar.activation(top[:, 3, :], top[:, 2, :], ACT.Exp).then_inc(s("exp_out"), 1)
            gate_scalar(nc, m, act, s, gateT, acc, NE)
            act.wait_ge(s("tables"), 1)
            act.wait_ge(s("rows_sorted"), 1)
            for h in range(2):
                act.dma_start(xb[h][:, :], xs_d[h * P:(h + 1) * P, :]).then_inc(s(f"xb{h}"), 16)
            with act.Fori(0, NB // 2) as i:
                word = turn_of(act, i)
                for h in range(2):
                    e = expert_of(word, h)
                    with act.If(used(word, h)):
                        for c in range(4):
                            if c % 2 == 0:
                                act.wait_ge(s(f"h_made{c // 2}{h}"), i + 2)
                                act.nop(nofuse=True)
                            nc.scalar.activation(hT[h][:, c, :], m.ps[:, 2 + c // 2 * 2 + h, (c % 2) * P:(c % 2 + 1) * P], ACT.Relu,
                                                 bias=m.col("L2_ffn_b1")[:, bass.ds(e * 4 + c, 1)]).then_inc(s(f"hT{h}"), 1)
                        act.wait_ge(s(f"x_turned{h}"), i + 2)
                        act.dma_start(xb[h][:, :], xs_d[bass.ds((i * 2 + (h + 2)) * P, P), :]).then_inc(s(f"xb{h}"), 16)

            for h in range(2):
                n = act.value_load(uses_i[0:1, h:h + 1], min_val=1, max_val=NB // 2)
                act.wait_ge(s(f"xb{h}"), n * 16 + 16)
                act.nop(nofuse=True)

        @block.vector
        def _(dve):
            def wide(ap):
                return ap.unsqueeze(2).to_broadcast([TP, NT, NE])

            steps = Steps(dve, s("dve"))
            st.credit(dve, "y_taken0", "y_taken1")
            steps(nc.vector.memset(all16[:, :], 1.0))
            steps(nc.vector.tensor_scalar(lower[:, :], m.iota16[0:TP, 0:TP], m.pcol[0:TP, :], None, ALU.is_gt), s("lower"))
            norm_vector(nc, m, dve, st, steps)
            dve.wait_ge(s("scores"), NT)
            steps.do(nc.vector.tensor_copy(score[:, :, :], m.ps[0:TP, 3, 0:NT * NE].rearrange("p (t e) -> p t e", t=NT)))
            iota = m.iota[0:TP, 0:NE].unsqueeze(1).to_broadcast([TP, NT, NE])
            src = score
            for j in range(2):
                steps.do(nc.vector.tensor_reduce(top[:, j, :], src[:, :, :], AX.X, ALU.max))
                steps.do(nc.vector.tensor_tensor(low[:, :, :], src[:, :, :], wide(top[:, j, :]), ALU.is_equal))
                steps.do(nc.vector.tensor_scalar(low[:, :, :], low[:, :, :], -1000.0, None, ALU.mult))
                steps.do(nc.vector.tensor_tensor(low[:, :, :], low[:, :, :], iota, ALU.add))
                steps.do(nc.vector.tensor_reduce(top[:, 4 + j, :], low[:, :, :], AX.X, ALU.min))
                steps.do(nc.vector.tensor_tensor(pick[:, j, :, :], low[:, :, :], wide(top[:, 4 + j, :]), ALU.is_equal))
                if j == 0:
                    steps.do(nc.vector.tensor_scalar(low[:, :, :], pick[:, 0, :, :], -1e30, None, ALU.mult))
                    steps.do(nc.vector.tensor_tensor(left[:, :, :], score[:, :, :], low[:, :, :], ALU.add))
                    src = left
            steps(nc.vector.tensor_tensor(chosen[:, :, :], pick[:, 0, :, :], pick[:, 1, :, :], ALU.add), s("chosen"))
            steps(nc.vector.tensor_tensor(top[:, 2, :], top[:, 1, :], top[:, 0, :], ALU.subtract), s("exp_in"))
            dve.wait_ge(s("ranked"), 1)
            nodes = m.ps[0:TP, 7, 0:NE]
            steps.do(nc.vector.tensor_scalar(blocks[:, :], nodes, 0.5, None, ALU.is_ge))
            for k in range(1, NT):
                steps.do(nc.vector.scalar_tensor_tensor(blocks[:, :], nodes, k * P + 0.5, blocks[:, :], ALU.is_ge, ALU.add))
            src, d = blocks, 1
            while d < NE:
                dst = ends[1] if src is ends[0] else ends[0]
                steps(nc.vector.tensor_copy(dst[:, 0:d], src[:, 0:d]))
                steps.do(nc.vector.tensor_tensor(dst[:, d:NE], src[:, d:NE], src[:, 0:NE - d], ALU.add))
                src, d = dst, 2 * d
            end = src
            steps.do(nc.vector.tensor_tensor(first[:, :], end[:, :], blocks[:, :], ALU.subtract))
            steps.do(nc.vector.scalar_tensor_tensor(low[:, :, :], first[:, :].unsqueeze(1).to_broadcast([TP, NT, NE]), float(P),
                                                    m.ps[0:TP, 6, 0:NT * NE].rearrange("p (t e) -> p t e", t=NT), ALU.mult, ALU.add))
            for j in range(2):
                steps(nc.vector.tensor_tensor(at[:, j, :, :], pick[:, j, :, :], low[:, :, :], ALU.mult))
            steps.settle()
            steps.do(nc.vector.tensor_reduce(slot[:, :, :], at[:, :, :, :], AX.X, ALU.add))
            steps(nc.vector.tensor_copy(slot_i[:, :, :], slot[:, :, :]), s("slots"))
            steps.do(nc.vector.tensor_tensor(after[:, :, :], m.iota[0:1, 0:NB].unsqueeze(2).to_broadcast([1, NB, NE]),
                                             end[0:1, :].unsqueeze(1).to_broadcast([1, NB, NE]), ALU.is_ge))
            steps.do(nc.vector.tensor_reduce(owner[:, :], after[:, :, :], AX.X, ALU.add))
            steps(nc.vector.tensor_scalar(info[:, :], owner[:, :], float(NE - 1), None, ALU.min))
            steps.do(nc.vector.tensor_scalar(owner[:, :], owner[:, :], NE - 0.5, None, ALU.is_lt))
            steps.do(nc.vector.scalar_tensor_tensor(info[:, :], owner[:, :], float(NE), info[:, :], ALU.mult, ALU.add))
            pair = info[:, :].rearrange("p (i h) -> p i h", h=2)
            steps.do(nc.vector.scalar_tensor_tensor(info2[:, :], pair[:, :, 1], float(2 * NE), pair[:, :, 0], ALU.mult, ALU.add))
            steps(nc.vector.tensor_copy(table[:, :], info2[:, :]))
            steps.do(nc.vector.tensor_reduce(uses[:, :], owner[:, :].rearrange("p (i h) -> p h i", h=2), AX.X, ALU.add))
            steps.do(nc.vector.tensor_copy(uses_i[:, :], uses[:, :]), s("tables"))
            dve.wait_ge(s("exp_out"), 1)
            steps.do(nc.vector.tensor_scalar(top[:, 6, :], top[:, 3, :], 1.0, None, ALU.add))
            steps.do(nc.vector.reciprocal(top[:, 7, :], top[:, 6, :]))
            steps.do(nc.vector.tensor_tensor(top[:, 6, :], top[:, 3, :], top[:, 7, :], ALU.mult))
            steps.do(nc.vector.tensor_tensor(low[:, :, :], pick[:, 0, :, :], wide(top[:, 7, :]), ALU.mult))
            steps.do(nc.vector.tensor_tensor(left[:, :, :], pick[:, 1, :, :], wide(top[:, 6, :]), ALU.mult))
            steps(nc.vector.tensor_tensor(gate[:, :, :], low[:, :, :], left[:, :, :], ALU.add), s("gate"))

            def turned(i, h, more):
                dve.wait_ge(s(f"x_turned{h}"), i + (more + 1))
                nc.vector.tensor_copy(xT[h][:, :, :], m.ps[:, h, 0:KC * P].rearrange("p (k n) -> p k n", k=KC))\
                    .then_inc(s(f"xT{h}"), 1)

            dve.wait_ge(s("acc"), NT)
            for t in range(NT):
                steps(nc.vector.tensor_tensor(acc[:, t, :], acc[:, t, :], m.xn[:, t, :], ALU.add))
            turned(0, 0, 1)
            with dve.Fori(0, NB // 2) as i:
                word = turn_of(dve, i)
                for h in range(2):
                    with dve.If(used(word, h)):
                        turned(i, 1 - h, h + 1)
                        dve.wait_ge(s(f"y_made{h}"), i + 2)
                        dve.wait_ge(s(f"yb_free{h}"), i + 1)
                        nc.vector.tensor_copy(yb[h][:, :], m.ps[:, 6 + h, 0:C]).then_inc(s(f"y_taken{h}"), 1)

            def weigh(t):
                dve.wait_ge(s(f"yg{t}"), 32)
                for j in range(2):
                    steps.do(nc.vector.scalar_tensor_tensor(acc[:, t, :], yg[:, j, t, :], top[:, 7 - j, t:t + 1], acc[:, t, :],
                                                            ALU.mult, ALU.add))

            norm_tail(nc, m, dve, s, steps, acc, z, "L2_ffn_gamma", "L2_ffn_beta", make=weigh)

        @block.tensor
        def _(pe):
            st.credit(pe, *[f"{n}{h}" for n in ("x_turned", "h_made0", "h_made1", "y_made") for h in range(2)])
            norm_tensor(nc, m, pe, st)
            gate_tensor(nc, m, pe, s, wr, NE, "L2_ffn_gate_b", b2)
            pe.wait_ge(s("lower"), 1)
            pe.wait_ge(s("chosen"), 1)
            for t in range(NT):
                for u in range(t + 1):
                    nc.tensor.matmul(m.ps[0:TP, 6, t * NE:(t + 1) * NE], (lower if u == t else all16)[:, :], chosen[:, u, :],
                                     start=u == 0, stop=u == t)
            for u in range(NT):
                ins = nc.tensor.matmul(m.ps[0:TP, 7, 0:NE], all16[:, :], chosen[:, u, :], start=u == 0, stop=u == NT - 1)
            ins.then_inc(s("ranked"), 1)
            pe.wait_ge(s("slots"), 1)
            gate_turn(nc, m, pe, s, gate, gateT, NE, b2)
            pe.wait_ge(s("acc"), NT)

            def turn(i, h, more):
                pe.wait_ge(s(f"xb{h}"), i * 16 + 16 * more)
                for k in range(KC):
                    ins = nc.tensor.transpose(m.ps[:, h, k * P:(k + 1) * P], xb[h][:, k * P:(k + 1) * P], m.ident[:, :])
                ins.then_inc(s(f"x_turned{h}"), 1)

            turn(0, 0, 1)
            with pe.Fori(0, NB // 2) as i:
                word = turn_of(pe, i)
                for h in range(2):
                    with pe.If(used(word, h)):
                        pe.wait_ge(s(f"w0{h}"), (i + 1) * 16)
                        pe.wait_ge(s(f"xT{h}"), i + 1)
                        pe.wait_ge(s(f"hT{h}"), i * 4 + 1)
                        for c in range(4):
                            for k in range(KC):
                                ins = nc.tensor.matmul(m.ps[:, 2 + c // 2 * 2 + h, (c % 2) * P:(c % 2 + 1) * P],
                                                       w1[h][:, (k * 4 + c) * P:(k * 4 + c + 1) * P], xT[h][:, k, :],
                                                       start=k == 0, stop=k == KC - 1)
                            if c % 2:
                                ins.then_inc(s(f"h_made{c // 2}{h}"), 1)
                        turn(i, 1 - h, h + 1)
                        pe.wait_ge(s(f"w1{h}"), (i + 1) * 16)
                        pe.wait_ge(s(f"y_taken{h}"), i + 1)
                        for c in range(4):
                            pe.wait_ge(s(f"hT{h}"), i * 4 + (c + 2))
                            ins = nc.tensor.matmul(m.ps[:, 6 + h, 0:C], hT[h][:, c, :], w2[h][:, c * C:(c + 1) * C],
                                                   start=c == 0, stop=c == 3)
                        ins.then_inc(s(f"y_made{h}"), 1)


def norm_tail(nc, m, dve, s, steps, z, other, gamma, beta, extra=None, make=None):
    for t in range(NT):
        if make:
            make(t)
        steps(nc.vector.bn_stats(m.stats[:, t, :], z[:, t, :]))
    steps.settle()
    for t in range(NT):
        steps(nc.vector.bn_aggr(m.mv[:, t, :], m.stats[:, t, :]), s("z_stats"))
    for t in range(NT):
        steps(nc.vector.tensor_tensor(m.x[:, t, :], m.x[:, t, :], m.row(beta), ALU.add))
    steps.settle()
    for t in range(NT):
        if extra is not None:
            steps(nc.vector.tensor_tensor(m.x[:, t, :], m.x[:, t, :], extra[:, t, :], ALU.add))
        steps(nc.vector.scalar_tensor_tensor(other[:, t, :], z[:, t, :], m.mv[:, t, 0:1], m.row(gamma), ALU.subtract, ALU.mult))
    steps.settle()
    dve.wait_ge(s("z_rstd"), 1)
    for t in range(NT):
        steps(nc.vector.scalar_tensor_tensor(m.x[:, t, :], other[:, t, :], m.rstd[0:TP, t:t + 1], m.x[:, t, :],
                                             ALU.mult, ALU.add))
    steps.settle()



def l3_gnn(nc, m, A):
    with ExitStack() as ctx:
        st = Stage(nc, ctx, "l3g")
        s, sb = st.sem, st.sb
        W = sb("W", [P, 1024])
        wl = W[:, 0:512].rearrange("p (k n) -> p k n", k=KC)
        wr = W[:, 512:1024].rearrange("p (k n) -> p k n", k=KC)
        rdeg = sb("rdeg", [P, N])
        aggT = sb("aggT", [P, KC, N])
        f = sb("f", [TP, NT, C])
        g = sb("g", [TP, NT, C])
        block = ctx.enter_context(nc.Block())

        @block.sync
        def _(sp):
            sp.dma_start(W[:, 0:1024], A["w_l3g"]).then_inc(s("w"), 16)

        @block.gpsimd
        def _(pool):
            steps = Steps(pool, s("pool"))
            norm_pool(nc, m, pool, st, steps)
            pool.wait_ge(s("z_stats"), NT)
            steps.do(nc.gpsimd.tensor_scalar(m.veps[0:TP, :], m.mv[:, :, 1], 1e-5, None, ALU.add))
            steps(nc.gpsimd.tensor_tensor(m.rstd[0:TP, :], m.veps[0:TP, :], m.mhalf[0:TP, 0:NT], ALU.pow), s("z_rstd"))

        @block.scalar
        def _(act):
            norm_scalar(nc, m, act, st)
            for t in range(NT):
                act.wait_ge(s("f_made"), t + 1)
                nc.scalar.activation(f[:, t, :], m.ps[0:TP, t, 0:C], ACT.Gelu).then_inc(s("f"), 1)

        @block.vector
        def _(dve):
            steps = Steps(dve, s("dve"))
            norm_vector(nc, m, dve, st, steps)
            for n, (a, b) in enumerate(HALF):
                dve.wait_ge(s("deg_made"), n + 1)
                steps.do(nc.vector.tensor_scalar(rdeg[:, a:b], m.ps[:, 3 + n, 0:b - a], 1.0, None, ALU.max))
            steps.do(nc.vector.reciprocal(rdeg[:, :], rdeg[:, :]))
            unit = 0
            for c in range(KC):
                for (a, b) in HALF:
                    dve.wait_ge(s("agg_made"), unit + 1)
                    steps(nc.vector.tensor_tensor(aggT[:, c, a:b], m.ps[:, 3 + unit, 0:b - a], rdeg[:, a:b], ALU.mult), s("aggT"))
                    unit += 1
            dve.wait_ge(s("f"), NT)
            norm_tail(nc, m, dve, s, steps, f, g, "L3_gnn_ln_gamma", "L3_gnn_ln_beta", extra=m.xn)

        @block.tensor
        def _(pe):
            for n, (a, b) in enumerate(HALF):
                for t in range(NT):
                    ins = nc.tensor.matmul(m.ps[:, 3 + n, 0:b - a], m.ones[0:TP, :], m.count[:, t, a:b], start=t == 0,
                                           stop=t == NT - 1)
                ins.then_inc(s("deg_made"), 1)
            norm_tensor(nc, m, pe, st)
            pe.wait_ge(s("dve"), NT + 2)
            unit = 0
            for c in range(KC):
                for (a, b) in HALF:
                    for t in range(NT):
                        ins = nc.tensor.matmul(m.ps[:, 3 + unit, 0:b - a], m.xn[:, t, c * P:(c + 1) * P], m.count[:, t, a:b],
                                               start=t == 0, stop=t == NT - 1)
                    ins.then_inc(s("agg_made"), 1)
                    unit += 1
            pe.wait_ge(s("w"), 16)
            pe.wait_ge(s("xnT_done"), XNT)
            pe.wait_ge(s("aggT"), 4)
            for t in range(NT):
                cols = slice(t * TP, (t + 1) * TP)
                parts = [(aggT[:, k, cols], wl[:, k, :]) for k in range(KC)] + [(m.xnT[:, k, cols], wr[:, k, :]) for k in range(KC)] + \
                    [(m.ones[0:1, 0:TP], m.row("L3_gnn_b_l", 1))]
                for j, (lhsT, rhs) in enumerate(parts):
                    ins = nc.tensor.matmul(m.ps[0:TP, t, 0:C], lhsT, rhs, start=j == 0, stop=j == len(parts) - 1)
                ins.then_inc(s("f_made"), 1)



def l3_ffn(nc, m, A):
    NH, D, G = 8, 64, 64
    SCALE = D ** -0.5
    with ExitStack() as ctx:
        st = Stage(nc, ctx, "l3f")
        s, sb = st.sem, st.sb
        wbig = sb("wbig", [P, 1024])
        w64 = sb("w64", [D, 2048 + 4 * D + NH])
        wfx = wbig[:, 0:1024].rearrange("p (k n) -> p k n", k=KC)
        wxT = w64[:, 0:2048].rearrange("p (h c) -> p h c", h=NH)
        small = w64[:, 2048:2048 + 4 * D + NH]
        wsl, wq, wk, wv = [small[:, D * i:D * (i + 1)] for i in range(4)]
        bxT = small[:, 4 * D:4 * D + NH]
        itemp = sb("itemp", [P, NH])
        wc = sb("wc", [P, KC, NH, G])
        bc = sb("bc", [1, NH, G])
        sw = sb("sw", [TP, NT, NH, G])
        mx = sb("mx", [TP, NT, NH])
        rs = sb("rs", [TP, NT, NH])
        zT = sb("zT", [P, KC, NH * G])
        norm = sb("norm", [G, NH * G])
        rnorm = sb("rnorm", [G, NH * G])
        tokT = sb("tokT", [D, NH * G])
        qT = sb("qT", [D, NH * G])
        kT = sb("kT", [D, NH * G])
        v = sb("v", [G, NH, D])
        at = sb("at", [G, NH, G])
        amx = sb("amx", [G, NH])
        atT = sb("atT", [G, NH, G])
        osT = sb("osT", [P, NH // 2, P])
        pw = sb("pw", [P, NH // 2, C])
        swT = sb("swT", [P, NH // 2, N])
        wout = sb("wout", [P, NH // 2, C])
        block = ctx.enter_context(nc.Block())

        @block.sync
        def _(sp):
            sp.dma_start(wbig[:, :], A["l3f_wfx"]).then_inc(s("w"), 16)
            sp.dma_start(w64[:, :], A["l3f_w64"]).then_inc(s("w"), 16)
            sp.dma_start(wout[:, :, :], A["l3f_wout"].rearrange("p (j c) -> p j c", j=NH // 2)).then_inc(s("wout"), 16)

        @block.gpsimd
        def _(pool):
            steps = Steps(pool, s("pool"))
            steps(nc.gpsimd.memset(osT[:, :, :], 0.0), s("osT_clear"))
            norm_pool(nc, m, pool, st, steps)

        @block.scalar
        def _(act):
            norm_scalar(nc, m, act, st)
            for t in range(NT):
                act.wait_ge(s("sw_in"), t + 1)
                nc.scalar.activation(sw[:, t, :, :], sw[:, t, :, :], ACT.Exp).then_inc(s("sw_exp"), 1)
            for j in range(2):
                act.wait_ge(s("qk_made"), j + 1)
                nc.scalar.activation((qT, kT)[j][:, :], m.ps[0:D, 2 + j, :], ACT.Copy).then_inc(s("qk"), 1)
            act.wait_ge(s("v_made"), 1)
            nc.scalar.activation(v[:, :, :], m.ps[0:G, 4, :].rearrange("p (h d) -> p h d", h=NH), ACT.Copy).then_inc(s("v"), 1)
            for j in range(NH // 2):
                for n in range(2):
                    act.wait_ge(s("sw_turned"), 2 * j + n + 1)
                    a, b = ((0, 4 * TP), (4 * TP, N))[n]
                    nc.scalar.activation(swT[:, j, a:b], m.ps[:, 6 + n, 0:b - a], ACT.Copy).then_inc(s("swT"), 1)
            act.wait_ge(s("at_in"), 1)
            nc.scalar.activation(at[:, :, :], at[:, :, :], ACT.Exp, scale=SCALE).then_inc(s("at_exp"), 1)
            act.wait_ge(s("atT_made"), 1)
            nc.scalar.activation(atT[:, :, :], m.ps[0:G, 0, :].rearrange("p (h d) -> p h d", h=NH), ACT.Copy).then_inc(s("atT"), 1)
            act.wait_ge(s("osT_made"), 1)
            act.wait_ge(s("osT_clear"), 1)
            for r in range(2):
                rows = slice(r * D, (r + 1) * D)
                heads = m.ps[rows, 1, :].rearrange("p (j r g) -> p j r g", r=2, g=G)
                nc.scalar.activation(osT[rows, :, rows], heads[:, :, r, :], ACT.Copy).then_inc(s("osT"), 1)
            for j in range(NH // 2):
                act.wait_ge(s("pw_made"), j + 1)
                nc.scalar.activation(pw[:, j, :], m.ps[:, 2 + j, 0:C], ACT.Copy).then_inc(s("pw"), 1)

        @block.vector
        def _(dve):
            steps = Steps(dve, s("dve"))
            steps.do(nc.vector.tensor_scalar(itemp[:, :], m.row("L3_ffn_temperature", P), 0.1, 5.0, ALU.max, ALU.min))
            steps.do(nc.vector.reciprocal(itemp[:, :], itemp[:, :]))
            for c in range(KC):
                dve.wait_ge(s("wc_made"), c + 1)
                steps(nc.vector.tensor_tensor(wc[:, c, :, :], m.ps[:, 3 + c, :].rearrange("p (h g) -> p h g", h=NH),
                                              itemp[:, :].unsqueeze(2).to_broadcast([P, NH, G]), ALU.mult), s("wc"))
            dve.wait_ge(s("bc_made"), 1)
            steps.do(nc.vector.tensor_tensor(bc[:, :, :], m.ps[0:1, 5, :].rearrange("p (h g) -> p h g", h=NH),
                                             m.row("L3_ffn_b_slice", 1).unsqueeze(1).to_broadcast([1, NH, G]), ALU.add))
            steps(nc.vector.tensor_tensor(bc[:, :, :], bc[:, :, :], itemp[0:1, :].unsqueeze(2).to_broadcast([1, NH, G]),
                                          ALU.mult), s("wc"))
            norm_vector(nc, m, dve, st, steps)
            for t in range(NT):
                dve.wait_ge(s("logits"), t + 1)
                lg = m.ps[0:TP, (3, 4, 5, 6, 7)[t], :].rearrange("p (h g) -> p h g", h=NH)
                steps.do(nc.vector.tensor_reduce(mx[:, t, :], lg, AX.X, ALU.max))
                steps(nc.vector.tensor_tensor(sw[:, t, :, :], lg, mx[:, t, :].unsqueeze(2).to_broadcast([TP, NH, G]),
                                              ALU.subtract), s("sw_in"))
            for t in range(NT):
                dve.wait_ge(s("sw_exp"), t + 1)
                steps.do(nc.vector.tensor_reduce(mx[:, t, :], sw[:, t, :, :], AX.X, ALU.add))
                steps.do(nc.vector.reciprocal(rs[:, t, :], mx[:, t, :]))
                steps(nc.vector.tensor_tensor(sw[:, t, :, :], sw[:, t, :, :], rs[:, t, :].unsqueeze(2).to_broadcast([TP, NH, G]),
                                              ALU.mult), s("sw"))
            dve.wait_ge(s("norm_made"), 1)
            steps(nc.vector.tensor_copy(norm[:, :], m.ps[0:G, 2, :]), s("norm"))
            steps.settle()
            steps.do(nc.vector.tensor_scalar(rnorm[:, :], norm[:, :], 1e-5, None, ALU.add))
            steps.do(nc.vector.reciprocal(rnorm[:, :], rnorm[:, :]))
            for c in range(KC):
                dve.wait_ge(s("z_made"), c + 1)
                steps(nc.vector.tensor_copy(zT[:, c, :], m.ps[:, c, :]), s("zT"))
            dve.wait_ge(s("tok_made"), 1)
            steps(nc.vector.tensor_tensor(tokT[:, :], m.ps[0:D, 5, :], rnorm[:, :], ALU.mult), s("tokT"))
            dve.wait_ge(s("att_made"), 1)
            lg = m.ps[0:G, 5, :].rearrange("p (h g) -> p h g", h=NH)
            steps.do(nc.vector.tensor_reduce(amx[:, :], lg, AX.X, ALU.max))
            steps(nc.vector.tensor_tensor(at[:, :, :], lg, amx[:, :].unsqueeze(2).to_broadcast([G, NH, G]), ALU.subtract), s("at_in"))
            dve.wait_ge(s("at_exp"), 1)
            steps.do(nc.vector.tensor_reduce(amx[:, :], at[:, :, :], AX.X, ALU.add))
            steps.do(nc.vector.reciprocal(amx[:, :], amx[:, :]))
            steps(nc.vector.tensor_tensor(at[:, :, :], at[:, :, :], amx[:, :].unsqueeze(2).to_broadcast([G, NH, G]), ALU.mult), s("at"))
            for t in range(NT):
                dve.wait_ge(s("out_made"), t + 1)
                steps(nc.vector.tensor_tensor(m.x[:, t, :], m.x[:, t, :], m.ps[0:TP, (6, 7, 0, 1, 2)[t], 0:C], ALU.add))
            steps.settle()

        @block.tensor
        def _(pe):
            pe.wait_ge(s("w"), 32)
            for c in range(KC):
                for h in range(NH):
                    ins = nc.tensor.matmul(m.ps[:, 3 + c, h * G:(h + 1) * G], wxT[:, h, c * P:(c + 1) * P], wsl, start=True, stop=True)
                ins.then_inc(s("wc_made"), 1)
            for h in range(NH):
                ins = nc.tensor.matmul(m.ps[0:1, 5, h * G:(h + 1) * G], bxT[:, h:h + 1], wsl, start=True, stop=True)
            ins.then_inc(s("bc_made"), 1)
            norm_tensor(nc, m, pe, st)
            pe.wait_ge(s("xnT_done"), XNT)
            pe.wait_ge(s("wc"), 3)
            for t in range(NT):
                b = (3, 4, 5, 6, 7)[t]
                for k in range(KC):
                    nc.tensor.matmul(m.ps[0:TP, b, :], m.xnT[:, k, t * TP:(t + 1) * TP], wc[:, k, :, :].rearrange("p h g -> p (h g)"),
                                     start=k == 0, stop=False)
                nc.tensor.matmul(m.ps[0:TP, b, :], m.ones[0:1, 0:TP], bc[:, :, :].rearrange("p h g -> p (h g)"), start=False,
                                 stop=True).then_inc(s("logits"), 1)
            for t in range(NT):
                pe.wait_ge(s("sw"), t + 1)
                w = sw[:, t, :, :].rearrange("p h g -> p (h g)")
                ins0 = nc.tensor.matmul(m.ps[0:G, 2, :], m.ones[0:TP, 0:G], w, start=t == 0, stop=t == NT - 1)
                for c in range(KC):
                    ins = nc.tensor.matmul(m.ps[:, c, :], m.xn[:, t, c * P:(c + 1) * P], w, start=t == 0, stop=t == NT - 1)
                    if t == NT - 1:
                        ins.then_inc(s("z_made"), 1)
                if t == NT - 1:
                    ins0.then_inc(s("norm_made"), 1)
            pe.wait_ge(s("norm"), 1)
            pe.wait_ge(s("zT"), KC)
            for h in range(NH):
                o = m.ps[0:D, 5, h * G:(h + 1) * G]
                for k in range(KC):
                    nc.tensor.matmul(o, wfx[:, k, h * D:(h + 1) * D], zT[:, k, h * G:(h + 1) * G], start=k == 0, stop=False)
                ins = nc.tensor.matmul(o, m.row("L3_ffn_b_fx", 1)[:, h * D:(h + 1) * D], norm[0:1, h * G:(h + 1) * G], start=False,
                                       stop=True)
            ins.then_inc(s("tok_made"), 1)
            pe.wait_ge(s("tokT"), 1)
            for j, wt in enumerate((wq, wk)):
                nc.tensor.matmul(m.ps[0:D, 2 + j, :], wt, tokT[:, :], start=True, stop=True).then_inc(s("qk_made"), 1)
            for h in range(NH):
                ins = nc.tensor.matmul(m.ps[0:G, 4, h * D:(h + 1) * D], tokT[:, h * G:(h + 1) * G], wv, start=True, stop=True)
            ins.then_inc(s("v_made"), 1)
            pe.wait_ge(s("qk"), 2)
            for h in range(NH):
                hg = slice(h * G, (h + 1) * G)
                ins = nc.tensor.matmul(m.ps[0:G, 5, hg], qT[:, hg], kT[:, hg], start=True, stop=True)
            ins.then_inc(s("att_made"), 1)
            for j in range(NH // 2):
                for t in range(NT):
                    b, c = (6, t * TP) if t < 4 else (7, 0)
                    if t in (0, 4) and j:
                        pe.wait_ge(s("swT"), 2 * j - 1 + (t == 4))
                    ins = nc.tensor.transpose(m.ps[:, b, c:c + TP], sw[:, t, 2 * j:2 * j + 2, :].rearrange("p r g -> p (r g)"),
                                              m.ident[0:TP, 0:TP])
                    if t >= 3:
                        ins.then_inc(s("sw_turned"), 1)
            pe.wait_ge(s("at"), 1)
            for h in range(NH):
                ins = nc.tensor.transpose(m.ps[0:G, 0, h * G:(h + 1) * G], at[:, h, :], m.ident[0:G, 0:G])
            ins.then_inc(s("atT_made"), 1)
            pe.wait_ge(s("atT"), 1)
            pe.wait_ge(s("v"), 1)
            for h in range(NH):
                pair = v[:, h // 2 * 2:h // 2 * 2 + 2, :].rearrange("p r d -> p (r d)")
                ins = nc.tensor.matmul(m.ps[:, 1, h * G:(h + 1) * G], pair, atT[:, h, :], start=True, stop=True)
            ins.then_inc(s("osT_made"), 1)
            pe.wait_ge(s("osT"), 2)
            pe.wait_ge(s("wout"), 16)
            for j in range(NH // 2):
                nc.tensor.matmul(m.ps[:, 2 + j, 0:C], osT[:, j, :], wout[:, j, :], start=True, stop=True).then_inc(s("pw_made"), 1)
            pe.wait_ge(s("pw"), NH // 2)
            pe.wait_ge(s("swT"), NH)
            for t in range(NT):
                b = (6, 7, 0, 1, 2)[t]
                for j in range(NH // 2):
                    nc.tensor.matmul(m.ps[0:TP, b, 0:C], swT[:, j, t * TP:(t + 1) * TP], pw[:, j, :], start=j == 0, stop=False)
                nc.tensor.matmul(m.ps[0:TP, b, 0:C], m.ones[0:1, 0:TP], m.row("L3_ffn_b_out", 1), start=False, stop=True)\
                    .then_inc(s("out_made"), 1)


LAYERS = [l0_gnn, l0_ffn, l1_gnn, l1_ffn, l2_gnn, l2_ffn, l3_gnn, l3_ffn]


def build(nc, A, out, upto=99):
    with ExitStack() as ctx:
        m = Memory(nc, ctx)
        setup(nc, m, A)
        edges(nc, m, A)
        for layer in LAYERS[:upto]:
            layer(nc, m, A)
        with ExitStack() as last:
            done = last.enter_context(nc.semaphore("stored"))
            block = last.enter_context(nc.Block())

            @block.sync
            def _(sp):
                sp.dma_start(out.rearrange("(t p) c -> p t c", p=TP), m.x[:, :, :]).then_inc(done, 16)
                sp.wait_ge(done, 16)



def chunks(w):
    return w.reshape(-1, P, w.shape[-1]).transpose(1, 0, 2).reshape(P, -1)


def laid_out(inputs):
    a = {k: np.asarray(v) for k, v in inputs.items()}
    out = {n: a[n] for n in ["x", "edge_attr_256", "edge_attr_128", "L0_gnn_w_f1b"]}
    cols = []
    for n in COLS:
        v = a[n].reshape(-1, P)
        cols.append(v.T)
    out["cols"] = np.concatenate(cols, axis=1)
    out["rows"] = np.concatenate([a[n].reshape(-1) for n in ROWS])
    out["w_f1aT"] = a["L0_gnn_w_f1a"].T
    out["featT"] = a["edge_attr_54"].T
    out["src_t"] = a["src"].reshape(ET, TP).T
    out["dst_t"] = a["dst"].reshape(ET, TP).T
    g = lambda n: a["L0_gnn_" + n]
    out["w_l0g"] = np.concatenate([chunks(g(n)) for n in ["c1_wl", "c1_wr", "c2_wl", "c2_wr", "lin1_w", "lin2_w", "cat_w"]], axis=1)
    out["dst"] = a["dst"]
    out["wn"] = chunks(a["L1_gnn_Wn"])
    out["wnT"] = chunks(a["L1_gnn_Wn"].T)
    out["we_be"] = chunks(np.concatenate([a["L1_gnn_We"], a["L1_gnn_be"][:, None]], axis=1))
    out["l1f_wr"] = chunks(a["L1_ffn_Wr"])
    out["L1_ffn_bo"] = a["L1_ffn_bo"]
    out["l1f_w"] = np.stack([np.stack([chunks(a["L1_ffn_" + n][e]) for n in ("W1", "W2", "Wo")]) for e in range(8)])
    fc = a["L2_gnn_Wfc"]
    fc = np.concatenate([fc, np.zeros((512 - fc.shape[0], fc.shape[1]), fc.dtype)])
    out["w_l2g"] = np.concatenate([chunks(a["L2_gnn_W1"]), chunks(fc), a["L2_gnn_W2"]], axis=1)
    out["l2g_small"] = np.stack([a["L2_gnn_" + n] for n in ("b2", "g2", "be2")], axis=1)
    out["l2f_wr"] = chunks(a["L2_ffn_gate_w"])
    out["L2_ffn_b2"] = a["L2_ffn_b2"]
    out["l2f_w"] = np.stack([np.stack([chunks(a["L2_ffn_" + n][e]) for n in ("w1", "w2")]) for e in range(16)])
    out["w_l3g"] = np.concatenate([chunks(a["L3_gnn_W_l"].T), chunks(a["L3_gnn_W_r"].T)], axis=1)
    f = lambda n: a["L3_ffn_" + n]
    heads = lambda w: w.reshape(8, 64, C).transpose(1, 0, 2).reshape(64, -1)
    out["l3f_wfx"] = chunks(f("W_fx"))
    out["l3f_w64"] = np.concatenate([heads(f("W_x").T), f("W_slice"), f("W_q"), f("W_k"), f("W_v"),
                                     f("b_x").reshape(8, 64).T], axis=1)
    out["l3f_wout"] = chunks(f("W_out"))
    out["l0f_wr"] = chunks(a["L0_ffn_Wr"])
    out["L0_ffn_b2"] = a["L0_ffn_b2"]
    out["l0f_experts"] = np.concatenate(
        [np.concatenate([chunks(a["L0_ffn_W1"][e]), chunks(a["L0_ffn_W2"][e]), a["L0_ffn_b1"][e].reshape(4, P).T], axis=1)
         for e in range(8)], axis=0)
    return {k: np.ascontiguousarray(v) for k, v in out.items()}


def kernel(**inputs):
    import concourse.bacc as bacc
    from concourse.bass_utils import run_bass_kernel_spmd

    nc = bacc.Bacc("TRN2", target_bir_lowering=False, num_devices=1)
    arrays = laid_out(inputs)
    A = {n: nc.dram_tensor("in_" + n, a.shape, mybir.dt.from_np(a.dtype), kind="ExternalInput").ap()
         for n, a in arrays.items()}
    out = nc.dram_tensor("out_x", (N, C), F32, kind="ExternalOutput").ap()
    build(nc, A, out)
    r = run_bass_kernel_spmd(nc, [{"in_" + n: a for n, a in arrays.items()}], core_ids=[0])
    return r.results[0]["out_x"]
```
